# Optimizing a Trainium2 kernel written in Bass

```python
import numpy as np
import jax
import jax.numpy as jnp

def _softmax(x, axis=-1):
    return jax.nn.softmax(x, axis=axis)

def _gelu(x):
    return jax.nn.gelu(x, approximate=True)

def _silu(x):
    return jax.nn.silu(x)

def _sigmoid(x):
    return jax.nn.sigmoid(x)

def _layernorm(x, axis=-1, eps=1e-05):
    m = jnp.mean(x, axis=axis, keepdims=True)
    v = jnp.var(x, axis=axis, keepdims=True)
    return (x - m) / jnp.sqrt(v + eps)

def _scatter_add(tgt, idx, src, axis=0):
    return tgt.at[idx].add(src)

def _segment_sum(src, seg, n):
    return jax.ops.segment_sum(src, seg, n)
kernel_name = 'mk_decoder_preln_d4_seqx_r8_9fa614'

def setup_inputs(seed: int=0):
    np.random.seed(seed)
    _w = jnp.asarray

    def _rec_inputs():
        import jax
        import jax.numpy as jnp
        _rk = jax.random.key(seed)
        x = -9.806e-05 + 1 * jax.random.normal(jax.random.fold_in(_rk, 1), (8, 100, 128), jnp.float32)
        _lenS = 100 - jax.random.randint(jax.random.fold_in(_rk, 7), (8,), 0, max(1, 100 // 4) + 1, jnp.int32)
        _lenS2 = 1444 - jax.random.randint(jax.random.fold_in(_rk, 8), (8,), 0, max(1, 1444 // 4) + 1, jnp.int32)
        _ctx_1024P = jax.random.normal(jax.random.fold_in(_rk, 11), (8, 16, 128), jnp.float32)
        _ctx_1024c = jax.random.dirichlet(jax.random.fold_in(_rk, 511), 0.3 * jnp.ones((16,), jnp.float32), (8, 1444))
        _ctx_1024t = jnp.einsum('bsk,bkd->bsd', _ctx_1024c, _ctx_1024P)
        _ctx_1024t = _ctx_1024t * jax.lax.rsqrt(jnp.mean(jnp.square(_ctx_1024t)) + 1e-12) * 0.953939
        ctx_1024 = -1.52775e-05 + 0.999936 * (_ctx_1024t + 0.3 * jax.random.normal(jax.random.fold_in(_rk, 611), (8, 1444, 128), jnp.float32))
        return (x, ctx_1024)
    x, ctx_1024 = _rec_inputs()

    def _L0_attn_setup():
        import jax, jax.numpy as jnp
        import numpy as np
        EMBED = 128
        WIN = 128
        NUM_HEADS = 16
        HQ = 16
        HKV = 4
        HEAD_DIM = EMBED // NUM_HEADS
        G = HQ // HKV
        key = jax.random.key(seed)
        k = jax.random.split(key, 5)
        B, S = (1, 256)
        x = jax.random.normal(k[0], (B, S, EMBED), dtype=jnp.float32)
        Wq = jax.random.normal(k[1], (HQ * HEAD_DIM, EMBED), dtype=jnp.float32) * 0.02
        Wk = jax.random.normal(k[2], (HKV * HEAD_DIM, EMBED), dtype=jnp.float32) * 0.02
        Wv = jax.random.normal(k[3], (HKV * HEAD_DIM, EMBED), dtype=jnp.float32) * 0.02
        Wo = jax.random.normal(k[4], (EMBED, HQ * HEAD_DIM), dtype=jnp.float32) * 0.02
        return {'x': x, 'Wq': Wq, 'Wk': Wk, 'Wv': Wv, 'Wo': Wo}
    _L0_attn_all = _L0_attn_setup()
    _L0_attn_in = {k: v for k, v in _L0_attn_all.items() if k in ('Wq', 'Wk', 'Wv', 'Wo')}
    del _L0_attn_all

    def _L0_xattn_setup():
        import jax, jax.numpy as jnp
        import numpy as np
        D = 128
        NUM_ITERS = 3
        EPS = 1e-06
        SCALE = D ** (-0.5)

        def rmsnorm(x, w, eps=EPS):
            return x * jax.lax.rsqrt(jnp.mean(x * x, axis=-1, keepdims=True) + eps) * w

        def gru_cell(x, h, wih, whh, bih, bhh):
            gx = x @ wih.T + bih
            gh = h @ whh.T + bhh
            xr, xz, xn = jnp.split(gx, 3, axis=-1)
            hr, hz, hn = jnp.split(gh, 3, axis=-1)
            r = jax.nn.sigmoid(xr + hr)
            z = jax.nn.sigmoid(xz + hz)
            n = jnp.tanh(xn + r * hn)
            return (1.0 - z) * n + z * h
        key = jax.random.key(seed)
        ks = jax.random.split(key, 8)
        B, K, M, d = (8, 64, 512, D)
        w_std = d ** (-0.5)
        return {'slots': jax.random.normal(ks[0], (B, K, d), jnp.float32), 'P': jax.random.normal(ks[1], (B, M, d), jnp.float32), 'Wq': jax.random.normal(ks[2], (d, d), jnp.float32) * w_std, 'Wk': jax.random.normal(ks[3], (d, d), jnp.float32) * w_std, 'Wv': jax.random.normal(ks[4], (d, d), jnp.float32) * w_std, 'gru_wih': jax.random.normal(ks[5], (3 * d, d), jnp.float32) * w_std, 'gru_whh': jax.random.normal(ks[6], (3 * d, d), jnp.float32) * w_std, 'gru_bih': jnp.zeros((3 * d,), jnp.float32), 'gru_bhh': jnp.zeros((3 * d,), jnp.float32), 'slot_norm_w': jnp.ones((d,), jnp.float32), 'input_norm_w': jnp.ones((d,), jnp.float32)}
    _L0_xattn_all = _L0_xattn_setup()
    _L0_xattn_in = {k: v for k, v in _L0_xattn_all.items() if k in ('Wq', 'Wk', 'Wv', 'gru_wih', 'gru_whh', 'gru_bih', 'gru_bhh', 'slot_norm_w', 'input_norm_w')}
    del _L0_xattn_all

    def _L0_ffn_setup():
        import jax, jax.numpy as jnp
        import numpy as np
        import math
        GOLDEN_CENTER = 1.0 / math.e
        GOLDEN_LOWER = 0.5 - math.log(4.0 / 3.0)
        GOLDEN_UPPER = 0.5
        B, T, D = (4, 256, 128)
        E = 8
        I = 512 // (E // 2)

        def _routing_weights(x, Wr, temperature):
            inh = jax.nn.sigmoid(x @ Wr / temperature)
            in_zone = (inh >= GOLDEN_LOWER) & (inh <= GOLDEN_UPPER)
            dist = jnp.abs(inh - GOLDEN_CENTER)
            w = jnp.exp(-dist / 0.1) * in_zone.astype(x.dtype)
            wsum = w.sum(axis=-1, keepdims=True)
            no_expert = wsum < 1e-08
            fb = jnp.exp(-dist / 0.3)
            _, top2 = jax.lax.top_k(fb, 2)
            fb_mask = jax.nn.one_hot(top2, E, dtype=x.dtype).sum(axis=-2)
            fb_w = fb * fb_mask
            fb_w = fb_w / jnp.clip(fb_w.sum(axis=-1, keepdims=True), 1e-08)
            w = jnp.where(no_expert, fb_w, w)
            wsum = w.sum(axis=-1, keepdims=True)
            return w / jnp.clip(wsum, 1e-08)
        key = jax.random.key(seed)
        k = jax.random.split(key, 6)
        s_d = 1.0 / math.sqrt(D)
        s_i = 1.0 / math.sqrt(I)
        return {'x': jax.random.normal(k[0], (B, T, D), jnp.float32), 'Wg': jax.random.normal(k[1], (E, D, I), jnp.float32) * s_d, 'Wu': jax.random.normal(k[2], (E, D, I), jnp.float32) * s_d, 'Wd': jax.random.normal(k[3], (E, I, D), jnp.float32) * s_i, 'Wr': jax.random.normal(k[4], (D, E), jnp.float32) * s_d, 'temperature': jnp.ones((1,), jnp.float32)}
    _L0_ffn_all = _L0_ffn_setup()
    _L0_ffn_in = {k: v for k, v in _L0_ffn_all.items() if k in ('Wg', 'Wu', 'Wd', 'Wr', 'temperature')}
    del _L0_ffn_all

    def _L1_attn_setup():
        import jax, jax.numpy as jnp
        import numpy as np
        H = 16
        G = 4
        DIM = 128
        HD = DIM // H // G
        key = jax.random.key(seed)
        k1, k2, k3 = jax.random.split(key, 3)
        x = jax.random.normal(k1, (8, 512, DIM), dtype=jnp.float32)
        w_qkvw = jax.random.normal(k2, (DIM, 4 * DIM), dtype=jnp.float32) * 0.02
        w_out = jax.random.normal(k3, (DIM, DIM), dtype=jnp.float32) * 0.02
        return {'x': x, 'w_qkvw': w_qkvw, 'w_out': w_out}
    _L1_attn_all = _L1_attn_setup()
    _L1_attn_in = {k: v for k, v in _L1_attn_all.items() if k in ('w_qkvw', 'w_out')}
    del _L1_attn_all

    def _L1_xattn_setup():
        import jax, jax.numpy as jnp
        import numpy as np
        import math
        D_MODEL = 128
        N_HEADS = 16
        key = jax.random.key(seed)
        ks = jax.random.split(key, 11)
        N, L, S = (2, 256, 256)
        d = D_MODEL
        s = 1.0 / math.sqrt(d)
        return {'queries': jax.random.normal(ks[0], (N, L, d), dtype=jnp.float32), 'keys': jax.random.normal(ks[1], (N, S, d), dtype=jnp.float32), 'values': jax.random.normal(ks[2], (N, S, d), dtype=jnp.float32), 'Wq': jax.random.normal(ks[3], (d, d), dtype=jnp.float32) * s, 'bq': jax.random.normal(ks[4], (d,), dtype=jnp.float32) * s, 'Wk': jax.random.normal(ks[5], (d, d), dtype=jnp.float32) * s, 'bk': jax.random.normal(ks[6], (d,), dtype=jnp.float32) * s, 'Wv': jax.random.normal(ks[7], (d, d), dtype=jnp.float32) * s, 'bv': jax.random.normal(ks[8], (d,), dtype=jnp.float32) * s, 'Wo': jax.random.normal(ks[9], (d, d), dtype=jnp.float32) * s, 'bo': jax.random.normal(ks[10], (d,), dtype=jnp.float32) * s}
    _L1_xattn_all = _L1_xattn_setup()
    _L1_xattn_in = {k: v for k, v in _L1_xattn_all.items() if k in ('Wq', 'bq', 'Wk', 'bk', 'Wv', 'bv', 'Wo', 'bo')}
    del _L1_xattn_all

    def _L1_ffn_setup():
        import jax, jax.numpy as jnp
        import numpy as np
        QMAX = 127.0

        def _ste_round(v):
            return v + jax.lax.stop_gradient(jnp.round(v) - v)

        def _act_fake_quant(x, clip_factor):
            scale = jax.nn.sigmoid(clip_factor) * jnp.max(jnp.abs(x)) / QMAX
            return jnp.clip(_ste_round(x / scale), -QMAX - 1.0, QMAX) * scale

        def _weight_fake_quant(w):
            scale = jnp.max(jnp.abs(w), axis=1, keepdims=True) / QMAX
            return jnp.clip(_ste_round(w / scale), -QMAX - 1.0, QMAX) * scale
        key = jax.random.key(seed)
        k1, k2, k3, k4 = jax.random.split(key, 4)
        B, S, H, I = (8, 1024, 128, 352)
        return {'x': jax.random.normal(k1, (B, S, H), dtype=jnp.float32), 'clip_x': jnp.full((1,), 4.0, dtype=jnp.float32), 'clip_down': jnp.full((1,), 4.0, dtype=jnp.float32), 'w_gate': jax.random.normal(k2, (I, H), dtype=jnp.float32) * 0.02, 'w_up': jax.random.normal(k3, (I, H), dtype=jnp.float32) * 0.02, 'w_down': jax.random.normal(k4, (H, I), dtype=jnp.float32) * 0.02}
    _L1_ffn_all = _L1_ffn_setup()
    _L1_ffn_in = {k: v for k, v in _L1_ffn_all.items() if k in ('clip_x', 'clip_down', 'w_gate', 'w_up', 'w_down')}
    del _L1_ffn_all

    def _L2_attn_setup():
        import jax, jax.numpy as jnp
        import numpy as np
        B, T, C = (4, 256, 128)
        QH = 4
        D = C // QH
        EPS = 1e-05

        def _layernorm(x, g, b):
            mu = jnp.mean(x, axis=-1, keepdims=True)
            var = jnp.mean(jnp.square(x - mu), axis=-1, keepdims=True)
            return (x - mu) * jax.lax.rsqrt(var + EPS) * g + b
        key = jax.random.key(seed)
        k1, k2, k3 = jax.random.split(key, 3)
        residual = jax.random.normal(k1, (B, T, C), dtype=jnp.float32)
        w_fc = jax.random.normal(k2, (C, C), dtype=jnp.float32) * (1.0 / np.sqrt(C))
        w_proj = jax.random.normal(k3, (C, C), dtype=jnp.float32) * (1.0 / np.sqrt(C))
        ln_g = jnp.ones((C,), dtype=jnp.float32)
        ln_b = jnp.zeros((C,), dtype=jnp.float32)
        return {'residual': residual, 'w_fc': w_fc, 'w_proj': w_proj, 'ln_g': ln_g, 'ln_b': ln_b}
    _L2_attn_all = _L2_attn_setup()
    _L2_attn_in = {k: v for k, v in _L2_attn_all.items() if k in ('w_fc', 'w_proj', 'ln_g', 'ln_b')}
    del _L2_attn_all

    def _L2_xattn_setup():
        import jax, jax.numpy as jnp
        import numpy as np
        EMB = 128
        key = jax.random.key(seed)
        k1, k2, k3, k4, k5 = jax.random.split(key, 5)
        batch = jax.random.normal(k1, (8, 512, EMB), dtype=jnp.float32)
        latent = jax.random.normal(k2, (8, 128, EMB), dtype=jnp.float32)
        s = 1.0 / np.sqrt(EMB)
        Wk = jax.random.normal(k3, (EMB, EMB), dtype=jnp.float32) * s
        Wq = jax.random.normal(k4, (EMB, EMB), dtype=jnp.float32) * s
        Wv = jax.random.normal(k5, (EMB, EMB), dtype=jnp.float32) * s
        return {'batch': batch, 'latent': latent, 'Wk': Wk, 'Wq': Wq, 'Wv': Wv}
    _L2_xattn_all = _L2_xattn_setup()
    _L2_xattn_in = {k: v for k, v in _L2_xattn_all.items() if k in ('Wk', 'Wq', 'Wv')}
    del _L2_xattn_all

    def _L2_ffn_setup():
        import jax, jax.numpy as jnp
        import numpy as np
        B, L, H, E, I = (4, 256, 128, 8, 512)
        S = B * L
        CAP_FACTOR_EVAL = 2.0
        MIN_CAP = 4
        _cap = int(np.floor(CAP_FACTOR_EVAL * S / E))
        _cap += _cap % 2
        CAPACITY = max(_cap, MIN_CAP)

        def _layer_norm(x, g, b, eps=1e-05):
            mu = x.mean(-1, keepdims=True)
            var = ((x - mu) ** 2).mean(-1, keepdims=True)
            return (x - mu) * jax.lax.rsqrt(var + eps) * g + b
        key = jax.random.key(seed)
        ks = jax.random.split(key, 8)
        gate_std = float(np.sqrt(0.1 / H))
        return {'inputs': jax.random.normal(ks[0], (B, L, H), jnp.float32), 'gate_weight': jax.random.normal(ks[1], (E, H), jnp.float32) * gate_std, 'ln_gamma': jnp.ones((H,), jnp.float32), 'ln_beta': jnp.zeros((H,), jnp.float32), 'wi': jax.random.normal(ks[2], (E, H, I), jnp.float32) * float(1.0 / np.sqrt(H)), 'wo': jax.random.normal(ks[3], (E, I, H), jnp.float32) * float(1.0 / np.sqrt(I)), 'conf_w1': jax.random.normal(ks[4], (H // 2, H), jnp.float32) * float(np.sqrt(2.0 / (H + H // 2))), 'conf_b1': -jnp.ones((H // 2,), jnp.float32), 'conf_w2': jax.random.normal(ks[5], (1, H // 2), jnp.float32) * float(np.sqrt(2.0 / (1 + H // 2))), 'conf_b2': -jnp.ones((1,), jnp.float32), 'comp_w': jax.random.normal(ks[6], (1, H), jnp.float32) * float(1.0 / np.sqrt(H)), 'comp_b': jnp.zeros((1,), jnp.float32)}
    _L2_ffn_all = _L2_ffn_setup()
    _L2_ffn_in = {k: v for k, v in _L2_ffn_all.items() if k in ('gate_weight', 'ln_gamma', 'ln_beta', 'wi', 'wo', 'conf_w1', 'conf_b1', 'conf_w2', 'conf_b2', 'comp_w', 'comp_b')}
    del _L2_ffn_all

    def _L3_attn_setup():
        import jax, jax.numpy as jnp
        import numpy as np
        TTT_LR = 0.01
        LN_EPS = 1e-05
        key = jax.random.key(seed)
        ks = jax.random.split(key, 4)
        B, S, D, DS = (4, 256, 128, 64)
        sc = 1.0 / np.sqrt(D).astype(np.float32)
        return {'x': jax.random.normal(ks[0], (B, S, D), dtype=jnp.float32), 'Wk': jax.random.normal(ks[1], (DS, D), dtype=jnp.float32) * sc, 'bk': jnp.zeros((DS,), jnp.float32), 'Wv': jax.random.normal(ks[2], (D, D), dtype=jnp.float32) * sc, 'bv': jnp.zeros((D,), jnp.float32), 'Wq': jax.random.normal(ks[3], (DS, D), dtype=jnp.float32) * sc, 'bq': jnp.zeros((DS,), jnp.float32), 'gamma': jnp.ones((D,), jnp.float32), 'beta': jnp.zeros((D,), jnp.float32)}
    _L3_attn_all = _L3_attn_setup()
    _L3_attn_in = {k: v for k, v in _L3_attn_all.items() if k in ('Wk', 'bk', 'Wv', 'bv', 'Wq', 'bq', 'gamma', 'beta')}
    del _L3_attn_all

    def _L3_xattn_setup():
        import jax, jax.numpy as jnp
        import numpy as np
        B, S, D = (4, 256, 128)
        H, HK = (16, 4)
        HD = D // H
        G = H // HK
        key = jax.random.key(seed)
        ks = jax.random.split(key, 7)
        s = 0.02
        return {'query': jax.random.normal(ks[0], (B, S, D), jnp.float32), 'key': jax.random.normal(ks[1], (B, S, D), jnp.float32), 'value': jax.random.normal(ks[2], (B, S, D), jnp.float32), 'Wq': jax.random.normal(ks[3], (D, H * HD), jnp.float32) * s, 'Wk': jax.random.normal(ks[4], (D, HK * HD), jnp.float32) * s, 'Wv': jax.random.normal(ks[5], (D, HK * HD), jnp.float32) * s, 'Wo': jax.random.normal(ks[6], (H * HD, D), jnp.float32) * s}
    _L3_xattn_all = _L3_xattn_setup()
    _L3_xattn_in = {k: v for k, v in _L3_xattn_all.items() if k in ('Wq', 'Wk', 'Wv', 'Wo')}
    del _L3_xattn_all

    def _L3_ffn_setup():
        import jax, jax.numpy as jnp
        import numpy as np

        def _binarize(w):
            alpha = jax.lax.stop_gradient(jnp.mean(jnp.abs(w), axis=1, keepdims=True))
            bw = alpha * jnp.sign(w)
            return w + jax.lax.stop_gradient(bw - w)
        key = jax.random.key(seed)
        k1, k2, k3, k4, k5 = jax.random.split(key, 5)
        D, H = (128, 512)
        x = jax.random.normal(k1, (64, 196, D), dtype=jnp.float32)
        w1 = jax.random.normal(k2, (H, D), dtype=jnp.float32) * 0.02
        b1 = jax.random.normal(k3, (H,), dtype=jnp.float32) * 0.02
        w2 = jax.random.normal(k4, (D, H), dtype=jnp.float32) * 0.02
        b2 = jax.random.normal(k5, (D,), dtype=jnp.float32) * 0.02
        return {'x': x, 'w1': w1, 'b1': b1, 'w2': w2, 'b2': b2}
    _L3_ffn_all = _L3_ffn_setup()
    _L3_ffn_in = {k: v for k, v in _L3_ffn_all.items() if k in ('w1', 'b1', 'w2', 'b2')}
    del _L3_ffn_all
    return {'x': x, 'ctx_1024': ctx_1024, 'L0_attn_Wq': _L0_attn_in['Wq'], 'L0_attn_Wk': _L0_attn_in['Wk'], 'L0_attn_Wv': _L0_attn_in['Wv'], 'L0_attn_Wo': _L0_attn_in['Wo'], 'L0_xattn_Wq': _L0_xattn_in['Wq'], 'L0_xattn_Wk': _L0_xattn_in['Wk'], 'L0_xattn_Wv': _L0_xattn_in['Wv'], 'L0_xattn_gru_wih': _L0_xattn_in['gru_wih'], 'L0_xattn_gru_whh': _L0_xattn_in['gru_whh'], 'L0_xattn_gru_bih': _L0_xattn_in['gru_bih'], 'L0_xattn_gru_bhh': _L0_xattn_in['gru_bhh'], 'L0_xattn_slot_norm_w': _L0_xattn_in['slot_norm_w'], 'L0_xattn_input_norm_w': _L0_xattn_in['input_norm_w'], 'L0_ffn_Wg': _L0_ffn_in['Wg'], 'L0_ffn_Wu': _L0_ffn_in['Wu'], 'L0_ffn_Wd': _L0_ffn_in['Wd'], 'L0_ffn_Wr': _L0_ffn_in['Wr'], 'L0_ffn_temperature': _L0_ffn_in['temperature'], 'L1_attn_w_qkvw': _L1_attn_in['w_qkvw'], 'L1_attn_w_out': _L1_attn_in['w_out'], 'L1_xattn_Wq': _L1_xattn_in['Wq'], 'L1_xattn_bq': _L1_xattn_in['bq'], 'L1_xattn_Wk': _L1_xattn_in['Wk'], 'L1_xattn_bk': _L1_xattn_in['bk'], 'L1_xattn_Wv': _L1_xattn_in['Wv'], 'L1_xattn_bv': _L1_xattn_in['bv'], 'L1_xattn_Wo': _L1_xattn_in['Wo'], 'L1_xattn_bo': _L1_xattn_in['bo'], 'L1_ffn_clip_x': _L1_ffn_in['clip_x'], 'L1_ffn_clip_down': _L1_ffn_in['clip_down'], 'L1_ffn_w_gate': _L1_ffn_in['w_gate'], 'L1_ffn_w_up': _L1_ffn_in['w_up'], 'L1_ffn_w_down': _L1_ffn_in['w_down'], 'L2_attn_w_fc': _L2_attn_in['w_fc'], 'L2_attn_w_proj': _L2_attn_in['w_proj'], 'L2_attn_ln_g': _L2_attn_in['ln_g'], 'L2_attn_ln_b': _L2_attn_in['ln_b'], 'L2_xattn_Wk': _L2_xattn_in['Wk'], 'L2_xattn_Wq': _L2_xattn_in['Wq'], 'L2_xattn_Wv': _L2_xattn_in['Wv'], 'L2_ffn_gate_weight': _L2_ffn_in['gate_weight'], 'L2_ffn_ln_gamma': _L2_ffn_in['ln_gamma'], 'L2_ffn_ln_beta': _L2_ffn_in['ln_beta'], 'L2_ffn_wi': _L2_ffn_in['wi'], 'L2_ffn_wo': _L2_ffn_in['wo'], 'L2_ffn_conf_w1': _L2_ffn_in['conf_w1'], 'L2_ffn_conf_b1': _L2_ffn_in['conf_b1'], 'L2_ffn_conf_w2': _L2_ffn_in['conf_w2'], 'L2_ffn_conf_b2': _L2_ffn_in['conf_b2'], 'L2_ffn_comp_w': _L2_ffn_in['comp_w'], 'L2_ffn_comp_b': _L2_ffn_in['comp_b'], 'L3_attn_Wk': _L3_attn_in['Wk'], 'L3_attn_bk': _L3_attn_in['bk'], 'L3_attn_Wv': _L3_attn_in['Wv'], 'L3_attn_bv': _L3_attn_in['bv'], 'L3_attn_Wq': _L3_attn_in['Wq'], 'L3_attn_bq': _L3_attn_in['bq'], 'L3_attn_gamma': _L3_attn_in['gamma'], 'L3_attn_beta': _L3_attn_in['beta'], 'L3_xattn_Wq': _L3_xattn_in['Wq'], 'L3_xattn_Wk': _L3_xattn_in['Wk'], 'L3_xattn_Wv': _L3_xattn_in['Wv'], 'L3_xattn_Wo': _L3_xattn_in['Wo'], 'L3_ffn_w1': _L3_ffn_in['w1'], 'L3_ffn_b1': _L3_ffn_in['b1'], 'L3_ffn_w2': _L3_ffn_in['w2'], 'L3_ffn_b2': _L3_ffn_in['b2']}

def reference(x, ctx_1024, L0_attn_Wq, L0_attn_Wk, L0_attn_Wv, L0_attn_Wo, L0_xattn_Wq, L0_xattn_Wk, L0_xattn_Wv, L0_xattn_gru_wih, L0_xattn_gru_whh, L0_xattn_gru_bih, L0_xattn_gru_bhh, L0_xattn_slot_norm_w, L0_xattn_input_norm_w, L0_ffn_Wg, L0_ffn_Wu, L0_ffn_Wd, L0_ffn_Wr, L0_ffn_temperature, L1_attn_w_qkvw, L1_attn_w_out, L1_xattn_Wq, L1_xattn_bq, L1_xattn_Wk, L1_xattn_bk, L1_xattn_Wv, L1_xattn_bv, L1_xattn_Wo, L1_xattn_bo, L1_ffn_clip_x, L1_ffn_clip_down, L1_ffn_w_gate, L1_ffn_w_up, L1_ffn_w_down, L2_attn_w_fc, L2_attn_w_proj, L2_attn_ln_g, L2_attn_ln_b, L2_xattn_Wk, L2_xattn_Wq, L2_xattn_Wv, L2_ffn_gate_weight, L2_ffn_ln_gamma, L2_ffn_ln_beta, L2_ffn_wi, L2_ffn_wo, L2_ffn_conf_w1, L2_ffn_conf_b1, L2_ffn_conf_w2, L2_ffn_conf_b2, L2_ffn_comp_w, L2_ffn_comp_b, L3_attn_Wk, L3_attn_bk, L3_attn_Wv, L3_attn_bv, L3_attn_Wq, L3_attn_bq, L3_attn_gamma, L3_attn_beta, L3_xattn_Wq, L3_xattn_Wk, L3_xattn_Wv, L3_xattn_Wo, L3_ffn_w1, L3_ffn_b1, L3_ffn_w2, L3_ffn_b2):
    import jax
    import jax.numpy as jnp

    def _L0_attn_ref(x, Wq, Wk, Wv, Wo):
        import jax, jax.numpy as jnp
        import numpy as np
        EMBED = 128
        WIN = 128
        NUM_HEADS = 16
        HQ = 16
        HKV = 4
        HEAD_DIM = EMBED // NUM_HEADS
        G = HQ // HKV
        B, S, _ = x.shape
        W = 2 * WIN + 1
        scale = 1.0 / np.sqrt(HEAD_DIM).astype(np.float32)
        Q = (x @ Wq.T).reshape(B, S, HKV, G, HEAD_DIM)
        K = (x @ Wk.T).reshape(B, S, HKV, HEAD_DIM)
        V = (x @ Wv.T).reshape(B, S, HKV, HEAD_DIM)
        offs = jnp.arange(W) - WIN
        idx = jnp.arange(S)[:, None] + offs[None, :]
        valid = (idx >= 0) & (idx < S)
        idxc = jnp.clip(idx, 0, S - 1)
        K_win = K[:, idxc]
        V_win = V[:, idxc]
        scores = jnp.einsum('bskgd,bswkd->bskgw', Q, K_win) * scale
        scores = jnp.where(valid[None, :, None, None, :], scores, jnp.float32(-jnp.inf))
        attn = jax.nn.softmax(scores, axis=-1)
        out = jnp.einsum('bskgw,bswkd->bskgd', attn, V_win)
        out = out.reshape(B, S, HQ * HEAD_DIM)
        return out @ Wo.T

    def _L0_xattn_ref(slots, P, Wq, Wk, Wv, gru_wih, gru_whh, gru_bih, gru_bhh, slot_norm_w, input_norm_w):
        import jax, jax.numpy as jnp
        import numpy as np
        D = 128
        NUM_ITERS = 3
        EPS = 1e-06
        SCALE = D ** (-0.5)

        def rmsnorm(x, w, eps=EPS):
            return x * jax.lax.rsqrt(jnp.mean(x * x, axis=-1, keepdims=True) + eps) * w

        def gru_cell(x, h, wih, whh, bih, bhh):
            gx = x @ wih.T + bih
            gh = h @ whh.T + bhh
            xr, xz, xn = jnp.split(gx, 3, axis=-1)
            hr, hz, hn = jnp.split(gh, 3, axis=-1)
            r = jax.nn.sigmoid(xr + hr)
            z = jax.nn.sigmoid(xz + hz)
            n = jnp.tanh(xn + r * hn)
            return (1.0 - z) * n + z * h
        Pn = rmsnorm(P, input_norm_w)
        k_proj = Pn @ Wk.T
        v_proj = Pn @ Wv.T
        for _ in range(NUM_ITERS):
            sn = rmsnorm(slots, slot_norm_w)
            q_proj = sn @ Wq.T
            scores = jnp.einsum('bkd,bmd->bkm', q_proj, k_proj) * SCALE
            attn = jax.nn.softmax(scores, axis=-2)
            attn = attn / (jnp.sum(attn, axis=-1, keepdims=True) + EPS)
            updates = jnp.einsum('bkm,bmd->bkd', attn, v_proj)
            slots = gru_cell(updates, slots, gru_wih, gru_whh, gru_bih, gru_bhh)
        return slots

    def _L0_ffn_ref(x, Wg, Wu, Wd, Wr, temperature):
        import jax, jax.numpy as jnp
        import numpy as np
        import math
        GOLDEN_CENTER = 1.0 / math.e
        GOLDEN_LOWER = 0.5 - math.log(4.0 / 3.0)
        GOLDEN_UPPER = 0.5
        B, T, D = (4, 256, 128)
        E = 8
        I = 512 // (E // 2)

        def _routing_weights(x, Wr, temperature):
            inh = jax.nn.sigmoid(x @ Wr / temperature)
            in_zone = (inh >= GOLDEN_LOWER) & (inh <= GOLDEN_UPPER)
            dist = jnp.abs(inh - GOLDEN_CENTER)
            w = jnp.exp(-dist / 0.1) * in_zone.astype(x.dtype)
            wsum = w.sum(axis=-1, keepdims=True)
            no_expert = wsum < 1e-08
            fb = jnp.exp(-dist / 0.3)
            _, top2 = jax.lax.top_k(fb, 2)
            fb_mask = jax.nn.one_hot(top2, E, dtype=x.dtype).sum(axis=-2)
            fb_w = fb * fb_mask
            fb_w = fb_w / jnp.clip(fb_w.sum(axis=-1, keepdims=True), 1e-08)
            w = jnp.where(no_expert, fb_w, w)
            wsum = w.sum(axis=-1, keepdims=True)
            return w / jnp.clip(wsum, 1e-08)
        weights = _routing_weights(x, Wr, temperature)
        gate = jnp.einsum('btd,edi->beti', x, Wg)
        up = jnp.einsum('btd,edi->beti', x, Wu)
        h = jax.nn.silu(gate) * up
        e_out = jnp.einsum('beti,eid->betd', h, Wd)
        out = jnp.einsum('bte,betd->btd', weights, e_out)
        return out

    def _L1_attn_ref(x, w_qkvw, w_out):
        import jax, jax.numpy as jnp
        import numpy as np
        H = 16
        G = 4
        DIM = 128
        HD = DIM // H // G
        B, S, dim = x.shape
        qkvw = x @ w_qkvw
        chunks = jnp.split(qkvw, G, axis=-1)
        subs = [jnp.split(t, G, axis=-1) for t in chunks]
        q = jnp.concatenate([subs[i][0] for i in range(4)], axis=0)
        k = jnp.concatenate([subs[i][1] for i in range(4)], axis=0)
        v = jnp.concatenate([subs[i][2] for i in range(4)], axis=0)
        w = jnp.concatenate([subs[i][3] for i in range(4)], axis=0)

        def shp(t):
            return t.reshape(B * G, H, -1, HD).swapaxes(1, 2)
        q, k, v = (shp(q), shp(k), shp(v))
        w = w.reshape(B * G, H, -1, HD)
        scale = HD ** (-0.5)
        scores = q @ k.swapaxes(-2, -1) * scale
        attn = jax.nn.softmax(scores, axis=-1)
        o = (attn @ v).swapaxes(1, 2).reshape(B, S, dim)
        return o * w.reshape(B, S, dim) @ w_out

    def _L1_xattn_ref(queries, keys, values, Wq, bq, Wk, bk, Wv, bv, Wo, bo):
        import jax, jax.numpy as jnp
        import numpy as np
        import math
        D_MODEL = 128
        N_HEADS = 16
        N, L, _ = queries.shape
        S = keys.shape[1]
        H = N_HEADS
        q = (queries @ Wq.T + bq).reshape(N, L, H, -1)
        k = (keys @ Wk.T + bk).reshape(N, S, H, -1)
        v = (values @ Wv.T + bv).reshape(N, S, H, -1)
        D = k.shape[-1]
        sm = jnp.einsum('nlhd,nshd->nlhs', q, k) / math.sqrt(D)
        causal_mask = jnp.triu(jnp.ones((L, S), dtype=bool), k=1)
        sm = jnp.where(causal_mask[None, :, None, :], -jnp.inf, sm)
        sm = jax.nn.softmax(sm, axis=-1)
        attn = jnp.einsum('nlhs,nshd->nlhd', sm, v)
        new_values = attn.reshape(N, L, H * D)
        return new_values @ Wo.T + bo

    def _L1_ffn_ref(x, clip_x, clip_down, w_gate, w_up, w_down):
        import jax, jax.numpy as jnp
        import numpy as np
        QMAX = 127.0

        def _ste_round(v):
            return v + jax.lax.stop_gradient(jnp.round(v) - v)

        def _act_fake_quant(x, clip_factor):
            scale = jax.nn.sigmoid(clip_factor) * jnp.max(jnp.abs(x)) / QMAX
            return jnp.clip(_ste_round(x / scale), -QMAX - 1.0, QMAX) * scale

        def _weight_fake_quant(w):
            scale = jnp.max(jnp.abs(w), axis=1, keepdims=True) / QMAX
            return jnp.clip(_ste_round(w / scale), -QMAX - 1.0, QMAX) * scale
        xq = _act_fake_quant(x, clip_x[0])
        gate = jnp.einsum('bsh,ih->bsi', xq, _weight_fake_quant(w_gate))
        up = jnp.einsum('bsh,ih->bsi', xq, _weight_fake_quant(w_up))
        h = _act_fake_quant(jax.nn.silu(gate) * up, clip_down[0])
        return jnp.einsum('bsi,hi->bsh', h, _weight_fake_quant(w_down))

    def _L2_attn_ref(residual, w_fc, w_proj, ln_g, ln_b):
        import jax, jax.numpy as jnp
        import numpy as np
        B, T, C = (4, 256, 128)
        QH = 4
        D = C // QH
        EPS = 1e-05

        def _layernorm(x, g, b):
            mu = jnp.mean(x, axis=-1, keepdims=True)
            var = jnp.mean(jnp.square(x - mu), axis=-1, keepdims=True)
            return (x - mu) * jax.lax.rsqrt(var + EPS) * g + b
        Bx, Tx, Cx = residual.shape
        x = _layernorm(residual, ln_g, ln_b)
        q = x.reshape(Bx, Tx, QH, D).transpose(0, 2, 1, 3)
        k = w_fc.reshape(-1, D)
        v = w_proj.T.reshape(-1, D)
        scores = jnp.einsum('bhtd,sd->bhts', q, k)
        p = jnp.square(jax.nn.relu(scores))
        out = jnp.einsum('bhts,sd->bhtd', p, v)
        out = out.transpose(0, 2, 1, 3).reshape(Bx, Tx, Cx)
        return residual + out

    def _L2_xattn_ref(batch, latent, Wk, Wq, Wv):
        import jax, jax.numpy as jnp
        import numpy as np
        EMB = 128
        keys = jnp.einsum('bpe,fe->bpf', batch, Wk)
        queries = jnp.einsum('ble,fe->blf', latent, Wq)
        values = jnp.einsum('bpe,fe->bpf', batch, Wv)
        scale = 1.0 / jnp.sqrt(jnp.asarray(batch.shape[-1], dtype=batch.dtype))
        weights = jnp.einsum('ble,bpe->blp', queries, keys) * scale
        weights = jax.nn.softmax(weights, axis=-1)
        attention = jnp.einsum('blp,bpe->ble', weights, values)
        return attention

    def _L2_ffn_ref(inputs, gate_weight, ln_gamma, ln_beta, wi, wo, conf_w1, conf_b1, conf_w2, conf_b2, comp_w, comp_b):
        import jax, jax.numpy as jnp
        import numpy as np
        B, L, H, E, I = (4, 256, 128, 8, 512)
        S = B * L
        CAP_FACTOR_EVAL = 2.0
        MIN_CAP = 4
        _cap = int(np.floor(CAP_FACTOR_EVAL * S / E))
        _cap += _cap % 2
        CAPACITY = max(_cap, MIN_CAP)

        def _layer_norm(x, g, b, eps=1e-05):
            mu = x.mean(-1, keepdims=True)
            var = ((x - mu) ** 2).mean(-1, keepdims=True)
            return (x - mu) * jax.lax.rsqrt(var + eps) * g + b
        tokens = inputs.reshape(-1, H)
        residual = tokens
        tokens = _layer_norm(tokens, ln_gamma, ln_beta)
        complexity_score = jax.nn.sigmoid(tokens @ comp_w.T + comp_b).mean()
        hdn = jax.nn.relu(tokens @ conf_w1.T + conf_b1)
        confidence_score = jax.nn.sigmoid(hdn @ conf_w2.T + conf_b2).mean()
        logits = tokens.astype(jnp.float32) @ gate_weight.astype(jnp.float32).T
        probs = jax.nn.softmax(logits, axis=-1)
        top1 = jnp.argmax(logits, axis=-1)
        onehot = jax.nn.one_hot(top1, E, dtype=jnp.int32)
        rank_e = jnp.cumsum(onehot, axis=0) - onehot
        rank = jnp.sum(rank_e * onehot, axis=-1)
        keep = rank < CAPACITY
        weight = jnp.take_along_axis(probs, top1[:, None], axis=-1)[:, 0]
        weight = (weight * keep).astype(tokens.dtype)
        slot = jnp.where(keep, rank, 0)
        dispatch = jnp.zeros((E, CAPACITY, H), tokens.dtype)
        dispatch = dispatch.at[top1, slot].add(tokens * keep[:, None])
        h = jax.nn.gelu(jnp.einsum('ech,ehi->eci', dispatch, wi), approximate=False)
        expert_out = jnp.einsum('eci,eih->ech', h, wo)
        combined = weight[:, None] * expert_out[top1, slot]
        out = (residual + combined).reshape(inputs.shape)
        return out

    def _L3_attn_ref(x, Wk, bk, Wv, bv, Wq, bq, gamma, beta):
        import jax, jax.numpy as jnp
        import numpy as np
        TTT_LR = 0.01
        LN_EPS = 1e-05
        B, S, D = x.shape
        DS = Wk.shape[0]
        mu = jnp.mean(x, axis=-1, keepdims=True)
        var = jnp.mean((x - mu) ** 2, axis=-1, keepdims=True)
        h = (x - mu) * jax.lax.rsqrt(var + LN_EPS) * gamma + beta
        keys = jnp.einsum('bsd,ed->bse', h, Wk) + bk
        values = jnp.einsum('bsd,ed->bse', h, Wv) + bv
        queries = jnp.einsum('bsd,ed->bse', h, Wq) + bq

        def step(W, qkv):
            q_t, k_t, v_t = qkv
            y_t = jnp.einsum('bds,bs->bd', W, q_t)
            pred = jnp.einsum('bds,bs->bd', W, k_t)
            err = pred - v_t
            W = W - TTT_LR * err[:, :, None] * k_t[:, None, :]
            return (W, y_t)
        W0 = jnp.zeros((B, D, DS), x.dtype)
        qs = jnp.swapaxes(queries, 0, 1)
        ks_ = jnp.swapaxes(keys, 0, 1)
        vs = jnp.swapaxes(values, 0, 1)
        _, ys = jax.lax.scan(step, W0, (qs, ks_, vs))
        y = jnp.swapaxes(ys, 0, 1)
        return x + y

    def _L3_xattn_ref(query, key, value, Wq, Wk, Wv, Wo):
        import jax, jax.numpy as jnp
        import numpy as np
        B, S, D = (4, 256, 128)
        H, HK = (16, 4)
        HD = D // H
        G = H // HK
        b, qlen, _ = query.shape
        kvlen = key.shape[1]
        q = (query @ Wq).reshape(b, qlen, H, HD)
        k = (key @ Wk).reshape(b, kvlen, HK, HD)
        v = (value @ Wv).reshape(b, kvlen, HK, HD)
        qg = q.reshape(b, qlen, HK, G, HD)
        scale = 1.0 / jnp.sqrt(jnp.asarray(HD, q.dtype))
        scores = jnp.einsum('bqkgd,bskd->bkgqs', qg, k) * scale
        attn = jax.nn.softmax(scores, axis=-1)
        out = jnp.einsum('bkgqs,bskd->bqkgd', attn, v)
        out = out.reshape(b, qlen, H * HD)
        return out @ Wo

    def _L3_ffn_ref(x, w1, b1, w2, b2):
        import jax, jax.numpy as jnp
        import numpy as np

        def _binarize(w):
            alpha = jax.lax.stop_gradient(jnp.mean(jnp.abs(w), axis=1, keepdims=True))
            bw = alpha * jnp.sign(w)
            return w + jax.lax.stop_gradient(bw - w)
        bw1 = _binarize(w1)
        h = jnp.einsum('bsd,hd->bsh', x, bw1) + b1
        h = jax.nn.gelu(h, approximate=False)
        bw2 = _binarize(w2)
        out = jnp.einsum('bsh,dh->bsd', h, bw2) + b2
        return out
    x = x + _L0_attn_ref(_layernorm(x, axis=-1), L0_attn_Wq, L0_attn_Wk, L0_attn_Wv, L0_attn_Wo)
    x = x + _L0_xattn_ref(_layernorm(x, axis=-1), ctx_1024, L0_xattn_Wq, L0_xattn_Wk, L0_xattn_Wv, L0_xattn_gru_wih, L0_xattn_gru_whh, L0_xattn_gru_bih, L0_xattn_gru_bhh, L0_xattn_slot_norm_w, L0_xattn_input_norm_w)
    x = x + _L0_ffn_ref(_layernorm(x, axis=-1), L0_ffn_Wg, L0_ffn_Wu, L0_ffn_Wd, L0_ffn_Wr, L0_ffn_temperature)
    x = x + _L1_attn_ref(_layernorm(x, axis=-1), L1_attn_w_qkvw, L1_attn_w_out)
    x = x + _L1_xattn_ref(_layernorm(x, axis=-1), ctx_1024, ctx_1024, L1_xattn_Wq, L1_xattn_bq, L1_xattn_Wk, L1_xattn_bk, L1_xattn_Wv, L1_xattn_bv, L1_xattn_Wo, L1_xattn_bo)
    x = x + _L1_ffn_ref(_layernorm(x, axis=-1), L1_ffn_clip_x, L1_ffn_clip_down, L1_ffn_w_gate, L1_ffn_w_up, L1_ffn_w_down)
    x = x + _L2_attn_ref(_layernorm(x, axis=-1), L2_attn_w_fc, L2_attn_w_proj, L2_attn_ln_g, L2_attn_ln_b)
    x = x + _L2_xattn_ref(ctx_1024, _layernorm(x, axis=-1), L2_xattn_Wk, L2_xattn_Wq, L2_xattn_Wv)
    x = x + _L2_ffn_ref(_layernorm(x, axis=-1), L2_ffn_gate_weight, L2_ffn_ln_gamma, L2_ffn_ln_beta, L2_ffn_wi, L2_ffn_wo, L2_ffn_conf_w1, L2_ffn_conf_b1, L2_ffn_conf_w2, L2_ffn_conf_b2, L2_ffn_comp_w, L2_ffn_comp_b)
    x = x + _L3_attn_ref(_layernorm(x, axis=-1), L3_attn_Wk, L3_attn_bk, L3_attn_Wv, L3_attn_bv, L3_attn_Wq, L3_attn_bq, L3_attn_gamma, L3_attn_beta)
    x = x + _L3_xattn_ref(_layernorm(x, axis=-1), ctx_1024, ctx_1024, L3_xattn_Wq, L3_xattn_Wk, L3_xattn_Wv, L3_xattn_Wo)
    x = x + _L3_ffn_ref(_layernorm(x, axis=-1), L3_ffn_w1, L3_ffn_b1, L3_ffn_w2, L3_ffn_b2)
    return x

_drawn_inputs = setup_inputs


def setup_inputs(seed=0):
    import zlib

    import numpy as np

    out = dict(_drawn_inputs(seed))
    spreads = {'L0_xattn_gru_bih': (0.0, 0.1),
     'L0_xattn_gru_bhh': (0.0, 0.1),
     'L0_xattn_slot_norm_w': (1.0, 0.2),
     'L0_xattn_input_norm_w': (1.0, 0.2),
     'L2_attn_ln_g': (1.0, 0.6),
     'L2_attn_ln_b': (0.0, 0.308),
     'L2_ffn_ln_gamma': (1.0, 0.6),
     'L2_ffn_ln_beta': (0.0, 1.779),
     'L2_ffn_conf_b1': (-1.0, 0.2),
     'L3_attn_bk': (0.0, 0.8),
     'L3_attn_bv': (0.0, 2.0),
     'L3_attn_bq': (0.0, 0.676),
     'L3_attn_gamma': (1.0, 0.2),
     'L3_attn_beta': (0.0, 0.548)}
    factors = {'L0_attn_Wq': 8.0,
     'L0_attn_Wk': 8.0,
     'L0_attn_Wv': 4.499,
     'L0_attn_Wo': 5.126,
     'L1_attn_w_qkvw': 8.0,
     'L1_attn_w_out': 8.0,
     'L1_xattn_bq': 3.065,
     'L1_xattn_bk': 64.0,
     'L1_ffn_w_gate': 6.77,
     'L1_ffn_w_up': 6.511,
     'L1_ffn_w_down': 6.466,
     'L3_xattn_Wq': 8.0,
     'L3_xattn_Wk': 8.0,
     'L3_xattn_Wv': 8.0,
     'L3_xattn_Wo': 8.0,
     'L3_ffn_w1': 7.514,
     'L3_ffn_b1': 8.0,
     'L3_ffn_w2': 7.094,
     'L3_ffn_b2': 27.287}
    for name, (base, spread) in spreads.items():
        noise = np.random.default_rng([zlib.crc32(name.encode()), seed]).standard_normal(out[name].shape)
        drawn = base * np.exp(spread * noise) if base else spread * noise
        out[name] = jnp.asarray(drawn.astype(out[name].dtype))
    for name, factor in factors.items():
        out[name] = (out[name] * factor).astype(out[name].dtype)
    return out
```

```python
from contextlib import ExitStack

import concourse.bass as bass
from concourse import mybir

ALU = mybir.AluOpType
ACT = mybir.ActivationFunctionType
F32 = mybir.dt.float32
BF16 = mybir.dt.bfloat16
AX = mybir.AxisListType

B, T, D = 8, 100, 128
TOK = B * T
HALF = TOK // 2
HB = B // 2
SC = 1444
KT_FULL = SC // 128
TAIL = SC - KT_FULL * 128
NKT = KT_FULL + 1
TILES = [128] * KT_FULL + [TAIL]
VGROUPS = [(0, 4, 128), (4, 8, 128), (8, KT_FULL, 128), (KT_FULL, NKT, TAIL)]
LN_EPS = 1e-5
ROUND = 12582912.0


class Names:
    pass


class Chain:

    def __init__(self, eng, sem):
        self.eng, self.sem, self.n = eng, sem, 0

    def then(self, ins):
        self.n += 1
        ins.then_inc(self.sem, 1)
        self.eng.wait_ge(self.sem, self.n)


class Stage:

    FIRST_SEM = 160

    def __init__(self, nc, ctx, name):
        self.nc, self.ctx, self.name, self.next = nc, ctx, name, self.FIRST_SEM
        ctx.callback(self.clear)

    def clear(self):
        self.nc.all_engine_barrier(sems_to_clear=range(self.FIRST_SEM, self.next))

    def sb(self, name, shape, dt=F32):
        return self.ctx.enter_context(self.nc.sbuf_tensor(f"{self.name}_{name}", shape, dt))

    def sem(self, name):
        self.next += 1
        return self.ctx.enter_context(self.nc.semaphore(f"{self.name}_{name}", num=self.next - 1))

    def ps(self, name, shape, dt=F32):
        return self.ctx.enter_context(self.nc.psum_tensor(f"{self.name}_{name}", shape, dt))



def ln_sems(s, name="ln"):
    q = Names()
    q.var, q.rstd, q.norm = s.sem(name + "_var"), s.sem(name + "_rstd"), s.sem(name + "_norm")
    q.xT, q.xTs = s.sem(name + "_xT_in_psum"), s.sem(name + "_xT_in_sbuf")
    return q


def ln_vector(nc, dve, chain, m, q, src=None, dst=None):
    src = m.X if src is None else src
    dst = m.XN if dst is None else dst
    for b in range(B):
        last = nc.vector.bn_stats(m.stats[:, b, :], src[:, b, :])
    chain.then(last)
    for b in range(B):
        last = nc.vector.bn_aggr(m.mv[:, b, :], m.stats[:, b, :])
    chain.then(last)
    nc.vector.tensor_scalar(m.veps[:, :], m.mv[:, :, 1], LN_EPS, None, ALU.add).then_inc(q.var, 1)
    dve.wait_ge(q.rstd, 1)
    for b in range(B):
        nc.vector.tensor_scalar(dst[:, b, :], src[:, b, :], m.mv[:, b, 0:1], m.rstd[:, b:b + 1],
                                ALU.subtract, ALU.mult).then_inc(q.norm, 1)


def ln_gpsimd(nc, pool, m, q):
    pool.wait_ge(q.var, 1)
    nc.gpsimd.tensor_tensor(m.rstd[:, :], m.veps[:, :], m.neg_half[0:T, 0:B], ALU.pow).then_inc(q.rstd, 1)


def ln_tensor(nc, pe, m, q, banks, src=None):
    src = m.XN if src is None else src
    for b in range(B):
        pe.wait_ge(q.norm, b + 1)
        nc.tensor.transpose(banks[b // HB][:, (b % HB) * T:(b % HB + 1) * T], src[:, b, :],
                            m.ident[0:T, 0:T]).then_inc(q.xT, 1)


def ln_scalar(nc, act, m, q, banks, affine=None):
    for h in range(2):
        act.wait_ge(q.xT, HB * (h + 1))
        dst = m.XNT[:, h * HALF:(h + 1) * HALF]
        if affine is None:
            nc.scalar.copy(dst, banks[h][:, 0:HALF]).then_inc(q.xTs, 1)
        else:
            nc.scalar.activation(dst, banks[h][:, 0:HALF], ACT.Identity, bias=affine[1][:, 0:1],
                                 scale=affine[0][:, 0:1]).then_inc(q.xTs, 1)



NH, HD = 16, 8
NJ = 4
NG = NH // NJ
SCALE8 = float(HD) ** -0.5


def attention16(nc, m, name, wq, wk, wv, wo, out_dram=None, weights_natural=False, keys="self",
                bias=None):
    grouped = keys != "causal"
    NK = 1 if grouped else NG
    long = keys == "context"
    tiles = TILES if long else [T]
    nt = len(tiles)
    HV = NJ if grouped else NH
    with ExitStack() as ctx:
        s = Stage(nc, ctx, name)
        q = ln_sems(s)
        wT = s.sb("wT", [128, 4, 128])
        wqp = s.sb("wqp", [128, NG, 128])
        wkp = s.sb("wkp", [128, NK, 128])
        QT = s.sb("QT", [128, NG, TOK])
        MXP = s.sb("MXP", [T, 2, NG, 128])
        QA = s.sb("QA", [128, 2, NG, T])
        E = s.sb("E", [128, 2, NJ * T])
        rden = s.sb("rden", [T, NH])
        ON = s.sb("ON", [T, D])
        OT = s.sb("OT", [128, T])
        bcol = s.sb("bcol", [128, 2, NG])
        brow = s.sb("brow", [1, 2, NG, 128])
        if long:
            KT = s.sb("KT", [128, 2, SC])
            V = s.sb("V", [128, 2, NKT, NJ, HD + 1])
            MH = s.sb("MH", [T, 2, NG, NJ, 2])
        else:
            KT = s.sb("KT", [128, NK, TOK])
            V = s.sb("V", [T, B, HV, HD + 1])
        pM = s.ps("pM", [128, 4, 512])
        pA = s.ps("pA", [128, 512])
        pS = s.ps("pS", [128, 2, 512])
        pO = s.ps("pO", [128, 512])
        banks = [pM[:, 0, :], pM[:, 1, :]]
        O = pO[0:T, 0:NH * (HD + 1)]
        O3 = O.rearrange("p (h e) -> p h e", e=HD + 1)
        OTp = pO[:, 160:160 + T]
        Y = pO[0:T, 384:512]
        dch, ach = s.sem("vector_own"), s.sem("scalar_own")
        s_wT, s_w = s.sem("weights_transposed"), s.sem("weights_ready")
        s_row, s_col, s_bias = s.sem("bias_rows"), s.sem("bias_columns_psum"), s.sem("bias_columns")
        s_q, s_qs = s.sem("q_psum"), s.sem("q_sbuf")
        s_k, s_ks = s.sem("k_psum"), s.sem("k_sbuf")
        s_v, s_vs = s.sem("v_psum"), s.sem("v_sbuf")
        s_m, s_mr = s.sem("scores_for_max"), s.sem("max_taken")
        s_mx = s.sem("maxima_ready")
        s_a, s_qa = s.sem("max_rows_psum"), s.sem("q_with_max")
        s_s, s_e = s.sem("scores"), s.sem("exps")
        s_eu = s.sem("exps_used")
        s_on = s.sem("out_normalised")
        s_ot, s_ots = s.sem("outT_psum"), s.sem("outT_sbuf")
        s_y, s_x = s.sem("y_psum"), s.sem("residual_added")
        s_out = s.sem("stored")
        names = [] if weights_natural else [n for n in (0, 1, 2, 3)]
        srcs = [wq, wk, wv, wo]
        KD = NJ * HD * NK
        rows = [128, KD, KD, 128]
        MU = 2 * NH if long else NJ

        with nc.Block(no_gpsimd_drain=True) as block:

            @block.sync
            def _(sp):
                if out_dram is not None:
                    sp.wait_ge(s_x, B)

            @block.gpsimd
            def _(pool):
                ln_gpsimd(nc, pool, m, q)

            @block.vector
            def _(dve):
                chain = Chain(dve, dch)
                for buf in (wqp, wkp, MXP, brow):
                    last = nc.vector.memset(buf[:], 0.0)
                last = nc.vector.memset(V[:], 1.0)
                chain.then(last)
                last = nc.vector.memset(brow[0:1, 1, :, HD:128:32], 1.0)
                if bias is not None:
                    dve.wait_ge(m.loaded[name], m.load_total[name])
                    for g in range(NG):
                        for i in range(2):
                            last = nc.vector.tensor_copy(
                                brow[0:1, i, g, :].rearrange("p (j r) -> p j r", r=32)[:, :, 0:HD],
                                bias[i][0:1, :].rearrange("p (j g d) -> p j g d", g=NG, d=HD)[:, :, g, :])
                last.then_inc(s_row, 1)
                ln_vector(nc, dve, chain, m, q)
                if names:
                    dve.wait_ge(s_wT, 4)
                    src = [pM[:, 2 + n // 2, (n % 2) * 128:(n % 2) * 128 + rows[n]] for n in range(4)]
                else:
                    dve.wait_ge(m.loaded[name], m.load_total[name])
                    src = [w[:, :] for w in srcs]
                for g in range(NG):
                    last = nc.vector.tensor_copy(
                        wqp[:, g, :].rearrange("p (j r) -> p j r", r=32)[:, :, 0:HD],
                        src[0].rearrange("p (j g d) -> p j g d", g=NG, d=HD)[:, :, g, :])
                for g in range(NK):
                    last = nc.vector.tensor_copy(
                        wkp[:, g, :].rearrange("p (j r) -> p j r", r=32)[:, :, 0:HD],
                        src[1].rearrange("p (j g d) -> p j g d", g=NK, d=HD)[:, :, g, :])
                if names:
                    for n in (2, 3):
                        last = nc.vector.tensor_copy(wT[:, n, 0:rows[n]], src[n])
                last.then_inc(s_w, 1)
                dve.wait_ge(s_col, 1)
                nc.vector.tensor_copy(bcol[:, :, :], pA[:, 0:2 * NG].rearrange("p (i g) -> p i g", g=NG))\
                  .then_inc(s_bias, 1)

                def values(n):
                    dve.wait_ge(s_v, n + 1)
                    if long:
                        b, (k0, k1, rows_v) = n // len(VGROUPS), VGROUPS[n % len(VGROUPS)]
                        if b >= 2 and k0 == 0:
                            dve.wait_ge(s_eu, nt * NJ * (b - 1))
                        dst = V[0:rows_v, b % 2, k0:k1, :, 0:HD]
                        src = pO[0:rows_v, 256 + 32 * (k0 % 4):256 + 32 * (k0 % 4) + 32 * (k1 - k0)]
                        nc.vector.tensor_copy(dst, src.rearrange("p (k j d) -> p k j d", j=NJ, d=HD))\
                          .then_inc(s_vs, 1)
                        return
                    else:
                        dst = V[:, n, :, 0:HD]
                        src = pO[0:T, 0:HV * HD]
                    nc.vector.tensor_copy(dst, src.rearrange("p (h d) -> p h d", d=HD)).then_inc(s_vs, 1)

                def maxima(b):
                    if b >= 2:
                        dve.wait_ge(s_a, b - 1)
                    for u in range(MU):
                        dve.wait_ge(s_m, MU * b + u + 1)
                        if long:
                            g, j, h = u // (2 * NJ), u // 2 % NJ, u % 2
                            last = nc.vector.tensor_reduce(
                                MH[:, b % 2, g, j, h:h + 1], pM[0:T, 2 * h:2 * h + 2, 0:SC // 4],
                                AX.XY, ALU.max, negate=True)
                        else:
                            last = nc.vector.tensor_reduce(
                                MXP[:, b % 2, :, 32 * u + HD],
                                pM[0:T, u, 0:NG * T].rearrange("p (g k) -> p g k", k=T),
                                AX.X, ALU.max, negate=True)
                        last.then_inc(s_mr, 1)
                    if long:
                        dve.wait_ge(s_mr, MU * (b + 1))
                        nc.vector.tensor_tensor(
                            MXP[:, b % 2, :, HD:128:32], MH[:, b % 2, :, :, 0], MH[:, b % 2, :, :, 1],
                            ALU.min).then_inc(s_mx, 1)

                def with_max(b):
                    dve.wait_ge(s_a, b + 1)
                    if b >= 2:
                        dve.wait_ge(s_eu, nt * NJ * (b - 1))
                    nc.vector.tensor_tensor(QA[:, b % 2, :, :], QT[:, :, b * T:(b + 1) * T],
                                            pA[:, 0:NG * T].rearrange("p (g t) -> p g t", t=T),
                                            ALU.add).then_inc(s_qa, 1)

                def finish(b):
                    dve.wait_ge(s_eu, nt * NJ * (b + 1))
                    chain.then(nc.vector.reciprocal(rden[:, :], O3[:, :, HD]))
                    nc.vector.tensor_tensor(
                        ON[:, :].rearrange("p (h d) -> p h d", d=HD), O3[:, :, 0:HD],
                        rden[:, :].unsqueeze(2).broadcast_to((T, NH, HD)), ALU.mult).then_inc(s_on, 1)

                def residual(b):
                    dve.wait_ge(s_y, b + 1)
                    nc.vector.tensor_tensor(m.X[:, b, :], m.X[:, b, :], Y, ALU.add).then_inc(s_x, 1)

                if long:
                    dve.wait_ge(s_qs, 8)
                    for i in range(len(VGROUPS)):
                        values(i)
                else:
                    for b in range(B):
                        values(b)
                    dve.wait_ge(s_qs, 8)
                maxima(0)
                for b in range(B):
                    with_max(b)
                    if b + 1 < B:
                        if long:
                            for i in range(len(VGROUPS)):
                                values((b + 1) * len(VGROUPS) + i)
                        maxima(b + 1)
                    finish(b)
                    residual(b)

            @block.scalar
            def _(act):
                chain = Chain(act, ach)
                ln_scalar(nc, act, m, q, banks)
                act.wait_ge(s_bias, 1)
                for n in range(2 * NG):
                    act.wait_ge(s_q, n + 1)
                    g, h = n // 2, n % 2
                    nc.scalar.activation(QT[:, g, h * HALF:(h + 1) * HALF], pS[:, n % 2, 0:HALF],
                                         ACT.Identity, bias=bcol[:, 0, g:g + 1]).then_inc(s_qs, 1)
                if not long:
                    for n in range(2 * NK):
                        act.wait_ge(s_k, n + 1)
                        g, h = n // 2, n % 2
                        nc.scalar.activation(KT[:, g, h * HALF:(h + 1) * HALF], pS[:, n % 2, 0:HALF],
                                             ACT.Identity, bias=bcol[:, 1, g:g + 1]).then_inc(s_ks, 1)

                def keys_of(b):
                    for n in range(4):
                        act.wait_ge(s_k, 4 * b + n + 1)
                        if b >= 2 and n == 0:
                            act.wait_ge(s_eu, nt * NJ * (b - 1))
                        nc.scalar.activation(KT[:, b % 2, n * (SC // 4):(n + 1) * (SC // 4)],
                                             pS[:, n % 2, 0:SC // 4], ACT.Identity,
                                             bias=bcol[:, 1, 0:1]).then_inc(s_ks, 1)

                def outT(b):
                    act.wait_ge(s_ot, b + 1)
                    nc.scalar.copy(OT[:, :], OTp).then_inc(s_ots, 1)

                if long:
                    keys_of(0)
                for b in range(B):
                    if long and b + 1 < B:
                        keys_of(b + 1)
                    for u in range(nt * NJ):
                        n = nt * NJ * b + u
                        k = u // NJ
                        act.wait_ge(s_s, n + 1)
                        if n >= 2:
                            act.wait_ge(s_eu, n - 1)
                        nc.scalar.activation(E[0:tiles[k], n % 2, :], pS[0:tiles[k], n % 2, 0:NJ * T],
                                             ACT.Exp, scale=SCALE8).then_inc(s_e, 1)
                    outT(b)

            @block.tensor
            def _(pe):
                pe.wait_ge(s_row, 1)
                for i in range(2):
                    for g in range(NG):
                        last = nc.tensor.matmul(pA[:, i * NG + g:i * NG + g + 1], brow[0:1, i, g, :],
                                                m.ones[0:1, 0:1], start=(i == 0 and g == 0), stop=True,
                                                skip_group_check=True)
                last.then_inc(s_col, 1)
                pe.wait_ge(m.loaded[name], m.load_total[name])
                for n in names:
                    nc.tensor.transpose(pM[:, 2 + n // 2, (n % 2) * 128:(n % 2) * 128 + rows[n]],
                                        srcs[n][0:rows[n], :], m.ident[0:rows[n], 0:rows[n]]).then_inc(s_wT, 1)
                ln_tensor(nc, pe, m, q, banks)
                pe.wait_ge(s_w, 1)
                pe.wait_ge(q.xTs, 2)
                for n in range(2 * NG):
                    if n >= 2:
                        pe.wait_ge(s_qs, n - 1)
                    g, h = n // 2, n % 2
                    nc.tensor.matmul(pS[:, n % 2, 0:HALF], wqp[:, g, :], m.XNT[:, h * HALF:(h + 1) * HALF],
                                     start=True, stop=True).then_inc(s_q, 1)

                def kv_src(b, n):
                    if keys == "self":
                        return m.XNT[:, b * T:(b + n) * T]
                    return m.CT[:, b:b + n, 0:T] if n > 1 else m.CT[:, b, 0:T]

                wv_ap = wT[:, 2, 0:HV * HD] if names else srcs[2][:, :]
                wo_ap = wT[:, 3, :] if names else srcs[3][:, :]
                if not long:
                    for n in range(2 * NK):
                        if n == 0:
                            pe.wait_ge(s_qs, 2 * NG)
                        if n >= 2:
                            pe.wait_ge(s_ks, n - 1)
                        g, h = n // 2, n % 2
                        nc.tensor.matmul(pS[:, n % 2, 0:HALF], wkp[:, g, :], kv_src(h * HB, HB),
                                         start=True, stop=True).then_inc(s_k, 1)
                    for b in range(B):
                        if b >= 1:
                            pe.wait_ge(s_vs, b)
                        last = nc.tensor.matmul(pO[0:T, 0:HV * HD], kv_src(b, 1), wv_ap,
                                                start=True, stop=bias is None)
                        if bias is not None:
                            last = nc.tensor.matmul(pO[0:T, 0:HV * HD], m.ones[0:1, 0:T], bias[2][0:1, :],
                                                    start=False, stop=True)
                        last.then_inc(s_v, 1)
                    pe.wait_ge(s_ks, 2 * NK)
                    pe.wait_ge(s_vs, B)

                def project_kv(b):
                    for n in range(4):
                        if b == 0 and n == 0:
                            pe.wait_ge(s_qs, 2 * NG)
                        if b >= 2 and n == 0:
                            pe.wait_ge(s_e, nt * NJ * (b - 1))
                        if 4 * b + n >= 2:
                            pe.wait_ge(s_ks, 4 * b + n - 1)
                        nc.tensor.matmul(pS[:, n % 2, 0:SC // 4], wkp[:, 0, :],
                                         m.CT[:, b, n * (SC // 4):(n + 1) * (SC // 4)],
                                         start=True, stop=True).then_inc(s_k, 1)
                    for i, (k0, k1, _) in enumerate(VGROUPS):
                        n = b * len(VGROUPS) + i
                        if n >= 1:
                            pe.wait_ge(s_vs, n)
                        if i == 0 and b >= 2:
                            pe.wait_ge(s_x, b - 1)
                        for k in range(k0, k1):
                            last = nc.tensor.matmul(
                                pO[0:TILES[k], 256 + 32 * (k % 4):256 + 32 * (k % 4) + 32],
                                m.CT[:, b, k * 128:k * 128 + TILES[k]], wv_ap,
                                start=True, stop=True)
                        last.then_inc(s_v, 1)

                def max_scores(b):
                    if long:
                        pe.wait_ge(s_ks, 4 * (b + 1))
                    for u in range(MU):
                        if long:
                            g, j, h = u // (2 * NJ), u // 2 % NJ, u % 2
                            if MU * b + u >= 2:
                                pe.wait_ge(s_mr, MU * b + u - 1)
                            for c in range(2):
                                k0 = (2 * h + c) * (SC // 4)
                                last = nc.tensor.matmul(
                                    pM[0:T, 2 * h + c, 0:SC // 4], QT[32 * j:32 * j + HD, g, b * T:(b + 1) * T],
                                    KT[32 * j:32 * j + HD, b % 2, k0:k0 + SC // 4],
                                    start=True, stop=True)
                        else:
                            if b >= 1:
                                pe.wait_ge(s_mr, MU * (b - 1) + u + 1)
                            if not grouped:
                                nc.tensor.matmul(pM[0:T, u, 0:NJ * T], m.ident[0:T, 0:T], m.mask[:, 0, :],
                                                 start=True, stop=False, skip_group_check=True)
                            for g in range(NG):
                                last = nc.tensor.matmul(
                                    pM[0:T, u, g * T:(g + 1) * T],
                                    QT[32 * u:32 * u + HD, g, b * T:(b + 1) * T],
                                    KT[32 * u:32 * u + HD, g if NK > 1 else 0, b * T:(b + 1) * T],
                                    start=(grouped and g == 0), stop=True, skip_group_check=True)
                        last.then_inc(s_m, 1)

                def max_rows(b):
                    if long:
                        pe.wait_ge(s_mx, b + 1)
                    else:
                        pe.wait_ge(s_mr, MU * (b + 1))
                    if b >= 1:
                        pe.wait_ge(s_qa, b)
                    else:
                        pe.wait_ge(s_bias, 1)
                    for g in range(NG):
                        last = nc.tensor.matmul(pA[:, g * T:(g + 1) * T], MXP[:, b % 2, g, :],
                                                m.ident[0:T, 0:T], start=(g == 0), stop=True,
                                                skip_group_check=True)
                    last.then_inc(s_a, 1)

                def score(b, u):
                    n = nt * NJ * b + u
                    k, j = u // NJ, u % NJ
                    if n >= 2:
                        pe.wait_ge(s_e, n - 1)
                    if grouped:
                        kt = KT[32 * j:32 * j + HD + 1, b % 2, k * 128:k * 128 + tiles[k]] if long else \
                            KT[32 * j:32 * j + HD + 1, 0, b * T:(b + 1) * T]
                        last = nc.tensor.matmul(pS[0:tiles[k], n % 2, 0:NG * T], kt,
                                                QA[32 * j:32 * j + HD + 1, b % 2, :, :], start=True, stop=True)
                    else:
                        nc.tensor.matmul(pS[0:T, n % 2, 0:NG * T], m.ident[0:T, 0:T], m.mask[:, 1, :],
                                         start=True, stop=False, skip_group_check=True)
                        for g in range(NG):
                            last = nc.tensor.matmul(
                                pS[0:T, n % 2, g * T:(g + 1) * T],
                                KT[32 * j:32 * j + HD + 1, g, b * T:(b + 1) * T],
                                QA[32 * j:32 * j + HD + 1, b % 2, g, :], start=False, stop=True,
                                skip_group_check=True)
                    last.then_inc(s_s, 1)

                def weigh(b, u):
                    n = nt * NJ * b + u
                    k, j = u // NJ, u % NJ
                    pe.wait_ge(s_e, n + 1)
                    for g in range(NG):
                        h = NG * j + g
                        if long:
                            v = V[0:TILES[k], b % 2, k, j, :]
                        else:
                            v = V[:, b, j if grouped else h, :]
                        last = nc.tensor.matmul(O[:, h * (HD + 1):(h + 1) * (HD + 1)],
                                                E[0:tiles[k], n % 2, g * T:(g + 1) * T], v,
                                                start=(k == 0 and j == 0 and g == 0), stop=(k == nt - 1),
                                                skip_group_check=True)
                    last.then_inc(s_eu, 1)

                def project(b):
                    pe.wait_ge(s_on, b + 1)
                    nc.tensor.transpose(OTp, ON[:, :], m.ident[0:T, 0:T]).then_inc(s_ot, 1)
                    pe.wait_ge(s_ots, b + 1)
                    last = nc.tensor.matmul(Y, OT[:, :], wo_ap, start=True, stop=bias is None)
                    if bias is not None:
                        last = nc.tensor.matmul(Y, m.ones[0:1, 0:T], bias[3][0:1, :], start=False, stop=True)
                    last.then_inc(s_y, 1)

                if long:
                    project_kv(0)
                else:
                    pe.wait_ge(s_qs, 2 * NG)
                max_scores(0)
                for b in range(B):
                    max_rows(b)
                    if b + 1 < B:
                        if long:
                            project_kv(b + 1)
                        max_scores(b + 1)
                    if long:
                        pe.wait_ge(s_vs, (b + 1) * len(VGROUPS))
                    pe.wait_ge(s_qa, b + 1)
                    if b >= 1:
                        pe.wait_ge(s_x, b)
                    score(b, 0)
                    for u in range(nt * NJ):
                        if u + 1 < nt * NJ:
                            score(b, u + 1)
                        weigh(b, u)
                    project(b)



def context_block(nc, m, name, normalise, nth):
    with ExitStack() as ctx:
        s = Stage(nc, ctx, name)
        pT = s.ps("pT", [128, 6, 512])
        junk = s.sb("junk", [128, NKT, D])
        ss = s.sb("ss", [128, B, NKT])
        rs = s.sb("rs", [128, B, NKT])
        s_sq, s_sq2, s_ms = s.sem("squares_vector"), s.sem("squares_scalar"), s.sem("mean_squares")
        s_r, s_n = s.sem("rstd"), s.sem("normalised")
        s_t, s_c = s.sem("transposed"), s.sem("copied_even")
        s_c2 = s.sem("copied_odd")
        groups = [(b, g) for b in range(B) for g in range(3)]

        with nc.Block(no_gpsimd_drain=True) as block:

            @block.sync
            def _(sp):
                if nth > 1:
                    for b in range(B):
                        load_context(sp, m, b)

            @block.gpsimd
            def _(pool):
                if not normalise:
                    return
                for b in range(B):
                    pool.wait_ge(s_ms, b + 1)
                    nc.gpsimd.tensor_tensor(rs[:, b, :], ss[:, b, :], m.neg_half[:, 0:NKT], ALU.pow)\
                      .then_inc(s_r, 1)

            @block.vector
            def _(dve):
                def copies(b):
                    for g in range(3):
                        i = 3 * b + g
                        if i % 2 == 0:
                            dve.wait_ge(s_t, i + 1)
                            nc.vector.tensor_copy(m.CT[:, b, g * 512:(g + 1) * 512], pT[:, i % 6, :])\
                              .then_inc(s_c, 1)

                for b in range(B):
                    if normalise:
                        dve.wait_ge(m.ctx_loaded[b], 32 * nth)
                        for k in range(NKT // 2):
                            last = nc.vector.scalar_tensor_tensor(
                                out=junk[:, k, :], in0=m.ctx_tm[:, b, k, 0:D], scalar=1.0,
                                in1=m.ctx_tm[:, b, k, 0:D], op0=ALU.mult, op1=ALU.mult,
                                accum_out=ss[:, b, k:k + 1])
                        last.then_inc(s_sq, 1)
                        dve.wait_ge(s_sq, b + 1)
                        dve.wait_ge(s_sq2, b + 1)
                        nc.vector.tensor_scalar(ss[:, b, :], ss[:, b, :], 1.0 / D, 1e-6, ALU.mult, ALU.add)\
                          .then_inc(s_ms, 1)
                        if b >= 1:
                            copies(b - 1)
                        dve.wait_ge(s_r, b + 1)
                        nc.vector.tensor_tensor(m.ctx_tm[:, b, :, 0:D], m.ctx_tm[:, b, :, 0:D],
                                                rs[:, b, :].unsqueeze(2).broadcast_to((128, NKT, D)),
                                                ALU.mult).then_inc(s_n, 1)
                    else:
                        copies(b)
                if normalise:
                    copies(B - 1)

            @block.scalar
            def _(act):
                def copies(b):
                    for g in range(3):
                        i = 3 * b + g
                        if i % 2 == 1:
                            act.wait_ge(s_t, i + 1)
                            nc.scalar.copy(m.CT[:, b, g * 512:(g + 1) * 512], pT[:, i % 6, :])\
                              .then_inc(s_c2, 1)

                for b in range(B):
                    if normalise:
                        act.wait_ge(m.ctx_loaded[b], 32 * nth)
                        if b >= 1:
                            act.wait_ge(s_sq2, b)
                        for k in range(NKT // 2, NKT):
                            last = nc.scalar.activation(junk[:, k, :], m.ctx_tm[:, b, k, 0:D], ACT.Square,
                                                        accum_out=ss[:, b, k:k + 1])
                        last.then_inc(s_sq2, 1)
                        if b >= 1:
                            copies(b - 1)
                    else:
                        copies(b)
                if normalise:
                    copies(B - 1)

            @block.tensor
            def _(pe):
                for i, (b, g) in enumerate(groups):
                    if normalise:
                        pe.wait_ge(s_n, b + 1)
                    else:
                        pe.wait_ge(m.ctx_loaded[b], 32 * nth)
                    if i >= 6:
                        if i % 2 == 0:
                            pe.wait_ge(s_c, (i - 6) // 2 + 1)
                        else:
                            pe.wait_ge(s_c2, (i - 6) // 2 + 1)
                    for k in range(4):
                        last = nc.tensor.transpose(pT[:, i % 6, k * 128:(k + 1) * 128],
                                                   m.ctx_tm[:, b, 4 * g + k, 0:D], m.ident[:, :])
                    last.then_inc(s_t, 1)


def load_context(sp, m, b):
    src = m.a["ctx_1024"]
    sp.dma_start(m.ctx_tm[:, b, 0:KT_FULL, 0:D],
                 src[b, 0:KT_FULL * 128, :].rearrange("(k p) d -> p k d", p=128)).then_inc(m.ctx_loaded[b], 16)
    sp.dma_start(m.ctx_tm[0:TAIL, b, KT_FULL, 0:D], src[b, KT_FULL * 128:SC, :]).then_inc(m.ctx_loaded[b], 16)



def slot_attention(nc, m):
    name = "L0x"
    w = m.w
    ITERS = 3
    N = ITERS * B
    G4 = 512
    with ExitStack() as ctx:
        s = Stage(nc, ctx, name)
        q = ln_sems(s)
        Mqk = s.sb("Mqk", [128, 128])
        G = s.sb("G", [128, 3 * D])
        wihT = s.sb("wihT", [128, 3 * D])
        whhT = s.sb("whhT", [128, 3 * D])
        grow = s.sb("gate_bias", [1, G4])
        ssq = s.sb("ssq", [T, 2])
        rsl = s.sb("rsl", [T, 2])
        junk = s.sb("junk", [T, D])
        SN = s.sb("SN", [T, 2, D])
        STs = s.sb("STs", [128, 2, 2, T])
        QS = s.sb("QS", [128, 2, T])
        mx = s.sb("mx", [128, 2, 12])
        E = s.sb("E", [128, 2, 12, T])
        Z = s.sb("Z", [128, 2, 12])
        RZ = s.sb("RZ", [128, 2, 12])
        den = s.sb("den", [T, 2])
        U = s.sb("U", [T, D])
        UT = s.sb("UT", [128, T])
        rz = s.sb("rz", [T, 2, 2 * D])
        nn = s.sb("nn", [T, 2, 3, D])
        pS = s.ps("pS", [128, 2, 3, 512])
        pT = s.ps("pT", [128, 512])
        pG = s.ps("pG", [128, 512])
        vch = s.sem("vector_own")
        gch = s.sem("gpsimd_own")
        s_wt, s_wc, s_w2, s_wr = s.sem("gru_transposed"), s.sem("gru_copied"), s.sem("products"), s.sem("weights")
        s_sq, s_r, s_sn = s.sem("slot_squares"), s.sem("slot_rstd"), s.sem("slots_normalised")
        s_t, s_ts = s.sem("slotsT_psum"), s.sem("slotsT_sbuf")
        s_q, s_qs = s.sem("q_psum"), s.sem("q_sbuf")
        s_s, s_sub, s_e = s.sem("scores"), s.sem("less_max"), s.sem("exps")
        s_rz, s_en = s.sem("rec_of_sums"), s.sem("attention")
        s_u, s_us = s.sem("update_psum"), s.sem("update_sbuf")
        s_ut, s_uts = s.sem("updateT_psum"), s.sem("updateT_sbuf")
        s_g, s_th = s.sem("gates_psum"), s.sem("tanh_rz")
        s_ni, s_n = s.sem("n_argument"), s.sem("n")
        s_slot = s.sem("slots_updated")

        with nc.Block(no_gpsimd_drain=True) as block:

            @block.gpsimd
            def _(pool):
                ln_gpsimd(nc, pool, m, q)
                chain = Chain(pool, gch)

                def rstd(n):
                    pool.wait_ge(s_sq, n + 1)
                    nc.gpsimd.tensor_tensor(rsl[:, n % 2:n % 2 + 1], ssq[:, n % 2:n % 2 + 1],
                                            m.neg_half[0:T, 0:1], ALU.pow).then_inc(s_r, 1)

                def normalise(n):
                    pool.wait_ge(s_rz, n + 1)
                    nc.gpsimd.tensor_tensor(E[:, n % 2, :, :], E[:, n % 2, :, :],
                                            RZ[:, n % 2, :].unsqueeze(2).broadcast_to((128, 12, T)),
                                            ALU.mult).then_inc(s_en, 1)

                def update(n):
                    b = n % B
                    pool.wait_ge(s_n, n + 1)
                    chain.then(nc.gpsimd.tensor_tensor(nn[:, n % 2, 2, :], m.XN[:, b, :], nn[:, n % 2, 1, :],
                                                       ALU.subtract))
                    chain.then(nc.gpsimd.tensor_tensor(nn[:, n % 2, 2, :], nn[:, n % 2, 2, :],
                                                       rz[:, n % 2, D:2 * D], ALU.mult))
                    nc.gpsimd.tensor_tensor(m.XN[:, b, :], nn[:, n % 2, 2, :], nn[:, n % 2, 1, :],
                                            ALU.add).then_inc(s_slot, 1)

                rstd(0)
                for n in range(N):
                    if n + 1 < N:
                        rstd(n + 1)
                    normalise(n)
                    if n >= 1:
                        update(n - 1)
                update(N - 1)

            @block.vector
            def _(dve):
                chain = Chain(dve, vch)
                ln_vector(nc, dve, chain, m, q)
                dve.wait_ge(m.loaded[name], m.load_total[name])
                bi, bh = w["x0bi"], w["x0bh"]
                nc.vector.tensor_tensor(grow[0:1, 0:2 * D], bi[0:1, 0:2 * D], bh[0:1, 0:2 * D], ALU.add)
                nc.vector.tensor_copy(grow[0:1, 2 * D:3 * D], bi[0:1, 2 * D:3 * D])
                nc.vector.tensor_copy(grow[0:1, 3 * D:4 * D], bh[0:1, 2 * D:3 * D])
                dve.wait_ge(s_wt, 2)
                nc.vector.tensor_copy(wihT[:, :], pS[:, 0, 0, 0:3 * D])
                nc.vector.tensor_copy(whhT[:, :], pS[:, 0, 1, 0:3 * D]).then_inc(s_wc, 1)
                dve.wait_ge(s_w2, 1)
                nc.vector.tensor_scalar(G[:, :], pS[:, 0, 2, 0:3 * D], w["x0iw"][:, 0:1], None, ALU.mult)
                nc.vector.tensor_scalar(Mqk[:, :], pS[:, 1, 0, 0:D], w["x0sw"][:, 0:1], float(D) ** -0.5,
                                        ALU.mult, ALU.mult).then_inc(s_wr, 1)
                dve.wait_ge(q.norm, B)

                def slot_stats(n):
                    b = n % B
                    if n >= B:
                        dve.wait_ge(s_slot, n - B + 1)
                    chain.then(nc.vector.scalar_tensor_tensor(
                        out=junk[:, :], in0=m.XN[:, b, :], scalar=1.0, in1=m.XN[:, b, :],
                        op0=ALU.mult, op1=ALU.mult, accum_out=ssq[:, n % 2:n % 2 + 1]))
                    nc.vector.tensor_scalar(ssq[:, n % 2:n % 2 + 1], ssq[:, n % 2:n % 2 + 1], 1.0 / D, 1e-6,
                                            ALU.mult, ALU.add).then_inc(s_sq, 1)

                def slot_norm(n):
                    dve.wait_ge(s_r, n + 1)
                    if n >= 2:
                        dve.wait_ge(s_t, n - 1)
                    nc.vector.tensor_scalar(SN[:, n % 2, :], m.XN[:, n % B, :], rsl[:, n % 2:n % 2 + 1], None,
                                            ALU.mult).then_inc(s_sn, 1)

                def less_max(n):
                    dve.wait_ge(s_s, n + 1)
                    sc = pS[:, n % 2, :, 0:4 * T].rearrange("p c (k t) -> p c k t", t=T)
                    mxv = mx[:, n % 2, :].rearrange("p (c k) -> p c k", k=4)
                    chain.then(nc.vector.tensor_reduce(mxv, sc, AX.X, ALU.max))
                    if n >= 2:
                        dve.wait_ge(s_u, n - 1)
                    nc.vector.tensor_tensor(E[:, n % 2, :, :].rearrange("p (c k) t -> p c k t", k=4), sc,
                                            mxv.unsqueeze(3).broadcast_to((128, 3, 4, T)),
                                            ALU.subtract).then_inc(s_sub, 1)

                def sums(n):
                    dve.wait_ge(s_e, n + 1)
                    chain.then(nc.vector.tensor_reduce(Z[:, n % 2, :], E[:, n % 2, :, :], AX.X, ALU.add))
                    nc.vector.reciprocal(RZ[:, n % 2, :], Z[:, n % 2, :]).then_inc(s_rz, 1)

                def scale_update(n):
                    dve.wait_ge(s_u, n + 1)
                    chain.then(nc.vector.tensor_scalar(den[:, 0:1], pG[0:T, D:D + 1], 1e-6, None, ALU.add))
                    chain.then(nc.vector.reciprocal(den[:, 1:2], den[:, 0:1]))
                    nc.vector.tensor_scalar(U[:, :], pG[0:T, 0:D], den[:, 1:2], None, ALU.mult).then_inc(s_us, 1)

                def gates(n):
                    dve.wait_ge(s_th, n + 1)
                    if n >= 2:
                        dve.wait_ge(s_slot, n - 1)
                    chain.then(nc.vector.tensor_scalar(rz[:, n % 2, :], rz[:, n % 2, :], 0.5, 0.5,
                                                       ALU.mult, ALU.add))
                    chain.then(nc.vector.tensor_tensor(nn[:, n % 2, 0, :], pG[0:T, 3 * D:4 * D],
                                                       rz[:, n % 2, 0:D], ALU.mult))
                    nc.vector.tensor_tensor(nn[:, n % 2, 0, :], pG[0:T, 2 * D:3 * D], nn[:, n % 2, 0, :],
                                            ALU.add).then_inc(s_ni, 1)

                slot_stats(0)
                slot_norm(0)
                slot_stats(1)
                slot_norm(1)
                less_max(0)
                for n in range(N):
                    sums(n)
                    if n + 2 < N:
                        slot_stats(n + 2)
                    if n + 1 < N:
                        less_max(n + 1)
                    if n + 2 < N:
                        slot_norm(n + 2)
                    scale_update(n)
                    gates(n)
                for b in range(B):
                    dve.wait_ge(s_slot, N - B + b + 1)
                    nc.vector.tensor_tensor(m.X[:, b, :], m.X[:, b, :], m.XN[:, b, :], ALU.add)

            @block.scalar
            def _(act):
                def slotsT(n):
                    act.wait_ge(s_t, n + 1)
                    if n >= 2:
                        act.wait_ge(s_g, n - 1)
                    nc.scalar.copy(STs[:, n % 2, :, :],
                                   pT[:, 0:256].rearrange("p (i t) -> p i t", i=2)[:, :, 0:T]).then_inc(s_ts, 1)

                def queries(n):
                    act.wait_ge(s_q, n + 1)
                    nc.scalar.activation(QS[:, n % 2, :], pT[:, 256:256 + T], ACT.Copy,
                                         scale=w["x0iw"][:, 0:1]).then_inc(s_qs, 1)

                def exps(n):
                    act.wait_ge(s_sub, n + 1)
                    nc.scalar.activation(E[:, n % 2, :, :], E[:, n % 2, :, :], ACT.Exp).then_inc(s_e, 1)

                def after(n):
                    act.wait_ge(s_ut, n + 1)
                    nc.scalar.copy(UT[:, :], pT[:, 384:384 + T]).then_inc(s_uts, 1)
                    act.wait_ge(s_g, n + 1)
                    if n >= 2:
                        act.wait_ge(s_slot, n - 1)
                    nc.scalar.activation(rz[:, n % 2, :], pG[0:T, 0:2 * D], ACT.Tanh, scale=0.5)\
                      .then_inc(s_th, 1)
                    act.wait_ge(s_ni, n + 1)
                    nc.scalar.activation(nn[:, n % 2, 1, :], nn[:, n % 2, 0, :], ACT.Tanh).then_inc(s_n, 1)

                act.wait_ge(m.loaded[name], m.load_total[name])
                slotsT(0)
                queries(0)
                exps(0)
                for n in range(N):
                    if n + 1 < N:
                        slotsT(n + 1)
                        queries(n + 1)
                        exps(n + 1)
                    after(n)

            @block.tensor
            def _(pe):
                pe.wait_ge(m.loaded[name], m.load_total[name])
                for i, key in enumerate(("x0ih", "x0hh")):
                    for c in range(3):
                        last = nc.tensor.transpose(pS[:, 0, i, c * D:(c + 1) * D], w[key][:, c, :], m.ident[:, :])
                    last.then_inc(s_wt, 1)
                nc.tensor.matmul(pS[:, 1, 0, 0:D], w["x0q"][:, :], w["x0k"][:, :], start=True, stop=True)
                pe.wait_ge(s_wc, 1)
                nc.tensor.matmul(pS[:, 0, 2, 0:3 * D], w["x0v"][:, :], wihT[:, :], start=True, stop=True)\
                  .then_inc(s_w2, 1)
                pe.wait_ge(s_wr, 1)

                def scores(n):
                    b = n % B
                    pe.wait_ge(s_sn, n + 1)
                    nc.tensor.transpose(pT[:, 0:T], m.XN[:, b, :], m.ident[0:T, 0:T])
                    nc.tensor.transpose(pT[:, 128:128 + T], SN[:, n % 2, :], m.ident[0:T, 0:T]).then_inc(s_t, 1)
                    pe.wait_ge(s_ts, n + 1)
                    nc.tensor.matmul(pT[:, 256:256 + T], Mqk[:, :], STs[:, n % 2, 1, :],
                                     start=True, stop=True).then_inc(s_q, 1)
                    pe.wait_ge(s_qs, n + 1)
                    if n >= 2:
                        pe.wait_ge(s_sub, n - 1)
                    for k in range(12):
                        last = nc.tensor.matmul(pS[:, n % 2, k // 4, (k % 4) * T:(k % 4 + 1) * T],
                                                m.CT[:, b, k * 128:(k + 1) * 128], QS[:, n % 2, :],
                                                start=True, stop=True)
                    last.then_inc(s_s, 1)

                def update(n):
                    b = n % B
                    pe.wait_ge(s_en, n + 1)
                    if n >= 1:
                        pe.wait_ge(s_ni, n)
                    for k, rows in enumerate(TILES):
                        last = nc.tensor.matmul(pG[0:T, 0:D + 1], E[0:rows, n % 2, k, :],
                                                m.ctx_tm[0:rows, b, k, :], start=(k == 0), stop=(k == NKT - 1))
                    last.then_inc(s_u, 1)
                    pe.wait_ge(s_us, n + 1)
                    nc.tensor.transpose(pT[:, 384:384 + T], U[:, :], m.ident[0:T, 0:T]).then_inc(s_ut, 1)
                    pe.wait_ge(s_uts, n + 1)
                    nc.tensor.matmul(pG[0:T, :], m.ones[0:1, 0:T], grow[0:1, :], start=True, stop=False,
                                     skip_group_check=True)
                    nc.tensor.matmul(pG[0:T, 0:3 * D], UT[:, :], G[:, :], start=False, stop=False,
                                     skip_group_check=True)
                    nc.tensor.matmul(pG[0:T, 0:2 * D], STs[:, n % 2, 0, :], whhT[:, 0:2 * D], start=False,
                                     stop=False, skip_group_check=True)
                    nc.tensor.matmul(pG[0:T, 3 * D:4 * D], STs[:, n % 2, 0, :], whhT[:, 2 * D:3 * D],
                                     start=False, stop=True, skip_group_check=True).then_inc(s_g, 1)

                scores(0)
                for n in range(N):
                    if n + 1 < N:
                        scores(n + 1)
                    update(n)



NE = 8


def first_largest(nc, chain, m, val, top, eq, best, onehot):
    chain.then(nc.vector.tensor_reduce(top, val, AX.X, ALU.max))
    chain.then(nc.vector.tensor_tensor(eq, val, top.unsqueeze(2).broadcast_to((T, B, NE)), ALU.is_equal))
    chain.then(nc.vector.tensor_tensor(eq, eq, m.order[:, :, :], ALU.mult))
    chain.then(nc.vector.tensor_reduce(best, eq, AX.X, ALU.max))
    chain.then(nc.vector.tensor_tensor(onehot, eq, best.unsqueeze(2).broadcast_to((T, B, NE)), ALU.is_equal))


def mixture_golden(nc, m):
    name = "L0f"
    w = m.w
    CENTER, LOWER, UPPER = 0.36787944117144233, 0.5 - 0.28768207245178085, 0.5
    N = 2 * NE
    with ExitStack() as ctx:
        s = Stage(nc, ctx, name)
        q = ln_sems(s)
        small = [s.sb(f"r{i}", [T, B, NE]) for i in range(8)]
        inh, dist, wz, fb, mask, t1, t2, zone = small
        sums = [s.sb(f"s{i}", [T, B]) for i in range(4)]
        itemp = s.sb("itemp", [T, 1])
        WT = s.sb("WT", [NE, TOK])
        SG = s.sb("SG", [128, 2, HALF])
        H = s.sb("H", [128, 2, HALF])
        pG = s.ps("pG", [128, 2, 512])
        pU = s.ps("pU", [128, 2, 512])
        pW = s.ps("pW", [128, 2, 512])
        pY = s.ps("pY", [128, 2, 512])
        vch = s.sem("vector_own")
        s_tp, s_lg, s_it = s.sem("temperature_psum"), s.sem("logits"), s.sem("inverse_temperature")
        s_ex, s_ds, s_fw = s.sem("exp_of_logits"), s.sem("distances"), s.sem("exp_of_distances")
        s_rw, s_wt, s_wts = s.sem("routing_weights"), s.sem("weightsT_psum"), s.sem("weightsT_sbuf")
        s_g, s_sg, s_h, s_y = s.sem("gate_up"), s.sem("silu"), s.sem("hidden"), s.sem("out")

        with nc.Block(no_gpsimd_drain=True) as block:

            @block.gpsimd
            def _(pool):
                ln_gpsimd(nc, pool, m, q)

            @block.vector
            def _(dve):
                chain = Chain(dve, vch)
                ln_vector(nc, dve, chain, m, q)
                dve.wait_ge(s_tp, 1)
                chain.then(nc.vector.reciprocal(itemp[:, :], pU[0:T, 0, 0:1]))
                nc.vector.tensor_scalar(itemp[:, :], itemp[:, :], -1.0, None, ALU.mult).then_inc(s_it, 1)
                dve.wait_ge(s_ex, 1)
                chain.then(nc.vector.tensor_scalar(inh[:, :, :], inh[:, :, :], 1.0, None, ALU.add))
                chain.then(nc.vector.reciprocal(inh[:, :, :], inh[:, :, :]))
                chain.then(nc.vector.tensor_scalar(t1[:, :, :], inh[:, :, :], CENTER, None, ALU.subtract))
                nc.vector.scalar_tensor_tensor(out=dist[:, :, :], in0=t1[:, :, :], scalar=-1.0,
                                               in1=t1[:, :, :], op0=ALU.mult, op1=ALU.max).then_inc(s_ds, 1)
                chain.then(nc.vector.tensor_scalar(zone[:, :, :], inh[:, :, :], LOWER, None, ALU.is_ge))
                chain.then(nc.vector.scalar_tensor_tensor(
                    out=zone[:, :, :], in0=inh[:, :, :], scalar=UPPER, in1=zone[:, :, :],
                    op0=ALU.is_le, op1=ALU.mult))
                dve.wait_ge(s_fw, 2)
                chain.then(nc.vector.tensor_tensor(wz[:, :, :], wz[:, :, :], zone[:, :, :], ALU.mult))
                first_largest(nc, chain, m, fb[:, :, :], sums[0][:, :], t1[:, :, :], sums[1][:, :],
                              mask[:, :, :])
                chain.then(nc.vector.scalar_tensor_tensor(
                    out=zone[:, :, :], in0=mask[:, :, :], scalar=-2.0, in1=fb[:, :, :],
                    op0=ALU.mult, op1=ALU.add))
                first_largest(nc, chain, m, zone[:, :, :], sums[0][:, :], t1[:, :, :], sums[1][:, :],
                              t2[:, :, :])
                chain.then(nc.vector.tensor_tensor(mask[:, :, :], mask[:, :, :], t2[:, :, :], ALU.add))
                chain.then(nc.vector.tensor_tensor(fb[:, :, :], fb[:, :, :], mask[:, :, :], ALU.mult))

                def over_sum(v, sm):
                    chain.then(nc.vector.tensor_reduce(sm, v, AX.X, ALU.add))
                    chain.then(nc.vector.tensor_scalar(sm, sm, 1e-8, None, ALU.max))
                    chain.then(nc.vector.reciprocal(sm, sm))
                    chain.then(nc.vector.tensor_tensor(v, v, sm.unsqueeze(2).broadcast_to((T, B, NE)), ALU.mult))

                over_sum(fb[:, :, :], sums[0][:, :])
                chain.then(nc.vector.tensor_reduce(sums[2][:, :], wz[:, :, :], AX.X, ALU.add))
                chain.then(nc.vector.tensor_scalar(sums[3][:, :], sums[2][:, :], 1e-8, None, ALU.is_lt))
                chain.then(nc.vector.tensor_tensor(t1[:, :, :], fb[:, :, :], wz[:, :, :], ALU.subtract))
                chain.then(nc.vector.tensor_tensor(
                    t1[:, :, :], t1[:, :, :], sums[3][:, :].unsqueeze(2).broadcast_to((T, B, NE)), ALU.mult))
                chain.then(nc.vector.tensor_tensor(wz[:, :, :], wz[:, :, :], t1[:, :, :], ALU.add))
                over_sum(wz[:, :, :], sums[0][:, :])
                nc.vector.memset(itemp[:, :], 0.0).then_inc(s_rw, 1)
                dve.wait_ge(s_wt, 1)
                nc.vector.tensor_copy(WT[:, 0:HALF], pG[0:NE, 0, 0:HALF])
                nc.vector.tensor_copy(WT[:, HALF:TOK], pG[0:NE, 1, 0:HALF]).then_inc(s_wts, 1)
                for n in range(N):
                    dve.wait_ge(s_sg, n + 1)
                    if n >= 2:
                        dve.wait_ge(s_y, n - 1)
                    chain.then(nc.vector.tensor_tensor(H[:, n % 2, :], SG[:, n % 2, :], pU[:, n % 2, 0:HALF],
                                                       ALU.mult))
                    nc.vector.tensor_tensor(H[:, n % 2, :], H[:, n % 2, :], pW[:, n % 2, 0:HALF],
                                            ALU.mult).then_inc(s_h, 1)
                for h in range(2):
                    dve.wait_ge(s_y, N - 1 + h)
                    nc.vector.tensor_tensor(m.X[:, h * HB:(h + 1) * HB, :], m.X[:, h * HB:(h + 1) * HB, :],
                                            pY[0:T, h, :].rearrange("p (b d) -> p b d", d=D), ALU.add)

            @block.scalar
            def _(act):
                ln_scalar(nc, act, m, q, [pG[:, 0, :], pG[:, 1, :]])
                act.wait_ge(s_lg, 1)
                act.wait_ge(s_it, 1)
                nc.scalar.activation(inh[:, :, :], pW[0:T, 0, 0:B * NE].rearrange("p (b e) -> p b e", e=NE),
                                     ACT.Exp, scale=itemp[:, 0:1]).then_inc(s_ex, 1)
                act.wait_ge(s_ds, 1)
                nc.scalar.activation(wz[:, :, :], dist[:, :, :], ACT.Exp, scale=-10.0).then_inc(s_fw, 1)
                nc.scalar.activation(fb[:, :, :], dist[:, :, :], ACT.Exp, scale=-1.0 / 0.3).then_inc(s_fw, 1)
                for n in range(N):
                    act.wait_ge(s_g, n + 1)
                    if n >= 2:
                        act.wait_ge(s_h, n - 1)
                    nc.scalar.activation(SG[:, n % 2, :], pG[:, n % 2, 0:HALF], ACT.Silu).then_inc(s_sg, 1)

            @block.tensor
            def _(pe):
                pe.wait_ge(m.loaded[name], m.load_total[name])
                nc.tensor.matmul(pU[0:T, 0, 0:1], m.ones[0:1, 0:T], w["f0t"][:, :], start=True, stop=True)\
                  .then_inc(s_tp, 1)
                ln_tensor(nc, pe, m, q, [pG[:, 0, :], pG[:, 1, :]])
                pe.wait_ge(q.xTs, 2)
                for b in range(B):
                    last = nc.tensor.matmul(pW[0:T, 0, b * NE:(b + 1) * NE], m.XNT[:, b * T:(b + 1) * T],
                                            w["f0r"][:, :], start=True, stop=True)
                last.then_inc(s_lg, 1)
                pe.wait_ge(s_rw, 1)
                for b in range(B):
                    last = nc.tensor.transpose(pG[0:NE, b // HB, (b % HB) * T:(b % HB + 1) * T], wz[:, b, :],
                                               m.ident[0:T, 0:T])
                last.then_inc(s_wt, 1)
                pe.wait_ge(s_wts, 1)

                def up(n):
                    e, h = n // 2, n % 2
                    if n >= 2:
                        pe.wait_ge(s_h, n - 1)
                    x = m.XNT[:, h * HALF:(h + 1) * HALF]
                    nc.tensor.matmul(pG[:, n % 2, 0:HALF], w["f0g"][:, e, :], x, start=True, stop=True)
                    nc.tensor.matmul(pU[:, n % 2, 0:HALF], w["f0u"][:, e, :], x, start=True, stop=True)
                    nc.tensor.matmul(pW[:, n % 2, 0:HALF], m.sel[:, e, :], WT[:, h * HALF:(h + 1) * HALF],
                                     start=True, stop=True).then_inc(s_g, 1)

                up(0)
                for n in range(N):
                    if n + 1 < N:
                        up(n + 1)
                    e, h = n // 2, n % 2
                    pe.wait_ge(s_h, n + 1)
                    for i in range(HB):
                        last = nc.tensor.matmul(pY[0:T, h, i * D:(i + 1) * D], H[:, n % 2, i * T:(i + 1) * T],
                                                w["f0d"][:, e, :], start=(e == 0 and i == 0),
                                                stop=(e == NE - 1), skip_group_check=True)
                    last.then_inc(s_y, 1)



def attention_regrouped(nc, m):
    name = "L1a"
    w = m.w
    R = T // 4
    FL = T * 32
    RC = 5
    N = R // RC
    with ExitStack() as ctx:
        s = Stage(nc, ctx, name)
        q = ln_sems(s)
        scr = nc.dram_tensor("regroup_in", (32, 4, FL), F32).ap()
        scr2 = nc.dram_tensor("regroup_out", (32, FL), F32).ap()
        free = m.CT[:, :, :].rearrange("p b k -> p (b k)")
        QK = free[0:T, 0:B * 512].rearrange("t (b c) -> t b c", b=B)
        S1, S2 = [free[:, B * 512 * (i + 1):B * 512 * (i + 1) + 2 * RC * NH * NH]
                  .rearrange("p (u r h k) -> p u r h k", u=2, r=RC, h=NH) for i in (0, 1)]
        L = s.sb("L", [128, 4, NH, R, 2])
        mx = s.sb("mx", [128, 2, RC, NH])
        den = s.sb("den", [128, 2, RC, NH])
        OA = s.sb("OA", [128, 2, 2, RC, NH])
        O = s.sb("O", [128, NH, R, 2])
        OX = s.sb("OX", [T, B, D])
        pT = s.ps("pT", [128, 2, 512])
        pQ = s.ps("pQ", [128, 4, 512])
        pY = s.ps("pY", [128, 2, 512])
        vch, gch = s.sem("vector_own"), s.sem("gpsimd_own")
        s_q, s_qs = s.sem("qkvw_psum"), s.sem("qkvw_sbuf")
        s_d, s_l = s.sem("in_dram"), s.sem("regrouped")
        s_p0, s_sc = s.sem("products_d1"), s.sem("less_max")
        s_e, s_pv, s_dn = s.sem("exps"), s.sem("weighted_d1"), s.sem("used")
        s_o, s_od, s_ox = s.sem("out_sbuf"), s.sem("out_in_dram"), s.sem("out_token_major")
        s_t, s_ts, s_y = s.sem("outT_psum"), s.sem("outT_sbuf"), s.sem("y_psum")

        def at(i, n, d):
            return L[:, i, :, n * RC:(n + 1) * RC, d].rearrange("p h r -> p r h")

        def rows(ap):
            return ap.unsqueeze(3).broadcast_to((128, RC, NH, NH))

        def cols(ap):
            return ap.unsqueeze(2).broadcast_to((128, RC, NH, NH))

        with nc.Block(no_gpsimd_drain=True) as block:

            @block.sync
            def _(sp):
                for b in range(B):
                    sp.wait_ge(s_qs, b + 1)
                    for i in range(4):
                        sp.dma_start(scr[i * B + b].rearrange("j (t c) -> t j c", c=32),
                                     QK[:, b, i * 128:(i + 1) * 128].rearrange("t (j c) -> t j c", c=32))\
                          .then_inc(s_d, 16)
                sp.wait_ge(s_d, 16 * 4 * B)
                for rq in range(4):
                    sp.dma_start(L[rq * 32:(rq + 1) * 32, :, :, :, :].rearrange("n j h r d -> n (j h) (r d)"),
                                 scr.rearrange("n j (h x) -> n (j h) x", x=2 * T)[:, :, 2 * R * rq:2 * R * (rq + 1)])\
                      .then_inc(s_l, 16)
                sp.wait_ge(s_o, 1)
                for rq in range(4):
                    sp.dma_start(scr2.rearrange("n (h x) -> n h x", x=2 * T)[:, :, 2 * R * rq:2 * R * (rq + 1)],
                                 O[rq * 32:(rq + 1) * 32, :, :, :].rearrange("n h r d -> n h (r d)"))\
                      .then_inc(s_od, 16)
                sp.wait_ge(s_od, 64)
                sp.dma_start(OX[:, :, :], scr2.rearrange("n x -> (n x)").rearrange("(b t d) -> t b d", t=T, d=D))\
                  .then_inc(s_ox, 16)

            @block.gpsimd
            def _(pool):
                ln_gpsimd(nc, pool, m, q)
                pool.wait_ge(s_l, 64)

                def products(n):
                    if n >= 2:
                        pool.wait_ge(s_dn, n - 1)
                    nc.gpsimd.tensor_tensor(S2[:, n % 2], rows(at(0, n, 1)), cols(at(1, n, 1)), ALU.mult)\
                      .then_inc(s_p0, 1)

                products(0)
                for n in range(N):
                    if n + 1 < N:
                        products(n + 1)
                    pool.wait_ge(s_e, n + 1)
                    nc.gpsimd.tensor_tensor(S2[:, n % 2], S1[:, n % 2], cols(at(2, n, 1)), ALU.mult)\
                      .then_inc(s_pv, 1)

            @block.vector
            def _(dve):
                chain = Chain(dve, vch)
                ln_vector(nc, dve, chain, m, q)
                dve.wait_ge(s_l, 64)

                def scores(n):
                    if n >= 2:
                        dve.wait_ge(s_pv, n - 1)
                    chain.then(nc.vector.tensor_tensor(S1[:, n % 2], rows(at(0, n, 0)), cols(at(1, n, 0)), ALU.mult))
                    dve.wait_ge(s_p0, n + 1)
                    chain.then(nc.vector.tensor_tensor(S1[:, n % 2], S1[:, n % 2], S2[:, n % 2], ALU.add))
                    chain.then(nc.vector.tensor_reduce(mx[:, n % 2], S1[:, n % 2], AX.X, ALU.max))
                    nc.vector.tensor_tensor(S1[:, n % 2], S1[:, n % 2], rows(mx[:, n % 2]),
                                            ALU.subtract).then_inc(s_sc, 1)

                scores(0)
                for n in range(N):
                    if n + 1 < N:
                        scores(n + 1)
                    dve.wait_ge(s_e, n + 1)
                    chain.then(nc.vector.tensor_reduce(den[:, n % 2], S1[:, n % 2], AX.X, ALU.add))
                    chain.then(nc.vector.reciprocal(den[:, n % 2], den[:, n % 2]))
                    dve.wait_ge(s_pv, n + 1)
                    chain.then(nc.vector.tensor_reduce(OA[:, n % 2, 1], S2[:, n % 2], AX.X, ALU.add))
                    chain.then(nc.vector.tensor_tensor(S1[:, n % 2], S1[:, n % 2], cols(at(2, n, 0)), ALU.mult))
                    chain.then(nc.vector.tensor_reduce(OA[:, n % 2, 0], S1[:, n % 2], AX.X, ALU.add))
                    nc.vector.tensor_tensor(OA[:, n % 2, 0], OA[:, n % 2, 0], den[:, n % 2], ALU.mult)
                    chain.then(nc.vector.tensor_tensor(OA[:, n % 2, 1], OA[:, n % 2, 1], den[:, n % 2], ALU.mult))
                    for d in range(2):
                        last = nc.vector.tensor_tensor(
                            O[:, :, n * RC:(n + 1) * RC, d].rearrange("p h r -> p r h"), OA[:, n % 2, d],
                            at(3, n, d), ALU.mult)
                    last.then_inc(s_dn, 1)
                dve.wait_ge(s_dn, N)
                nc.vector.memset(mx[:, 0], 0.0).then_inc(s_o, 1)
                for h in range(2):
                    dve.wait_ge(s_y, h + 1)
                    nc.vector.tensor_tensor(m.X[:, h * HB:(h + 1) * HB, :], m.X[:, h * HB:(h + 1) * HB, :],
                                            pY[0:T, h, :].rearrange("p (b d) -> p b d", d=D), ALU.add)

            @block.scalar
            def _(act):
                ln_scalar(nc, act, m, q, [pT[:, 0, :], pT[:, 1, :]])
                for b in range(B):
                    act.wait_ge(s_q, b + 1)
                    nc.scalar.copy(QK[:, b, :], pQ[0:T, b % 4, :]).then_inc(s_qs, 1)
                for n in range(N):
                    act.wait_ge(s_sc, n + 1)
                    nc.scalar.activation(S1[:, n % 2], S1[:, n % 2], ACT.Exp, scale=2.0 ** -0.5).then_inc(s_e, 1)
                for h in range(2):
                    act.wait_ge(s_t, h + 1)
                    nc.scalar.copy(m.XNT[:, h * HALF:(h + 1) * HALF], pT[:, h, 0:HALF]).then_inc(s_ts, 1)

            @block.tensor
            def _(pe):
                ln_tensor(nc, pe, m, q, [pT[:, 0, :], pT[:, 1, :]])
                pe.wait_ge(m.loaded[name], m.load_total[name])
                pe.wait_ge(q.xTs, 2)
                for b in range(B):
                    if b >= 4:
                        pe.wait_ge(s_qs, b - 3)
                    nc.tensor.matmul(pQ[0:T, b % 4, :], m.XNT[:, b * T:(b + 1) * T], w["a1w"][:, :],
                                     start=True, stop=True).then_inc(s_q, 1)
                pe.wait_ge(s_qs, B)
                pe.wait_ge(s_ox, 16)
                for h in range(2):
                    for i in range(HB):
                        last = nc.tensor.transpose(pT[:, h, i * T:(i + 1) * T], OX[:, h * HB + i, :],
                                                   m.ident[0:T, 0:T])
                    last.then_inc(s_t, 1)
                for h in range(2):
                    pe.wait_ge(s_ts, h + 1)
                    for i in range(HB):
                        b = h * HB + i
                        last = nc.tensor.matmul(pY[0:T, h, i * D:(i + 1) * D], m.XNT[:, b * T:(b + 1) * T],
                                                w["a1o"][:, :], start=True, stop=True)
                    last.then_inc(s_y, 1)



def attention_wide(nc, m):
    name = "L2x"
    w = m.w
    C = SC // 4
    SCALE = float(D) ** -0.5
    with ExitStack() as ctx:
        s = Stage(nc, ctx, name)
        q = ln_sems(s)
        Mqk = s.sb("Mqk", [128, 128])
        WvT = s.sb("WvT", [128, 128])
        QS = s.sb("QS", [128, TOK])
        nmx = s.sb("nmx", [T, 2])
        E = s.sb("E", [T, 2, SC])
        sm = s.sb("sm", [T, 4])
        ET = s.sb("ET", [128, NKT, T])
        U = s.sb("U", [T, D])
        UT = s.sb("UT", [128, T])
        pS = s.ps("pS", [128, 4, 512])
        pE = s.ps("pE", [128, 3, 512])
        pO = s.ps("pO", [128, 512])
        vch = s.sem("vector_own")
        s_w, s_ws = s.sem("weights_psum"), s.sem("weights_ready")
        s_q, s_qs = s.sem("q_psum"), s.sem("q_sbuf")
        s_s, s_m, s_e = s.sem("scores"), s.sem("maximum"), s.sem("exps")
        s_t, s_tc, s_tc2 = s.sem("expsT_psum"), s.sem("expsT_vector"), s.sem("expsT_scalar")
        s_u, s_us = s.sem("sums_psum"), s.sem("sums_scaled")
        s_ut, s_uts, s_y, s_x = s.sem("sumsT_psum"), s.sem("sumsT_sbuf"), s.sem("y_psum"), s.sem("added")

        with nc.Block(no_gpsimd_drain=True) as block:

            @block.gpsimd
            def _(pool):
                ln_gpsimd(nc, pool, m, q)

            @block.vector
            def _(dve):
                chain = Chain(dve, vch)
                dve.wait_ge(s_w, 1)
                nc.vector.tensor_copy(Mqk[:, :], pE[:, 2, 0:128])
                nc.vector.tensor_copy(WvT[:, :], pE[:, 2, 128:256]).then_inc(s_ws, 1)
                ln_vector(nc, dve, chain, m, q)

                def maximum(b):
                    dve.wait_ge(s_s, b + 1)
                    if b >= 2:
                        dve.wait_ge(s_e, b - 1)
                    chain.then(nc.vector.tensor_reduce(nmx[:, b % 2:b % 2 + 1], pS[0:T, :, 0:C], AX.XY,
                                                       ALU.max, negate=True))
                    nc.vector.tensor_scalar(nmx[:, b % 2:b % 2 + 1], nmx[:, b % 2:b % 2 + 1], SCALE, None,
                                            ALU.mult).then_inc(s_m, 1)

                maximum(0)
                for b in range(B):
                    dve.wait_ge(s_t, 3 * b + 1)
                    if b >= 1:
                        dve.wait_ge(s_u, b)
                    nc.vector.tensor_copy(ET[:, 0:4, :], pE[:, 0, 0:4 * T].rearrange("p (k t) -> p k t", t=T))\
                      .then_inc(s_tc, 1)
                    if b + 1 < B:
                        maximum(b + 1)
                    dve.wait_ge(s_t, 3 * b + 3)
                    nc.vector.tensor_copy(ET[:, 8:11, :], pE[:, 2, 0:3 * T].rearrange("p (k t) -> p k t", t=T))
                    nc.vector.tensor_copy(ET[0:TAIL, 11, :], pE[0:TAIL, 2, 3 * T:4 * T]).then_inc(s_tc, 1)
                    chain.then(nc.vector.reciprocal(sm[:, 2:3], sm[:, b % 2:b % 2 + 1]))
                    dve.wait_ge(s_u, b + 1)
                    nc.vector.tensor_scalar(U[:, :], pO[0:T, 0:D], sm[:, 2:3], None, ALU.mult).then_inc(s_us, 1)
                    dve.wait_ge(s_y, b + 1)
                    nc.vector.tensor_tensor(m.X[:, b, :], m.X[:, b, :], pO[0:T, 256:256 + D], ALU.add)\
                      .then_inc(s_x, 1)

            @block.scalar
            def _(act):
                ln_scalar(nc, act, m, q, [pE[:, 0, :], pE[:, 1, :]])
                for h in range(2):
                    act.wait_ge(s_q, h + 1)
                    nc.scalar.copy(QS[:, h * HALF:(h + 1) * HALF], pS[:, h, 0:HALF]).then_inc(s_qs, 1)

                def exps(b):
                    act.wait_ge(s_m, b + 1)
                    if b >= 2:
                        act.wait_ge(s_us, b - 1)
                    nc.scalar.activation(E[:, b % 2, :].rearrange("p (c k) -> p c k", k=C), pS[0:T, :, 0:C],
                                         ACT.Exp, bias=nmx[:, b % 2:b % 2 + 1], scale=SCALE,
                                         accum_out=sm[:, b % 2:b % 2 + 1]).then_inc(s_e, 1)

                exps(0)
                for b in range(B):
                    if b + 1 < B:
                        exps(b + 1)
                    act.wait_ge(s_t, 3 * b + 2)
                    nc.scalar.copy(ET[:, 4:8, :], pE[:, 1, 0:4 * T].rearrange("p (k t) -> p k t", t=T))\
                      .then_inc(s_tc2, 1)
                    act.wait_ge(s_ut, b + 1)
                    nc.scalar.copy(UT[:, :], pO[:, 128:128 + T]).then_inc(s_uts, 1)

            @block.tensor
            def _(pe):
                pe.wait_ge(m.loaded[name], m.load_total[name])
                nc.tensor.matmul(pE[:, 2, 0:128], w["x2q"][:, :], w["x2k"][:, :], start=True, stop=True)
                nc.tensor.transpose(pE[:, 2, 128:256], w["x2v"][:, :], m.ident[:, :]).then_inc(s_w, 1)
                ln_tensor(nc, pe, m, q, [pE[:, 0, :], pE[:, 1, :]])
                pe.wait_ge(s_ws, 1)
                for h in range(2):
                    pe.wait_ge(q.xTs, h + 1)
                    nc.tensor.matmul(pS[:, h, 0:HALF], Mqk[:, :], m.XNT[:, h * HALF:(h + 1) * HALF],
                                     start=True, stop=True).then_inc(s_q, 1)
                pe.wait_ge(s_qs, 2)

                def scores(b):
                    if b >= 1:
                        pe.wait_ge(s_e, b)
                    for c in range(4):
                        last = nc.tensor.matmul(pS[0:T, c, 0:C], QS[:, b * T:(b + 1) * T],
                                                m.CT[:, b, c * C:(c + 1) * C], start=True, stop=True)
                    last.then_inc(s_s, 1)

                scores(0)
                for b in range(B):
                    pe.wait_ge(s_e, b + 1)
                    for g in range(3):
                        if b >= 1:
                            if g == 1:
                                pe.wait_ge(s_tc2, b)
                            else:
                                pe.wait_ge(s_tc, 2 * b - (1 if g == 0 else 0))
                        for k in range(4 * g, 4 * g + 4):
                            last = nc.tensor.transpose(pE[0:TILES[k], g, (k % 4) * T:(k % 4 + 1) * T],
                                                       E[:, b % 2, k * 128:k * 128 + TILES[k]],
                                                       m.ident[0:T, 0:T])
                        last.then_inc(s_t, 1)
                    if b + 1 < B:
                        scores(b + 1)
                    pe.wait_ge(s_tc, 2 * b + 2)
                    pe.wait_ge(s_tc2, b + 1)
                    if b >= 1:
                        pe.wait_ge(s_x, b)
                    for k in range(NKT):
                        last = nc.tensor.matmul(pO[0:T, 0:D], ET[0:TILES[k], k, :],
                                                m.ctx_tm[0:TILES[k], b, k, 0:D],
                                                start=(k == 0), stop=(k == NKT - 1))
                    last.then_inc(s_u, 1)
                    pe.wait_ge(s_us, b + 1)
                    nc.tensor.transpose(pO[:, 128:128 + T], U[:, :], m.ident[0:T, 0:T]).then_inc(s_ut, 1)
                    pe.wait_ge(s_uts, b + 1)
                    nc.tensor.matmul(pO[0:T, 256:256 + D], UT[:, :], WvT[:, :], start=True, stop=True)\
                      .then_inc(s_y, 1)



def two_norms_vector(nc, dve, chain, m, q, q2):
    ln_vector(nc, dve, chain, m, q)
    dve.wait_ge(q.norm, B)
    ln_vector(nc, dve, chain, m, q2, src=m.XN, dst=m.XN2)


def add_psum(nc, dve, chain, m, h, out):
    x, xn = m.X[:, h * HB:(h + 1) * HB, :], m.XN[:, h * HB:(h + 1) * HB, :]
    chain.then(nc.vector.tensor_tensor(x, x, xn, ALU.add))
    return nc.vector.tensor_tensor(x, x, out.rearrange("p (b d) -> p b d", d=D), ALU.add)



def attention_fixed_keys(nc, m):
    name = "L2a"
    w = m.w
    N = 32
    W = 32
    with ExitStack() as ctx:
        s = Stage(nc, ctx, name)
        q, q2 = ln_sems(s), ln_sems(s, "ln2")
        wf4 = s.sb("wf4", [128, 4, 4, W])
        KF = s.sb("KF", [128, 4, 128])
        VF = s.sb("VF", [128, 128])
        RL = s.sb("RL", [128, 2, HALF])
        P = s.sb("P", [128, 2, HALF])
        pT = s.ps("pT", [128, 2, 512])
        pS = s.ps("pS", [128, 4, 512])
        pY = s.ps("pY", [128, 2, 512])
        vch = s.sem("vector_own")
        s_w4, s_wt, s_ws = s.sem("keys_repeated"), s.sem("weights_transposed"), s.sem("weights_ready")
        s_s, s_r, s_p, s_y = s.sem("scores"), s.sem("relu"), s.sem("squares"), s.sem("out")

        with nc.Block(no_gpsimd_drain=True) as block:

            @block.gpsimd
            def _(pool):
                ln_gpsimd(nc, pool, m, q)
                ln_gpsimd(nc, pool, m, q2)

            @block.vector
            def _(dve):
                chain = Chain(dve, vch)
                dve.wait_ge(m.loaded[name], m.load_total[name])
                for h in range(4):
                    last = nc.vector.tensor_copy(wf4[:, :, h, :], w["a2f"][:, :].rearrange("c (j d) -> c j d", d=W))
                last.then_inc(s_w4, 1)
                two_norms_vector(nc, dve, chain, m, q, q2)
                dve.wait_ge(s_wt, 1)
                nc.vector.tensor_copy(KF[:, :, :], pS[:, 0, :].rearrange("p (j c) -> p j c", c=128))
                nc.vector.tensor_copy(VF[:, :], pS[:, 1, 0:128]).then_inc(s_ws, 1)
                for n in range(N):
                    dve.wait_ge(s_r, n + 1)
                    if n >= 2:
                        dve.wait_ge(s_y, n - 1)
                    nc.vector.tensor_tensor(P[:, n % 2, :], RL[:, n % 2, :], pS[:, n % 4, 0:HALF],
                                            ALU.mult).then_inc(s_p, 1)
                for h in range(2):
                    dve.wait_ge(s_y, N // 2 * (h + 1))
                    add_psum(nc, dve, chain, m, h, pY[0:T, h, :])

            @block.scalar
            def _(act):
                ln_scalar(nc, act, m, q2, [pT[:, 0, :], pT[:, 1, :]], (w["a2g"], w["a2b"]))
                for n in range(N):
                    act.wait_ge(s_s, n + 1)
                    if n >= 2:
                        act.wait_ge(s_p, n - 1)
                    nc.scalar.activation(RL[:, n % 2, :], pS[:, n % 4, 0:HALF], ACT.Relu).then_inc(s_r, 1)

            @block.tensor
            def _(pe):
                pe.wait_ge(s_w4, 1)
                for j in range(4):
                    nc.tensor.transpose(pS[:, 0, j * 128:(j + 1) * 128], wf4[:, j, :, :], m.ident[:, :])
                nc.tensor.transpose(pS[:, 1, 0:128], w["a2p"][:, :], m.ident[:, :]).then_inc(s_wt, 1)
                ln_tensor(nc, pe, m, q2, [pT[:, 0, :], pT[:, 1, :]], m.XN2)
                pe.wait_ge(s_ws, 1)
                pe.wait_ge(q2.xTs, 2)

                def scores(n):
                    h, j = n // 4 % 4, n % 4
                    half = n // 16
                    if n >= 4:
                        pe.wait_ge(s_p, n - 3)
                    nc.tensor.matmul(pS[:, n % 4, 0:HALF], KF[W * h:W * (h + 1), j, :],
                                     m.XNT[W * h:W * (h + 1), half * HALF:(half + 1) * HALF],
                                     start=True, stop=True).then_inc(s_s, 1)

                for n in range(3):
                    scores(n)
                for n in range(N):
                    if n + 3 < N:
                        scores(n + 3)
                    h, j, half = n // 4 % 4, n % 4, n // 16
                    pe.wait_ge(s_p, n + 1)
                    for i in range(HB):
                        last = nc.tensor.matmul(pY[0:T, half, i * D + W * h:i * D + W * (h + 1)],
                                                P[:, n % 2, i * T:(i + 1) * T], VF[:, W * j:W * (j + 1)],
                                                start=(n % 16 == 0 and i == 0), stop=(j == 3),
                                                skip_group_check=True)
                    last.then_inc(s_y, 1)



def mixture_top1(nc, m):
    name = "L2f"
    w = m.w
    CAPACITY = 256
    IT = 4
    N = 2 * NE
    with ExitStack() as ctx:
        s = Stage(nc, ctx, name)
        q, q2 = ln_sems(s), ln_sems(s, "ln2")
        gwT = s.sb("gwT", [128, NE])
        lg, eq, oh, pre, rk = [s.sb(f"r{i}", [T, B, NE]) for i in range(5)]
        top, best, wt, keep = [s.sb(f"s{i}", [T, B]) for i in range(4)]
        OHT = s.sb("OHT", [NE, TOK])
        XM = s.sb("XM", [128, 2, HALF])
        H = s.sb("H", [128, 2, IT, HALF])
        YW = s.sb("YW", [T, HB, D])
        pC = s.ps("pC", [128, 2, 512])
        pU = s.ps("pU", [128, 4, 512])
        pY = s.ps("pY", [128, 2, 512])
        vch = s.sem("vector_own")
        s_wt, s_ws, s_lg, s_oh = s.sem("router_transposed"), s.sem("router_ready"), s.sem("logits"), s.sem("one_hot")
        s_dl, s_ex, s_rk = s.sem("logits_less_max"), s.sem("exp_of_logits"), s.sem("ranks")
        s_ot, s_ots = s.sem("one_hotT_psum"), s.sem("one_hotT_sbuf")
        s_c, s_xm = s.sem("mask_spread"), s.sem("tokens_masked")
        s_u, s_h, s_y = s.sem("up"), s.sem("gelu"), s.sem("out")

        free = m.ctx_tm[:, :, :, :].rearrange("p b k d -> p (b k d)")
        wi = free[:, 0:NE * 512].rearrange("p (e i) -> p e i", e=NE)
        wo = free[:, NE * 512:2 * NE * 512].rearrange("p (e i d) -> p e i d", e=NE, d=D)
        s_wi, s_wo = s.sem("wi_loaded"), s.sem("wo_loaded")

        with nc.Block(no_gpsimd_drain=True) as block:

            @block.sync
            def _(sp):
                for b in range(B):
                    sp.wait_ge(m.ctx_loaded[b], 32 * m.ctx_times)
                for e in range(0, NE, 2):
                    sp.dma_start(wi[:, e:e + 2, :], m.a["L2_ffn_wi"][e:e + 2].rearrange("e d i -> d e i"))\
                      .then_inc(s_wi, 16)
                    sp.dma_start(wo[:, e:e + 2, :, :].rearrange("p e i d -> p (e i) d"),
                                 m.a["L2_ffn_wo"][e:e + 2].rearrange("e (i p) d -> p (e i) d", p=128))\
                      .then_inc(s_wo, 16)

            @block.gpsimd
            def _(pool):
                ln_gpsimd(nc, pool, m, q)
                ln_gpsimd(nc, pool, m, q2)

            @block.vector
            def _(dve):
                chain = Chain(dve, vch)
                dve.wait_ge(s_wt, 1)
                nc.vector.tensor_copy(gwT[:, :], pU[:, 0, 0:NE]).then_inc(s_ws, 1)
                two_norms_vector(nc, dve, chain, m, q, q2)
                dve.wait_ge(s_lg, 1)
                chain.then(nc.vector.tensor_copy(lg[:, :, :], pU[0:T, 1, 0:B * NE].rearrange("p (b e) -> p b e", e=NE)))
                first_largest(nc, chain, m, lg[:, :, :], top[:, :], eq[:, :, :], best[:, :], oh[:, :, :])
                chain.then(nc.vector.memset(pre[:, 0, :], 0.0))
                for b in range(1, B):
                    ins = nc.vector.tensor_tensor(pre[:, b, :], pre[:, b - 1, :], oh[:, b - 1, :], ALU.add)
                    if b < B - 1:
                        chain.then(ins)
                ins.then_inc(s_oh, 1)
                nc.vector.tensor_tensor(lg[:, :, :], lg[:, :, :], top[:, :].unsqueeze(2).broadcast_to((T, B, NE)),
                                        ALU.subtract).then_inc(s_dl, 1)
                dve.wait_ge(s_ot, 1)
                nc.vector.tensor_copy(OHT[:, 0:HALF], pC[0:NE, 0, 0:HALF])
                nc.vector.tensor_copy(OHT[:, HALF:TOK], pC[0:NE, 1, 0:HALF]).then_inc(s_ots, 1)
                dve.wait_ge(s_ex, 1)
                chain.then(nc.vector.tensor_reduce(wt[:, :], eq[:, :, :], AX.X, ALU.add))
                chain.then(nc.vector.reciprocal(wt[:, :], wt[:, :]))
                dve.wait_ge(s_rk, 1)
                chain.then(nc.vector.tensor_tensor(
                    rk[:, :, :], pU[0:T, 2, 0:B * NE].rearrange("p (b e) -> p b e", e=NE), oh[:, :, :], ALU.mult))
                chain.then(nc.vector.tensor_reduce(keep[:, :], rk[:, :, :], AX.X, ALU.add))
                chain.then(nc.vector.tensor_scalar(keep[:, :], keep[:, :], float(CAPACITY), None, ALU.is_lt))
                chain.then(nc.vector.tensor_tensor(wt[:, :], wt[:, :], keep[:, :], ALU.mult))
                for n in range(N):
                    h = n % 2
                    dve.wait_ge(s_c, n + 1)
                    if n >= 2:
                        dve.wait_ge(s_u, IT * (n - 1))
                    nc.vector.tensor_tensor(XM[:, n % 2, :], m.XNT[:, h * HALF:(h + 1) * HALF],
                                            pC[:, n % 2, 0:HALF], ALU.mult).then_inc(s_xm, 1)
                for h in range(2):
                    dve.wait_ge(s_y, N - 1 + h)
                    x, xn = m.X[:, h * HB:(h + 1) * HB, :], m.XN[:, h * HB:(h + 1) * HB, :]
                    nc.vector.tensor_tensor(x, x, xn, ALU.add)
                    chain.then(nc.vector.tensor_tensor(
                        YW[:, :, :], pY[0:T, h, :].rearrange("p (b d) -> p b d", d=D),
                        wt[:, h * HB:(h + 1) * HB].unsqueeze(2).broadcast_to((T, HB, D)), ALU.mult))
                    chain.then(nc.vector.tensor_tensor(x, x, YW[:, :, :], ALU.add))

            @block.scalar
            def _(act):
                act.wait_ge(m.loaded[name], m.load_total[name])
                ln_scalar(nc, act, m, q2, [pC[:, 0, :], pC[:, 1, :]], (w["f2g"], w["f2b"]))
                act.wait_ge(s_dl, 1)
                nc.scalar.activation(eq[:, :, :], lg[:, :, :], ACT.Exp).then_inc(s_ex, 1)
                for u in range(N * IT):
                    act.wait_ge(s_u, u + 1)
                    n = u // IT
                    if n >= 2:
                        act.wait_ge(s_y, n - 1)
                    nc.scalar.activation(H[:, n % 2, u % IT, :], pU[:, u % 4, 0:HALF], ACT.Gelu).then_inc(s_h, 1)

            @block.tensor
            def _(pe):
                pe.wait_ge(m.loaded[name], m.load_total[name])
                nc.tensor.transpose(pU[:, 0, 0:NE], w["f2r"][:, :], m.ident[0:NE, 0:NE]).then_inc(s_wt, 1)
                ln_tensor(nc, pe, m, q2, [pC[:, 0, :], pC[:, 1, :]], m.XN2)
                pe.wait_ge(s_ws, 1)
                pe.wait_ge(q2.xTs, 2)
                for b in range(B):
                    last = nc.tensor.matmul(pU[0:T, 1, b * NE:(b + 1) * NE], m.XNT[:, b * T:(b + 1) * T],
                                            gwT[:, :], start=True, stop=True)
                last.then_inc(s_lg, 1)
                pe.wait_ge(s_oh, 1)
                for b in range(B):
                    last = nc.tensor.transpose(pC[0:NE, b // HB, (b % HB) * T:(b % HB + 1) * T], oh[:, b, :],
                                               m.ident[0:T, 0:T])
                last.then_inc(s_ot, 1)
                nc.tensor.matmul(pU[0:T, 2, 0:B * NE], m.before[:, :], oh[:, :, :].rearrange("p b e -> p (b e)"),
                                 start=True, stop=False)
                nc.tensor.matmul(pU[0:T, 2, 0:B * NE], m.ones[0:T, 0:T], pre[:, :, :].rearrange("p b e -> p (b e)"),
                                 start=False, stop=True).then_inc(s_rk, 1)
                pe.wait_ge(s_ots, 1)
                pe.wait_ge(s_ex, 1)

                def spread(n):
                    e, h = n // 2, n % 2
                    if n >= 2:
                        pe.wait_ge(s_xm, n - 1)
                    nc.tensor.matmul(pC[:, n % 2, 0:HALF], m.sel[:, e, :], OHT[:, h * HALF:(h + 1) * HALF],
                                     start=True, stop=True).then_inc(s_c, 1)

                def up(n, i):
                    e = n // 2
                    u = n * IT + i
                    if i == 0:
                        pe.wait_ge(s_xm, n + 1)
                    if u >= 4:
                        pe.wait_ge(s_h, u - 3)
                    nc.tensor.matmul(pU[:, u % 4, 0:HALF], wi[:, e, i * 128:(i + 1) * 128],
                                     XM[:, n % 2, :], start=True, stop=True).then_inc(s_u, 1)

                def down(n, i):
                    e, h = n // 2, n % 2
                    pe.wait_ge(s_h, n * IT + i + 1)
                    for k in range(HB):
                        last = nc.tensor.matmul(pY[0:T, h, k * D:(k + 1) * D], H[:, n % 2, i, k * T:(k + 1) * T],
                                                wo[:, e, i, :], start=(e == 0 and i == 0 and k == 0),
                                                stop=(e == NE - 1 and i == IT - 1), skip_group_check=True)
                    if i == IT - 1:
                        last.then_inc(s_y, 1)

                pe.wait_ge(s_wi, 64)
                pe.wait_ge(s_wo, 64)
                spread(0)
                for n in range(N + 1):
                    if n + 1 < N:
                        spread(n + 1)
                    for i in range(IT):
                        if n < N:
                            up(n, i)
                        if n >= 1:
                            down(n - 1, i)



LEVELS = [1, 2, 4, 8, 16, 32, 64]
TTT_LR = 0.01
DS = 64


def attention_delta_rule(nc, m):
    name = "L3a"
    w = m.w
    NL = len(LEVELS)
    with ExitStack() as ctx:
        s = Stage(nc, ctx, name)
        q, q2 = ln_sems(s), ln_sems(s, "ln2")
        wkT = s.sb("wkT", [128, DS])
        wqT = s.sb("wqT", [128, DS])
        wvT = s.sb("wvT", [128, D])
        KT = s.sb("KT", [DS, TOK])
        QT = s.sb("QT", [DS, TOK])
        V = s.sb("V", [T, B, D])
        LT = m.ctx_tm[0:T, :, :, :].rearrange("p b k d -> p (b k d)")[:, 0:B * NL * T]\
            .rearrange("p (b l t) -> p b l t", b=B, l=NL)
        SQ = s.sb("SQ", [T, B, T])
        X = s.sb("X", [T, 2, HB, T])
        XT = s.sb("XT", [T, 2, HB, T])
        TP = s.sb("TP", [T, 2, HB, T])
        U = s.sb("U", [T, 2, HB, D])
        pA = s.ps("pA", [128, 2, 512])
        pB = s.ps("pB", [128, 2, 512])
        pC = s.ps("pC", [128, 2, 512])
        pD = s.ps("pD", [128, 2, 512])
        vch = s.sem("vector_own")
        s_wt, s_ws = s.sem("weights_transposed"), s.sem("weights_ready")
        s_kq, s_kqs, s_v, s_vs = s.sem("k_q_psum"), s.sem("k_q_sbuf"), s.sem("v_psum"), s.sem("v_sbuf")
        s_kk, s_l = s.sem("k_k_and_k_q"), s.sem("masked")
        s_x0 = s.sem("first_inverse")
        s_t, s_tp = s.sem("l_x_psum"), s.sem("l_x_sbuf")
        s_xx, s_x = s.sem("x_l_x"), s.sem("inverse_updated")
        s_u, s_us, s_y = s.sem("updates_psum"), s.sem("updates_sbuf"), s.sem("y_psum")

        with nc.Block(no_gpsimd_drain=True) as block:

            @block.gpsimd
            def _(pool):
                ln_gpsimd(nc, pool, m, q)
                ln_gpsimd(nc, pool, m, q2)

            @block.vector
            def _(dve):
                chain = Chain(dve, vch)
                dve.wait_ge(s_wt, 1)
                nc.vector.tensor_copy(wkT[:, :], pB[:, 0, 0:DS])
                nc.vector.tensor_copy(wqT[:, :], pB[:, 0, 128:128 + DS])
                nc.vector.tensor_copy(wvT[:, :], pB[:, 0, 256:256 + D]).then_inc(s_ws, 1)
                two_norms_vector(nc, dve, chain, m, q, q2)
                for h in range(2):
                    dve.wait_ge(s_v, h + 1)
                    nc.vector.tensor_scalar(V[:, h * HB:(h + 1) * HB, :],
                                            pD[0:T, h, :].rearrange("p (b d) -> p b d", d=D), TTT_LR, None,
                                            ALU.mult).then_inc(s_vs, 1)
                for b in range(B):
                    dve.wait_ge(m.ctx_loaded[b], 32 * m.ctx_times)
                for b in range(B):
                    dve.wait_ge(s_kk, b + 1)
                    kk = pC[0:T, b % 2, 0:T].unsqueeze(1)
                    chain.then(nc.vector.tensor_tensor(LT[:, b, :, :], kk.broadcast_to((T, NL, T)),
                                                       m.below[0:T, 1:NL + 1, 0:T], ALU.mult))
                    nc.vector.tensor_tensor(SQ[:, b, :], pC[0:T, b % 2, 128:128 + T], m.before[:, :], ALU.mult)
                    nc.vector.tensor_tensor(X[:, b // HB, b % HB, :], pC[0:T, b % 2, 0:T],
                                            m.below[0:T, 0, 0:T], ALU.mult)
                    chain.then(nc.vector.tensor_tensor(XT[:, b // HB, b % HB, :], m.ident[0:T, 0:T],
                                                       LT[:, b, 0, :], ALU.subtract))
                    nc.vector.tensor_tensor(X[:, b // HB, b % HB, :], m.ident[0:T, 0:T],
                                            X[:, b // HB, b % HB, :], ALU.subtract).then_inc(s_l, 1)
                for l in range(1, NL):
                    for h in range(2):
                        n = 2 * (l - 1) + h
                        dve.wait_ge(s_xx, n + 1)
                        pv = lambda p: p[0:T, h, 0:HALF].rearrange("p (b t) -> p b t", t=T)
                        if l < NL - 1:
                            nc.vector.tensor_tensor(X[:, h], X[:, h], pv(pB), ALU.subtract)
                        nc.vector.tensor_tensor(XT[:, h], XT[:, h], pv(pC), ALU.subtract).then_inc(s_x, 1)
                for h in range(2):
                    dve.wait_ge(s_y, h + 1)
                    add_psum(nc, dve, chain, m, h, pD[0:T, h, :])

            @block.scalar
            def _(act):
                act.wait_ge(m.loaded[name], m.load_total[name])
                ln_scalar(nc, act, m, q2, [pA[:, 0, :], pA[:, 1, :]], (w["a3g"], w["a3b"]))
                for h in range(2):
                    cols = slice(h * HALF, (h + 1) * HALF)
                    act.wait_ge(s_kq, 2 * h + 1)
                    nc.scalar.activation(KT[:, cols], pA[0:DS, h, 0:HALF], ACT.Identity,
                                         bias=w["a3bk"][:, 0:1]).then_inc(s_kqs, 1)
                    act.wait_ge(s_kq, 2 * h + 2)
                    nc.scalar.activation(QT[:, cols], pB[0:DS, h, 0:HALF], ACT.Identity,
                                         bias=w["a3bq"][:, 0:1]).then_inc(s_kqs, 1)
                for n in range(2 * (NL - 1)):
                    act.wait_ge(s_t, n + 1)
                    nc.scalar.copy(TP[:, n % 2], pA[0:T, n % 2, 0:HALF].rearrange("p (b t) -> p b t", t=T))\
                      .then_inc(s_tp, 1)
                for h in range(2):
                    act.wait_ge(s_u, h + 1)
                    nc.scalar.copy(U[:, h], pA[0:T, h, :].rearrange("p (b d) -> p b d", d=D)).then_inc(s_us, 1)

            @block.tensor
            def _(pe):
                pe.wait_ge(m.loaded[name], m.load_total[name])
                nc.tensor.transpose(pB[:, 0, 0:DS], w["a3k"][:, :], m.ident[0:DS, 0:DS])
                nc.tensor.transpose(pB[:, 0, 128:128 + DS], w["a3q"][:, :], m.ident[0:DS, 0:DS])
                nc.tensor.transpose(pB[:, 0, 256:256 + D], w["a3v"][:, :], m.ident[:, :]).then_inc(s_wt, 1)
                ln_tensor(nc, pe, m, q2, [pA[:, 0, :], pA[:, 1, :]], m.XN2)
                pe.wait_ge(s_ws, 1)
                for h in range(2):
                    pe.wait_ge(q2.xTs, 2)
                    x = m.XNT[:, h * HALF:(h + 1) * HALF]
                    nc.tensor.matmul(pA[0:DS, h, 0:HALF], wkT[:, :], x, start=True, stop=True).then_inc(s_kq, 1)
                    nc.tensor.matmul(pB[0:DS, h, 0:HALF], wqT[:, :], x, start=True, stop=True).then_inc(s_kq, 1)
                for h in range(2):
                    for i in range(HB):
                        b = h * HB + i
                        nc.tensor.matmul(pD[0:T, h, i * D:(i + 1) * D], m.XNT[:, b * T:(b + 1) * T], wvT[:, :],
                                         start=(i == 0), stop=False, skip_group_check=True)
                        last = nc.tensor.matmul(pD[0:T, h, i * D:(i + 1) * D], m.ones[0:1, 0:T],
                                                w["a3bv"][:, :], start=False, stop=True, skip_group_check=True)
                    last.then_inc(s_v, 1)
                pe.wait_ge(s_kqs, 4)
                for b in range(B):
                    if b >= 2:
                        pe.wait_ge(s_l, b - 1)
                    c = slice(b * T, (b + 1) * T)
                    nc.tensor.matmul(pC[0:T, b % 2, 0:T], KT[:, c], KT[:, c], start=True, stop=True)
                    nc.tensor.matmul(pC[0:T, b % 2, 128:128 + T], KT[:, c], QT[:, c], start=True, stop=True)\
                      .then_inc(s_kk, 1)
                pe.wait_ge(s_l, B)
                for l in range(1, NL):
                    for h in range(2):
                        n = 2 * (l - 1) + h
                        if n >= 2:
                            pe.wait_ge(s_x, n - 1)
                        for i in range(HB):
                            last = nc.tensor.matmul(pA[0:T, h, i * T:(i + 1) * T], LT[:, h * HB + i, l, :],
                                                    X[:, h, i, :], start=True, stop=True)
                        last.then_inc(s_t, 1)
                    for h in range(2):
                        n = 2 * (l - 1) + h
                        pe.wait_ge(s_tp, n + 1)
                        for i in range(HB):
                            if l < NL - 1:
                                nc.tensor.matmul(pB[0:T, h, i * T:(i + 1) * T], XT[:, h, i, :],
                                                 TP[:, h, i, :], start=True, stop=True)
                            last = nc.tensor.matmul(pC[0:T, h, i * T:(i + 1) * T], TP[:, h, i, :],
                                                    XT[:, h, i, :], start=True, stop=True)
                        last.then_inc(s_xx, 1)
                pe.wait_ge(s_vs, 2)
                for h in range(2):
                    pe.wait_ge(s_x, 2 * (NL - 2) + h + 1)
                    for i in range(HB):
                        last = nc.tensor.matmul(pA[0:T, h, i * D:(i + 1) * D], XT[:, h, i, :],
                                                V[:, h * HB + i, :], start=True, stop=True)
                    last.then_inc(s_u, 1)
                for h in range(2):
                    pe.wait_ge(s_us, h + 1)
                    for i in range(HB):
                        last = nc.tensor.matmul(pD[0:T, h, i * D:(i + 1) * D], SQ[:, h * HB + i, :],
                                                U[:, h, i, :], start=True, stop=True)
                    last.then_inc(s_y, 1)



def ffn_binary(nc, m):
    name = "L3f"
    w = m.w
    IT = 4
    N = 2 * IT
    with ExitStack() as ctx:
        s = Stage(nc, ctx, name)
        q = ln_sems(s)
        S1 = s.sb("S1", [128, IT, D])
        S2 = s.sb("S2", [128, IT * 128])
        S1T = s.sb("S1T", [128, IT, 128])
        S2T = s.sb("S2T", [128, IT, 128])
        al = s.sb("al", [128, IT + 1])
        H = s.sb("H", [128, 2, HALF])
        YT = s.sb("YT", [128, TOK])
        pT = s.ps("pT", [128, 2, 512])
        pW = s.ps("pW", [128, 2, 512])
        pH = s.ps("pH", [128, 2, 512])
        pY = s.ps("pY", [128, 2, 512])
        vch = s.sem("vector_own")
        s_al, s_sg = s.sem("mean_magnitudes"), s.sem("signs")
        s_wt, s_ws, s_h, s_g = s.sem("signs_transposed"), s.sem("weights_ready"), s.sem("hidden"), s.sem("gelu")
        s_y, s_yt, s_yy = s.sem("outT_psum"), s.sem("outT_sbuf"), s.sem("out")

        with nc.Block(no_gpsimd_drain=True) as block:

            @block.gpsimd
            def _(pool):
                ln_gpsimd(nc, pool, m, q)

            @block.vector
            def _(dve):
                chain = Chain(dve, vch)
                dve.wait_ge(m.loaded[name], m.load_total[name])
                nc.vector.tensor_reduce(al[:, 0:IT], w["f31"][:, :, :], AX.X, ALU.add, apply_absolute_value=True)
                chain.then(nc.vector.tensor_reduce(al[:, IT:IT + 1], w["f32"][:, :], AX.X, ALU.add,
                                                   apply_absolute_value=True))
                nc.vector.tensor_scalar(al[:, 0:IT], al[:, 0:IT], 1.0 / D, None, ALU.mult)
                nc.vector.tensor_scalar(al[:, IT:IT + 1], al[:, IT:IT + 1], 1.0 / (IT * 128), None, ALU.mult)\
                  .then_inc(s_al, 1)
                ln_vector(nc, dve, chain, m, q)
                dve.wait_ge(s_wt, 2)
                nc.vector.tensor_copy(S1T[:, :, :], pW[:, 0, :].rearrange("p (i c) -> p i c", c=128))
                nc.vector.tensor_copy(S2T[:, :, :], pW[:, 1, :].rearrange("p (i c) -> p i c", c=128)).then_inc(s_ws, 1)
                for h in range(2):
                    dve.wait_ge(s_y, IT * (h + 1))
                    nc.vector.tensor_scalar(YT[:, h * HALF:(h + 1) * HALF], pY[:, h, 0:HALF],
                                            al[:, IT:IT + 1], w["f3b2"][:, 0:1], ALU.mult, ALU.add)\
                      .then_inc(s_yt, 1)
                for h in range(2):
                    dve.wait_ge(s_yy, h + 1)
                    x = m.X[:, h * HB:(h + 1) * HB, :]
                    nc.vector.tensor_tensor(x, x, pT[0:T, h, :].rearrange("p (b d) -> p b d", d=D), ALU.add)

            @block.scalar
            def _(act):
                act.wait_ge(m.loaded[name], m.load_total[name])
                nc.scalar.activation(S1[:, :, :], w["f31"][:, :, :], ACT.Sign).then_inc(s_sg, 1)
                nc.scalar.activation(S2[:, :], w["f32"][:, :], ACT.Sign).then_inc(s_sg, 1)
                ln_scalar(nc, act, m, q, [pT[:, 0, :], pT[:, 1, :]])
                act.wait_ge(s_al, 1)
                for n in range(N):
                    act.wait_ge(s_h, n + 1)
                    if n >= 2:
                        act.wait_ge(s_y, n - 1)
                    i = n % IT
                    nc.scalar.activation(H[:, n % 2, :], pH[:, n % 2, 0:HALF], ACT.Gelu,
                                         bias=w["f3b1"][:, i:i + 1], scale=al[:, i:i + 1]).then_inc(s_g, 1)

            @block.tensor
            def _(pe):
                pe.wait_ge(s_sg, 2)
                for i in range(IT):
                    last = nc.tensor.transpose(pW[:, 0, i * 128:(i + 1) * 128], S1[:, i, :], m.ident[:, :])
                last.then_inc(s_wt, 1)
                for i in range(IT):
                    last = nc.tensor.transpose(pW[:, 1, i * 128:(i + 1) * 128], S2[:, i * 128:(i + 1) * 128],
                                               m.ident[:, :])
                last.then_inc(s_wt, 1)
                ln_tensor(nc, pe, m, q, [pT[:, 0, :], pT[:, 1, :]])
                pe.wait_ge(s_ws, 1)
                pe.wait_ge(q.xTs, 2)

                def up(n):
                    if n >= 2:
                        pe.wait_ge(s_g, n - 1)
                    h = n // IT
                    nc.tensor.matmul(pH[:, n % 2, 0:HALF], S1T[:, n % IT, :], m.XNT[:, h * HALF:(h + 1) * HALF],
                                     start=True, stop=True).then_inc(s_h, 1)

                up(0)
                for n in range(N):
                    if n + 1 < N:
                        up(n + 1)
                    pe.wait_ge(s_g, n + 1)
                    h, i = n // IT, n % IT
                    last = nc.tensor.matmul(pY[:, h, 0:HALF], S2T[:, i, :], H[:, n % 2, :],
                                            start=(i == 0), stop=(i == IT - 1))
                    last.then_inc(s_y, 1)
                for h in range(2):
                    pe.wait_ge(s_yt, h + 1)
                    for i in range(HB):
                        b = h * HB + i
                        last = nc.tensor.transpose(pT[0:T, h, i * D:(i + 1) * D], YT[:, b * T:(b + 1) * T],
                                                   m.ident[:, :])
                    last.then_inc(s_yy, 1)



def ffn_quantised(nc, m):
    name = "L1f"
    w = m.w
    QMAX = 127.0
    ROWS = [128, 128, 96]
    NI = 352
    N = 6
    with ExitStack() as ctx:
        s = Stage(nc, ctx, name)
        q = ln_sems(s)
        ident16 = s.sb("ident16", [128, 128], BF16)
        scw = s.sb("scw", [128, 7])
        inw = s.sb("inw", [128, 7])
        wq = s.sb("wq", [128, 6, 128])
        wqd = s.sb("wqd", [128, NI])
        wq16 = s.sb("wq16", [128, 6, 128], BF16)
        wqd16 = s.sb("wqd16", [128, NI], BF16)
        WT = s.sb("WT", [128, 6, 128], BF16)
        WDT = s.sb("WDT", [128, 3, 128], BF16)
        col = s.sb("col", [128, 16])
        one = s.sb("one", [1, 4])
        XQ = s.sb("XQ", [128, TOK])
        XQ16 = s.sb("XQ16", [128, TOK], BF16)
        SG = s.sb("SG", [128, 2, HALF])
        H = s.sb("H", [128, N, HALF])
        H16 = s.sb("H16", [128, N, HALF], BF16)
        MH = s.sb("MH", [128, N])
        sg = s.sb("sg", [128, 7])
        YT = s.sb("YT", [128, TOK])
        p16 = s.ps("p16", [128, 2, 1024], BF16)
        pT = s.ps("pT", [128, 2, 512])
        pG = s.ps("pG", [128, 2, 512])
        pU = s.ps("pU", [128, 2, 512])
        vch = s.sem("vector_own")
        s_id, s_q16, s_wt, s_wts = s.sem("ident_bf16"), s.sem("weights_rounded"), s.sem("weights_transposed"), s.sem("weights_sbuf")
        s_cl, s_ce = s.sem("clips_spread"), s.sem("exp_of_clips")
        s_m, s_mt, s_m1, s_mb = s.sem("token_max"), s.sem("max_as_row"), s.sem("overall_max"), s.sem("max_spread")
        s_xq, s_gu, s_si, s_h = s.sem("x_rounded"), s.sem("gate_up"), s.sem("silu"), s.sem("hidden")
        s_hr, s_hq = s.sem("hidden_scaled"), s.sem("hidden_rounded")
        s_y, s_yt, s_yy = s.sem("outT_psum"), s.sem("outT_sbuf"), s.sem("out")
        src = [(w["f1g"], i) for i in range(3)] + [(w["f1u"], i) for i in range(3)]

        def tile(buf, k):
            return buf[0:ROWS[k % 3], k, :]

        with nc.Block(no_gpsimd_drain=True) as block:

            @block.gpsimd
            def _(pool):
                ln_gpsimd(nc, pool, m, q)
                for n in range(N):
                    pool.wait_ge(s_hr, n + 1)
                    r = ROWS[n % 3]
                    nc.gpsimd.tensor_scalar(H16[0:r, n, :], H[0:r, n, :], ROUND, None, ALU.subtract)\
                      .then_inc(s_hq, 1)

            @block.vector
            def _(dve):
                chain = Chain(dve, vch)
                nc.vector.tensor_copy(ident16[:, :], m.ident[:, :]).then_inc(s_id, 1)
                chain.then(nc.vector.memset(scw[:, :], 1.0))
                chain.then(nc.vector.memset(MH[:, :], 0.0))
                dve.wait_ge(m.loaded[name], m.load_total[name])
                for k, (buf, i) in enumerate(src):
                    r = ROWS[i]
                    nc.vector.tensor_reduce(scw[0:r, k:k + 1], buf[0:r, i, :], AX.X, ALU.max,
                                            apply_absolute_value=True)
                chain.then(nc.vector.tensor_reduce(scw[:, 6:7], w["f1d"][:, :], AX.X, ALU.max,
                                                   apply_absolute_value=True))
                chain.then(nc.vector.tensor_scalar(scw[:, :], scw[:, :], 1.0 / QMAX, None, ALU.mult))
                chain.then(nc.vector.reciprocal(inw[:, :], scw[:, :]))

                def rounded(dst, val, inv, out):
                    yield lambda: nc.vector.tensor_scalar(dst, val, inv, QMAX, ALU.mult, ALU.min)
                    yield lambda: nc.vector.tensor_scalar(dst, dst, -QMAX - 1.0, ROUND, ALU.max, ALU.add)
                    if out is not None:
                        yield lambda: nc.vector.tensor_scalar(out, dst, ROUND, None, ALU.subtract)

                todo = [rounded(tile(wq, k), buf[0:ROWS[i], i, :], inw[0:ROWS[i], k:k + 1], tile(wq16, k))
                        for k, (buf, i) in enumerate(src)]
                todo.append(rounded(wqd[:, :], w["f1d"][:, :], inw[:, 6:7], wqd16[:, :]))
                for steps in zip(*todo):
                    for step in steps[:-1]:
                        step()
                    chain.then(steps[-1]())
                nc.vector.tensor_copy(scw[:, :], scw[:, :]).then_inc(s_q16, 1)
                ln_vector(nc, dve, chain, m, q)
                dve.wait_ge(q.norm, B)
                nc.vector.tensor_reduce(col[0:T, 0:1], m.XN[:, :, :], AX.XY, ALU.max,
                                        apply_absolute_value=True).then_inc(s_m, 1)
                dve.wait_ge(s_wt, 1)
                for k in range(6):
                    nc.vector.tensor_copy(WT[:, k, 0:ROWS[k % 3]], p16[:, 0, k * 128:k * 128 + ROWS[k % 3]])
                for i in range(3):
                    last = nc.vector.tensor_copy(WDT[0:ROWS[i], i, :], p16[0:ROWS[i], 1, i * 128:(i + 1) * 128])
                last.then_inc(s_wts, 1)
                dve.wait_ge(s_ce, 1)
                chain.then(nc.vector.tensor_scalar(col[:, 1:3], col[:, 1:3], 1.0, None, ALU.add))
                chain.then(nc.vector.reciprocal(col[:, 1:3], col[:, 1:3]))
                chain.then(nc.vector.tensor_scalar(col[:, 1:3], col[:, 1:3], 1.0 / QMAX, None, ALU.mult))

                def overall(i):
                    dve.wait_ge(s_mt, i + 1)
                    nc.vector.tensor_reduce(one[0:1, i:i + 1], pU[0:1, 0, 0:128 if i else T], AX.X,
                                            ALU.max).then_inc(s_m1, 1)
                    dve.wait_ge(s_mb, i + 1)
                    chain.then(nc.vector.tensor_tensor(col[:, 3 + 2 * i:4 + 2 * i], pU[:, 1, 0:1],
                                                       col[:, 1 + i:2 + i], ALU.mult))
                    chain.then(nc.vector.reciprocal(col[:, 4 + 2 * i:5 + 2 * i], col[:, 3 + 2 * i:4 + 2 * i]))

                overall(0)
                nc.vector.tensor_scalar(sg[:, 0:6], scw[:, 0:6], col[:, 3:4], None, ALU.mult)
                dve.wait_ge(q.xTs, 2)
                for step in rounded(XQ[:, :], m.XNT[:, :], col[:, 4:5], XQ16[:, :]):
                    ins = step()
                    chain.then(ins)
                nc.vector.tensor_copy(col[:, 10:11], col[:, 4:5]).then_inc(s_xq, 1)
                for n in range(N):
                    r, k = ROWS[n % 3], n % 3
                    dve.wait_ge(s_si, n + 1)
                    ins = nc.vector.scalar_tensor_tensor(
                        out=H[0:r, n, :], in0=pU[0:r, n % 2, 0:HALF], scalar=sg[0:r, 3 + k:4 + k],
                        in1=SG[0:r, n % 2, :], op0=ALU.mult, op1=ALU.mult)
                    ins.then_inc(s_h, 1)
                    dve.wait_ge(s_h, n + 1)
                    last = nc.vector.tensor_reduce(MH[0:r, n:n + 1], H[0:r, n, :], AX.X, ALU.max,
                                                   apply_absolute_value=True)
                chain.then(last)
                nc.vector.tensor_reduce(col[:, 0:1], MH[:, :], AX.X, ALU.max).then_inc(s_m, 1)
                overall(1)
                for n in range(N):
                    r = ROWS[n % 3]
                    steps = list(rounded(H[0:r, n, :], H[0:r, n, :], col[0:r, 6:7], None))
                    chain.then(steps[0]())
                    steps[1]().then_inc(s_hr, 1)
                chain.then(nc.vector.tensor_tensor(sg[:, 6:7], scw[:, 6:7], col[:, 5:6], ALU.mult))
                for h in range(2):
                    dve.wait_ge(s_y, h + 1)
                    nc.vector.tensor_scalar(YT[:, h * HALF:(h + 1) * HALF], pG[:, h, 0:HALF], sg[:, 6:7],
                                            None, ALU.mult).then_inc(s_yt, 1)
                for h in range(2):
                    dve.wait_ge(s_yy, h + 1)
                    x = m.X[:, h * HB:(h + 1) * HB, :]
                    nc.vector.tensor_tensor(x, x, pT[0:T, h, :].rearrange("p (b d) -> p b d", d=D), ALU.add)

            @block.scalar
            def _(act):
                act.wait_ge(s_cl, 1)
                nc.scalar.activation(col[:, 1:3], pU[:, 0, 128:130], ACT.Exp, scale=-1.0).then_inc(s_ce, 1)
                ln_scalar(nc, act, m, q, [pT[:, 0, :], pT[:, 1, :]])
                act.wait_ge(s_xq, 1)
                for n in range(N):
                    r, k = ROWS[n % 3], n % 3
                    act.wait_ge(s_gu, n + 1)
                    if n >= 2:
                        act.wait_ge(s_h, n - 1)
                    nc.scalar.activation(SG[0:r, n % 2, :], pG[0:r, n % 2, 0:HALF], ACT.Silu,
                                         scale=sg[0:r, k:k + 1]).then_inc(s_si, 1)

            @block.tensor
            def _(pe):
                pe.wait_ge(m.loaded[name], m.load_total[name])
                nc.tensor.matmul(pU[:, 0, 128:130], m.ones[0:1, 0:128], w["f1c"][0:1, :], start=True, stop=True)\
                  .then_inc(s_cl, 1)
                pe.wait_ge(s_id, 1)
                pe.wait_ge(s_q16, 1)
                for k in range(6):
                    r = ROWS[k % 3]
                    nc.tensor.transpose(p16[:, 0, k * 128:k * 128 + r], tile(wq16, k), ident16[0:r, 0:r])
                for i in range(3):
                    last = nc.tensor.transpose(p16[0:ROWS[i], 1, i * 128:(i + 1) * 128],
                                               wqd16[:, i * 128:i * 128 + ROWS[i]], ident16[:, :])
                last.then_inc(s_wt, 1)
                ln_tensor(nc, pe, m, q, [pT[:, 0, :], pT[:, 1, :]])

                def overall(i):
                    n = 128 if i else T
                    pe.wait_ge(s_m, i + 1)
                    if i == 0:
                        pe.wait_ge(s_ce, 1)
                    nc.tensor.transpose(pU[0:1, 0, 0:n], col[0:n, 0:1], m.ident[0:n, 0:n]).then_inc(s_mt, 1)
                    pe.wait_ge(s_m1, i + 1)
                    nc.tensor.matmul(pU[:, 1, 0:1], m.ones[0:1, 0:128], one[0:1, i:i + 1], start=True,
                                     stop=True).then_inc(s_mb, 1)

                overall(0)
                pe.wait_ge(s_wts, 1)
                pe.wait_ge(s_xq, 1)
                for n in range(N):
                    r, k, h = ROWS[n % 3], n % 3, n // 3
                    if n >= 2:
                        pe.wait_ge(s_h, n - 1)
                    x = XQ16[:, h * HALF:(h + 1) * HALF]
                    nc.tensor.matmul(pG[0:r, n % 2, 0:HALF], WT[:, k, 0:r], x, start=True, stop=True)
                    nc.tensor.matmul(pU[0:r, n % 2, 0:HALF], WT[:, 3 + k, 0:r], x, start=True, stop=True)\
                      .then_inc(s_gu, 1)
                overall(1)
                for h in range(2):
                    for k in range(3):
                        n, r = 3 * h + k, ROWS[k]
                        pe.wait_ge(s_hq, n + 1)
                        last = nc.tensor.matmul(pG[:, h, 0:HALF], WDT[0:r, k, :], H16[0:r, n, :],
                                                start=(k == 0), stop=(k == 2))
                    last.then_inc(s_y, 1)
                for h in range(2):
                    pe.wait_ge(s_yt, h + 1)
                    for i in range(HB):
                        b = h * HB + i
                        last = nc.tensor.transpose(pT[0:T, h, i * D:(i + 1) * D], YT[:, b * T:(b + 1) * T],
                                                   m.ident[:, :])
                    last.then_inc(s_yy, 1)



NAMES = ['x', 'ctx_1024', 'L0_attn_Wq', 'L0_attn_Wk', 'L0_attn_Wv', 'L0_attn_Wo', 'L0_xattn_Wq', 'L0_xattn_Wk', 'L0_xattn_Wv', 'L0_xattn_gru_wih', 'L0_xattn_gru_whh', 'L0_xattn_gru_bih', 'L0_xattn_gru_bhh', 'L0_xattn_slot_norm_w', 'L0_xattn_input_norm_w', 'L0_ffn_Wg', 'L0_ffn_Wu', 'L0_ffn_Wd', 'L0_ffn_Wr', 'L0_ffn_temperature', 'L1_attn_w_qkvw', 'L1_attn_w_out', 'L1_xattn_Wq', 'L1_xattn_bq', 'L1_xattn_Wk', 'L1_xattn_bk', 'L1_xattn_Wv', 'L1_xattn_bv', 'L1_xattn_Wo', 'L1_xattn_bo', 'L1_ffn_clip_x', 'L1_ffn_clip_down', 'L1_ffn_w_gate', 'L1_ffn_w_up', 'L1_ffn_w_down', 'L2_attn_w_fc', 'L2_attn_w_proj', 'L2_attn_ln_g', 'L2_attn_ln_b', 'L2_xattn_Wk', 'L2_xattn_Wq', 'L2_xattn_Wv', 'L2_ffn_gate_weight', 'L2_ffn_ln_gamma', 'L2_ffn_ln_beta', 'L2_ffn_wi', 'L2_ffn_wo', 'L3_attn_Wk', 'L3_attn_bk', 'L3_attn_Wv', 'L3_attn_bv', 'L3_attn_Wq', 'L3_attn_bq', 'L3_attn_gamma', 'L3_attn_beta', 'L3_xattn_Wq', 'L3_xattn_Wk', 'L3_xattn_Wv', 'L3_xattn_Wo', 'L3_ffn_w1', 'L3_ffn_b1', 'L3_ffn_w2', 'L3_ffn_b2']

SUBLAYERS = [1, 2, 3, 4, 5, 6, 7, 8, 9, 10, 11, 12]


def decoder(nc, a, out):
    with ExitStack() as ctx:
        def sb(name, shape, dt=F32):
            return ctx.enter_context(nc.sbuf_tensor(name, shape, dt))

        def sem(name):
            return ctx.enter_context(nc.semaphore(name))

        m = Names()
        m.X = sb("X", [T, B, D])
        m.XN = sb("XN", [T, B, D])
        m.XNT = sb("XNT", [128, TOK])
        m.XN2 = sb("XN2", [T, B, D])
        m.stats = sb("stats", [T, B, 6])
        m.mv = sb("mv", [T, B, 2])
        m.veps = sb("veps", [T, B])
        m.rstd = sb("rstd", [T, B])
        m.ident = sb("ident", [128, 128])
        m.ones = sb("ones", [128, 512])
        m.neg_half = sb("neg_half", [128, 96])
        m.mask = sb("mask", [T, 2, NJ * T])
        m.order = sb("order", [T, B, NE])
        m.before = sb("before", [T, T])
        m.below = sb("below", [128, 8, 128])
        m.sel = sb("sel", [8, 8, 128])
        m.ctx_tm = sb("ctx_tm", [128, B, NKT, D + 1])
        m.CT = sb("CT", [128, B, NKT * 128])
        m.loaded, m.load_total = {}, {}
        w = {}
        specs = []

        def want(stage, key, shape, src, slot=None, part=None):
            if slot is not None:
                part = (slice(None), slice(slot, slot + 1))
            specs.append((stage, key, shape, src, part if part is not None else slice(None)))

        def row(v):
            return v.rearrange("(a n) -> a n", a=1)

        want_all(a, want, row)
        order = []
        for spec in specs:
            if spec[0] not in order:
                order.append(spec[0])
        held = {stage: ctx.enter_context(ExitStack()) for stage in reversed(order)}
        for stage in reversed(order):
            for st, key, shape, _, _ in specs:
                if st == stage and shape is not None:
                    w[key] = held[stage].enter_context(nc.sbuf_tensor("w_" + key, shape, F32))
        loads = [(stage, w[key][part], src) for stage, key, _, src, part in specs]
        for stage in order:
            m.loaded[stage] = sem("loaded_" + stage)
            m.load_total[stage] = 16 * sum(spec[0] == stage for spec in specs)
        m.w = w
        m.loads = loads
        m.a = a
        m.x_loaded = sem("x_loaded")
        m.stored = sem("result_stored")
        m.ctx_loaded = [sem(f"ctx_loaded_{b}") for b in range(B)]
        first_block(nc, m, a["x"])
        n = SUBLAYERS
        m.ctx_times = 2 if 2 in n else 1
        if 1 in n:
            attention16(nc, m, "L0a", w["a0q"][:, :], w["a0k"][:, :], w["a0v"][:, :], w["a0o"][:, :])
        held["L0a"].close()
        if 2 in n:
            context_block(nc, m, "ctxn", True, 1)
            slot_attention(nc, m)
        held["L0x"].close()
        if 3 in n:
            mixture_golden(nc, m)
        held["L0f"].close()
        if 4 in n:
            attention_regrouped(nc, m)
        held["L1a"].close()
        if set(n) & {5, 8, 11}:
            context_block(nc, m, "ctxr", False, m.ctx_times)
        if 5 in n:
            attention16(nc, m, "L1x", w["x1q"][:, :], w["x1k"][:, :], w["x1v"][:, :], w["x1o"][:, :],
                        keys="causal", bias=(w["x1bq"], w["x1bk"], w["x1bv"], w["x1bo"]))
        held["L1x"].close()
        if 6 in n:
            ffn_quantised(nc, m)
        held["L1f"].close()
        if 7 in n:
            attention_fixed_keys(nc, m)
        held["L2a"].close()
        if 8 in n:
            attention_wide(nc, m)
        held["L2x"].close()
        if 9 in n:
            mixture_top1(nc, m)
        held["L2f"].close()
        if 10 in n:
            attention_delta_rule(nc, m)
        held["L3a"].close()
        if 11 in n:
            attention16(nc, m, "L3x", w["x3q"][:, :], w["x3k"][:, :], w["x3v"][:, :], w["x3o"][:, :],
                        weights_natural=True, keys="context")
        held["L3x"].close()
        if 12 in n:
            ffn_binary(nc, m)
        held["L3f"].close()
        store_block(nc, m, out)


def want_all(a, want, row):
    want("L0a", "a0q", [128, 128], a["L0_attn_Wq"])
    want("L0a", "a0k", [32, 128], a["L0_attn_Wk"])
    want("L0a", "a0v", [32, 128], a["L0_attn_Wv"])
    want("L0a", "a0o", [128, 128], a["L0_attn_Wo"])
    want("L0x", "x0q", [128, 128], a["L0_xattn_Wq"])
    want("L0x", "x0k", [128, 128], a["L0_xattn_Wk"])
    want("L0x", "x0v", [128, 128], a["L0_xattn_Wv"])
    want("L0x", "x0ih", [128, 3, 128], a["L0_xattn_gru_wih"].rearrange("(c p) d -> p c d", p=128))
    want("L0x", "x0hh", [128, 3, 128], a["L0_xattn_gru_whh"].rearrange("(c p) d -> p c d", p=128))
    want("L0x", "x0bi", [1, 384], row(a["L0_xattn_gru_bih"]))
    want("L0x", "x0bh", [1, 384], row(a["L0_xattn_gru_bhh"]))
    want("L0x", "x0sw", [128, 1], a["L0_xattn_slot_norm_w"].rearrange("(p a) -> p a", a=1))
    want("L0x", "x0iw", [128, 1], a["L0_xattn_input_norm_w"].rearrange("(p a) -> p a", a=1))
    want("L0f", "f0t", [1, 1], row(a["L0_ffn_temperature"]))
    want("L0f", "f0r", [128, NE], a["L0_ffn_Wr"])
    want("L0f", "f0g", [128, NE, 128], a["L0_ffn_Wg"].rearrange("e d i -> d e i"))
    want("L0f", "f0u", [128, NE, 128], a["L0_ffn_Wu"].rearrange("e d i -> d e i"))
    want("L0f", "f0d", [128, NE, 128], a["L0_ffn_Wd"].rearrange("e i d -> i e d"))
    want("L1a", "a1w", [128, 512], a["L1_attn_w_qkvw"])
    want("L1a", "a1o", [128, 128], a["L1_attn_w_out"])
    for key, src in (("q", "Wq"), ("k", "Wk"), ("v", "Wv"), ("o", "Wo")):
        want("L1x", "x1" + key, [128, 128], a["L1_xattn_" + src])
        want("L1x", "x1b" + key, [1, 128], row(a["L1_xattn_b" + key]))

    def column(v, p=128):
        return v.rearrange("(c p) -> p c", p=p)

    for key, src in (("f1g", "w_gate"), ("f1u", "w_up")):
        v = a["L1_ffn_" + src]
        want("L1f", key, [128, 3, 128], v[0:256, :].rearrange("(i p) d -> p i d", p=128),
             part=(slice(0, 128), slice(0, 2)))
        want("L1f", key, None, v[256:352, :], part=(slice(0, 96), 2))
    want("L1f", "f1d", [128, 352], a["L1_ffn_w_down"])
    want("L1f", "f1c", [1, 2], row(a["L1_ffn_clip_x"]), slot=0)
    want("L1f", "f1c", None, row(a["L1_ffn_clip_down"]), slot=1)
    want("L2a", "a2f", [128, 128], a["L2_attn_w_fc"])
    want("L2a", "a2p", [128, 128], a["L2_attn_w_proj"])
    want("L2a", "a2g", [128, 1], column(a["L2_attn_ln_g"]))
    want("L2a", "a2b", [128, 1], column(a["L2_attn_ln_b"]))
    want("L2x", "x2q", [128, 128], a["L2_xattn_Wq"])
    want("L2x", "x2k", [128, 128], a["L2_xattn_Wk"])
    want("L2x", "x2v", [128, 128], a["L2_xattn_Wv"])
    want("L2f", "f2r", [NE, 128], a["L2_ffn_gate_weight"])
    want("L2f", "f2g", [128, 1], column(a["L2_ffn_ln_gamma"]))
    want("L2f", "f2b", [128, 1], column(a["L2_ffn_ln_beta"]))
    want("L3a", "a3k", [DS, 128], a["L3_attn_Wk"])
    want("L3a", "a3q", [DS, 128], a["L3_attn_Wq"])
    want("L3a", "a3v", [128, 128], a["L3_attn_Wv"])
    want("L3a", "a3bk", [DS, 1], column(a["L3_attn_bk"], DS))
    want("L3a", "a3bq", [DS, 1], column(a["L3_attn_bq"], DS))
    want("L3a", "a3bv", [1, 128], row(a["L3_attn_bv"]))
    want("L3a", "a3g", [128, 1], column(a["L3_attn_gamma"]))
    want("L3a", "a3b", [128, 1], column(a["L3_attn_beta"]))
    for key, src, f in (("q", "Wq", 128), ("k", "Wk", 32), ("v", "Wv", 32), ("o", "Wo", 128)):
        want("L3x", "x3" + key, [128, f], a["L3_xattn_" + src])
    want("L3f", "f31", [128, 4, 128], a["L3_ffn_w1"].rearrange("(i p) d -> p i d", p=128))
    want("L3f", "f32", [128, 512], a["L3_ffn_w2"])
    want("L3f", "f3b1", [128, 4], column(a["L3_ffn_b1"][0:128]), slot=0)
    for i in range(1, 4):
        want("L3f", "f3b1", None, column(a["L3_ffn_b1"][i * 128:(i + 1) * 128]), slot=i)
    want("L3f", "f3b2", [128, 1], column(a["L3_ffn_b2"]))


def first_block(nc, m, x):
    with ExitStack() as ctx:
        s = Stage(nc, ctx, "first")
        s_set = s.sem("cleared")
        s_pad = s.sem("context_padded")
        with nc.Block(no_gpsimd_drain=True) as block:

            @block.sync
            def _(sp):
                sp.dma_start(m.X[:, :, :], x.rearrange("b t d -> t b d")).then_inc(m.x_loaded, 16)
                sp.wait_ge(s_pad, 1)
                for b in range(B):
                    load_context(sp, m, b)
                for stage, dst, src in m.loads:
                    sp.dma_start(dst, src).then_inc(m.loaded[stage], 16)

            @block.vector
            def _(dve):
                nc.vector.memset(m.ctx_tm[:, :, KT_FULL, :], 0.0).then_inc(s_pad, 1)
                dve.wait_ge(s_pad, 1)
                nc.vector.memset(m.ctx_tm[:, :, :, D], 1.0).then_inc(s_pad, 1)
                dve.wait_ge(s_pad, 2)
                dve.wait_ge(m.x_loaded, 16)

            @block.gpsimd
            def _(pool):
                nc.gpsimd.memset(m.ident[:, :], 0.0)
                nc.gpsimd.memset(m.mask[:, :, :], 0.0)
                nc.gpsimd.memset(m.sel[:, :, :], 0.0)
                nc.gpsimd.memset(m.before[:, :], 1.0)
                nc.gpsimd.memset(m.below[:, :, :], 0.0)
                nc.gpsimd.memset(m.ones[:, :], 1.0)
                nc.gpsimd.memset(m.neg_half[:, :], -0.5).then_inc(s_set, 1)
                for e in range(NE):
                    last = nc.gpsimd.memset(m.order[:, :, e], float(NE - e))
                last.then_inc(s_set, 1)
                pool.wait_ge(s_set, 2)
                nc.gpsimd.affine_select(out=m.ident[:, :], in_=m.ident[:, :], compare_op=ALU.not_equal,
                                        fill=1.0, base=0, pattern=[[-1, 128]], channel_multiplier=1)
                nc.gpsimd.affine_select(out=m.mask[:, 0, :], in_=m.mask[:, 0, :], compare_op=ALU.is_ge,
                                        fill=-1e30, base=0, pattern=[[0, NJ], [-1, T]],
                                        channel_multiplier=1)
                nc.gpsimd.affine_select(out=m.mask[:, 1, :], in_=m.mask[:, 1, :], compare_op=ALU.is_ge,
                                        fill=-1e30, base=0, pattern=[[0, NG], [1, T]],
                                        channel_multiplier=-1)
                nc.gpsimd.affine_select(out=m.sel[:, :, :], in_=m.sel[:, :, :], compare_op=ALU.not_equal,
                                        fill=1.0, base=0, pattern=[[-1, 8], [0, 128]],
                                        channel_multiplier=1).then_inc(s_set, 1)
                nc.gpsimd.affine_select(out=m.before[:, :], in_=m.before[:, :], compare_op=ALU.is_ge,
                                        fill=0.0, base=-1, pattern=[[1, T]], channel_multiplier=-1)
                n = 3
                for i, sz in [(0, 1)] + [(k + 1, v) for k, v in enumerate(LEVELS)]:
                    blocks = 128 // (2 * sz)
                    cols = slice(0, sz) if i == 0 else slice(sz, 2 * sz)
                    lo = sz if i == 0 else 0
                    kept = [p for p in ([2 * sz, blocks], [0, sz]) if p[1] > 1]
                    v = m.below[:, i, :].rearrange("p (k c) -> p k c", c=2 * sz)[:, :, cols]
                    pool.wait_ge(s_set, n)
                    nc.gpsimd.memset(v, TTT_LR).then_inc(s_set, 1)
                    pool.wait_ge(s_set, n + 1)
                    nc.gpsimd.affine_select(out=v, in_=v, compare_op=ALU.is_ge, fill=0.0, base=-lo,
                                            pattern=[[-p[0], p[1]] for p in kept], channel_multiplier=1)\
                        .then_inc(s_set, 1)
                    pool.wait_ge(s_set, n + 2)
                    nc.gpsimd.affine_select(out=v, in_=v, compare_op=ALU.is_ge, fill=0.0, base=lo + sz - 1,
                                            pattern=kept, channel_multiplier=-1)\
                        .then_inc(s_set, 1)
                    n += 3
                pool.wait_ge(s_set, n)


def store_block(nc, m, out):
    with nc.Block(no_gpsimd_drain=True) as block:

        @block.sync
        def _(sp):
            for stage in m.loaded:
                sp.wait_ge(m.loaded[stage], m.load_total[stage])
            for b in range(B):
                sp.wait_ge(m.ctx_loaded[b], 32 * m.ctx_times)
            sp.dma_start(out.rearrange("b t d -> t b d"), m.X[:, :, :]).then_inc(m.stored, 16)
            sp.wait_ge(m.stored, 16)



def kernel(**inputs):
    import numpy as _np
    import concourse.bacc as _bacc
    from concourse.bass_utils import run_bass_kernel_spmd as _run

    nc = _bacc.Bacc("TRN2", target_bir_lowering=False, num_devices=1)
    arrays, args = {}, {}
    for name in NAMES:
        arr = _np.ascontiguousarray(inputs[name])
        arrays[f"in_{name}"] = arr
        args[name] = nc.dram_tensor(f"in_{name}", arr.shape, mybir.dt.from_np(arr.dtype), kind="ExternalInput").ap()
    out = nc.dram_tensor("decoded", (B, T, D), F32, kind="ExternalOutput").ap()
    decoder(nc, args, out)
    r = _run(nc, [arrays], core_ids=[0])
    return r.results[0]["decoded"]
```

```python
from contextlib import ExitStack

import concourse.bass as bass
from concourse import mybir

ALU = mybir.AluOpType
ACT = mybir.ActivationFunctionType
F32 = mybir.dt.float32
BF16 = mybir.dt.bfloat16
AX = mybir.AxisListType

B, T, D = 8, 100, 128
TOK = B * T
HALF = TOK // 2
HB = B // 2
SC = 1444
KT_FULL = SC // 128
TAIL = SC - KT_FULL * 128
NKT = KT_FULL + 1
TILES = [128] * KT_FULL + [TAIL]
VGROUPS = [(0, 4, 128), (4, 8, 128), (8, KT_FULL, 128), (KT_FULL, NKT, TAIL)]
LN_EPS = 1e-5
ROUND = 12582912.0


class Names:
    pass


class Chain:

    def __init__(self, eng, sem):
        self.eng, self.sem, self.n = eng, sem, 0

    def then(self, ins):
        self.n += 1
        ins.then_inc(self.sem, 1)
        self.eng.wait_ge(self.sem, self.n)


class Stage:

    FIRST_SEM = 160

    def __init__(self, nc, ctx, name):
        self.nc, self.ctx, self.name, self.next = nc, ctx, name, self.FIRST_SEM
        ctx.callback(self.clear)

    def clear(self):
        self.nc.all_engine_barrier(sems_to_clear=range(self.FIRST_SEM, self.next))

    def sb(self, name, shape, dt=F32):
        return self.ctx.enter_context(self.nc.sbuf_tensor(f"{self.name}_{name}", shape, dt))

    def sem(self, name):
        self.next += 1
        return self.ctx.enter_context(self.nc.semaphore(f"{self.name}_{name}", num=self.next - 1))

    def ps(self, name, shape, dt=F32):
        return self.ctx.enter_context(self.nc.psum_tensor(f"{self.name}_{name}", shape, dt))



def ln_sems(s, name="ln"):
    q = Names()
    q.var, q.rstd, q.norm = s.sem(name + "_var"), s.sem(name + "_rstd"), s.sem(name + "_norm")
    q.xT, q.xTs = s.sem(name + "_xT_in_psum"), s.sem(name + "_xT_in_sbuf")
    return q


def ln_vector(nc, dve, chain, m, q, src=None, dst=None):
    src = m.X if src is None else src
    dst = m.XN if dst is None else dst
    for b in range(B):
        last = nc.vector.bn_stats(m.stats[:, b, :], src[:, b, :])
    chain.then(last)
    for b in range(B):
        last = nc.vector.bn_aggr(m.mv[:, b, :], m.stats[:, b, :])
    chain.then(last)
    nc.vector.tensor_scalar(m.veps[:, :], m.mv[:, :, 1], LN_EPS, None, ALU.add).then_inc(q.var, 1)
    dve.wait_ge(q.rstd, 1)
    for b in range(B):
        nc.vector.tensor_scalar(dst[:, b, :], src[:, b, :], m.mv[:, b, 0:1], m.rstd[:, b:b + 1],
                                ALU.subtract, ALU.mult).then_inc(q.norm, 1)


def ln_gpsimd(nc, pool, m, q):
    pool.wait_ge(q.var, 1)
    nc.gpsimd.tensor_tensor(m.rstd[:, :], m.veps[:, :], m.neg_half[0:T, 0:B], ALU.pow).then_inc(q.rstd, 1)


def ln_tensor(nc, pe, m, q, banks, src=None):
    src = m.XN if src is None else src
    for b in range(B):
        pe.wait_ge(q.norm, b + 1)
        nc.tensor.transpose(banks[b // HB][:, (b % HB) * T:(b % HB + 1) * T], src[:, b, :],
                            m.ident[0:T, 0:T]).then_inc(q.xT, 1)


def ln_scalar(nc, act, m, q, banks, affine=None):
    for h in range(2):
        act.wait_ge(q.xT, HB * (h + 1))
        dst = m.XNT[:, h * HALF:(h + 1) * HALF]
        if affine is None:
            nc.scalar.copy(dst, banks[h][:, 0:HALF]).then_inc(q.xTs, 1)
        else:
            nc.scalar.activation(dst, banks[h][:, 0:HALF], ACT.Identity, bias=affine[1][:, 0:1],
                                 scale=affine[0][:, 0:1]).then_inc(q.xTs, 1)



NH, HD = 16, 8
NJ = 4
NG = NH // NJ
SCALE8 = float(HD) ** -0.5
KEY_TERM = [1, 2, 1, 2, 3, 1]
QUERY_TERM = [1, 1, 2, 2, 1, 3]
SLOTS = len(KEY_TERM)
MAXROW = SLOTS * HD
PAIRS = 2


MASK = 2 * PAIRS * NG
NCOLS = MASK + 4


def term_rows(nc, brow):
    for a in range(2):
        c = 64 * a + MAXROW
        last = nc.vector.memset(brow[0:1, PAIRS * NG:MASK, c:c + 3], 1.0)
        for side, term in ((0, KEY_TERM), (2, QUERY_TERM)):
            for k, v in enumerate(term):
                if v >= 2:
                    last = nc.vector.memset(brow[0:1, MASK + side, c - MAXROW + HD * k:c - MAXROW + HD * k + HD],
                                            1.0)
                if v == 3:
                    last = nc.vector.memset(
                        brow[0:1, MASK + side + 1, c - MAXROW + HD * k:c - MAXROW + HD * k + HD], 1.0)
        last = nc.vector.memset(brow[0:1, MASK + 2, c + 1:c + 3], 1.0)
        last = nc.vector.memset(brow[0:1, MASK + 3, c + 2:c + 3], 1.0)
    return last


def bias_times_mask(nc, mcol, bcol):
    half = PAIRS * NG
    nc.vector.tensor_scalar(mcol[:, 0:half], bcol[:, 0:half], bcol[:, MASK + 2:MASK + 3], None, ALU.mult)
    return nc.vector.tensor_scalar(mcol[:, half:MASK], bcol[:, half:MASK], bcol[:, MASK:MASK + 1], None,
                                   ALU.mult)


def attention16(nc, m, name, wq, wk, wv, wo, spare, weights_natural=False, keys="self", bias=None,
                beside=None):
    grouped = keys != "causal"
    NK = 1 if grouped else NG
    long = keys == "context"
    tiles = TILES if long else [T]
    nt = len(tiles)
    NU = nt * NJ
    CH = [482, 482, 480]
    MU = NU
    LAG = MU + 20 if long else MU + 11
    TM_AT, NORM_AT, TURN_AT, OT_AT, PROJ_AT, RES_AT = (3, 4, 7, 8, 11, 12) if long else (1, 1, 2, 2, 3, 3)
    DELAY = 1
    KB = 3 if long else 1
    UW = max(CH) if long else NG * T
    EB = 2 * NJ
    with ExitStack() as ctx:
        s = Stage(nc, ctx, name)
        q = ln_sems(s)
        wT = s.sb("wT", [128, 2, 128])
        wqe = s.sb("wqe", [128, PAIRS, NG, 128])
        wke = s.sb("wke", [128, PAIRS, NK, 128]) if grouped else \
            spare[:, 11000:11000 + PAIRS * NK * 128].rearrange("p (i g c) -> p i g c", i=PAIRS, g=NK)
        if bias is None:
            bcol, mcol = m.cols, m.mcols
        else:
            brow = s.sb("brow", [1, MASK, 128])
            bcol = s.sb("bcol", [128, NCOLS])
            mcol = s.sb("mcol", [128, MASK])
        at0 = NJ * NG * TOK // 2
        QS = spare[:, 0:at0].bitcast(BF16).rearrange("p (j g t) -> p j g t", j=NJ, g=NG)
        T1 = s.sb("T1", [128, 2, UW], BF16)
        X1 = s.sb("X1", [128, 2, UW])
        T2 = s.sb("T2", [128, 2, UW], BF16)
        M3 = s.sb("M3", [128, 2, NG * T], BF16)
        MH = s.sb("MH", [T, 2, NJ, NG, 3]) if long else None
        nm = s.sb("nm", [T, 2, NJ, NG])
        MXP = s.sb("MXP", [T, 2, PAIRS, NG, 128])
        OC = s.sb("OC", [128, NG * T])
        rden = s.sb("rden", [T, NG, NJ])
        ON = s.sb("ON", [T, D])
        OT = s.sb("OT", [128, T])
        if long:
            at1 = at0 + KB * PAIRS * SC // 2
            KS = spare[:, at0:at1].bitcast(BF16).rearrange("p (k i t) -> p k i t", k=KB, i=PAIRS)
            V = s.sb("V", [128, 2, NKT, NJ, 32])
            E = s.sb("E", [128, EB, NG * T])
        else:
            at1 = at0 + NK * PAIRS * TOK // 2
            KS = spare[:, at0:at1].bitcast(BF16).rearrange("p (g i t) -> p g i t", g=NK, i=PAIRS)
            if grouped:
                at2 = at1 + B * NJ * 32
                V = spare[0:T, at1:at2].rearrange("p (b j d) -> p b j d", b=B, j=NJ)
                E = spare[:, at2:at2 + EB * NG * T].rearrange("p (i t) -> p i t", i=EB)
            else:
                CX = spare[:, at1:at1 + TOK]
                V = s.sb("V", [T, B, NH, 32])
                E = s.sb("E", [128, EB, NG * T])
        if not grouped:
            ident16 = s.sb("ident16", [T, T], BF16)
            mask16 = m.XN2[:, :, :].rearrange("t b d -> t (b d)").bitcast(BF16)[:, 0:2 * NG * T]\
                .rearrange("t (i k) -> t i k", i=2)
        pM = s.ps("pM", [128, 3, 512])
        pS = s.ps("pS", [128, 2, 512])
        pO = s.ps("pO", [128, 512])
        pP = s.ps("pP", [128, 2, 512])
        banks = [pM[:, 0, :], pM[:, 1, :]]
        dch, gch = s.sem("vector_own"), s.sem("gpsimd_own")
        s_wT, s_w = s.sem("weights_transposed"), s.sem("weights_ready")
        s_row, s_col, s_bias = s.sem("bias_rows"), s.sem("bias_columns_psum"), s.sem("bias_columns")
        s_set, s_clear = s.sem("buffers_cleared"), s.sem("queries_cleared")
        s_table = s.sem("tables")
        s_qv = s.sem("query_half_written")
        s_up, s_t1, s_x1 = s.sem("unit_psum"), s.sem("first_terms"), s.sem("unit_read")
        s_t2, s_fin = s.sem("second_terms"), s.sem("unit_split")
        s_m, s_mr, s_mx = s.sem("scores_for_max"), s.sem("max_taken"), s.sem("maxima_ready")
        s_s, s_e, s_eu = s.sem("scores"), s.sem("exps"), s.sem("exps_used")
        s_oc, s_tt, s_on = s.sem("out_sbuf"), s.sem("out_token_major"), s.sem("out_normalised")
        s_ot, s_ots = s.sem("outT_psum"), s.sem("outT_sbuf")
        s_y, s_x = s.sem("y_psum"), s.sem("residual_added")
        s_cx, s_cxs = s.sem("context_turned"), s.sem("context_turned_sbuf")
        KD = NJ * HD * NK
        rows = [128, KD, KD, 128]
        srcs = [wq, wk, wv, wo]
        wTs = [pM[:, 2, 0:128], pP[:, 0, 0:KD], pP[:, 0, 128:128 + KD], pP[:, 0, 256:384]]
        if weights_natural:
            wTs = srcs

        units = [("Q", p, g, h) for p in range(PAIRS) for g in range(NG) for h in range(2)]
        if long:
            units += [("K", p, 0, c) for p in range(PAIRS) for c in range(3)]
            units += [("V", 0, i) for i in range(2)]
        else:
            units += [("K", p, g, h) for p in range(PAIRS) for g in range(NK) for h in range(2)]
            units += [("V", b, 0) for b in range(B)]
        FIRST = len(units)
        STEPS = B * NU
        steps = range(-LAG, STEPS)
        at = {t: [] for t in range(-LAG, STEPS + DELAY)}
        later = []
        for b in range(B):
            first = b * MU - LAG
            if long and b >= 1:
                later += [(first - MU + 18 + 4 * i, ("K", i // 3, b, i % 3)) for i in range(6)]
                later += [((b - 1) * NU + 22 + 4 * i, ("V", b, i)) for i in range(2)]
            later += [(first + MU + (2 + 4 * p if long else 2 * p), ("M", p, b, 0)) for p in range(PAIRS)]
        for t, unit in sorted(later):
            at[t].append(len(units))
            units.append(unit)

        def split_before(n, kinds="QKM"):
            return sum(units[i][0] in kinds for i in range(n))

        def keys_ready(b):
            n = [n for n, x in enumerate(units) if x[0] == "K" and (x[2] == b or not long)]
            return 1 + split_before(max(n))

        def values_ready(b):
            n = [n for n, x in enumerate(units) if x[0] == "V" and x[1] == b]
            return 1 + max(n)

        NQ = 2 * PAIRS * NG

        def bias_column(unit):
            g = unit[2] if unit[0] == "Q" or not long else 0
            return (PAIRS * NG if unit[0] == "K" else 0) + unit[1] * NG + g

        def width(unit):
            return CH[unit[3]] if unit[0] == "K" and long else NG * T

        with nc.Block(no_gpsimd_drain=True) as block:

            @block.sync
            def _(sp):
                if beside is not None:
                    beside[0](sp, m)

            @block.gpsimd
            def _(pool):
                chain = Chain(pool, gch)
                if long:
                    for b in range(B):
                        pool.wait_ge(m.ctx_loaded[b], 32 * m.ctx_times)
                nc.gpsimd.memset(wke[:], 0.0).then_inc(s_set, 1)
                nc.gpsimd.memset(V[:], 0.0).then_inc(s_set, 1)
                nc.gpsimd.memset(spare[:, 0:at0], 0.0)
                nc.gpsimd.memset(MXP[:], 0.0).then_inc(s_clear, 1)
                ln_gpsimd(nc, pool, m, q)
                pool.wait_ge(s_clear, 1)
                if bias is not None:
                    pool.wait_ge(s_bias, 1)

                def split(n):
                    unit = units[n]
                    kind, p = unit[0], unit[1]
                    if kind == "V":
                        return
                    i = split_before(n)
                    W = width(unit)
                    pool.wait_ge(s_x1, n + 1)
                    if i >= 1:
                        pool.wait_ge(s_fin, i)
                    if n < FIRST or not long:
                        pool.wait_ge(s_t2, i + 1)
                    else:
                        c = MASK + (1 if kind == "K" else 3)
                        chain.then(nc.gpsimd.tensor_scalar(T2[:, i % 2, 0:W], X1[:, i % 2, 0:W],
                                                           bcol[:, c:c + 1], None, ALU.mult))
                    if kind == "K":
                        if long:
                            b, c = unit[2], unit[3]
                            if b >= KB:
                                pool.wait_ge(s_s, NU * (b - KB + 1))
                            dst = KS[:, b % KB, p, CH[0] * c:CH[0] * c + W]
                        else:
                            dst = KS[:, unit[2], p, unit[3] * HALF:(unit[3] + 1) * HALF]
                        nc.gpsimd.tensor_tensor(dst, X1[:, i % 2, 0:W], T2[:, i % 2, 0:W], ALU.subtract)\
                          .then_inc(s_fin, 1)
                        return
                    if kind == "Q":
                        nc.gpsimd.tensor_tensor(
                            QS[64:128, 2 * p + 1, unit[2], unit[3] * HALF:(unit[3] + 1) * HALF],
                            X1[64:128, i % 2, 0:W], T2[64:128, i % 2, 0:W], ALU.subtract)\
                            .then_inc(s_fin, 1)
                        return
                    b = unit[2]
                    chain.then(nc.gpsimd.tensor_tensor(M3[:, i % 2, :], X1[:, i % 2, 0:W],
                                                       T2[:, i % 2, 0:W], ALU.subtract))
                    for a in range(2):
                        r = slice(64 * a + 32, 64 * a + 64)
                        v = QS[r, 2 * p + a, :, b * T:(b + 1) * T]
                        last = nc.gpsimd.tensor_tensor(
                            v, v, M3[r, i % 2, :].rearrange("p (g t) -> p g t", t=T), ALU.add)
                        if a == 0:
                            chain.then(last)
                    last.then_inc(s_fin, 1)

                for n in range(FIRST):
                    split(n)
                pool.wait_ge(s_qv, NQ)
                for t in steps:
                    for n in at[t]:
                        split(n)
                if beside is not None:
                    pool.wait_ge(s_fin, split_before(len(units)))
                    beside[1](nc, pool, m, s_table)

            @block.vector
            def _(dve):
                chain = Chain(dve, dch)
                if bias is not None:
                    chain.then(nc.vector.memset(brow[:], 0.0))
                    for a in range(2):
                        c = 64 * a + MAXROW
                        nc.vector.memset(brow[0:1, PAIRS * NG:MASK, c:c + 3], 1.0)
                    dve.wait_ge(m.loaded[name], m.load_total[name])
                    for i in range(2):
                        for j in range(NJ):
                            p, a = j // 2, j % 2
                            last = nc.vector.tensor_copy(
                                brow[0:1, i * PAIRS * NG + p * NG:i * PAIRS * NG + (p + 1) * NG,
                                     64 * a:64 * a + MAXROW].rearrange("o g (k d) -> o g k d", d=HD),
                                bias[i][0:1, j * NG * HD:(j + 1) * NG * HD]
                                .rearrange("o (g d) -> o g d", d=HD).unsqueeze(2)
                                .broadcast_to((1, NG, SLOTS, HD)))
                    last.then_inc(s_row, 1)
                if not grouped:
                    nc.vector.tensor_copy(ident16[:, :], m.ident[0:T, 0:T])
                    nc.vector.tensor_copy(mask16[:, :, :], m.mask[:, :, :])
                nc.vector.memset(wqe[:], 0.0)
                ln_vector(nc, dve, chain, m, q)
                dve.wait_ge(s_set, 2)
                nc.vector.memset(V[:, :, :, HD] if not long else V[:, :, :, :, HD], 1.0)
                if keys == "causal":
                    for h in range(2):
                        dve.wait_ge(s_cx, h + 1)
                        nc.vector.tensor_copy(CX[:, h * HALF:(h + 1) * HALF], pS[:, h, 0:HALF])\
                          .then_inc(s_cxs, 1)
                if not weights_natural:
                    dve.wait_ge(s_wT, 4)
                else:
                    dve.wait_ge(m.loaded[name], m.load_total[name])
                for dst, src, n in ((wqe, wTs[0], NG), (wke, wTs[1], NK)):
                    for j in range(NJ):
                        p, a = j // 2, j % 2
                        last = nc.vector.tensor_copy(
                            dst[:, p, :, 64 * a:64 * a + MAXROW].rearrange("p g (k d) -> p g k d", d=HD),
                            src[:, j * n * HD:(j + 1) * n * HD].rearrange("p (g d) -> p g d", d=HD)
                            .unsqueeze(2).broadcast_to((128, n, SLOTS, HD)))
                if not weights_natural:
                    for n in (2, 3):
                        last = nc.vector.tensor_copy(wT[:, n - 2, 0:rows[n]], wTs[n])
                last.then_inc(s_w, 1)
                if bias is not None:
                    dve.wait_ge(s_col, 1)
                    nc.vector.tensor_copy(bcol[:, MASK:NCOLS], m.cols[:, MASK:NCOLS])
                    chain.then(nc.vector.tensor_copy(bcol[:, 0:MASK], pO[:, 0:MASK]))
                    bias_times_mask(nc, mcol, bcol).then_inc(s_bias, 1)

                def read(n):
                    unit = units[n]
                    kind = unit[0]
                    bank = n % 2 if n < FIRST else 0
                    if kind == "V":
                        dve.wait_ge(s_up, n + 1)
                        if long:
                            b, k0 = unit[1], NKT // 2 * unit[2]
                            if b >= 2 and k0 == 0:
                                dve.wait_ge(s_eu, NU * (b - 1))
                            parts = [(k0, k0 + 6, 128)] if k0 == 0 else [(k0, k0 + 5, 128), (k0 + 5, NKT, TAIL)]
                            for ka, kb, r in parts:
                                last = nc.vector.tensor_copy(
                                    V[0:r, b % 2, ka:kb, :, 0:HD],
                                    pP[0:r, bank, 32 * (ka - k0):32 * (kb - k0)]
                                    .rearrange("p (k j d) -> p k j d", j=NJ, d=HD))
                            last.then_inc(s_x1, 1)
                        else:
                            nc.vector.tensor_copy(V[:, unit[1], :, 0:HD],
                                                  pP[0:T, bank, 0:KD].rearrange("p (h d) -> p h d", d=HD))\
                              .then_inc(s_x1, 1)
                        return
                    i = split_before(n)
                    W = width(unit)
                    dve.wait_ge(s_t1, i + 1)
                    if i >= 2:
                        dve.wait_ge(s_fin, i - 1)
                        dve.wait_ge(s_qv, min(i - 1, NQ))
                    if kind == "M":
                        nc.vector.tensor_tensor(X1[:, i % 2, 0:W], pP[:, bank, 0:W], T1[:, i % 2, 0:W],
                                                ALU.subtract).then_inc(s_x1, 1)
                    else:
                        c = bias_column(unit)
                        nc.vector.scalar_tensor_tensor(
                            out=X1[:, i % 2, 0:W], in0=pP[:, bank, 0:W], scalar=bcol[:, c:c + 1],
                            in1=T1[:, i % 2, 0:W], op0=ALU.add, op1=ALU.subtract).then_inc(s_x1, 1)

                def maximum(n):
                    b, u = n // MU, n % MU
                    dve.wait_ge(s_m, n + 1)
                    if long:
                        j, g, c = u // (3 * NG), u // 3 % NG, u % 3
                        nc.vector.tensor_reduce(MH[:, b % 2, j, g, c:c + 1], pM[0:T, n % 3, 0:CH[c]],
                                                AX.X, ALU.max, negate=True).then_inc(s_mr, 1)
                    else:
                        nc.vector.tensor_reduce(nm[:, b % 2, u, :],
                                                pM[0:T, n % 3, 0:NG * T].rearrange("p (g k) -> p g k", k=T),
                                                AX.X, ALU.max, negate=True).then_inc(s_mr, 1)
                    if u == MU - 1:
                        dve.wait_ge(s_mr, n + 1)
                        if long:
                            chain.then(nc.vector.tensor_reduce(nm[:, b % 2], MH[:, b % 2], AX.X, ALU.min))
                        for p in range(PAIRS):
                            last = nc.vector.tensor_copy(
                                MXP[:, b % 2, p].rearrange("t g (a c) -> t g a c", a=2)[:, :, :, MAXROW:MAXROW + 3],
                                nm[:, b % 2, 2 * p:2 * p + 2, :].rearrange("t a g -> t g a").unsqueeze(3)
                                .broadcast_to((T, NG, 2, 3)))
                        last.then_inc(s_mx, 1)

                def out_copied(b):
                    dve.wait_ge(s_eu, NU * (b + 1))
                    nc.vector.tensor_copy(OC[:, :], pO[:, 0:NG * T]).then_inc(s_oc, 1)

                def normalised(b):
                    dve.wait_ge(s_tt, b + 1)
                    v = pP[0:T, 1, :].rearrange("t (g j r) -> t g j r", g=NG, j=NJ)
                    chain.then(nc.vector.reciprocal(rden[:, :, :], v[:, :, :, HD]))
                    for g in range(NG):
                        last = nc.vector.tensor_tensor(
                            ON[:, :].rearrange("t (j g d) -> t j g d", g=NG, d=HD)[:, :, g, :],
                            v[:, g, :, 0:HD], rden[:, g, :].unsqueeze(2).broadcast_to((T, NJ, HD)), ALU.mult)
                    last.then_inc(s_on, 1)

                def residual(b):
                    dve.wait_ge(s_y, b + 1)
                    nc.vector.tensor_tensor(m.X[:, b, :], m.X[:, b, :], pP[0:T, 1, 128:256], ALU.add)\
                      .then_inc(s_x, 1)

                def query_half(n):
                    if units[n][0] != "Q":
                        return
                    _, p, g, h = units[n]
                    dve.wait_ge(s_t2, n + 1)
                    if n == 0:
                        dve.wait_ge(s_clear, 1)
                    nc.vector.tensor_tensor(QS[0:64, 2 * p, g, h * HALF:(h + 1) * HALF],
                                            X1[0:64, n % 2, 0:HALF], T2[0:64, n % 2, 0:HALF],
                                            ALU.subtract).then_inc(s_qv, 1)

                for n in range(FIRST):
                    read(n)
                    if n >= 1:
                        query_half(n - 1)
                for t in steps:
                    b, u = t // NU, t % NU
                    for n in at.get(t - DELAY, []):
                        read(n)
                    if t + LAG < B * MU:
                        maximum(t + LAG)
                    if b >= 1 and u == 0:
                        out_copied(b - 1)
                    if b >= 1 and u == NORM_AT:
                        normalised(b - 1)
                    if b >= 1 and u == RES_AT:
                        residual(b - 1)
                out_copied(B - 1)
                normalised(B - 1)
                residual(B - 1)

            @block.scalar
            def _(act):
                ln_scalar(nc, act, m, q, banks)
                if bias is not None:
                    act.wait_ge(s_bias, 1)

                def first_terms(n):
                    unit = units[n]
                    if unit[0] == "V":
                        return
                    i = split_before(n)
                    W = width(unit)
                    bank = n % 2 if n < FIRST else 0
                    act.wait_ge(s_up, n + 1)
                    c = MASK + (0 if unit[0] == "K" else 2)
                    if unit[0] == "M":
                        nc.scalar.activation(T1[:, i % 2, 0:W], pP[:, bank, 0:W], ACT.Copy,
                                             scale=bcol[:, c:c + 1]).then_inc(s_t1, 1)
                    else:
                        k = bias_column(unit)
                        nc.scalar.activation(T1[:, i % 2, 0:W], pP[:, bank, 0:W], ACT.Identity,
                                             bias=mcol[:, k:k + 1], scale=bcol[:, c:c + 1]).then_inc(s_t1, 1)

                def second_terms(n):
                    if units[n][0] == "V":
                        return
                    act.wait_ge(s_x1, n + 1)
                    i = split_before(n)
                    if i >= 2:
                        act.wait_ge(s_fin, i - 1)
                        act.wait_ge(s_qv, min(i - 1, NQ))
                    c = MASK + (1 if units[n][0] == "K" else 3)
                    W = width(units[n])
                    nc.scalar.activation(T2[:, i % 2, 0:W], X1[:, i % 2, 0:W], ACT.Copy,
                                         scale=bcol[:, c:c + 1]).then_inc(s_t2, 1)

                def exps(n):
                    k = n % NU // NJ
                    act.wait_ge(s_s, n + 1)
                    if n >= EB:
                        act.wait_ge(s_eu, n - EB + 1)
                    nc.scalar.activation(E[0:tiles[k], n % EB, :], pS[0:tiles[k], n % 2, 0:NG * T],
                                         ACT.Exp, scale=SCALE8).then_inc(s_e, 1)

                def outT(b):
                    act.wait_ge(s_ot, b + 1)
                    nc.scalar.copy(OT[:, :], pP[:, 1, 0:T]).then_inc(s_ots, 1)

                for n in range(FIRST):
                    first_terms(n)
                    if n >= 1:
                        second_terms(n - 1)
                for t in steps:
                    for n in at[t]:
                        first_terms(n)
                    for n in at.get(t - DELAY, []):
                        if not long:
                            second_terms(n)
                    if 0 <= t + NJ < STEPS:
                        exps(t + NJ)
                    if t // NU >= 1 and t % NU == OT_AT:
                        outT(t // NU - 1)
                outT(B - 1)

            @block.tensor
            def _(pe):
                if bias is not None:
                    pe.wait_ge(s_row, 1)
                    for i in range(MASK):
                        last = nc.tensor.matmul(pO[:, i:i + 1], brow[0:1, i, :], m.ones[0:1, 0:1],
                                                start=(i == 0), stop=True, skip_group_check=True)
                    last.then_inc(s_col, 1)
                pe.wait_ge(m.loaded[name], m.load_total[name])
                if not weights_natural:
                    for n in range(4):
                        nc.tensor.transpose(wTs[n], srcs[n][0:rows[n], :], m.ident[0:rows[n], 0:rows[n]])\
                          .then_inc(s_wT, 1)
                if keys == "causal":
                    for b in range(B):
                        pe.wait_ge(m.ctx_loaded[b], 32 * m.ctx_times)
                        last = nc.tensor.transpose(pS[:, b // HB, (b % HB) * T:(b % HB + 1) * T],
                                                   m.ctx_tm[0:T, b, 0, 0:D], m.ident[0:T, 0:T])
                        if b % HB == HB - 1:
                            last.then_inc(s_cx, 1)
                ln_tensor(nc, pe, m, q, banks)
                if keys == "causal":
                    pe.wait_ge(s_cxs, 2)
                pe.wait_ge(s_w, 1)
                pe.wait_ge(q.xTs, 2)
                wv_ap = srcs[2][:, :] if weights_natural else wT[:, 0, 0:KD]
                wo_ap = srcs[3][:, :] if weights_natural else wT[:, 1, :]

                def kv_src(b, n):
                    if keys == "self":
                        return m.XNT[:, b * T:(b + n) * T]
                    return CX[:, b * T:(b + n) * T]

                def unit_matmul(n):
                    unit = units[n]
                    kind = unit[0]
                    bank = n % 2 if n < FIRST else 0
                    if n < FIRST and n >= 2:
                        pe.wait_ge(s_x1, n - 1)
                    if n >= FIRST:
                        pe.wait_ge(s_x1, n)
                    if kind == "Q":
                        last = nc.tensor.matmul(pP[:, bank, 0:HALF], wqe[:, unit[1], unit[2], :],
                                                m.XNT[:, unit[3] * HALF:(unit[3] + 1) * HALF],
                                                start=True, stop=True)
                    elif kind == "K" and long:
                        c0, W = CH[0] * unit[3], width(unit)
                        last = nc.tensor.matmul(pP[:, bank, 0:W], wke[:, unit[1], 0, :],
                                                m.CT[:, unit[2], c0:c0 + W],
                                                start=True, stop=True)
                    elif kind == "K":
                        last = nc.tensor.matmul(pP[:, bank, 0:HALF], wke[:, unit[1], unit[2], :],
                                                kv_src(unit[3] * HB, HB), start=True, stop=True)
                    elif kind == "V" and long:
                        k0 = NKT // 2 * unit[2]
                        for k in range(k0, k0 + NKT // 2):
                            last = nc.tensor.matmul(pP[0:TILES[k], bank, 32 * (k - k0):32 * (k - k0) + 32],
                                                    m.CT[:, unit[1], k * 128:k * 128 + TILES[k]], wv_ap,
                                                    start=True, stop=True)
                    elif kind == "V":
                        last = nc.tensor.matmul(pP[0:T, bank, 0:KD], kv_src(unit[1], 1), wv_ap,
                                                start=True, stop=bias is None)
                        if bias is not None:
                            last = nc.tensor.matmul(pP[0:T, bank, 0:KD], m.ones[0:1, 0:T], bias[2][0:1, :],
                                                    start=False, stop=True)
                    else:
                        pe.wait_ge(s_mx, unit[2] + 1)
                        for g in range(NG):
                            last = nc.tensor.matmul(pP[:, bank, g * T:(g + 1) * T],
                                                    MXP[:, unit[2] % 2, unit[1], g, :], m.ident[0:T, 0:T],
                                                    start=(g == 0), stop=True, skip_group_check=True)
                    last.then_inc(s_up, 1)

                def max_scores(n):
                    b, u = n // MU, n % MU
                    if n >= 3:
                        pe.wait_ge(s_mr, n - 2)
                    if u == 0:
                        pe.wait_ge(s_fin, keys_ready(b))
                    if long:
                        j, g, c = u // (3 * NG), u // 3 % NG, u % 3
                        k0 = sum(CH[:c])
                        last = nc.tensor.matmul(pM[0:T, n % 3, 0:CH[c]], QS[:, j, g, b * T:(b + 1) * T],
                                                KS[:, b % KB, j // 2, k0:k0 + CH[c]], start=True, stop=True)
                    else:
                        if not grouped:
                            nc.tensor.matmul(pM[0:T, n % 3, 0:NG * T], ident16[:, :], mask16[:, 0, :],
                                             start=True, stop=False, skip_group_check=True)
                        for g in range(NG):
                            last = nc.tensor.matmul(
                                pM[0:T, n % 3, g * T:(g + 1) * T], QS[:, u, g, b * T:(b + 1) * T],
                                KS[:, g if NK > 1 else 0, u // 2, b * T:(b + 1) * T],
                                start=(grouped and g == 0), stop=True, skip_group_check=True)
                    last.then_inc(s_m, 1)

                def score(n):
                    b, u = n // NU, n % NU
                    k, j = u // NJ, u % NJ
                    if u == 0:
                        pe.wait_ge(s_fin, rows_split(b))
                    if n >= 2:
                        pe.wait_ge(s_e, n - 1)
                    if long:
                        last = nc.tensor.matmul(pS[0:tiles[k], n % 2, 0:NG * T],
                                                KS[:, b % KB, j // 2, k * 128:k * 128 + tiles[k]],
                                                QS[:, j, :, b * T:(b + 1) * T], start=True, stop=True)
                    elif grouped:
                        last = nc.tensor.matmul(pS[0:T, n % 2, 0:NG * T], KS[:, 0, j // 2, b * T:(b + 1) * T],
                                                QS[:, j, :, b * T:(b + 1) * T], start=True, stop=True)
                    else:
                        nc.tensor.matmul(pS[0:T, n % 2, 0:NG * T], ident16[:, :], mask16[:, 1, :],
                                         start=True, stop=False, skip_group_check=True)
                        for g in range(NG):
                            last = nc.tensor.matmul(pS[0:T, n % 2, g * T:(g + 1) * T],
                                                    KS[:, g, j // 2, b * T:(b + 1) * T],
                                                    QS[:, j, g, b * T:(b + 1) * T], start=False, stop=True,
                                                    skip_group_check=True)
                    last.then_inc(s_s, 1)

                def rows_split(b):
                    n = max(n for n, x in enumerate(units) if x[0] == "M" and x[2] == b)
                    return 1 + split_before(n)

                def weigh(n):
                    b, u = n // NU, n % NU
                    k, j = u // NJ, u % NJ
                    pe.wait_ge(s_e, n + 1)
                    if u == 0:
                        pe.wait_ge(s_x1, values_ready(b))
                        if b >= 1:
                            pe.wait_ge(s_oc, b)
                    out = pO[32 * j:32 * j + 32, 0:NG * T]
                    if grouped:
                        v = V[0:tiles[k], b % 2, k, j, :] if long else V[:, b, j, :]
                        last = nc.tensor.matmul(out, v, E[0:tiles[k], n % EB, :], start=(k == 0),
                                                stop=(k == nt - 1), skip_group_check=True)
                    else:
                        for g in range(NG):
                            last = nc.tensor.matmul(out[:, g * T:(g + 1) * T], V[:, b, NG * j + g, :],
                                                    E[0:T, n % EB, g * T:(g + 1) * T], start=(g == 0),
                                                    stop=True, skip_group_check=True)
                    last.then_inc(s_eu, 1)

                def token_major(b):
                    pe.wait_ge(s_oc, b + 1)
                    if b >= 1:
                        pe.wait_ge(s_x, b)
                    for g in range(NG):
                        last = nc.tensor.transpose(pP[0:T, 1, g * 128:(g + 1) * 128], OC[:, g * T:(g + 1) * T],
                                                   m.ident[:, :])
                    last.then_inc(s_tt, 1)

                def turn(b):
                    pe.wait_ge(s_on, b + 1)
                    nc.tensor.transpose(pP[:, 1, 0:T], ON[:, :], m.ident[0:T, 0:T]).then_inc(s_ot, 1)

                def project(b):
                    pe.wait_ge(s_ots, b + 1)
                    last = nc.tensor.matmul(pP[0:T, 1, 128:256], OT[:, :], wo_ap, start=True,
                                            stop=bias is None)
                    if bias is not None:
                        last = nc.tensor.matmul(pP[0:T, 1, 128:256], m.ones[0:1, 0:T], bias[3][0:1, :],
                                                start=False, stop=True)
                    last.then_inc(s_y, 1)

                for n in range(FIRST):
                    unit_matmul(n)
                pe.wait_ge(s_qv, NQ)
                for t in steps:
                    b, u = t // NU, t % NU
                    for n in at[t]:
                        unit_matmul(n)
                    if t + LAG < B * MU:
                        max_scores(t + LAG)
                    if 0 <= t + NJ < STEPS:
                        score(t + NJ)
                    if b >= 1 and u == TM_AT:
                        token_major(b - 1)
                    if b >= 1 and u == TURN_AT:
                        turn(b - 1)
                    if b >= 1 and u == PROJ_AT:
                        project(b - 1)
                    if t >= 0 and u % NJ == NJ - 1:
                        for n in range(t - NJ + 1, t + 1):
                            weigh(n)
                token_major(B - 1)
                turn(B - 1)
                project(B - 1)



def context_block(nc, m, name, normalise, nth):
    with ExitStack() as ctx:
        s = Stage(nc, ctx, name)
        pT = s.ps("pT", [128, 6, 512])
        junk = s.sb("junk", [128, NKT, D])
        ss = s.sb("ss", [128, B, NKT])
        rs = s.sb("rs", [128, B, NKT])
        s_sq, s_sq2, s_ms = s.sem("squares_vector"), s.sem("squares_scalar"), s.sem("mean_squares")
        s_r, s_n = s.sem("rstd"), s.sem("normalised")
        s_t, s_c = s.sem("transposed"), s.sem("copied_even")
        s_c2 = s.sem("copied_odd")
        groups = [(b, g) for b in range(B) for g in range(3)]

        with nc.Block(no_gpsimd_drain=True) as block:

            @block.gpsimd
            def _(pool):
                if not normalise:
                    return
                for b in range(B):
                    pool.wait_ge(s_ms, b + 1)
                    nc.gpsimd.tensor_tensor(rs[:, b, :], ss[:, b, :], m.neg_half[:, 0:NKT], ALU.pow)\
                      .then_inc(s_r, 1)

            @block.vector
            def _(dve):
                def copies(b):
                    for g in range(3):
                        i = 3 * b + g
                        if i % 2 == 0:
                            dve.wait_ge(s_t, i + 1)
                            nc.vector.tensor_copy(m.CT[:, b, g * 512:(g + 1) * 512], pT[:, i % 6, :])\
                              .then_inc(s_c, 1)

                for b in range(B):
                    if normalise:
                        dve.wait_ge(m.ctx_loaded[b], 32 * nth)
                        for k in range(NKT // 2):
                            last = nc.vector.scalar_tensor_tensor(
                                out=junk[:, k, :], in0=m.ctx_tm[:, b, k, 0:D], scalar=1.0,
                                in1=m.ctx_tm[:, b, k, 0:D], op0=ALU.mult, op1=ALU.mult,
                                accum_out=ss[:, b, k:k + 1])
                        last.then_inc(s_sq, 1)
                        dve.wait_ge(s_sq, b + 1)
                        dve.wait_ge(s_sq2, b + 1)
                        nc.vector.tensor_scalar(ss[:, b, :], ss[:, b, :], 1.0 / D, 1e-6, ALU.mult, ALU.add)\
                          .then_inc(s_ms, 1)
                        if b >= 1:
                            copies(b - 1)
                        dve.wait_ge(s_r, b + 1)
                        nc.vector.tensor_tensor(m.ctx_tm[:, b, :, 0:D], m.ctx_tm[:, b, :, 0:D],
                                                rs[:, b, :].unsqueeze(2).broadcast_to((128, NKT, D)),
                                                ALU.mult).then_inc(s_n, 1)
                    else:
                        copies(b)
                if normalise:
                    copies(B - 1)

            @block.scalar
            def _(act):
                def copies(b):
                    for g in range(3):
                        i = 3 * b + g
                        if i % 2 == 1:
                            act.wait_ge(s_t, i + 1)
                            nc.scalar.copy(m.CT[:, b, g * 512:(g + 1) * 512], pT[:, i % 6, :])\
                              .then_inc(s_c2, 1)

                for b in range(B):
                    if normalise:
                        act.wait_ge(m.ctx_loaded[b], 32 * nth)
                        if b >= 1:
                            act.wait_ge(s_sq2, b)
                        for k in range(NKT // 2, NKT):
                            last = nc.scalar.activation(junk[:, k, :], m.ctx_tm[:, b, k, 0:D], ACT.Square,
                                                        accum_out=ss[:, b, k:k + 1])
                        last.then_inc(s_sq2, 1)
                        if b >= 1:
                            copies(b - 1)
                    else:
                        copies(b)
                if normalise:
                    copies(B - 1)

            @block.tensor
            def _(pe):
                for i, (b, g) in enumerate(groups):
                    if normalise:
                        pe.wait_ge(s_n, b + 1)
                    else:
                        pe.wait_ge(m.ctx_loaded[b], 32 * nth)
                    if i >= 6:
                        if i % 2 == 0:
                            pe.wait_ge(s_c, (i - 6) // 2 + 1)
                        else:
                            pe.wait_ge(s_c2, (i - 6) // 2 + 1)
                    for k in range(4):
                        last = nc.tensor.transpose(pT[:, i % 6, k * 128:(k + 1) * 128],
                                                   m.ctx_tm[:, b, 4 * g + k, 0:D], m.ident[:, :])
                    last.then_inc(s_t, 1)


def load_context(sp, m, b):
    src = m.a["ctx_1024"]
    sp.dma_start(m.ctx_tm[:, b, 0:KT_FULL, 0:D],
                 src[b, 0:KT_FULL * 128, :].rearrange("(k p) d -> p k d", p=128)).then_inc(m.ctx_loaded[b], 16)
    sp.dma_start(m.ctx_tm[0:TAIL, b, KT_FULL, 0:D], src[b, KT_FULL * 128:SC, :]).then_inc(m.ctx_loaded[b], 16)



def slot_attention(nc, m):
    name = "L0x"
    w = m.w
    ITERS = 3
    N = ITERS * B
    G4 = 512
    with ExitStack() as ctx:
        s = Stage(nc, ctx, name)
        q = ln_sems(s)
        Mqk = s.sb("Mqk", [128, 128])
        G = s.sb("G", [128, 3 * D])
        wihT = s.sb("wihT", [128, 3 * D])
        whhT = s.sb("whhT", [128, 3 * D])
        grow = s.sb("gate_bias", [1, G4])
        ssq = s.sb("ssq", [T, 2])
        rsl = s.sb("rsl", [T, 2])
        junk = s.sb("junk", [T, D])
        SN = s.sb("SN", [T, 2, D])
        STs = s.sb("STs", [128, 2, 2, T])
        QS = s.sb("QS", [128, 2, T])
        mx = s.sb("mx", [128, 2, 12])
        E = s.sb("E", [128, 2, 12, T])
        Z = s.sb("Z", [128, 2, 12])
        RZ = s.sb("RZ", [128, 2, 12])
        den = s.sb("den", [T, 2])
        U = s.sb("U", [T, D])
        UT = s.sb("UT", [128, T])
        rz = s.sb("rz", [T, 2, 2 * D])
        nn = s.sb("nn", [T, 2, 3, D])
        pS = s.ps("pS", [128, 2, 3, 512])
        pT = s.ps("pT", [128, 512])
        pG = s.ps("pG", [128, 512])
        vch = s.sem("vector_own")
        gch = s.sem("gpsimd_own")
        s_wt, s_wc, s_w2, s_wr = s.sem("gru_transposed"), s.sem("gru_copied"), s.sem("products"), s.sem("weights")
        s_sq, s_r, s_sn = s.sem("slot_squares"), s.sem("slot_rstd"), s.sem("slots_normalised")
        s_t, s_ts = s.sem("slotsT_psum"), s.sem("slotsT_sbuf")
        s_q, s_qs = s.sem("q_psum"), s.sem("q_sbuf")
        s_s, s_sub, s_e = s.sem("scores"), s.sem("less_max"), s.sem("exps")
        s_rz, s_en = s.sem("rec_of_sums"), s.sem("attention")
        s_u, s_us = s.sem("update_psum"), s.sem("update_sbuf")
        s_ut, s_uts = s.sem("updateT_psum"), s.sem("updateT_sbuf")
        s_g, s_th = s.sem("gates_psum"), s.sem("tanh_rz")
        s_ni, s_n = s.sem("n_argument"), s.sem("n")
        s_slot = s.sem("slots_updated")

        with nc.Block(no_gpsimd_drain=True) as block:

            @block.sync
            def _(sp):
                for b in range(B):
                    sp.wait_ge(s_u, N - B + b + 1)
                    load_context(sp, m, b)

            @block.gpsimd
            def _(pool):
                ln_gpsimd(nc, pool, m, q)
                chain = Chain(pool, gch)

                def rstd(n):
                    pool.wait_ge(s_sq, n + 1)
                    nc.gpsimd.tensor_tensor(rsl[:, n % 2:n % 2 + 1], ssq[:, n % 2:n % 2 + 1],
                                            m.neg_half[0:T, 0:1], ALU.pow).then_inc(s_r, 1)

                def normalise(n):
                    pool.wait_ge(s_rz, n + 1)
                    nc.gpsimd.tensor_tensor(E[:, n % 2, :, :], E[:, n % 2, :, :],
                                            RZ[:, n % 2, :].unsqueeze(2).broadcast_to((128, 12, T)),
                                            ALU.mult).then_inc(s_en, 1)

                def update(n):
                    b = n % B
                    pool.wait_ge(s_n, n + 1)
                    chain.then(nc.gpsimd.tensor_tensor(nn[:, n % 2, 2, :], m.XN[:, b, :], nn[:, n % 2, 1, :],
                                                       ALU.subtract))
                    chain.then(nc.gpsimd.tensor_tensor(nn[:, n % 2, 2, :], nn[:, n % 2, 2, :],
                                                       rz[:, n % 2, D:2 * D], ALU.mult))
                    nc.gpsimd.tensor_tensor(m.XN[:, b, :], nn[:, n % 2, 2, :], nn[:, n % 2, 1, :],
                                            ALU.add).then_inc(s_slot, 1)

                rstd(0)
                for n in range(N):
                    if n + 1 < N:
                        rstd(n + 1)
                    normalise(n)
                    if n >= 1:
                        update(n - 1)
                update(N - 1)

            @block.vector
            def _(dve):
                chain = Chain(dve, vch)
                ln_vector(nc, dve, chain, m, q)
                dve.wait_ge(m.loaded[name], m.load_total[name])
                bi, bh = w["x0bi"], w["x0bh"]
                nc.vector.tensor_tensor(grow[0:1, 0:2 * D], bi[0:1, 0:2 * D], bh[0:1, 0:2 * D], ALU.add)
                nc.vector.tensor_copy(grow[0:1, 2 * D:3 * D], bi[0:1, 2 * D:3 * D])
                nc.vector.tensor_copy(grow[0:1, 3 * D:4 * D], bh[0:1, 2 * D:3 * D])
                dve.wait_ge(s_wt, 2)
                nc.vector.tensor_copy(wihT[:, :], pS[:, 0, 0, 0:3 * D])
                nc.vector.tensor_copy(whhT[:, :], pS[:, 0, 1, 0:3 * D]).then_inc(s_wc, 1)
                dve.wait_ge(s_w2, 1)
                nc.vector.tensor_scalar(G[:, :], pS[:, 0, 2, 0:3 * D], w["x0iw"][:, 0:1], None, ALU.mult)
                nc.vector.tensor_scalar(Mqk[:, :], pS[:, 1, 0, 0:D], w["x0sw"][:, 0:1], float(D) ** -0.5,
                                        ALU.mult, ALU.mult).then_inc(s_wr, 1)
                dve.wait_ge(q.norm, B)

                def slot_stats(n):
                    b = n % B
                    if n >= B:
                        dve.wait_ge(s_slot, n - B + 1)
                    chain.then(nc.vector.scalar_tensor_tensor(
                        out=junk[:, :], in0=m.XN[:, b, :], scalar=1.0, in1=m.XN[:, b, :],
                        op0=ALU.mult, op1=ALU.mult, accum_out=ssq[:, n % 2:n % 2 + 1]))
                    nc.vector.tensor_scalar(ssq[:, n % 2:n % 2 + 1], ssq[:, n % 2:n % 2 + 1], 1.0 / D, 1e-6,
                                            ALU.mult, ALU.add).then_inc(s_sq, 1)

                def slot_norm(n):
                    dve.wait_ge(s_r, n + 1)
                    if n >= 2:
                        dve.wait_ge(s_t, n - 1)
                    nc.vector.tensor_scalar(SN[:, n % 2, :], m.XN[:, n % B, :], rsl[:, n % 2:n % 2 + 1], None,
                                            ALU.mult).then_inc(s_sn, 1)

                def less_max(n):
                    dve.wait_ge(s_s, n + 1)
                    sc = pS[:, n % 2, :, 0:4 * T].rearrange("p c (k t) -> p c k t", t=T)
                    mxv = mx[:, n % 2, :].rearrange("p (c k) -> p c k", k=4)
                    chain.then(nc.vector.tensor_reduce(mxv, sc, AX.X, ALU.max))
                    if n >= 2:
                        dve.wait_ge(s_u, n - 1)
                    nc.vector.tensor_tensor(E[:, n % 2, :, :].rearrange("p (c k) t -> p c k t", k=4), sc,
                                            mxv.unsqueeze(3).broadcast_to((128, 3, 4, T)),
                                            ALU.subtract).then_inc(s_sub, 1)

                def sums(n):
                    dve.wait_ge(s_e, n + 1)
                    chain.then(nc.vector.tensor_reduce(Z[:, n % 2, :], E[:, n % 2, :, :], AX.X, ALU.add))
                    nc.vector.reciprocal(RZ[:, n % 2, :], Z[:, n % 2, :]).then_inc(s_rz, 1)

                def scale_update(n):
                    dve.wait_ge(s_u, n + 1)
                    chain.then(nc.vector.tensor_scalar(den[:, 0:1], pG[0:T, D:D + 1], 1e-6, None, ALU.add))
                    chain.then(nc.vector.reciprocal(den[:, 1:2], den[:, 0:1]))
                    nc.vector.tensor_scalar(U[:, :], pG[0:T, 0:D], den[:, 1:2], None, ALU.mult).then_inc(s_us, 1)

                def gates(n):
                    dve.wait_ge(s_th, n + 1)
                    if n >= 2:
                        dve.wait_ge(s_slot, n - 1)
                    chain.then(nc.vector.tensor_scalar(rz[:, n % 2, :], rz[:, n % 2, :], 0.5, 0.5,
                                                       ALU.mult, ALU.add))
                    chain.then(nc.vector.tensor_tensor(nn[:, n % 2, 0, :], pG[0:T, 3 * D:4 * D],
                                                       rz[:, n % 2, 0:D], ALU.mult))
                    nc.vector.tensor_tensor(nn[:, n % 2, 0, :], pG[0:T, 2 * D:3 * D], nn[:, n % 2, 0, :],
                                            ALU.add).then_inc(s_ni, 1)

                slot_stats(0)
                slot_norm(0)
                slot_stats(1)
                slot_norm(1)
                less_max(0)
                for n in range(N):
                    sums(n)
                    if n + 2 < N:
                        slot_stats(n + 2)
                    if n + 1 < N:
                        less_max(n + 1)
                    if n + 2 < N:
                        slot_norm(n + 2)
                    scale_update(n)
                    gates(n)
                for b in range(B):
                    dve.wait_ge(s_slot, N - B + b + 1)
                    nc.vector.tensor_tensor(m.X[:, b, :], m.X[:, b, :], m.XN[:, b, :], ALU.add)

            @block.scalar
            def _(act):
                def slotsT(n):
                    act.wait_ge(s_t, n + 1)
                    if n >= 2:
                        act.wait_ge(s_g, n - 1)
                    nc.scalar.copy(STs[:, n % 2, :, :],
                                   pT[:, 0:256].rearrange("p (i t) -> p i t", i=2)[:, :, 0:T]).then_inc(s_ts, 1)

                def queries(n):
                    act.wait_ge(s_q, n + 1)
                    nc.scalar.activation(QS[:, n % 2, :], pT[:, 256:256 + T], ACT.Copy,
                                         scale=w["x0iw"][:, 0:1]).then_inc(s_qs, 1)

                def exps(n):
                    act.wait_ge(s_sub, n + 1)
                    nc.scalar.activation(E[:, n % 2, :, :], E[:, n % 2, :, :], ACT.Exp).then_inc(s_e, 1)

                def after(n):
                    act.wait_ge(s_ut, n + 1)
                    nc.scalar.copy(UT[:, :], pT[:, 384:384 + T]).then_inc(s_uts, 1)
                    act.wait_ge(s_g, n + 1)
                    if n >= 2:
                        act.wait_ge(s_slot, n - 1)
                    nc.scalar.activation(rz[:, n % 2, :], pG[0:T, 0:2 * D], ACT.Tanh, scale=0.5)\
                      .then_inc(s_th, 1)
                    act.wait_ge(s_ni, n + 1)
                    nc.scalar.activation(nn[:, n % 2, 1, :], nn[:, n % 2, 0, :], ACT.Tanh).then_inc(s_n, 1)

                act.wait_ge(m.loaded[name], m.load_total[name])
                slotsT(0)
                queries(0)
                exps(0)
                for n in range(N):
                    if n + 1 < N:
                        slotsT(n + 1)
                        queries(n + 1)
                        exps(n + 1)
                    after(n)

            @block.tensor
            def _(pe):
                pe.wait_ge(m.loaded[name], m.load_total[name])
                for i, key in enumerate(("x0ih", "x0hh")):
                    for c in range(3):
                        last = nc.tensor.transpose(pS[:, 0, i, c * D:(c + 1) * D], w[key][:, c, :], m.ident[:, :])
                    last.then_inc(s_wt, 1)
                nc.tensor.matmul(pS[:, 1, 0, 0:D], w["x0q"][:, :], w["x0k"][:, :], start=True, stop=True)
                pe.wait_ge(s_wc, 1)
                nc.tensor.matmul(pS[:, 0, 2, 0:3 * D], w["x0v"][:, :], wihT[:, :], start=True, stop=True)\
                  .then_inc(s_w2, 1)
                pe.wait_ge(s_wr, 1)

                def scores(n):
                    b = n % B
                    pe.wait_ge(s_sn, n + 1)
                    nc.tensor.transpose(pT[:, 0:T], m.XN[:, b, :], m.ident[0:T, 0:T])
                    nc.tensor.transpose(pT[:, 128:128 + T], SN[:, n % 2, :], m.ident[0:T, 0:T]).then_inc(s_t, 1)
                    pe.wait_ge(s_ts, n + 1)
                    nc.tensor.matmul(pT[:, 256:256 + T], Mqk[:, :], STs[:, n % 2, 1, :],
                                     start=True, stop=True).then_inc(s_q, 1)
                    pe.wait_ge(s_qs, n + 1)
                    if n >= 2:
                        pe.wait_ge(s_sub, n - 1)
                    for k in range(12):
                        last = nc.tensor.matmul(pS[:, n % 2, k // 4, (k % 4) * T:(k % 4 + 1) * T],
                                                m.CT[:, b, k * 128:(k + 1) * 128], QS[:, n % 2, :],
                                                start=True, stop=True)
                    last.then_inc(s_s, 1)

                def update(n):
                    b = n % B
                    pe.wait_ge(s_en, n + 1)
                    if n >= 1:
                        pe.wait_ge(s_ni, n)
                    for k, rows in enumerate(TILES):
                        last = nc.tensor.matmul(pG[0:T, 0:D + 1], E[0:rows, n % 2, k, :],
                                                m.ctx_tm[0:rows, b, k, :], start=(k == 0), stop=(k == NKT - 1))
                    last.then_inc(s_u, 1)
                    pe.wait_ge(s_us, n + 1)
                    nc.tensor.transpose(pT[:, 384:384 + T], U[:, :], m.ident[0:T, 0:T]).then_inc(s_ut, 1)
                    pe.wait_ge(s_uts, n + 1)
                    nc.tensor.matmul(pG[0:T, :], m.ones[0:1, 0:T], grow[0:1, :], start=True, stop=False,
                                     skip_group_check=True)
                    nc.tensor.matmul(pG[0:T, 0:3 * D], UT[:, :], G[:, :], start=False, stop=False,
                                     skip_group_check=True)
                    nc.tensor.matmul(pG[0:T, 0:2 * D], STs[:, n % 2, 0, :], whhT[:, 0:2 * D], start=False,
                                     stop=False, skip_group_check=True)
                    nc.tensor.matmul(pG[0:T, 3 * D:4 * D], STs[:, n % 2, 0, :], whhT[:, 2 * D:3 * D],
                                     start=False, stop=True, skip_group_check=True).then_inc(s_g, 1)

                scores(0)
                for n in range(N):
                    if n + 1 < N:
                        scores(n + 1)
                    update(n)



NE = 8


def first_largest(nc, chain, m, val, top, eq, best, onehot):
    chain.then(nc.vector.tensor_reduce(top, val, AX.X, ALU.max))
    chain.then(nc.vector.tensor_tensor(eq, val, top.unsqueeze(2).broadcast_to((T, B, NE)), ALU.is_equal))
    chain.then(nc.vector.tensor_tensor(eq, eq, m.order[:, :, :], ALU.mult))
    chain.then(nc.vector.tensor_reduce(best, eq, AX.X, ALU.max))
    chain.then(nc.vector.tensor_tensor(onehot, eq, best.unsqueeze(2).broadcast_to((T, B, NE)), ALU.is_equal))


def mixture_golden(nc, m):
    name = "L0f"
    w = m.w
    CENTER, LOWER, UPPER = 0.36787944117144233, 0.5 - 0.28768207245178085, 0.5
    N = 2 * NE
    with ExitStack() as ctx:
        s = Stage(nc, ctx, name)
        q = ln_sems(s)
        small = [s.sb(f"r{i}", [T, B, NE]) for i in range(8)]
        inh, dist, wz, fb, mask, t1, t2, zone = small
        sums = [s.sb(f"s{i}", [T, B]) for i in range(4)]
        itemp = s.sb("itemp", [T, 1])
        WT = s.sb("WT", [NE, TOK])
        SG = s.sb("SG", [128, 2, HALF])
        H = s.sb("H", [128, 2, HALF])
        pG = s.ps("pG", [128, 2, 512])
        pU = s.ps("pU", [128, 2, 512])
        pW = s.ps("pW", [128, 2, 512])
        pY = s.ps("pY", [128, 2, 512])
        vch = s.sem("vector_own")
        s_tp, s_lg, s_it = s.sem("temperature_psum"), s.sem("logits"), s.sem("inverse_temperature")
        s_ex, s_ds, s_fw = s.sem("exp_of_logits"), s.sem("distances"), s.sem("exp_of_distances")
        s_rw, s_wt, s_wts = s.sem("routing_weights"), s.sem("weightsT_psum"), s.sem("weightsT_sbuf")
        s_g, s_sg, s_h, s_y = s.sem("gate_up"), s.sem("silu"), s.sem("hidden"), s.sem("out")

        with nc.Block(no_gpsimd_drain=True) as block:

            @block.gpsimd
            def _(pool):
                ln_gpsimd(nc, pool, m, q)

            @block.vector
            def _(dve):
                chain = Chain(dve, vch)
                ln_vector(nc, dve, chain, m, q)
                dve.wait_ge(s_tp, 1)
                chain.then(nc.vector.reciprocal(itemp[:, :], pU[0:T, 0, 0:1]))
                nc.vector.tensor_scalar(itemp[:, :], itemp[:, :], -1.0, None, ALU.mult).then_inc(s_it, 1)
                dve.wait_ge(s_ex, 1)
                chain.then(nc.vector.tensor_scalar(inh[:, :, :], inh[:, :, :], 1.0, None, ALU.add))
                chain.then(nc.vector.reciprocal(inh[:, :, :], inh[:, :, :]))
                chain.then(nc.vector.tensor_scalar(t1[:, :, :], inh[:, :, :], CENTER, None, ALU.subtract))
                nc.vector.scalar_tensor_tensor(out=dist[:, :, :], in0=t1[:, :, :], scalar=-1.0,
                                               in1=t1[:, :, :], op0=ALU.mult, op1=ALU.max).then_inc(s_ds, 1)
                chain.then(nc.vector.tensor_scalar(zone[:, :, :], inh[:, :, :], LOWER, None, ALU.is_ge))
                chain.then(nc.vector.scalar_tensor_tensor(
                    out=zone[:, :, :], in0=inh[:, :, :], scalar=UPPER, in1=zone[:, :, :],
                    op0=ALU.is_le, op1=ALU.mult))
                dve.wait_ge(s_fw, 2)
                chain.then(nc.vector.tensor_tensor(wz[:, :, :], wz[:, :, :], zone[:, :, :], ALU.mult))
                first_largest(nc, chain, m, fb[:, :, :], sums[0][:, :], t1[:, :, :], sums[1][:, :],
                              mask[:, :, :])
                chain.then(nc.vector.scalar_tensor_tensor(
                    out=zone[:, :, :], in0=mask[:, :, :], scalar=-2.0, in1=fb[:, :, :],
                    op0=ALU.mult, op1=ALU.add))
                first_largest(nc, chain, m, zone[:, :, :], sums[0][:, :], t1[:, :, :], sums[1][:, :],
                              t2[:, :, :])
                chain.then(nc.vector.tensor_tensor(mask[:, :, :], mask[:, :, :], t2[:, :, :], ALU.add))
                chain.then(nc.vector.tensor_tensor(fb[:, :, :], fb[:, :, :], mask[:, :, :], ALU.mult))

                def over_sum(v, sm):
                    chain.then(nc.vector.tensor_reduce(sm, v, AX.X, ALU.add))
                    chain.then(nc.vector.tensor_scalar(sm, sm, 1e-8, None, ALU.max))
                    chain.then(nc.vector.reciprocal(sm, sm))
                    chain.then(nc.vector.tensor_tensor(v, v, sm.unsqueeze(2).broadcast_to((T, B, NE)), ALU.mult))

                over_sum(fb[:, :, :], sums[0][:, :])
                chain.then(nc.vector.tensor_reduce(sums[2][:, :], wz[:, :, :], AX.X, ALU.add))
                chain.then(nc.vector.tensor_scalar(sums[3][:, :], sums[2][:, :], 1e-8, None, ALU.is_lt))
                chain.then(nc.vector.tensor_tensor(t1[:, :, :], fb[:, :, :], wz[:, :, :], ALU.subtract))
                chain.then(nc.vector.tensor_tensor(
                    t1[:, :, :], t1[:, :, :], sums[3][:, :].unsqueeze(2).broadcast_to((T, B, NE)), ALU.mult))
                chain.then(nc.vector.tensor_tensor(wz[:, :, :], wz[:, :, :], t1[:, :, :], ALU.add))
                over_sum(wz[:, :, :], sums[0][:, :])
                nc.vector.memset(itemp[:, :], 0.0).then_inc(s_rw, 1)
                dve.wait_ge(s_wt, 1)
                nc.vector.tensor_copy(WT[:, 0:HALF], pG[0:NE, 0, 0:HALF])
                nc.vector.tensor_copy(WT[:, HALF:TOK], pG[0:NE, 1, 0:HALF]).then_inc(s_wts, 1)
                for n in range(N):
                    dve.wait_ge(s_sg, n + 1)
                    if n >= 2:
                        dve.wait_ge(s_y, n - 1)
                    chain.then(nc.vector.tensor_tensor(H[:, n % 2, :], SG[:, n % 2, :], pU[:, n % 2, 0:HALF],
                                                       ALU.mult))
                    nc.vector.tensor_tensor(H[:, n % 2, :], H[:, n % 2, :], pW[:, n % 2, 0:HALF],
                                            ALU.mult).then_inc(s_h, 1)
                for h in range(2):
                    dve.wait_ge(s_y, N - 1 + h)
                    nc.vector.tensor_tensor(m.X[:, h * HB:(h + 1) * HB, :], m.X[:, h * HB:(h + 1) * HB, :],
                                            pY[0:T, h, :].rearrange("p (b d) -> p b d", d=D), ALU.add)

            @block.scalar
            def _(act):
                ln_scalar(nc, act, m, q, [pG[:, 0, :], pG[:, 1, :]])
                act.wait_ge(s_lg, 1)
                act.wait_ge(s_it, 1)
                nc.scalar.activation(inh[:, :, :], pW[0:T, 0, 0:B * NE].rearrange("p (b e) -> p b e", e=NE),
                                     ACT.Exp, scale=itemp[:, 0:1]).then_inc(s_ex, 1)
                act.wait_ge(s_ds, 1)
                nc.scalar.activation(wz[:, :, :], dist[:, :, :], ACT.Exp, scale=-10.0).then_inc(s_fw, 1)
                nc.scalar.activation(fb[:, :, :], dist[:, :, :], ACT.Exp, scale=-1.0 / 0.3).then_inc(s_fw, 1)
                for n in range(N):
                    act.wait_ge(s_g, n + 1)
                    if n >= 2:
                        act.wait_ge(s_h, n - 1)
                    nc.scalar.activation(SG[:, n % 2, :], pG[:, n % 2, 0:HALF], ACT.Silu).then_inc(s_sg, 1)

            @block.tensor
            def _(pe):
                pe.wait_ge(m.loaded[name], m.load_total[name])
                nc.tensor.matmul(pU[0:T, 0, 0:1], m.ones[0:1, 0:T], w["f0t"][:, :], start=True, stop=True)\
                  .then_inc(s_tp, 1)
                ln_tensor(nc, pe, m, q, [pG[:, 0, :], pG[:, 1, :]])
                pe.wait_ge(q.xTs, 2)
                for b in range(B):
                    last = nc.tensor.matmul(pW[0:T, 0, b * NE:(b + 1) * NE], m.XNT[:, b * T:(b + 1) * T],
                                            w["f0r"][:, :], start=True, stop=True)
                last.then_inc(s_lg, 1)
                pe.wait_ge(s_rw, 1)
                for b in range(B):
                    last = nc.tensor.transpose(pG[0:NE, b // HB, (b % HB) * T:(b % HB + 1) * T], wz[:, b, :],
                                               m.ident[0:T, 0:T])
                last.then_inc(s_wt, 1)
                pe.wait_ge(s_wts, 1)

                def up(n):
                    e, h = n // 2, n % 2
                    if n >= 2:
                        pe.wait_ge(s_h, n - 1)
                    x = m.XNT[:, h * HALF:(h + 1) * HALF]
                    nc.tensor.matmul(pG[:, n % 2, 0:HALF], w["f0g"][:, e, :], x, start=True, stop=True)
                    nc.tensor.matmul(pU[:, n % 2, 0:HALF], w["f0u"][:, e, :], x, start=True, stop=True)
                    nc.tensor.matmul(pW[:, n % 2, 0:HALF], m.sel[:, e, :], WT[:, h * HALF:(h + 1) * HALF],
                                     start=True, stop=True).then_inc(s_g, 1)

                up(0)
                for n in range(N):
                    if n + 1 < N:
                        up(n + 1)
                    e, h = n // 2, n % 2
                    pe.wait_ge(s_h, n + 1)
                    for i in range(HB):
                        last = nc.tensor.matmul(pY[0:T, h, i * D:(i + 1) * D], H[:, n % 2, i * T:(i + 1) * T],
                                                w["f0d"][:, e, :], start=(e == 0 and i == 0),
                                                stop=(e == NE - 1), skip_group_check=True)
                    last.then_inc(s_y, 1)



def attention_regrouped(nc, m):
    name = "L1a"
    w = m.w
    R = T // 4
    FL = T * 32
    RC = 5
    N = R // RC
    with ExitStack() as ctx:
        s = Stage(nc, ctx, name)
        q = ln_sems(s)
        scr = nc.dram_tensor("regroup_in", (32, 4, FL), F32).ap()
        scr2 = nc.dram_tensor("regroup_out", (32, FL), F32).ap()
        free = m.CT[:, :, :].rearrange("p b k -> p (b k)")
        QK = free[0:T, 0:B * 512].rearrange("t (b c) -> t b c", b=B)
        S1, S2 = [free[:, B * 512 * (i + 1):B * 512 * (i + 1) + 2 * RC * NH * NH]
                  .rearrange("p (u r h k) -> p u r h k", u=2, r=RC, h=NH) for i in (0, 1)]
        L = s.sb("L", [128, 4, NH, R, 2])
        mx = s.sb("mx", [128, 2, RC, NH])
        den = s.sb("den", [128, 2, RC, NH])
        OA = s.sb("OA", [128, 2, 2, RC, NH])
        O = s.sb("O", [128, NH, R, 2])
        OX = s.sb("OX", [T, B, D])
        pT = s.ps("pT", [128, 2, 512])
        pQ = s.ps("pQ", [128, 4, 512])
        pY = s.ps("pY", [128, 2, 512])
        vch, gch = s.sem("vector_own"), s.sem("gpsimd_own")
        s_q, s_qs = s.sem("qkvw_psum"), s.sem("qkvw_sbuf")
        s_d, s_l = s.sem("in_dram"), s.sem("regrouped")
        s_p0, s_sc = s.sem("products_d1"), s.sem("less_max")
        s_e, s_pv, s_dn = s.sem("exps"), s.sem("weighted_d1"), s.sem("used")
        s_o, s_od, s_ox = s.sem("out_sbuf"), s.sem("out_in_dram"), s.sem("out_token_major")
        s_t, s_ts, s_y = s.sem("outT_psum"), s.sem("outT_sbuf"), s.sem("y_psum")

        def at(i, n, d):
            return L[:, i, :, n * RC:(n + 1) * RC, d].rearrange("p h r -> p r h")

        def rows(ap):
            return ap.unsqueeze(3).broadcast_to((128, RC, NH, NH))

        def cols(ap):
            return ap.unsqueeze(2).broadcast_to((128, RC, NH, NH))

        with nc.Block(no_gpsimd_drain=True) as block:

            @block.sync
            def _(sp):
                for b in range(B):
                    sp.wait_ge(s_qs, b + 1)
                    for i in range(4):
                        sp.dma_start(scr[i * B + b].rearrange("j (t c) -> t j c", c=32),
                                     QK[:, b, i * 128:(i + 1) * 128].rearrange("t (j c) -> t j c", c=32))\
                          .then_inc(s_d, 16)
                sp.wait_ge(s_d, 16 * 4 * B)
                for rq in range(4):
                    sp.dma_start(L[rq * 32:(rq + 1) * 32, :, :, :, :].rearrange("n j h r d -> n (j h) (r d)"),
                                 scr.rearrange("n j (h x) -> n (j h) x", x=2 * T)[:, :, 2 * R * rq:2 * R * (rq + 1)])\
                      .then_inc(s_l, 16)
                sp.wait_ge(s_o, 1)
                for rq in range(4):
                    sp.dma_start(scr2.rearrange("n (h x) -> n h x", x=2 * T)[:, :, 2 * R * rq:2 * R * (rq + 1)],
                                 O[rq * 32:(rq + 1) * 32, :, :, :].rearrange("n h r d -> n h (r d)"))\
                      .then_inc(s_od, 16)
                sp.wait_ge(s_od, 64)
                sp.dma_start(OX[:, :, :], scr2.rearrange("n x -> (n x)").rearrange("(b t d) -> t b d", t=T, d=D))\
                  .then_inc(s_ox, 16)

            @block.gpsimd
            def _(pool):
                ln_gpsimd(nc, pool, m, q)
                pool.wait_ge(s_l, 64)

                def products(n):
                    if n >= 2:
                        pool.wait_ge(s_dn, n - 1)
                    nc.gpsimd.tensor_tensor(S2[:, n % 2], rows(at(0, n, 1)), cols(at(1, n, 1)), ALU.mult)\
                      .then_inc(s_p0, 1)

                products(0)
                for n in range(N):
                    if n + 1 < N:
                        products(n + 1)
                    pool.wait_ge(s_e, n + 1)
                    nc.gpsimd.tensor_tensor(S2[:, n % 2], S1[:, n % 2], cols(at(2, n, 1)), ALU.mult)\
                      .then_inc(s_pv, 1)

            @block.vector
            def _(dve):
                chain = Chain(dve, vch)
                ln_vector(nc, dve, chain, m, q)
                dve.wait_ge(s_l, 64)

                def scores(n):
                    if n >= 2:
                        dve.wait_ge(s_pv, n - 1)
                    chain.then(nc.vector.tensor_tensor(S1[:, n % 2], rows(at(0, n, 0)), cols(at(1, n, 0)), ALU.mult))
                    dve.wait_ge(s_p0, n + 1)
                    chain.then(nc.vector.tensor_tensor(S1[:, n % 2], S1[:, n % 2], S2[:, n % 2], ALU.add))
                    chain.then(nc.vector.tensor_reduce(mx[:, n % 2], S1[:, n % 2], AX.X, ALU.max))
                    nc.vector.tensor_tensor(S1[:, n % 2], S1[:, n % 2], rows(mx[:, n % 2]),
                                            ALU.subtract).then_inc(s_sc, 1)

                scores(0)
                for n in range(N):
                    if n + 1 < N:
                        scores(n + 1)
                    dve.wait_ge(s_e, n + 1)
                    chain.then(nc.vector.tensor_reduce(den[:, n % 2], S1[:, n % 2], AX.X, ALU.add))
                    chain.then(nc.vector.reciprocal(den[:, n % 2], den[:, n % 2]))
                    dve.wait_ge(s_pv, n + 1)
                    chain.then(nc.vector.tensor_reduce(OA[:, n % 2, 1], S2[:, n % 2], AX.X, ALU.add))
                    chain.then(nc.vector.tensor_tensor(S1[:, n % 2], S1[:, n % 2], cols(at(2, n, 0)), ALU.mult))
                    chain.then(nc.vector.tensor_reduce(OA[:, n % 2, 0], S1[:, n % 2], AX.X, ALU.add))
                    nc.vector.tensor_tensor(OA[:, n % 2, 0], OA[:, n % 2, 0], den[:, n % 2], ALU.mult)
                    chain.then(nc.vector.tensor_tensor(OA[:, n % 2, 1], OA[:, n % 2, 1], den[:, n % 2], ALU.mult))
                    for d in range(2):
                        last = nc.vector.tensor_tensor(
                            O[:, :, n * RC:(n + 1) * RC, d].rearrange("p h r -> p r h"), OA[:, n % 2, d],
                            at(3, n, d), ALU.mult)
                    last.then_inc(s_dn, 1)
                dve.wait_ge(s_dn, N)
                nc.vector.memset(mx[:, 0], 0.0).then_inc(s_o, 1)
                for h in range(2):
                    dve.wait_ge(s_y, h + 1)
                    nc.vector.tensor_tensor(m.X[:, h * HB:(h + 1) * HB, :], m.X[:, h * HB:(h + 1) * HB, :],
                                            pY[0:T, h, :].rearrange("p (b d) -> p b d", d=D), ALU.add)

            @block.scalar
            def _(act):
                ln_scalar(nc, act, m, q, [pT[:, 0, :], pT[:, 1, :]])
                for b in range(B):
                    act.wait_ge(s_q, b + 1)
                    nc.scalar.copy(QK[:, b, :], pQ[0:T, b % 4, :]).then_inc(s_qs, 1)
                for n in range(N):
                    act.wait_ge(s_sc, n + 1)
                    nc.scalar.activation(S1[:, n % 2], S1[:, n % 2], ACT.Exp, scale=2.0 ** -0.5).then_inc(s_e, 1)
                for h in range(2):
                    act.wait_ge(s_t, h + 1)
                    nc.scalar.copy(m.XNT[:, h * HALF:(h + 1) * HALF], pT[:, h, 0:HALF]).then_inc(s_ts, 1)

            @block.tensor
            def _(pe):
                ln_tensor(nc, pe, m, q, [pT[:, 0, :], pT[:, 1, :]])
                pe.wait_ge(m.loaded[name], m.load_total[name])
                pe.wait_ge(q.xTs, 2)
                for b in range(B):
                    if b >= 4:
                        pe.wait_ge(s_qs, b - 3)
                    nc.tensor.matmul(pQ[0:T, b % 4, :], m.XNT[:, b * T:(b + 1) * T], w["a1w"][:, :],
                                     start=True, stop=True).then_inc(s_q, 1)
                pe.wait_ge(s_qs, B)
                pe.wait_ge(s_ox, 16)
                for h in range(2):
                    for i in range(HB):
                        last = nc.tensor.transpose(pT[:, h, i * T:(i + 1) * T], OX[:, h * HB + i, :],
                                                   m.ident[0:T, 0:T])
                    last.then_inc(s_t, 1)
                for h in range(2):
                    pe.wait_ge(s_ts, h + 1)
                    for i in range(HB):
                        b = h * HB + i
                        last = nc.tensor.matmul(pY[0:T, h, i * D:(i + 1) * D], m.XNT[:, b * T:(b + 1) * T],
                                                w["a1o"][:, :], start=True, stop=True)
                    last.then_inc(s_y, 1)



def attention_wide(nc, m):
    name = "L2x"
    w = m.w
    C = SC // 4
    SCALE = float(D) ** -0.5
    with ExitStack() as ctx:
        s = Stage(nc, ctx, name)
        q = ln_sems(s)
        Mqk = s.sb("Mqk", [128, 128])
        WvT = s.sb("WvT", [128, 128])
        QS = s.sb("QS", [128, TOK])
        nmx = s.sb("nmx", [T, 2])
        E = s.sb("E", [T, 2, SC])
        sm = s.sb("sm", [T, 4])
        ET = s.sb("ET", [128, NKT, T])
        U = s.sb("U", [T, D])
        UT = s.sb("UT", [128, T])
        pS = s.ps("pS", [128, 4, 512])
        pE = s.ps("pE", [128, 3, 512])
        pO = s.ps("pO", [128, 512])
        vch = s.sem("vector_own")
        s_w, s_ws = s.sem("weights_psum"), s.sem("weights_ready")
        s_q, s_qs = s.sem("q_psum"), s.sem("q_sbuf")
        s_s, s_m, s_e = s.sem("scores"), s.sem("maximum"), s.sem("exps")
        s_t, s_tc, s_tc2 = s.sem("expsT_psum"), s.sem("expsT_vector"), s.sem("expsT_scalar")
        s_u, s_us = s.sem("sums_psum"), s.sem("sums_scaled")
        s_ut, s_uts, s_y, s_x = s.sem("sumsT_psum"), s.sem("sumsT_sbuf"), s.sem("y_psum"), s.sem("added")

        with nc.Block(no_gpsimd_drain=True) as block:

            @block.gpsimd
            def _(pool):
                ln_gpsimd(nc, pool, m, q)

            @block.vector
            def _(dve):
                chain = Chain(dve, vch)
                dve.wait_ge(s_w, 1)
                nc.vector.tensor_copy(Mqk[:, :], pE[:, 2, 0:128])
                nc.vector.tensor_copy(WvT[:, :], pE[:, 2, 128:256]).then_inc(s_ws, 1)
                ln_vector(nc, dve, chain, m, q)

                def maximum(b):
                    dve.wait_ge(s_s, b + 1)
                    if b >= 2:
                        dve.wait_ge(s_e, b - 1)
                    chain.then(nc.vector.tensor_reduce(nmx[:, b % 2:b % 2 + 1], pS[0:T, :, 0:C], AX.XY,
                                                       ALU.max, negate=True))
                    nc.vector.tensor_scalar(nmx[:, b % 2:b % 2 + 1], nmx[:, b % 2:b % 2 + 1], SCALE, None,
                                            ALU.mult).then_inc(s_m, 1)

                maximum(0)
                for b in range(B):
                    dve.wait_ge(s_t, 3 * b + 1)
                    if b >= 1:
                        dve.wait_ge(s_u, b)
                    nc.vector.tensor_copy(ET[:, 0:4, :], pE[:, 0, 0:4 * T].rearrange("p (k t) -> p k t", t=T))\
                      .then_inc(s_tc, 1)
                    if b + 1 < B:
                        maximum(b + 1)
                    dve.wait_ge(s_t, 3 * b + 3)
                    nc.vector.tensor_copy(ET[:, 8:11, :], pE[:, 2, 0:3 * T].rearrange("p (k t) -> p k t", t=T))
                    nc.vector.tensor_copy(ET[0:TAIL, 11, :], pE[0:TAIL, 2, 3 * T:4 * T]).then_inc(s_tc, 1)
                    chain.then(nc.vector.reciprocal(sm[:, 2:3], sm[:, b % 2:b % 2 + 1]))
                    dve.wait_ge(s_u, b + 1)
                    nc.vector.tensor_scalar(U[:, :], pO[0:T, 0:D], sm[:, 2:3], None, ALU.mult).then_inc(s_us, 1)
                    dve.wait_ge(s_y, b + 1)
                    nc.vector.tensor_tensor(m.X[:, b, :], m.X[:, b, :], pO[0:T, 256:256 + D], ALU.add)\
                      .then_inc(s_x, 1)

            @block.scalar
            def _(act):
                ln_scalar(nc, act, m, q, [pE[:, 0, :], pE[:, 1, :]])
                for h in range(2):
                    act.wait_ge(s_q, h + 1)
                    nc.scalar.copy(QS[:, h * HALF:(h + 1) * HALF], pS[:, h, 0:HALF]).then_inc(s_qs, 1)

                def exps(b):
                    act.wait_ge(s_m, b + 1)
                    if b >= 2:
                        act.wait_ge(s_us, b - 1)
                    nc.scalar.activation(E[:, b % 2, :].rearrange("p (c k) -> p c k", k=C), pS[0:T, :, 0:C],
                                         ACT.Exp, bias=nmx[:, b % 2:b % 2 + 1], scale=SCALE,
                                         accum_out=sm[:, b % 2:b % 2 + 1]).then_inc(s_e, 1)

                exps(0)
                for b in range(B):
                    if b + 1 < B:
                        exps(b + 1)
                    act.wait_ge(s_t, 3 * b + 2)
                    nc.scalar.copy(ET[:, 4:8, :], pE[:, 1, 0:4 * T].rearrange("p (k t) -> p k t", t=T))\
                      .then_inc(s_tc2, 1)
                    act.wait_ge(s_ut, b + 1)
                    nc.scalar.copy(UT[:, :], pO[:, 128:128 + T]).then_inc(s_uts, 1)

            @block.tensor
            def _(pe):
                pe.wait_ge(m.loaded[name], m.load_total[name])
                nc.tensor.matmul(pE[:, 2, 0:128], w["x2q"][:, :], w["x2k"][:, :], start=True, stop=True)
                nc.tensor.transpose(pE[:, 2, 128:256], w["x2v"][:, :], m.ident[:, :]).then_inc(s_w, 1)
                ln_tensor(nc, pe, m, q, [pE[:, 0, :], pE[:, 1, :]])
                pe.wait_ge(s_ws, 1)
                for h in range(2):
                    pe.wait_ge(q.xTs, h + 1)
                    nc.tensor.matmul(pS[:, h, 0:HALF], Mqk[:, :], m.XNT[:, h * HALF:(h + 1) * HALF],
                                     start=True, stop=True).then_inc(s_q, 1)
                pe.wait_ge(s_qs, 2)

                def scores(b):
                    if b >= 1:
                        pe.wait_ge(s_e, b)
                    for c in range(4):
                        last = nc.tensor.matmul(pS[0:T, c, 0:C], QS[:, b * T:(b + 1) * T],
                                                m.CT[:, b, c * C:(c + 1) * C], start=True, stop=True)
                    last.then_inc(s_s, 1)

                scores(0)
                for b in range(B):
                    pe.wait_ge(s_e, b + 1)
                    for g in range(3):
                        if b >= 1:
                            if g == 1:
                                pe.wait_ge(s_tc2, b)
                            else:
                                pe.wait_ge(s_tc, 2 * b - (1 if g == 0 else 0))
                        for k in range(4 * g, 4 * g + 4):
                            last = nc.tensor.transpose(pE[0:TILES[k], g, (k % 4) * T:(k % 4 + 1) * T],
                                                       E[:, b % 2, k * 128:k * 128 + TILES[k]],
                                                       m.ident[0:T, 0:T])
                        last.then_inc(s_t, 1)
                    if b + 1 < B:
                        scores(b + 1)
                    pe.wait_ge(s_tc, 2 * b + 2)
                    pe.wait_ge(s_tc2, b + 1)
                    if b >= 1:
                        pe.wait_ge(s_x, b)
                    for k in range(NKT):
                        last = nc.tensor.matmul(pO[0:T, 0:D], ET[0:TILES[k], k, :],
                                                m.ctx_tm[0:TILES[k], b, k, 0:D],
                                                start=(k == 0), stop=(k == NKT - 1))
                    last.then_inc(s_u, 1)
                    pe.wait_ge(s_us, b + 1)
                    nc.tensor.transpose(pO[:, 128:128 + T], U[:, :], m.ident[0:T, 0:T]).then_inc(s_ut, 1)
                    pe.wait_ge(s_uts, b + 1)
                    nc.tensor.matmul(pO[0:T, 256:256 + D], UT[:, :], WvT[:, :], start=True, stop=True)\
                      .then_inc(s_y, 1)



def two_norms_vector(nc, dve, chain, m, q, q2):
    ln_vector(nc, dve, chain, m, q)
    dve.wait_ge(q.norm, B)
    ln_vector(nc, dve, chain, m, q2, src=m.XN, dst=m.XN2)


def add_psum(nc, dve, chain, m, h, out):
    x, xn = m.X[:, h * HB:(h + 1) * HB, :], m.XN[:, h * HB:(h + 1) * HB, :]
    chain.then(nc.vector.tensor_tensor(x, x, xn, ALU.add))
    return nc.vector.tensor_tensor(x, x, out.rearrange("p (b d) -> p b d", d=D), ALU.add)



def attention_fixed_keys(nc, m):
    name = "L2a"
    w = m.w
    N = 32
    W = 32
    with ExitStack() as ctx:
        s = Stage(nc, ctx, name)
        q, q2 = ln_sems(s), ln_sems(s, "ln2")
        wf4 = s.sb("wf4", [128, 4, 4, W])
        KF = s.sb("KF", [128, 4, 128])
        VF = s.sb("VF", [128, 128])
        RL = s.sb("RL", [128, 2, HALF])
        P = s.sb("P", [128, 2, HALF])
        pT = s.ps("pT", [128, 2, 512])
        pS = s.ps("pS", [128, 4, 512])
        pY = s.ps("pY", [128, 2, 512])
        vch = s.sem("vector_own")
        s_w4, s_wt, s_ws = s.sem("keys_repeated"), s.sem("weights_transposed"), s.sem("weights_ready")
        s_s, s_r, s_p, s_y = s.sem("scores"), s.sem("relu"), s.sem("squares"), s.sem("out")

        with nc.Block(no_gpsimd_drain=True) as block:

            @block.gpsimd
            def _(pool):
                ln_gpsimd(nc, pool, m, q)
                ln_gpsimd(nc, pool, m, q2)

            @block.vector
            def _(dve):
                chain = Chain(dve, vch)
                dve.wait_ge(m.loaded[name], m.load_total[name])
                for h in range(4):
                    last = nc.vector.tensor_copy(wf4[:, :, h, :], w["a2f"][:, :].rearrange("c (j d) -> c j d", d=W))
                last.then_inc(s_w4, 1)
                two_norms_vector(nc, dve, chain, m, q, q2)
                dve.wait_ge(s_wt, 1)
                nc.vector.tensor_copy(KF[:, :, :], pS[:, 0, :].rearrange("p (j c) -> p j c", c=128))
                nc.vector.tensor_copy(VF[:, :], pS[:, 1, 0:128]).then_inc(s_ws, 1)
                for n in range(N):
                    dve.wait_ge(s_r, n + 1)
                    if n >= 2:
                        dve.wait_ge(s_y, n - 1)
                    nc.vector.tensor_tensor(P[:, n % 2, :], RL[:, n % 2, :], pS[:, n % 4, 0:HALF],
                                            ALU.mult).then_inc(s_p, 1)
                for h in range(2):
                    dve.wait_ge(s_y, N // 2 * (h + 1))
                    add_psum(nc, dve, chain, m, h, pY[0:T, h, :])

            @block.scalar
            def _(act):
                ln_scalar(nc, act, m, q2, [pT[:, 0, :], pT[:, 1, :]], (w["a2g"], w["a2b"]))
                for n in range(N):
                    act.wait_ge(s_s, n + 1)
                    if n >= 2:
                        act.wait_ge(s_p, n - 1)
                    nc.scalar.activation(RL[:, n % 2, :], pS[:, n % 4, 0:HALF], ACT.Relu).then_inc(s_r, 1)

            @block.tensor
            def _(pe):
                pe.wait_ge(s_w4, 1)
                for j in range(4):
                    nc.tensor.transpose(pS[:, 0, j * 128:(j + 1) * 128], wf4[:, j, :, :], m.ident[:, :])
                nc.tensor.transpose(pS[:, 1, 0:128], w["a2p"][:, :], m.ident[:, :]).then_inc(s_wt, 1)
                ln_tensor(nc, pe, m, q2, [pT[:, 0, :], pT[:, 1, :]], m.XN2)
                pe.wait_ge(s_ws, 1)
                pe.wait_ge(q2.xTs, 2)

                def scores(n):
                    h, j = n // 4 % 4, n % 4
                    half = n // 16
                    if n >= 4:
                        pe.wait_ge(s_p, n - 3)
                    nc.tensor.matmul(pS[:, n % 4, 0:HALF], KF[W * h:W * (h + 1), j, :],
                                     m.XNT[W * h:W * (h + 1), half * HALF:(half + 1) * HALF],
                                     start=True, stop=True).then_inc(s_s, 1)

                for n in range(3):
                    scores(n)
                for n in range(N):
                    if n + 3 < N:
                        scores(n + 3)
                    h, j, half = n // 4 % 4, n % 4, n // 16
                    pe.wait_ge(s_p, n + 1)
                    for i in range(HB):
                        last = nc.tensor.matmul(pY[0:T, half, i * D + W * h:i * D + W * (h + 1)],
                                                P[:, n % 2, i * T:(i + 1) * T], VF[:, W * j:W * (j + 1)],
                                                start=(n % 16 == 0 and i == 0), stop=(j == 3),
                                                skip_group_check=True)
                    last.then_inc(s_y, 1)



def mixture_top1(nc, m):
    name = "L2f"
    w = m.w
    CAPACITY = 256
    IT = 4
    N = 2 * NE
    with ExitStack() as ctx:
        s = Stage(nc, ctx, name)
        q, q2 = ln_sems(s), ln_sems(s, "ln2")
        gwT = s.sb("gwT", [128, NE])
        lg, eq, oh, pre, rk = [s.sb(f"r{i}", [T, B, NE]) for i in range(5)]
        top, best, wt, keep = [s.sb(f"s{i}", [T, B]) for i in range(4)]
        OHT = s.sb("OHT", [NE, TOK])
        XM = s.sb("XM", [128, 2, HALF])
        H = s.sb("H", [128, 2, IT, HALF])
        YW = s.sb("YW", [T, HB, D])
        pC = s.ps("pC", [128, 2, 512])
        pU = s.ps("pU", [128, 4, 512])
        pY = s.ps("pY", [128, 2, 512])
        vch = s.sem("vector_own")
        s_wt, s_ws, s_lg, s_oh = s.sem("router_transposed"), s.sem("router_ready"), s.sem("logits"), s.sem("one_hot")
        s_dl, s_ex, s_rk = s.sem("logits_less_max"), s.sem("exp_of_logits"), s.sem("ranks")
        s_ot, s_ots = s.sem("one_hotT_psum"), s.sem("one_hotT_sbuf")
        s_c, s_xm = s.sem("mask_spread"), s.sem("tokens_masked")
        s_u, s_h, s_y = s.sem("up"), s.sem("gelu"), s.sem("out")

        free = m.ctx_tm[:, :, :, :].rearrange("p b k d -> p (b k d)")
        wi = free[:, 0:NE * 512].rearrange("p (e i) -> p e i", e=NE)
        wo = free[:, NE * 512:2 * NE * 512].rearrange("p (e i d) -> p e i d", e=NE, d=D)
        s_wi, s_wo = s.sem("wi_loaded"), s.sem("wo_loaded")

        with nc.Block(no_gpsimd_drain=True) as block:

            @block.sync
            def _(sp):
                for b in range(B):
                    sp.wait_ge(m.ctx_loaded[b], 32 * m.ctx_times)
                for e in range(0, NE, 2):
                    sp.dma_start(wi[:, e:e + 2, :], m.a["L2_ffn_wi"][e:e + 2].rearrange("e d i -> d e i"))\
                      .then_inc(s_wi, 16)
                    sp.dma_start(wo[:, e:e + 2, :, :].rearrange("p e i d -> p (e i) d"),
                                 m.a["L2_ffn_wo"][e:e + 2].rearrange("e (i p) d -> p (e i) d", p=128))\
                      .then_inc(s_wo, 16)

            @block.gpsimd
            def _(pool):
                ln_gpsimd(nc, pool, m, q)
                ln_gpsimd(nc, pool, m, q2)

            @block.vector
            def _(dve):
                chain = Chain(dve, vch)
                dve.wait_ge(s_wt, 1)
                nc.vector.tensor_copy(gwT[:, :], pU[:, 0, 0:NE]).then_inc(s_ws, 1)
                two_norms_vector(nc, dve, chain, m, q, q2)
                dve.wait_ge(s_lg, 1)
                chain.then(nc.vector.tensor_copy(lg[:, :, :], pU[0:T, 1, 0:B * NE].rearrange("p (b e) -> p b e", e=NE)))
                first_largest(nc, chain, m, lg[:, :, :], top[:, :], eq[:, :, :], best[:, :], oh[:, :, :])
                chain.then(nc.vector.memset(pre[:, 0, :], 0.0))
                for b in range(1, B):
                    ins = nc.vector.tensor_tensor(pre[:, b, :], pre[:, b - 1, :], oh[:, b - 1, :], ALU.add)
                    if b < B - 1:
                        chain.then(ins)
                ins.then_inc(s_oh, 1)
                nc.vector.tensor_tensor(lg[:, :, :], lg[:, :, :], top[:, :].unsqueeze(2).broadcast_to((T, B, NE)),
                                        ALU.subtract).then_inc(s_dl, 1)
                dve.wait_ge(s_ot, 1)
                nc.vector.tensor_copy(OHT[:, 0:HALF], pC[0:NE, 0, 0:HALF])
                nc.vector.tensor_copy(OHT[:, HALF:TOK], pC[0:NE, 1, 0:HALF]).then_inc(s_ots, 1)
                dve.wait_ge(s_ex, 1)
                chain.then(nc.vector.tensor_reduce(wt[:, :], eq[:, :, :], AX.X, ALU.add))
                chain.then(nc.vector.reciprocal(wt[:, :], wt[:, :]))
                dve.wait_ge(s_rk, 1)
                chain.then(nc.vector.tensor_tensor(
                    rk[:, :, :], pU[0:T, 2, 0:B * NE].rearrange("p (b e) -> p b e", e=NE), oh[:, :, :], ALU.mult))
                chain.then(nc.vector.tensor_reduce(keep[:, :], rk[:, :, :], AX.X, ALU.add))
                chain.then(nc.vector.tensor_scalar(keep[:, :], keep[:, :], float(CAPACITY), None, ALU.is_lt))
                chain.then(nc.vector.tensor_tensor(wt[:, :], wt[:, :], keep[:, :], ALU.mult))
                for n in range(N):
                    h = n % 2
                    dve.wait_ge(s_c, n + 1)
                    if n >= 2:
                        dve.wait_ge(s_u, IT * (n - 1))
                    nc.vector.tensor_tensor(XM[:, n % 2, :], m.XNT[:, h * HALF:(h + 1) * HALF],
                                            pC[:, n % 2, 0:HALF], ALU.mult).then_inc(s_xm, 1)
                for h in range(2):
                    dve.wait_ge(s_y, N - 1 + h)
                    x, xn = m.X[:, h * HB:(h + 1) * HB, :], m.XN[:, h * HB:(h + 1) * HB, :]
                    nc.vector.tensor_tensor(x, x, xn, ALU.add)
                    chain.then(nc.vector.tensor_tensor(
                        YW[:, :, :], pY[0:T, h, :].rearrange("p (b d) -> p b d", d=D),
                        wt[:, h * HB:(h + 1) * HB].unsqueeze(2).broadcast_to((T, HB, D)), ALU.mult))
                    chain.then(nc.vector.tensor_tensor(x, x, YW[:, :, :], ALU.add))

            @block.scalar
            def _(act):
                act.wait_ge(m.loaded[name], m.load_total[name])
                ln_scalar(nc, act, m, q2, [pC[:, 0, :], pC[:, 1, :]], (w["f2g"], w["f2b"]))
                act.wait_ge(s_dl, 1)
                nc.scalar.activation(eq[:, :, :], lg[:, :, :], ACT.Exp).then_inc(s_ex, 1)
                for u in range(N * IT):
                    act.wait_ge(s_u, u + 1)
                    n = u // IT
                    if n >= 2:
                        act.wait_ge(s_y, n - 1)
                    nc.scalar.activation(H[:, n % 2, u % IT, :], pU[:, u % 4, 0:HALF], ACT.Gelu).then_inc(s_h, 1)

            @block.tensor
            def _(pe):
                pe.wait_ge(m.loaded[name], m.load_total[name])
                nc.tensor.transpose(pU[:, 0, 0:NE], w["f2r"][:, :], m.ident[0:NE, 0:NE]).then_inc(s_wt, 1)
                ln_tensor(nc, pe, m, q2, [pC[:, 0, :], pC[:, 1, :]], m.XN2)
                pe.wait_ge(s_ws, 1)
                pe.wait_ge(q2.xTs, 2)
                for b in range(B):
                    last = nc.tensor.matmul(pU[0:T, 1, b * NE:(b + 1) * NE], m.XNT[:, b * T:(b + 1) * T],
                                            gwT[:, :], start=True, stop=True)
                last.then_inc(s_lg, 1)
                pe.wait_ge(s_oh, 1)
                for b in range(B):
                    last = nc.tensor.transpose(pC[0:NE, b // HB, (b % HB) * T:(b % HB + 1) * T], oh[:, b, :],
                                               m.ident[0:T, 0:T])
                last.then_inc(s_ot, 1)
                nc.tensor.matmul(pU[0:T, 2, 0:B * NE], m.before[:, :], oh[:, :, :].rearrange("p b e -> p (b e)"),
                                 start=True, stop=False)
                nc.tensor.matmul(pU[0:T, 2, 0:B * NE], m.ones[0:T, 0:T], pre[:, :, :].rearrange("p b e -> p (b e)"),
                                 start=False, stop=True).then_inc(s_rk, 1)
                pe.wait_ge(s_ots, 1)
                pe.wait_ge(s_ex, 1)

                def spread(n):
                    e, h = n // 2, n % 2
                    if n >= 2:
                        pe.wait_ge(s_xm, n - 1)
                    nc.tensor.matmul(pC[:, n % 2, 0:HALF], m.sel[:, e, :], OHT[:, h * HALF:(h + 1) * HALF],
                                     start=True, stop=True).then_inc(s_c, 1)

                def up(n, i):
                    e = n // 2
                    u = n * IT + i
                    if i == 0:
                        pe.wait_ge(s_xm, n + 1)
                    if u >= 4:
                        pe.wait_ge(s_h, u - 3)
                    nc.tensor.matmul(pU[:, u % 4, 0:HALF], wi[:, e, i * 128:(i + 1) * 128],
                                     XM[:, n % 2, :], start=True, stop=True).then_inc(s_u, 1)

                def down(n, i):
                    e, h = n // 2, n % 2
                    pe.wait_ge(s_h, n * IT + i + 1)
                    for k in range(HB):
                        last = nc.tensor.matmul(pY[0:T, h, k * D:(k + 1) * D], H[:, n % 2, i, k * T:(k + 1) * T],
                                                wo[:, e, i, :], start=(e == 0 and i == 0 and k == 0),
                                                stop=(e == NE - 1 and i == IT - 1), skip_group_check=True)
                    if i == IT - 1:
                        last.then_inc(s_y, 1)

                pe.wait_ge(s_wi, 64)
                pe.wait_ge(s_wo, 64)
                spread(0)
                for n in range(N + 1):
                    if n + 1 < N:
                        spread(n + 1)
                    for i in range(IT):
                        if n < N:
                            up(n, i)
                        if n >= 1:
                            down(n - 1, i)



LEVELS = [1, 2, 4, 8, 16, 32, 64]
TTT_LR = 0.01
DS = 64


def attention_delta_rule(nc, m):
    name = "L3a"
    w = m.w
    NL = len(LEVELS)
    with ExitStack() as ctx:
        s = Stage(nc, ctx, name)
        q, q2 = ln_sems(s), ln_sems(s, "ln2")
        wkT = s.sb("wkT", [128, DS])
        wqT = s.sb("wqT", [128, DS])
        wvT = s.sb("wvT", [128, D])
        KT = s.sb("KT", [DS, TOK])
        QT = s.sb("QT", [DS, TOK])
        V = s.sb("V", [T, B, D])
        LT = m.ctx_tm[0:T, :, :, :].rearrange("p b k d -> p (b k d)")[:, 0:B * NL * T]\
            .rearrange("p (b l t) -> p b l t", b=B, l=NL)
        SQ = s.sb("SQ", [T, B, T])
        X = s.sb("X", [T, 2, HB, T])
        XT = s.sb("XT", [T, 2, HB, T])
        TP = s.sb("TP", [T, 2, HB, T])
        U = s.sb("U", [T, 2, HB, D])
        pA = s.ps("pA", [128, 2, 512])
        pB = s.ps("pB", [128, 2, 512])
        pC = s.ps("pC", [128, 2, 512])
        pD = s.ps("pD", [128, 2, 512])
        vch = s.sem("vector_own")
        s_wt, s_ws = s.sem("weights_transposed"), s.sem("weights_ready")
        s_kq, s_kqs, s_v, s_vs = s.sem("k_q_psum"), s.sem("k_q_sbuf"), s.sem("v_psum"), s.sem("v_sbuf")
        s_kk, s_l = s.sem("k_k_and_k_q"), s.sem("masked")
        s_x0 = s.sem("first_inverse")
        s_t, s_tp = s.sem("l_x_psum"), s.sem("l_x_sbuf")
        s_xx, s_x = s.sem("x_l_x"), s.sem("inverse_updated")
        s_u, s_us, s_y = s.sem("updates_psum"), s.sem("updates_sbuf"), s.sem("y_psum")

        with nc.Block(no_gpsimd_drain=True) as block:

            @block.gpsimd
            def _(pool):
                ln_gpsimd(nc, pool, m, q)
                ln_gpsimd(nc, pool, m, q2)

            @block.vector
            def _(dve):
                chain = Chain(dve, vch)
                dve.wait_ge(s_wt, 1)
                nc.vector.tensor_copy(wkT[:, :], pB[:, 0, 0:DS])
                nc.vector.tensor_copy(wqT[:, :], pB[:, 0, 128:128 + DS])
                nc.vector.tensor_copy(wvT[:, :], pB[:, 0, 256:256 + D]).then_inc(s_ws, 1)
                two_norms_vector(nc, dve, chain, m, q, q2)
                for h in range(2):
                    dve.wait_ge(s_v, h + 1)
                    nc.vector.tensor_scalar(V[:, h * HB:(h + 1) * HB, :],
                                            pD[0:T, h, :].rearrange("p (b d) -> p b d", d=D), TTT_LR, None,
                                            ALU.mult).then_inc(s_vs, 1)
                for b in range(B):
                    dve.wait_ge(m.ctx_loaded[b], 32 * m.ctx_times)
                for b in range(B):
                    dve.wait_ge(s_kk, b + 1)
                    kk = pC[0:T, b % 2, 0:T].unsqueeze(1)
                    chain.then(nc.vector.tensor_tensor(LT[:, b, :, :], kk.broadcast_to((T, NL, T)),
                                                       m.below[0:T, 1:NL + 1, 0:T], ALU.mult))
                    nc.vector.tensor_tensor(SQ[:, b, :], pC[0:T, b % 2, 128:128 + T], m.before[:, :], ALU.mult)
                    nc.vector.tensor_tensor(X[:, b // HB, b % HB, :], pC[0:T, b % 2, 0:T],
                                            m.below[0:T, 0, 0:T], ALU.mult)
                    chain.then(nc.vector.tensor_tensor(XT[:, b // HB, b % HB, :], m.ident[0:T, 0:T],
                                                       LT[:, b, 0, :], ALU.subtract))
                    nc.vector.tensor_tensor(X[:, b // HB, b % HB, :], m.ident[0:T, 0:T],
                                            X[:, b // HB, b % HB, :], ALU.subtract).then_inc(s_l, 1)
                for l in range(1, NL):
                    for h in range(2):
                        n = 2 * (l - 1) + h
                        dve.wait_ge(s_xx, n + 1)
                        pv = lambda p: p[0:T, h, 0:HALF].rearrange("p (b t) -> p b t", t=T)
                        if l < NL - 1:
                            nc.vector.tensor_tensor(X[:, h], X[:, h], pv(pB), ALU.subtract)
                        nc.vector.tensor_tensor(XT[:, h], XT[:, h], pv(pC), ALU.subtract).then_inc(s_x, 1)
                for h in range(2):
                    dve.wait_ge(s_y, h + 1)
                    add_psum(nc, dve, chain, m, h, pD[0:T, h, :])

            @block.scalar
            def _(act):
                act.wait_ge(m.loaded[name], m.load_total[name])
                ln_scalar(nc, act, m, q2, [pA[:, 0, :], pA[:, 1, :]], (w["a3g"], w["a3b"]))
                for h in range(2):
                    cols = slice(h * HALF, (h + 1) * HALF)
                    act.wait_ge(s_kq, 2 * h + 1)
                    nc.scalar.activation(KT[:, cols], pA[0:DS, h, 0:HALF], ACT.Identity,
                                         bias=w["a3bk"][:, 0:1]).then_inc(s_kqs, 1)
                    act.wait_ge(s_kq, 2 * h + 2)
                    nc.scalar.activation(QT[:, cols], pB[0:DS, h, 0:HALF], ACT.Identity,
                                         bias=w["a3bq"][:, 0:1]).then_inc(s_kqs, 1)
                for n in range(2 * (NL - 1)):
                    act.wait_ge(s_t, n + 1)
                    nc.scalar.copy(TP[:, n % 2], pA[0:T, n % 2, 0:HALF].rearrange("p (b t) -> p b t", t=T))\
                      .then_inc(s_tp, 1)
                for h in range(2):
                    act.wait_ge(s_u, h + 1)
                    nc.scalar.copy(U[:, h], pA[0:T, h, :].rearrange("p (b d) -> p b d", d=D)).then_inc(s_us, 1)

            @block.tensor
            def _(pe):
                pe.wait_ge(m.loaded[name], m.load_total[name])
                nc.tensor.transpose(pB[:, 0, 0:DS], w["a3k"][:, :], m.ident[0:DS, 0:DS])
                nc.tensor.transpose(pB[:, 0, 128:128 + DS], w["a3q"][:, :], m.ident[0:DS, 0:DS])
                nc.tensor.transpose(pB[:, 0, 256:256 + D], w["a3v"][:, :], m.ident[:, :]).then_inc(s_wt, 1)
                ln_tensor(nc, pe, m, q2, [pA[:, 0, :], pA[:, 1, :]], m.XN2)
                pe.wait_ge(s_ws, 1)
                for h in range(2):
                    pe.wait_ge(q2.xTs, 2)
                    x = m.XNT[:, h * HALF:(h + 1) * HALF]
                    nc.tensor.matmul(pA[0:DS, h, 0:HALF], wkT[:, :], x, start=True, stop=True).then_inc(s_kq, 1)
                    nc.tensor.matmul(pB[0:DS, h, 0:HALF], wqT[:, :], x, start=True, stop=True).then_inc(s_kq, 1)
                for h in range(2):
                    for i in range(HB):
                        b = h * HB + i
                        nc.tensor.matmul(pD[0:T, h, i * D:(i + 1) * D], m.XNT[:, b * T:(b + 1) * T], wvT[:, :],
                                         start=(i == 0), stop=False, skip_group_check=True)
                        last = nc.tensor.matmul(pD[0:T, h, i * D:(i + 1) * D], m.ones[0:1, 0:T],
                                                w["a3bv"][:, :], start=False, stop=True, skip_group_check=True)
                    last.then_inc(s_v, 1)
                pe.wait_ge(s_kqs, 4)
                for b in range(B):
                    if b >= 2:
                        pe.wait_ge(s_l, b - 1)
                    c = slice(b * T, (b + 1) * T)
                    nc.tensor.matmul(pC[0:T, b % 2, 0:T], KT[:, c], KT[:, c], start=True, stop=True)
                    nc.tensor.matmul(pC[0:T, b % 2, 128:128 + T], KT[:, c], QT[:, c], start=True, stop=True)\
                      .then_inc(s_kk, 1)
                pe.wait_ge(s_l, B)
                for l in range(1, NL):
                    for h in range(2):
                        n = 2 * (l - 1) + h
                        if n >= 2:
                            pe.wait_ge(s_x, n - 1)
                        for i in range(HB):
                            last = nc.tensor.matmul(pA[0:T, h, i * T:(i + 1) * T], LT[:, h * HB + i, l, :],
                                                    X[:, h, i, :], start=True, stop=True)
                        last.then_inc(s_t, 1)
                    for h in range(2):
                        n = 2 * (l - 1) + h
                        pe.wait_ge(s_tp, n + 1)
                        for i in range(HB):
                            if l < NL - 1:
                                nc.tensor.matmul(pB[0:T, h, i * T:(i + 1) * T], XT[:, h, i, :],
                                                 TP[:, h, i, :], start=True, stop=True)
                            last = nc.tensor.matmul(pC[0:T, h, i * T:(i + 1) * T], TP[:, h, i, :],
                                                    XT[:, h, i, :], start=True, stop=True)
                        last.then_inc(s_xx, 1)
                pe.wait_ge(s_vs, 2)
                for h in range(2):
                    pe.wait_ge(s_x, 2 * (NL - 2) + h + 1)
                    for i in range(HB):
                        last = nc.tensor.matmul(pA[0:T, h, i * D:(i + 1) * D], XT[:, h, i, :],
                                                V[:, h * HB + i, :], start=True, stop=True)
                    last.then_inc(s_u, 1)
                for h in range(2):
                    pe.wait_ge(s_us, h + 1)
                    for i in range(HB):
                        last = nc.tensor.matmul(pD[0:T, h, i * D:(i + 1) * D], SQ[:, h * HB + i, :],
                                                U[:, h, i, :], start=True, stop=True)
                    last.then_inc(s_y, 1)



def ffn_binary(nc, m):
    name = "L3f"
    w = m.w
    IT = 4
    N = 2 * IT
    with ExitStack() as ctx:
        s = Stage(nc, ctx, name)
        q = ln_sems(s)
        S1 = s.sb("S1", [128, IT, D])
        S2 = s.sb("S2", [128, IT * 128])
        S1T = s.sb("S1T", [128, IT, 128])
        S2T = s.sb("S2T", [128, IT, 128])
        al = s.sb("al", [128, IT + 1])
        H = s.sb("H", [128, 2, HALF])
        YT = s.sb("YT", [128, TOK])
        pT = s.ps("pT", [128, 2, 512])
        pW = s.ps("pW", [128, 2, 512])
        pH = s.ps("pH", [128, 2, 512])
        pY = s.ps("pY", [128, 2, 512])
        vch = s.sem("vector_own")
        s_al, s_sg = s.sem("mean_magnitudes"), s.sem("signs")
        s_wt, s_ws, s_h, s_g = s.sem("signs_transposed"), s.sem("weights_ready"), s.sem("hidden"), s.sem("gelu")
        s_y, s_yt, s_yy = s.sem("outT_psum"), s.sem("outT_sbuf"), s.sem("out")

        with nc.Block(no_gpsimd_drain=True) as block:

            @block.gpsimd
            def _(pool):
                ln_gpsimd(nc, pool, m, q)

            @block.vector
            def _(dve):
                chain = Chain(dve, vch)
                dve.wait_ge(m.loaded[name], m.load_total[name])
                nc.vector.tensor_reduce(al[:, 0:IT], w["f31"][:, :, :], AX.X, ALU.add, apply_absolute_value=True)
                chain.then(nc.vector.tensor_reduce(al[:, IT:IT + 1], w["f32"][:, :], AX.X, ALU.add,
                                                   apply_absolute_value=True))
                nc.vector.tensor_scalar(al[:, 0:IT], al[:, 0:IT], 1.0 / D, None, ALU.mult)
                nc.vector.tensor_scalar(al[:, IT:IT + 1], al[:, IT:IT + 1], 1.0 / (IT * 128), None, ALU.mult)\
                  .then_inc(s_al, 1)
                ln_vector(nc, dve, chain, m, q)
                dve.wait_ge(s_wt, 2)
                nc.vector.tensor_copy(S1T[:, :, :], pW[:, 0, :].rearrange("p (i c) -> p i c", c=128))
                nc.vector.tensor_copy(S2T[:, :, :], pW[:, 1, :].rearrange("p (i c) -> p i c", c=128)).then_inc(s_ws, 1)
                for h in range(2):
                    dve.wait_ge(s_y, IT * (h + 1))
                    nc.vector.tensor_scalar(YT[:, h * HALF:(h + 1) * HALF], pY[:, h, 0:HALF],
                                            al[:, IT:IT + 1], w["f3b2"][:, 0:1], ALU.mult, ALU.add)\
                      .then_inc(s_yt, 1)
                for h in range(2):
                    dve.wait_ge(s_yy, h + 1)
                    x = m.X[:, h * HB:(h + 1) * HB, :]
                    nc.vector.tensor_tensor(x, x, pT[0:T, h, :].rearrange("p (b d) -> p b d", d=D), ALU.add)

            @block.scalar
            def _(act):
                act.wait_ge(m.loaded[name], m.load_total[name])
                nc.scalar.activation(S1[:, :, :], w["f31"][:, :, :], ACT.Sign).then_inc(s_sg, 1)
                nc.scalar.activation(S2[:, :], w["f32"][:, :], ACT.Sign).then_inc(s_sg, 1)
                ln_scalar(nc, act, m, q, [pT[:, 0, :], pT[:, 1, :]])
                act.wait_ge(s_al, 1)
                for n in range(N):
                    act.wait_ge(s_h, n + 1)
                    if n >= 2:
                        act.wait_ge(s_y, n - 1)
                    i = n % IT
                    nc.scalar.activation(H[:, n % 2, :], pH[:, n % 2, 0:HALF], ACT.Gelu,
                                         bias=w["f3b1"][:, i:i + 1], scale=al[:, i:i + 1]).then_inc(s_g, 1)

            @block.tensor
            def _(pe):
                pe.wait_ge(s_sg, 2)
                for i in range(IT):
                    last = nc.tensor.transpose(pW[:, 0, i * 128:(i + 1) * 128], S1[:, i, :], m.ident[:, :])
                last.then_inc(s_wt, 1)
                for i in range(IT):
                    last = nc.tensor.transpose(pW[:, 1, i * 128:(i + 1) * 128], S2[:, i * 128:(i + 1) * 128],
                                               m.ident[:, :])
                last.then_inc(s_wt, 1)
                ln_tensor(nc, pe, m, q, [pT[:, 0, :], pT[:, 1, :]])
                pe.wait_ge(s_ws, 1)
                pe.wait_ge(q.xTs, 2)

                def up(n):
                    if n >= 2:
                        pe.wait_ge(s_g, n - 1)
                    h = n // IT
                    nc.tensor.matmul(pH[:, n % 2, 0:HALF], S1T[:, n % IT, :], m.XNT[:, h * HALF:(h + 1) * HALF],
                                     start=True, stop=True).then_inc(s_h, 1)

                up(0)
                for n in range(N):
                    if n + 1 < N:
                        up(n + 1)
                    pe.wait_ge(s_g, n + 1)
                    h, i = n // IT, n % IT
                    last = nc.tensor.matmul(pY[:, h, 0:HALF], S2T[:, i, :], H[:, n % 2, :],
                                            start=(i == 0), stop=(i == IT - 1))
                    last.then_inc(s_y, 1)
                for h in range(2):
                    pe.wait_ge(s_yt, h + 1)
                    for i in range(HB):
                        b = h * HB + i
                        last = nc.tensor.transpose(pT[0:T, h, i * D:(i + 1) * D], YT[:, b * T:(b + 1) * T],
                                                   m.ident[:, :])
                    last.then_inc(s_yy, 1)



def ffn_quantised(nc, m):
    name = "L1f"
    w = m.w
    QMAX = 127.0
    ROWS = [128, 128, 96]
    NI = 352
    N = 6
    with ExitStack() as ctx:
        s = Stage(nc, ctx, name)
        q = ln_sems(s)
        ident16 = s.sb("ident16", [128, 128], BF16)
        scw = s.sb("scw", [128, 7])
        inw = s.sb("inw", [128, 7])
        wq = s.sb("wq", [128, 6, 128])
        wqd = s.sb("wqd", [128, NI])
        wq16 = s.sb("wq16", [128, 6, 128], BF16)
        wqd16 = s.sb("wqd16", [128, NI], BF16)
        WT = s.sb("WT", [128, 6, 128], BF16)
        WDT = s.sb("WDT", [128, 3, 128], BF16)
        col = s.sb("col", [128, 16])
        one = s.sb("one", [1, 4])
        XQ = s.sb("XQ", [128, TOK])
        XQ16 = s.sb("XQ16", [128, TOK], BF16)
        SG = s.sb("SG", [128, 2, HALF])
        H = s.sb("H", [128, N, HALF])
        H16 = s.sb("H16", [128, N, HALF], BF16)
        MH = s.sb("MH", [128, N])
        sg = s.sb("sg", [128, 7])
        YT = s.sb("YT", [128, TOK])
        p16 = s.ps("p16", [128, 2, 1024], BF16)
        pT = s.ps("pT", [128, 2, 512])
        pG = s.ps("pG", [128, 2, 512])
        pU = s.ps("pU", [128, 2, 512])
        vch = s.sem("vector_own")
        s_id, s_q16, s_wt, s_wts = s.sem("ident_bf16"), s.sem("weights_rounded"), s.sem("weights_transposed"), s.sem("weights_sbuf")
        s_cl, s_ce = s.sem("clips_spread"), s.sem("exp_of_clips")
        s_m, s_mt, s_m1, s_mb = s.sem("token_max"), s.sem("max_as_row"), s.sem("overall_max"), s.sem("max_spread")
        s_xq, s_gu, s_si, s_h = s.sem("x_rounded"), s.sem("gate_up"), s.sem("silu"), s.sem("hidden")
        s_hr, s_hq = s.sem("hidden_scaled"), s.sem("hidden_rounded")
        s_y, s_yt, s_yy = s.sem("outT_psum"), s.sem("outT_sbuf"), s.sem("out")
        src = [(w["f1g"], i) for i in range(3)] + [(w["f1u"], i) for i in range(3)]

        def tile(buf, k):
            return buf[0:ROWS[k % 3], k, :]

        with nc.Block(no_gpsimd_drain=True) as block:

            @block.gpsimd
            def _(pool):
                ln_gpsimd(nc, pool, m, q)
                for n in range(N):
                    pool.wait_ge(s_hr, n + 1)
                    r = ROWS[n % 3]
                    nc.gpsimd.tensor_scalar(H16[0:r, n, :], H[0:r, n, :], ROUND, None, ALU.subtract)\
                      .then_inc(s_hq, 1)

            @block.vector
            def _(dve):
                chain = Chain(dve, vch)
                nc.vector.tensor_copy(ident16[:, :], m.ident[:, :]).then_inc(s_id, 1)
                chain.then(nc.vector.memset(scw[:, :], 1.0))
                chain.then(nc.vector.memset(MH[:, :], 0.0))
                dve.wait_ge(m.loaded[name], m.load_total[name])
                for k, (buf, i) in enumerate(src):
                    r = ROWS[i]
                    nc.vector.tensor_reduce(scw[0:r, k:k + 1], buf[0:r, i, :], AX.X, ALU.max,
                                            apply_absolute_value=True)
                chain.then(nc.vector.tensor_reduce(scw[:, 6:7], w["f1d"][:, :], AX.X, ALU.max,
                                                   apply_absolute_value=True))
                chain.then(nc.vector.tensor_scalar(scw[:, :], scw[:, :], 1.0 / QMAX, None, ALU.mult))
                chain.then(nc.vector.reciprocal(inw[:, :], scw[:, :]))

                def rounded(dst, val, inv, out):
                    yield lambda: nc.vector.tensor_scalar(dst, val, inv, QMAX, ALU.mult, ALU.min)
                    yield lambda: nc.vector.tensor_scalar(dst, dst, -QMAX - 1.0, ROUND, ALU.max, ALU.add)
                    if out is not None:
                        yield lambda: nc.vector.tensor_scalar(out, dst, ROUND, None, ALU.subtract)

                todo = [rounded(tile(wq, k), buf[0:ROWS[i], i, :], inw[0:ROWS[i], k:k + 1], tile(wq16, k))
                        for k, (buf, i) in enumerate(src)]
                todo.append(rounded(wqd[:, :], w["f1d"][:, :], inw[:, 6:7], wqd16[:, :]))
                for steps in zip(*todo):
                    for step in steps[:-1]:
                        step()
                    chain.then(steps[-1]())
                nc.vector.tensor_copy(scw[:, :], scw[:, :]).then_inc(s_q16, 1)
                ln_vector(nc, dve, chain, m, q)
                dve.wait_ge(q.norm, B)
                nc.vector.tensor_reduce(col[0:T, 0:1], m.XN[:, :, :], AX.XY, ALU.max,
                                        apply_absolute_value=True).then_inc(s_m, 1)
                dve.wait_ge(s_wt, 1)
                for k in range(6):
                    nc.vector.tensor_copy(WT[:, k, 0:ROWS[k % 3]], p16[:, 0, k * 128:k * 128 + ROWS[k % 3]])
                for i in range(3):
                    last = nc.vector.tensor_copy(WDT[0:ROWS[i], i, :], p16[0:ROWS[i], 1, i * 128:(i + 1) * 128])
                last.then_inc(s_wts, 1)
                dve.wait_ge(s_ce, 1)
                chain.then(nc.vector.tensor_scalar(col[:, 1:3], col[:, 1:3], 1.0, None, ALU.add))
                chain.then(nc.vector.reciprocal(col[:, 1:3], col[:, 1:3]))
                chain.then(nc.vector.tensor_scalar(col[:, 1:3], col[:, 1:3], 1.0 / QMAX, None, ALU.mult))

                def overall(i):
                    dve.wait_ge(s_mt, i + 1)
                    nc.vector.tensor_reduce(one[0:1, i:i + 1], pU[0:1, 0, 0:128 if i else T], AX.X,
                                            ALU.max).then_inc(s_m1, 1)
                    dve.wait_ge(s_mb, i + 1)
                    chain.then(nc.vector.tensor_tensor(col[:, 3 + 2 * i:4 + 2 * i], pU[:, 1, 0:1],
                                                       col[:, 1 + i:2 + i], ALU.mult))
                    chain.then(nc.vector.reciprocal(col[:, 4 + 2 * i:5 + 2 * i], col[:, 3 + 2 * i:4 + 2 * i]))

                overall(0)
                nc.vector.tensor_scalar(sg[:, 0:6], scw[:, 0:6], col[:, 3:4], None, ALU.mult)
                dve.wait_ge(q.xTs, 2)
                for step in rounded(XQ[:, :], m.XNT[:, :], col[:, 4:5], XQ16[:, :]):
                    ins = step()
                    chain.then(ins)
                nc.vector.tensor_copy(col[:, 10:11], col[:, 4:5]).then_inc(s_xq, 1)
                for n in range(N):
                    r, k = ROWS[n % 3], n % 3
                    dve.wait_ge(s_si, n + 1)
                    ins = nc.vector.scalar_tensor_tensor(
                        out=H[0:r, n, :], in0=pU[0:r, n % 2, 0:HALF], scalar=sg[0:r, 3 + k:4 + k],
                        in1=SG[0:r, n % 2, :], op0=ALU.mult, op1=ALU.mult)
                    ins.then_inc(s_h, 1)
                    dve.wait_ge(s_h, n + 1)
                    last = nc.vector.tensor_reduce(MH[0:r, n:n + 1], H[0:r, n, :], AX.X, ALU.max,
                                                   apply_absolute_value=True)
                chain.then(last)
                nc.vector.tensor_reduce(col[:, 0:1], MH[:, :], AX.X, ALU.max).then_inc(s_m, 1)
                overall(1)
                for n in range(N):
                    r = ROWS[n % 3]
                    steps = list(rounded(H[0:r, n, :], H[0:r, n, :], col[0:r, 6:7], None))
                    chain.then(steps[0]())
                    steps[1]().then_inc(s_hr, 1)
                chain.then(nc.vector.tensor_tensor(sg[:, 6:7], scw[:, 6:7], col[:, 5:6], ALU.mult))
                for h in range(2):
                    dve.wait_ge(s_y, h + 1)
                    nc.vector.tensor_scalar(YT[:, h * HALF:(h + 1) * HALF], pG[:, h, 0:HALF], sg[:, 6:7],
                                            None, ALU.mult).then_inc(s_yt, 1)
                for h in range(2):
                    dve.wait_ge(s_yy, h + 1)
                    x = m.X[:, h * HB:(h + 1) * HB, :]
                    nc.vector.tensor_tensor(x, x, pT[0:T, h, :].rearrange("p (b d) -> p b d", d=D), ALU.add)

            @block.scalar
            def _(act):
                act.wait_ge(s_cl, 1)
                nc.scalar.activation(col[:, 1:3], pU[:, 0, 128:130], ACT.Exp, scale=-1.0).then_inc(s_ce, 1)
                ln_scalar(nc, act, m, q, [pT[:, 0, :], pT[:, 1, :]])
                act.wait_ge(s_xq, 1)
                for n in range(N):
                    r, k = ROWS[n % 3], n % 3
                    act.wait_ge(s_gu, n + 1)
                    if n >= 2:
                        act.wait_ge(s_h, n - 1)
                    nc.scalar.activation(SG[0:r, n % 2, :], pG[0:r, n % 2, 0:HALF], ACT.Silu,
                                         scale=sg[0:r, k:k + 1]).then_inc(s_si, 1)

            @block.tensor
            def _(pe):
                pe.wait_ge(m.loaded[name], m.load_total[name])
                nc.tensor.matmul(pU[:, 0, 128:130], m.ones[0:1, 0:128], w["f1c"][0:1, :], start=True, stop=True)\
                  .then_inc(s_cl, 1)
                pe.wait_ge(s_id, 1)
                pe.wait_ge(s_q16, 1)
                for k in range(6):
                    r = ROWS[k % 3]
                    nc.tensor.transpose(p16[:, 0, k * 128:k * 128 + r], tile(wq16, k), ident16[0:r, 0:r])
                for i in range(3):
                    last = nc.tensor.transpose(p16[0:ROWS[i], 1, i * 128:(i + 1) * 128],
                                               wqd16[:, i * 128:i * 128 + ROWS[i]], ident16[:, :])
                last.then_inc(s_wt, 1)
                ln_tensor(nc, pe, m, q, [pT[:, 0, :], pT[:, 1, :]])

                def overall(i):
                    n = 128 if i else T
                    pe.wait_ge(s_m, i + 1)
                    if i == 0:
                        pe.wait_ge(s_ce, 1)
                    nc.tensor.transpose(pU[0:1, 0, 0:n], col[0:n, 0:1], m.ident[0:n, 0:n]).then_inc(s_mt, 1)
                    pe.wait_ge(s_m1, i + 1)
                    nc.tensor.matmul(pU[:, 1, 0:1], m.ones[0:1, 0:128], one[0:1, i:i + 1], start=True,
                                     stop=True).then_inc(s_mb, 1)

                overall(0)
                pe.wait_ge(s_wts, 1)
                pe.wait_ge(s_xq, 1)
                for n in range(N):
                    r, k, h = ROWS[n % 3], n % 3, n // 3
                    if n >= 2:
                        pe.wait_ge(s_h, n - 1)
                    x = XQ16[:, h * HALF:(h + 1) * HALF]
                    nc.tensor.matmul(pG[0:r, n % 2, 0:HALF], WT[:, k, 0:r], x, start=True, stop=True)
                    nc.tensor.matmul(pU[0:r, n % 2, 0:HALF], WT[:, 3 + k, 0:r], x, start=True, stop=True)\
                      .then_inc(s_gu, 1)
                overall(1)
                for h in range(2):
                    for k in range(3):
                        n, r = 3 * h + k, ROWS[k]
                        pe.wait_ge(s_hq, n + 1)
                        last = nc.tensor.matmul(pG[:, h, 0:HALF], WDT[0:r, k, :], H16[0:r, n, :],
                                                start=(k == 0), stop=(k == 2))
                    last.then_inc(s_y, 1)
                for h in range(2):
                    pe.wait_ge(s_yt, h + 1)
                    for i in range(HB):
                        b = h * HB + i
                        last = nc.tensor.transpose(pT[0:T, h, i * D:(i + 1) * D], YT[:, b * T:(b + 1) * T],
                                                   m.ident[:, :])
                    last.then_inc(s_yy, 1)



NAMES = ['x', 'ctx_1024', 'L0_attn_Wq', 'L0_attn_Wk', 'L0_attn_Wv', 'L0_attn_Wo', 'L0_xattn_Wq', 'L0_xattn_Wk', 'L0_xattn_Wv', 'L0_xattn_gru_wih', 'L0_xattn_gru_whh', 'L0_xattn_gru_bih', 'L0_xattn_gru_bhh', 'L0_xattn_slot_norm_w', 'L0_xattn_input_norm_w', 'L0_ffn_Wg', 'L0_ffn_Wu', 'L0_ffn_Wd', 'L0_ffn_Wr', 'L0_ffn_temperature', 'L1_attn_w_qkvw', 'L1_attn_w_out', 'L1_xattn_Wq', 'L1_xattn_bq', 'L1_xattn_Wk', 'L1_xattn_bk', 'L1_xattn_Wv', 'L1_xattn_bv', 'L1_xattn_Wo', 'L1_xattn_bo', 'L1_ffn_clip_x', 'L1_ffn_clip_down', 'L1_ffn_w_gate', 'L1_ffn_w_up', 'L1_ffn_w_down', 'L2_attn_w_fc', 'L2_attn_w_proj', 'L2_attn_ln_g', 'L2_attn_ln_b', 'L2_xattn_Wk', 'L2_xattn_Wq', 'L2_xattn_Wv', 'L2_ffn_gate_weight', 'L2_ffn_ln_gamma', 'L2_ffn_ln_beta', 'L2_ffn_wi', 'L2_ffn_wo', 'L3_attn_Wk', 'L3_attn_bk', 'L3_attn_Wv', 'L3_attn_bv', 'L3_attn_Wq', 'L3_attn_bq', 'L3_attn_gamma', 'L3_attn_beta', 'L3_xattn_Wq', 'L3_xattn_Wk', 'L3_xattn_Wv', 'L3_xattn_Wo', 'L3_ffn_w1', 'L3_ffn_b1', 'L3_ffn_w2', 'L3_ffn_b2']

SUBLAYERS = [1, 2, 3, 4, 5, 6, 7, 8, 9, 10, 11, 12]


def decoder(nc, a, out):
    with ExitStack() as ctx:
        def sb(name, shape, dt=F32):
            return ctx.enter_context(nc.sbuf_tensor(name, shape, dt))

        def sem(name):
            return ctx.enter_context(nc.semaphore(name))

        m = Names()
        m.X = sb("X", [T, B, D])
        m.XN = sb("XN", [T, B, D])
        m.XNT = sb("XNT", [128, TOK])
        m.XN2 = sb("XN2", [T, B, D])
        m.stats = sb("stats", [T, B, 6])
        m.mv = sb("mv", [T, B, 2])
        m.veps = sb("veps", [T, B])
        m.rstd = sb("rstd", [T, B])
        m.ident = sb("ident", [128, 128])
        m.ones = sb("ones", [128, 512])
        m.neg_half = sb("neg_half", [128, 96])
        m.mask = sb("mask", [T, 2, NJ * T])
        m.order = sb("order", [T, B, NE])
        m.before = sb("before", [T, T])
        m.below = sb("below", [128, 8, 128])
        m.cols = sb("cols", [128, NCOLS])
        m.mcols = sb("mcols", [128, NCOLS - 4])
        m.sel = sb("sel", [8, 8, 128])
        m.ctx_tm = sb("ctx_tm", [128, B, NKT, D + 1])
        m.CT = sb("CT", [128, B, NKT * 128])
        m.loaded, m.load_total = {}, {}
        w = {}
        specs = []

        def want(stage, key, shape, src, slot=None, part=None):
            if slot is not None:
                part = (slice(None), slice(slot, slot + 1))
            specs.append((stage, key, shape, src, part if part is not None else slice(None)))

        def row(v):
            return v.rearrange("(a n) -> a n", a=1)

        want_all(a, want, row)
        order = []
        for spec in specs:
            if spec[0] not in order:
                order.append(spec[0])
        held = {stage: ctx.enter_context(ExitStack()) for stage in reversed(order)}
        for stage in reversed(order):
            for st, key, shape, _, _ in specs:
                if st == stage and shape is not None:
                    w[key] = held[stage].enter_context(nc.sbuf_tensor("w_" + key, shape, F32))
        loads = [(stage, w[key][part], src) for stage, key, _, src, part in specs]
        for stage in order:
            m.loaded[stage] = sem("loaded_" + stage)
            m.load_total[stage] = 16 * sum(spec[0] == stage for spec in specs)
        m.w = w
        m.loads = loads
        m.a = a
        m.x_loaded = sem("x_loaded")
        m.stored = sem("result_stored")
        m.padded = sem("context_padded")
        m.ctx_loaded = [sem(f"ctx_loaded_{b}") for b in range(B)]
        first_block(nc, m, a["x"])
        n = SUBLAYERS
        m.ctx_times = 2 if 2 in n else 1
        old_CT = m.CT[:, :, :].rearrange("p b k -> p (b k)")
        old_ctx = m.ctx_tm[:, :, :, :].rearrange("p b k d -> p (b k d)")
        if 1 in n:
            attention16(nc, m, "L0a", w["a0q"][:, :], w["a0k"][:, :], w["a0v"][:, :], w["a0o"][:, :], old_CT,
                        beside=(other_loads, other_tables))
        held["L0a"].close()
        if 2 in n:
            context_block(nc, m, "ctxn", True, 1)
            slot_attention(nc, m)
        held["L0x"].close()
        if 3 in n:
            mixture_golden(nc, m)
        held["L0f"].close()
        if 4 in n:
            attention_regrouped(nc, m)
        held["L1a"].close()
        if 5 in n:
            attention16(nc, m, "L1x", w["x1q"][:, :], w["x1k"][:, :], w["x1v"][:, :], w["x1o"][:, :], old_CT,
                        keys="causal", bias=(w["x1bq"], w["x1bk"], w["x1bv"], w["x1bo"]))
        held["L1x"].close()
        if set(n) & {8, 11}:
            context_block(nc, m, "ctxr", False, m.ctx_times)
        if 6 in n:
            ffn_quantised(nc, m)
        held["L1f"].close()
        if 7 in n:
            attention_fixed_keys(nc, m)
        held["L2a"].close()
        if 8 in n:
            attention_wide(nc, m)
        held["L2x"].close()
        if 9 in n:
            mixture_top1(nc, m)
        held["L2f"].close()
        if 10 in n:
            attention_delta_rule(nc, m)
        held["L3a"].close()
        if 11 in n:
            attention16(nc, m, "L3x", w["x3q"][:, :], w["x3k"][:, :], w["x3v"][:, :], w["x3o"][:, :], old_ctx,
                        weights_natural=True, keys="context")
        held["L3x"].close()
        if 12 in n:
            ffn_binary(nc, m)
        held["L3f"].close()
        store_block(nc, m, out)


def want_all(a, want, row):
    want("L0a", "a0q", [128, 128], a["L0_attn_Wq"])
    want("L0a", "a0k", [32, 128], a["L0_attn_Wk"])
    want("L0a", "a0v", [32, 128], a["L0_attn_Wv"])
    want("L0a", "a0o", [128, 128], a["L0_attn_Wo"])
    want("L0x", "x0q", [128, 128], a["L0_xattn_Wq"])
    want("L0x", "x0k", [128, 128], a["L0_xattn_Wk"])
    want("L0x", "x0v", [128, 128], a["L0_xattn_Wv"])
    want("L0x", "x0ih", [128, 3, 128], a["L0_xattn_gru_wih"].rearrange("(c p) d -> p c d", p=128))
    want("L0x", "x0hh", [128, 3, 128], a["L0_xattn_gru_whh"].rearrange("(c p) d -> p c d", p=128))
    want("L0x", "x0bi", [1, 384], row(a["L0_xattn_gru_bih"]))
    want("L0x", "x0bh", [1, 384], row(a["L0_xattn_gru_bhh"]))
    want("L0x", "x0sw", [128, 1], a["L0_xattn_slot_norm_w"].rearrange("(p a) -> p a", a=1))
    want("L0x", "x0iw", [128, 1], a["L0_xattn_input_norm_w"].rearrange("(p a) -> p a", a=1))
    want("L0f", "f0t", [1, 1], row(a["L0_ffn_temperature"]))
    want("L0f", "f0r", [128, NE], a["L0_ffn_Wr"])
    want("L0f", "f0g", [128, NE, 128], a["L0_ffn_Wg"].rearrange("e d i -> d e i"))
    want("L0f", "f0u", [128, NE, 128], a["L0_ffn_Wu"].rearrange("e d i -> d e i"))
    want("L0f", "f0d", [128, NE, 128], a["L0_ffn_Wd"].rearrange("e i d -> i e d"))
    want("L1a", "a1w", [128, 512], a["L1_attn_w_qkvw"])
    want("L1a", "a1o", [128, 128], a["L1_attn_w_out"])
    for key, src in (("q", "Wq"), ("k", "Wk"), ("v", "Wv"), ("o", "Wo")):
        want("L1x", "x1" + key, [128, 128], a["L1_xattn_" + src])
        want("L1x", "x1b" + key, [1, 128], row(a["L1_xattn_b" + key]))

    def column(v, p=128):
        return v.rearrange("(c p) -> p c", p=p)

    for key, src in (("f1g", "w_gate"), ("f1u", "w_up")):
        v = a["L1_ffn_" + src]
        want("L1f", key, [128, 3, 128], v[0:256, :].rearrange("(i p) d -> p i d", p=128),
             part=(slice(0, 128), slice(0, 2)))
        want("L1f", key, None, v[256:352, :], part=(slice(0, 96), 2))
    want("L1f", "f1d", [128, 352], a["L1_ffn_w_down"])
    want("L1f", "f1c", [1, 2], row(a["L1_ffn_clip_x"]), slot=0)
    want("L1f", "f1c", None, row(a["L1_ffn_clip_down"]), slot=1)
    want("L2a", "a2f", [128, 128], a["L2_attn_w_fc"])
    want("L2a", "a2p", [128, 128], a["L2_attn_w_proj"])
    want("L2a", "a2g", [128, 1], column(a["L2_attn_ln_g"]))
    want("L2a", "a2b", [128, 1], column(a["L2_attn_ln_b"]))
    want("L2x", "x2q", [128, 128], a["L2_xattn_Wq"])
    want("L2x", "x2k", [128, 128], a["L2_xattn_Wk"])
    want("L2x", "x2v", [128, 128], a["L2_xattn_Wv"])
    want("L2f", "f2r", [NE, 128], a["L2_ffn_gate_weight"])
    want("L2f", "f2g", [128, 1], column(a["L2_ffn_ln_gamma"]))
    want("L2f", "f2b", [128, 1], column(a["L2_ffn_ln_beta"]))
    want("L3a", "a3k", [DS, 128], a["L3_attn_Wk"])
    want("L3a", "a3q", [DS, 128], a["L3_attn_Wq"])
    want("L3a", "a3v", [128, 128], a["L3_attn_Wv"])
    want("L3a", "a3bk", [DS, 1], column(a["L3_attn_bk"], DS))
    want("L3a", "a3bq", [DS, 1], column(a["L3_attn_bq"], DS))
    want("L3a", "a3bv", [1, 128], row(a["L3_attn_bv"]))
    want("L3a", "a3g", [128, 1], column(a["L3_attn_gamma"]))
    want("L3a", "a3b", [128, 1], column(a["L3_attn_beta"]))
    for key, src, f in (("q", "Wq", 128), ("k", "Wk", 32), ("v", "Wv", 32), ("o", "Wo", 128)):
        want("L3x", "x3" + key, [128, f], a["L3_xattn_" + src])
    want("L3f", "f31", [128, 4, 128], a["L3_ffn_w1"].rearrange("(i p) d -> p i d", p=128))
    want("L3f", "f32", [128, 512], a["L3_ffn_w2"])
    want("L3f", "f3b1", [128, 4], column(a["L3_ffn_b1"][0:128]), slot=0)
    for i in range(1, 4):
        want("L3f", "f3b1", None, column(a["L3_ffn_b1"][i * 128:(i + 1) * 128]), slot=i)
    want("L3f", "f3b2", [128, 1], column(a["L3_ffn_b2"]))


def first_block(nc, m, x):
    with ExitStack() as ctx:
        s = Stage(nc, ctx, "first")
        brow = s.sb("brow", [1, NCOLS, 128])
        pc = s.ps("columns", [128, NCOLS])
        s_set = s.sem("cleared")
        s_row, s_row1, s_col, s_c = s.sem("rows_cleared"), s.sem("rows"), s.sem("columns_psum"), s.sem("columns")
        with nc.Block(no_gpsimd_drain=True) as block:

            @block.sync
            def _(sp):
                sp.dma_start(m.X[:, :, :], x.rearrange("b t d -> t b d")).then_inc(m.x_loaded, 16)
                for stage, dst, src in m.loads:
                    if stage == "L0a":
                        sp.dma_start(dst, src).then_inc(m.loaded[stage], 16)

            @block.vector
            def _(dve):
                nc.vector.memset(m.ones[:, :], 1.0)
                nc.vector.memset(brow[:], 0.0).then_inc(s_row, 1)
                dve.wait_ge(s_row, 1)
                term_rows(nc, brow).then_inc(s_row1, 1)
                nc.vector.memset(m.ctx_tm[:, :, KT_FULL, :], 0.0).then_inc(m.padded, 1)
                dve.wait_ge(m.padded, 1)
                nc.vector.memset(m.ctx_tm[:, :, :, D], 1.0).then_inc(m.padded, 1)
                dve.wait_ge(s_col, 1)
                nc.vector.tensor_copy(m.cols[:, :], pc[:, :]).then_inc(s_c, 1)
                dve.wait_ge(s_c, 1)
                bias_times_mask(nc, m.mcols, m.cols)
                dve.wait_ge(m.x_loaded, 16)

            @block.tensor
            def _(pe):
                pe.wait_ge(s_row1, 1)
                for i in range(NCOLS):
                    last = nc.tensor.matmul(pc[:, i:i + 1], brow[0:1, i, :], m.ones[0:1, 0:1],
                                            start=(i == 0), stop=True, skip_group_check=True)
                last.then_inc(s_col, 1)

            @block.gpsimd
            def _(pool):
                nc.gpsimd.memset(m.neg_half[:, :], -0.5)
                nc.gpsimd.memset(m.ident[:, :], 0.0).then_inc(s_set, 1)
                pool.wait_ge(s_set, 1)
                nc.gpsimd.affine_select(out=m.ident[:, :], in_=m.ident[:, :], compare_op=ALU.not_equal,
                                        fill=1.0, base=0, pattern=[[-1, 128]], channel_multiplier=1)


def other_loads(sp, m):
    sp.wait_ge(m.padded, 2)
    for b in range(B):
        load_context(sp, m, b)
    for stage, dst, src in m.loads:
        if stage != "L0a":
            sp.dma_start(dst, src).then_inc(m.loaded[stage], 16)


def other_tables(nc, pool, m, s_set):
    nc.gpsimd.memset(m.mask[:, :, :], 0.0)
    nc.gpsimd.memset(m.sel[:, :, :], 0.0)
    nc.gpsimd.memset(m.before[:, :], 1.0)
    nc.gpsimd.memset(m.below[:, :, :], 0.0).then_inc(s_set, 1)
    for e in range(NE):
        last = nc.gpsimd.memset(m.order[:, :, e], float(NE - e))
    last.then_inc(s_set, 1)
    pool.wait_ge(s_set, 2)
    nc.gpsimd.affine_select(out=m.mask[:, 0, :], in_=m.mask[:, 0, :], compare_op=ALU.is_ge,
                            fill=-1e30, base=0, pattern=[[0, NJ], [-1, T]],
                            channel_multiplier=1)
    nc.gpsimd.affine_select(out=m.mask[:, 1, :], in_=m.mask[:, 1, :], compare_op=ALU.is_ge,
                            fill=-1e30, base=0, pattern=[[0, NG], [1, T]],
                            channel_multiplier=-1)
    nc.gpsimd.affine_select(out=m.sel[:, :, :], in_=m.sel[:, :, :], compare_op=ALU.not_equal,
                            fill=1.0, base=0, pattern=[[-1, 8], [0, 128]],
                            channel_multiplier=1).then_inc(s_set, 1)
    nc.gpsimd.affine_select(out=m.before[:, :], in_=m.before[:, :], compare_op=ALU.is_ge,
                            fill=0.0, base=-1, pattern=[[1, T]], channel_multiplier=-1)
    n = 3
    for i, sz in [(0, 1)] + [(k + 1, v) for k, v in enumerate(LEVELS)]:
        blocks = 128 // (2 * sz)
        cols = slice(0, sz) if i == 0 else slice(sz, 2 * sz)
        lo = sz if i == 0 else 0
        kept = [p for p in ([2 * sz, blocks], [0, sz]) if p[1] > 1]
        v = m.below[:, i, :].rearrange("p (k c) -> p k c", c=2 * sz)[:, :, cols]
        pool.wait_ge(s_set, n)
        nc.gpsimd.memset(v, TTT_LR).then_inc(s_set, 1)
        pool.wait_ge(s_set, n + 1)
        nc.gpsimd.affine_select(out=v, in_=v, compare_op=ALU.is_ge, fill=0.0, base=-lo,
                                pattern=[[-p[0], p[1]] for p in kept], channel_multiplier=1)\
            .then_inc(s_set, 1)
        pool.wait_ge(s_set, n + 2)
        nc.gpsimd.affine_select(out=v, in_=v, compare_op=ALU.is_ge, fill=0.0, base=lo + sz - 1,
                                pattern=kept, channel_multiplier=-1)\
            .then_inc(s_set, 1)
        n += 3
    pool.wait_ge(s_set, n)


def store_block(nc, m, out):
    with nc.Block(no_gpsimd_drain=True) as block:

        @block.sync
        def _(sp):
            for stage in m.loaded:
                sp.wait_ge(m.loaded[stage], m.load_total[stage])
            for b in range(B):
                sp.wait_ge(m.ctx_loaded[b], 32 * m.ctx_times)
            sp.dma_start(out.rearrange("b t d -> t b d"), m.X[:, :, :]).then_inc(m.stored, 16)
            sp.wait_ge(m.stored, 16)



def kernel(**inputs):
    import numpy as _np
    import concourse.bacc as _bacc
    from concourse.bass_utils import run_bass_kernel_spmd as _run

    nc = _bacc.Bacc("TRN2", target_bir_lowering=False, num_devices=1)
    arrays, args = {}, {}
    for name in NAMES:
        arr = _np.ascontiguousarray(inputs[name])
        arrays[f"in_{name}"] = arr
        args[name] = nc.dram_tensor(f"in_{name}", arr.shape, mybir.dt.from_np(arr.dtype), kind="ExternalInput").ap()
    out = nc.dram_tensor("decoded", (B, T, D), F32, kind="ExternalOutput").ap()
    decoder(nc, args, out)
    r = _run(nc, [arrays], core_ids=[0])
    return r.results[0]["decoded"]
```

```python
from contextlib import ExitStack

import concourse.bass as bass
from concourse import mybir

ALU = mybir.AluOpType
ACT = mybir.ActivationFunctionType
F32 = mybir.dt.float32
BF16 = mybir.dt.bfloat16
AX = mybir.AxisListType

B, T, D = 8, 100, 128
TOK = B * T
HALF = TOK // 2
HB = B // 2
SC = 1444
KT_FULL = SC // 128
TAIL = SC - KT_FULL * 128
NKT = KT_FULL + 1
TILES = [128] * KT_FULL + [TAIL]
LN_EPS = 1e-5
ROUND = 12582912.0


class Names:
    pass


class Chain:

    def __init__(self, eng, sem):
        self.eng, self.sem, self.n = eng, sem, 0

    def then(self, ins):
        self.n += 1
        ins.then_inc(self.sem, 1)
        self.eng.wait_ge(self.sem, self.n)


class Stage:

    FIRST_SEM = 160

    def __init__(self, nc, ctx, name):
        self.nc, self.ctx, self.name, self.next = nc, ctx, name, self.FIRST_SEM
        ctx.callback(self.clear)

    def clear(self):
        self.nc.all_engine_barrier(sems_to_clear=range(self.FIRST_SEM, self.next))

    def sb(self, name, shape, dt=F32):
        return self.ctx.enter_context(self.nc.sbuf_tensor(f"{self.name}_{name}", shape, dt))

    def sem(self, name):
        self.next += 1
        return self.ctx.enter_context(self.nc.semaphore(f"{self.name}_{name}", num=self.next - 1))

    def ps(self, name, shape, dt=F32):
        return self.ctx.enter_context(self.nc.psum_tensor(f"{self.name}_{name}", shape, dt))



def ln_sems(s, name="ln"):
    q = Names()
    q.var, q.rstd, q.norm = s.sem(name + "_var"), s.sem(name + "_rstd"), s.sem(name + "_norm")
    q.xT, q.xTs = s.sem(name + "_xT_in_psum"), s.sem(name + "_xT_in_sbuf")
    return q


def ln_vector(nc, dve, chain, m, q, src=None, dst=None):
    src = m.X if src is None else src
    dst = m.XN if dst is None else dst
    for b in range(B):
        last = nc.vector.bn_stats(m.stats[:, b, :], src[:, b, :])
    chain.then(last)
    for b in range(B):
        last = nc.vector.bn_aggr(m.mv[:, b, :], m.stats[:, b, :])
    chain.then(last)
    nc.vector.tensor_scalar(m.veps[:, 0, :], m.mv[:, :, 1], LN_EPS, None, ALU.add).then_inc(q.var, 1)
    dve.wait_ge(q.rstd, 1)
    for b in range(B):
        nc.vector.tensor_scalar(dst[:, b, :], src[:, b, :], m.mv[:, b, 0:1], m.rstd[:, 0, b:b + 1],
                                ALU.subtract, ALU.mult).then_inc(q.norm, 1)


def ln_gpsimd(nc, pool, m, q):
    pool.wait_ge(q.var, 1)
    nc.gpsimd.tensor_tensor(m.rstd[:, 0, :], m.veps[:, 0, :], m.neg_half[0:T, 0:B], ALU.pow).then_inc(q.rstd, 1)


def ln_tensor(nc, pe, m, q, banks, src=None):
    src = m.XN if src is None else src
    for b in range(B):
        pe.wait_ge(q.norm, b + 1)
        nc.tensor.transpose(banks[b // HB][:, (b % HB) * T:(b % HB + 1) * T], src[:, b, :],
                            m.ident[0:T, 0:T]).then_inc(q.xT, 1)


def ln_scalar(nc, act, m, q, banks, affine=None):
    for h in range(2):
        act.wait_ge(q.xT, HB * (h + 1))
        dst = m.XNT[:, h * HALF:(h + 1) * HALF]
        if affine is None:
            nc.scalar.copy(dst, banks[h][:, 0:HALF]).then_inc(q.xTs, 1)
        else:
            nc.scalar.activation(dst, banks[h][:, 0:HALF], ACT.Identity, bias=affine[1][:, 0:1],
                                 scale=affine[0][:, 0:1]).then_inc(q.xTs, 1)



NH, HD = 16, 8
NJ = 4
NG = NH // NJ
SCALE8 = float(HD) ** -0.5
KEY_TERM = [1, 2, 1, 2, 3, 1]
QUERY_TERM = [1, 1, 2, 2, 1, 3]
SLOTS = len(KEY_TERM)
MAXROW = SLOTS * HD
PAIRS = 2


MASK = 2 * PAIRS * NG
NCOLS = MASK + 4


def term_rows(nc, brow):
    for a in range(2):
        c = 64 * a + MAXROW
        last = nc.vector.memset(brow[0:1, PAIRS * NG:MASK, c:c + 3], 1.0)
        for side, term in ((0, KEY_TERM), (2, QUERY_TERM)):
            for k, v in enumerate(term):
                if v >= 2:
                    last = nc.vector.memset(brow[0:1, MASK + side, c - MAXROW + HD * k:c - MAXROW + HD * k + HD],
                                            1.0)
                if v == 3:
                    last = nc.vector.memset(
                        brow[0:1, MASK + side + 1, c - MAXROW + HD * k:c - MAXROW + HD * k + HD], 1.0)
        last = nc.vector.memset(brow[0:1, MASK + 2, c + 1:c + 3], 1.0)
        last = nc.vector.memset(brow[0:1, MASK + 3, c + 2:c + 3], 1.0)
    return last


def bias_times_mask(nc, mcol, bcol):
    half = PAIRS * NG
    nc.vector.tensor_scalar(mcol[:, 0:half], bcol[:, 0:half], bcol[:, MASK + 2:MASK + 3], None, ALU.mult)
    return nc.vector.tensor_scalar(mcol[:, half:MASK], bcol[:, half:MASK], bcol[:, MASK:MASK + 1], None,
                                   ALU.mult)


def attention16(nc, m, name, wq, wk, wv, wo, spare, weights_natural=False, keys="self", bias=None,
                beside=None):
    grouped = keys != "causal"
    NK = 1 if grouped else NG
    long = keys == "context"
    tiles = TILES if long else [T]
    nt = len(tiles)
    NU = nt * NJ
    CH = [482, 482, 480]
    MU = NU
    LAG = MU + 20 if long else MU + 11
    TM_AT, NORM_AT, TURN_AT, OT_AT, PROJ_AT, RES_AT = (3, 4, 7, 8, 11, 12) if long else (1, 1, 2, 2, 3, 3)
    DELAY = 1
    KB = 3 if long else 1
    UW = max(CH) if long else NG * T
    EB = 2 * NJ
    with ExitStack() as ctx:
        s = Stage(nc, ctx, name)
        q = ln_sems(s)
        wT = s.sb("wT", [128, 2, 128])
        wqe = s.sb("wqe", [128, PAIRS, NG, 128])
        if bias is None:
            bcol, mcol = m.cols, m.mcols
        else:
            brow = s.sb("brow", [1, MASK, 128])
            bcol = s.sb("bcol", [128, NCOLS])
            mcol = s.sb("mcol", [128, MASK])
        at0 = NJ * NG * TOK // 2
        QS = spare[:, 0:at0].bitcast(BF16).rearrange("p (j g t) -> p j g t", j=NJ, g=NG)
        wke_at = spare.shape[-1] - PAIRS * NK * 128
        wke = s.sb("wke", [128, PAIRS, NK, 128]) if grouped else \
            spare[:, wke_at:wke_at + PAIRS * NK * 128].rearrange("p (i g c) -> p i g c", i=PAIRS, g=NK)
        T1 = s.sb("T1", [128, 2, UW], BF16)
        X1 = s.sb("X1", [128, 2, UW])
        T2 = s.sb("T2", [128, 2, UW], BF16)
        M3 = s.sb("M3", [128, 2, NG * T], BF16)
        MH = s.sb("MH", [T, 2, NJ, NG, 3]) if long else None
        nm = s.sb("nm", [T, 2, NJ, NG])
        MXP = s.sb("MXP", [T, 2, PAIRS, NG, 128])
        OC = s.sb("OC", [128, NG * T])
        rden = s.sb("rden", [T, NG, NJ])
        ON = s.sb("ON", [T, D])
        OT = s.sb("OT", [128, T])
        if long:
            at1 = at0 + KB * PAIRS * SC // 2
            KS = spare[:, at0:at1].bitcast(BF16).rearrange("p (k i t) -> p k i t", k=KB, i=PAIRS)
            V = s.sb("V", [128, 2, NKT, NJ, 32])
            E = s.sb("E", [128, EB, NG * T])
        else:
            at1 = at0 + NK * PAIRS * TOK // 2
            KS = spare[:, at0:at1].bitcast(BF16).rearrange("p (g i t) -> p g i t", g=NK, i=PAIRS)
            if grouped:
                at2 = at1 + B * NJ * 32
                V = spare[0:T, at1:at2].rearrange("p (b j d) -> p b j d", b=B, j=NJ)
                E = spare[:, at2:at2 + EB * NG * T].rearrange("p (i t) -> p i t", i=EB)
            else:
                CX = spare[:, at1:at1 + TOK]
                V = s.sb("V", [T, B, NH, 32])
                E = s.sb("E", [128, EB, NG * T])
        if not grouped:
            ident16 = s.sb("ident16", [T, T], BF16)
            mask16 = m.XN2[:, :, :].rearrange("t b d -> t (b d)").bitcast(BF16)[:, 0:2 * NG * T]\
                .rearrange("t (i k) -> t i k", i=2)
        pM = s.ps("pM", [128, 3, 512])
        pS = s.ps("pS", [128, 2, 512])
        pO = s.ps("pO", [128, 512])
        pP = s.ps("pP", [128, 2, 512])
        banks = [pM[:, 0, :], pM[:, 1, :]]
        dch, gch = s.sem("vector_own"), s.sem("gpsimd_own")
        s_wT, s_w = s.sem("weights_transposed"), s.sem("weights_ready")
        s_row, s_col, s_bias = s.sem("bias_rows"), s.sem("bias_columns_psum"), s.sem("bias_columns")
        s_set, s_clear = s.sem("buffers_cleared"), s.sem("queries_cleared")
        s_table = s.sem("tables")
        s_qv = s.sem("query_half_written")
        s_up, s_t1, s_x1 = s.sem("unit_psum"), s.sem("first_terms"), s.sem("unit_read")
        s_t2, s_fin = s.sem("second_terms"), s.sem("unit_split")
        s_m, s_mr, s_mx = s.sem("scores_for_max"), s.sem("max_taken"), s.sem("maxima_ready")
        s_s, s_e, s_eu = s.sem("scores"), s.sem("exps"), s.sem("exps_used")
        s_oc, s_tt, s_on = s.sem("out_sbuf"), s.sem("out_token_major"), s.sem("out_normalised")
        s_ot, s_ots = s.sem("outT_psum"), s.sem("outT_sbuf")
        s_y, s_x = s.sem("y_psum"), s.sem("residual_added")
        s_cx, s_cxs = s.sem("context_turned"), s.sem("context_turned_sbuf")
        KD = NJ * HD * NK
        rows = [128, KD, KD, 128]
        srcs = [wq, wk, wv, wo]
        wTs = [pM[:, 2, 0:128], pP[:, 0, 0:KD], pP[:, 0, 128:128 + KD], pP[:, 0, 256:384]]
        if weights_natural:
            wTs = srcs

        units = [("Q", p, g, h) for p in range(PAIRS) for g in range(NG) for h in range(2)]
        if long:
            units += [("K", p, 0, c) for p in range(PAIRS) for c in range(3)]
            units += [("V", 0, i) for i in range(2)]
        else:
            units += [("K", p, g, h) for p in range(PAIRS) for g in range(NK) for h in range(2)]
            units += [("V", b, 0) for b in range(B)]
        FIRST = len(units)
        STEPS = B * NU
        steps = range(-LAG, STEPS)
        at = {t: [] for t in range(-LAG, STEPS + DELAY)}
        later = []
        for b in range(B):
            first = b * MU - LAG
            if long and b >= 1:
                later += [(first - MU + 18 + 4 * i, ("K", i // 3, b, i % 3)) for i in range(6)]
                later += [((b - 1) * NU + 22 + 4 * i, ("V", b, i)) for i in range(2)]
            later += [(first + MU + (2 + 4 * p if long else 2 * p), ("M", p, b, 0)) for p in range(PAIRS)]
        for t, unit in sorted(later):
            at[t].append(len(units))
            units.append(unit)

        def split_before(n, kinds="QKM"):
            return sum(units[i][0] in kinds for i in range(n))

        def keys_ready(b):
            n = [n for n, x in enumerate(units) if x[0] == "K" and (x[2] == b or not long)]
            return 1 + split_before(max(n))

        def values_ready(b):
            n = [n for n, x in enumerate(units) if x[0] == "V" and x[1] == b]
            return 1 + max(n)

        NQ = 2 * PAIRS * NG

        def bias_column(unit):
            g = unit[2] if unit[0] == "Q" or not long else 0
            return (PAIRS * NG if unit[0] == "K" else 0) + unit[1] * NG + g

        def width(unit):
            return CH[unit[3]] if unit[0] == "K" and long else NG * T

        with nc.Block(no_gpsimd_drain=True) as block:

            @block.sync
            def _(sp):
                if beside is not None:
                    beside[0](sp, m)

            @block.gpsimd
            def _(pool):
                chain = Chain(pool, gch)
                if long:
                    for b in range(B):
                        pool.wait_ge(m.ctx_loaded[b], 32)
                nc.gpsimd.memset(wke[:], 0.0).then_inc(s_set, 1)
                nc.gpsimd.memset(V[:], 0.0).then_inc(s_set, 1)
                pool.wait_ge(s_set, 2)
                ln_gpsimd(nc, pool, m, q)
                nc.gpsimd.memset(spare[:, 0:at0], 0.0)
                nc.gpsimd.memset(MXP[:], 0.0).then_inc(s_clear, 1)
                pool.wait_ge(s_clear, 1)
                if bias is not None:
                    pool.wait_ge(s_bias, 1)

                def split(n):
                    unit = units[n]
                    kind, p = unit[0], unit[1]
                    if kind == "V":
                        return
                    i = split_before(n)
                    W = width(unit)
                    pool.wait_ge(s_x1, n + 1)
                    if i >= 1:
                        pool.wait_ge(s_fin, i)
                    if n < FIRST or not long:
                        pool.wait_ge(s_t2, i + 1)
                    else:
                        c = MASK + (1 if kind == "K" else 3)
                        chain.then(nc.gpsimd.tensor_scalar(T2[:, i % 2, 0:W], X1[:, i % 2, 0:W],
                                                           bcol[:, c:c + 1], None, ALU.mult))
                    if kind == "K":
                        if long:
                            b, c = unit[2], unit[3]
                            if b >= KB:
                                pool.wait_ge(s_s, NU * (b - KB + 1))
                            dst = KS[:, b % KB, p, CH[0] * c:CH[0] * c + W]
                        else:
                            dst = KS[:, unit[2], p, unit[3] * HALF:(unit[3] + 1) * HALF]
                        nc.gpsimd.tensor_tensor(dst, X1[:, i % 2, 0:W], T2[:, i % 2, 0:W], ALU.subtract)\
                          .then_inc(s_fin, 1)
                        return
                    if kind == "Q":
                        nc.gpsimd.tensor_tensor(
                            QS[64:128, 2 * p + 1, unit[2], unit[3] * HALF:(unit[3] + 1) * HALF],
                            X1[64:128, i % 2, 0:W], T2[64:128, i % 2, 0:W], ALU.subtract)\
                            .then_inc(s_fin, 1)
                        return
                    b = unit[2]
                    chain.then(nc.gpsimd.tensor_tensor(M3[:, i % 2, :], X1[:, i % 2, 0:W],
                                                       T2[:, i % 2, 0:W], ALU.subtract))
                    for a in range(2):
                        r = slice(64 * a + 32, 64 * a + 64)
                        v = QS[r, 2 * p + a, :, b * T:(b + 1) * T]
                        last = nc.gpsimd.tensor_tensor(
                            v, v, M3[r, i % 2, :].rearrange("p (g t) -> p g t", t=T), ALU.add)
                        if a == 0:
                            chain.then(last)
                    last.then_inc(s_fin, 1)

                for n in range(FIRST):
                    split(n)
                pool.wait_ge(s_qv, NQ)
                for t in steps:
                    for n in at[t]:
                        split(n)
                if beside is not None:
                    pool.wait_ge(s_fin, split_before(len(units)))
                    beside[1](nc, pool, m, s_table)

            @block.vector
            def _(dve):
                chain = Chain(dve, dch)
                if bias is not None:
                    chain.then(nc.vector.memset(brow[:], 0.0))
                    for a in range(2):
                        c = 64 * a + MAXROW
                        nc.vector.memset(brow[0:1, PAIRS * NG:MASK, c:c + 3], 1.0)
                    dve.wait_ge(m.loaded[name], m.load_total[name])
                    for i in range(2):
                        for j in range(NJ):
                            p, a = j // 2, j % 2
                            last = nc.vector.tensor_copy(
                                brow[0:1, i * PAIRS * NG + p * NG:i * PAIRS * NG + (p + 1) * NG,
                                     64 * a:64 * a + MAXROW].rearrange("o g (k d) -> o g k d", d=HD),
                                bias[i][0:1, j * NG * HD:(j + 1) * NG * HD]
                                .rearrange("o (g d) -> o g d", d=HD).unsqueeze(2)
                                .broadcast_to((1, NG, SLOTS, HD)))
                    last.then_inc(s_row, 1)
                if not grouped:
                    nc.vector.tensor_copy(ident16[:, :], m.ident[0:T, 0:T])
                    nc.vector.tensor_copy(mask16[:, :, :], m.mask[:, :, :])
                nc.vector.memset(wqe[:], 0.0)
                ln_vector(nc, dve, chain, m, q)
                dve.wait_ge(s_set, 2)
                nc.vector.memset(V[:, :, :, HD] if not long else V[:, :, :, :, HD], 1.0)
                if keys == "causal":
                    for h in range(2):
                        dve.wait_ge(s_cx, h + 1)
                        nc.vector.tensor_copy(CX[:, h * HALF:(h + 1) * HALF], pS[:, h, 0:HALF])\
                          .then_inc(s_cxs, 1)
                if not weights_natural:
                    dve.wait_ge(s_wT, 4)
                else:
                    dve.wait_ge(m.loaded[name], m.load_total[name])
                for dst, src, n in ((wqe, wTs[0], NG), (wke, wTs[1], NK)):
                    for j in range(NJ):
                        p, a = j // 2, j % 2
                        last = nc.vector.tensor_copy(
                            dst[:, p, :, 64 * a:64 * a + MAXROW].rearrange("p g (k d) -> p g k d", d=HD),
                            src[:, j * n * HD:(j + 1) * n * HD].rearrange("p (g d) -> p g d", d=HD)
                            .unsqueeze(2).broadcast_to((128, n, SLOTS, HD)))
                if not weights_natural:
                    for n in (2, 3):
                        last = nc.vector.tensor_copy(wT[:, n - 2, 0:rows[n]], wTs[n])
                last.then_inc(s_w, 1)
                if bias is not None:
                    dve.wait_ge(s_col, 1)
                    nc.vector.tensor_copy(bcol[:, MASK:NCOLS], m.cols[:, MASK:NCOLS])
                    chain.then(nc.vector.tensor_copy(bcol[:, 0:MASK], pO[:, 0:MASK]))
                    bias_times_mask(nc, mcol, bcol).then_inc(s_bias, 1)

                def read(n):
                    unit = units[n]
                    kind = unit[0]
                    bank = n % 2 if n < FIRST else 0
                    if kind == "V":
                        dve.wait_ge(s_up, n + 1)
                        if long:
                            b, k0 = unit[1], NKT // 2 * unit[2]
                            if b >= 2 and k0 == 0:
                                dve.wait_ge(s_eu, NU * (b - 1))
                            parts = [(k0, k0 + 6, 128)] if k0 == 0 else [(k0, k0 + 5, 128), (k0 + 5, NKT, TAIL)]
                            for ka, kb, r in parts:
                                last = nc.vector.tensor_copy(
                                    V[0:r, b % 2, ka:kb, :, 0:HD],
                                    pP[0:r, bank, 32 * (ka - k0):32 * (kb - k0)]
                                    .rearrange("p (k j d) -> p k j d", j=NJ, d=HD))
                            last.then_inc(s_x1, 1)
                        else:
                            nc.vector.tensor_copy(V[:, unit[1], :, 0:HD],
                                                  pP[0:T, bank, 0:KD].rearrange("p (h d) -> p h d", d=HD))\
                              .then_inc(s_x1, 1)
                        return
                    i = split_before(n)
                    W = width(unit)
                    dve.wait_ge(s_t1, i + 1)
                    if i >= 2:
                        dve.wait_ge(s_fin, i - 1)
                        dve.wait_ge(s_qv, min(i - 1, NQ))
                    if kind == "M":
                        nc.vector.tensor_tensor(X1[:, i % 2, 0:W], pP[:, bank, 0:W], T1[:, i % 2, 0:W],
                                                ALU.subtract).then_inc(s_x1, 1)
                    else:
                        c = bias_column(unit)
                        nc.vector.scalar_tensor_tensor(
                            out=X1[:, i % 2, 0:W], in0=pP[:, bank, 0:W], scalar=bcol[:, c:c + 1],
                            in1=T1[:, i % 2, 0:W], op0=ALU.add, op1=ALU.subtract).then_inc(s_x1, 1)

                def maximum(n):
                    b, u = n // MU, n % MU
                    dve.wait_ge(s_m, n + 1)
                    if long:
                        j, g, c = u // (3 * NG), u // 3 % NG, u % 3
                        nc.vector.tensor_reduce(MH[:, b % 2, j, g, c:c + 1], pM[0:T, n % 3, 0:CH[c]],
                                                AX.X, ALU.max, negate=True).then_inc(s_mr, 1)
                    else:
                        nc.vector.tensor_reduce(nm[:, b % 2, u, :],
                                                pM[0:T, n % 3, 0:NG * T].rearrange("p (g k) -> p g k", k=T),
                                                AX.X, ALU.max, negate=True).then_inc(s_mr, 1)
                    if u == MU - 1:
                        dve.wait_ge(s_mr, n + 1)
                        if long:
                            chain.then(nc.vector.tensor_reduce(nm[:, b % 2], MH[:, b % 2], AX.X, ALU.min))
                        for p in range(PAIRS):
                            last = nc.vector.tensor_copy(
                                MXP[:, b % 2, p].rearrange("t g (a c) -> t g a c", a=2)[:, :, :, MAXROW:MAXROW + 3],
                                nm[:, b % 2, 2 * p:2 * p + 2, :].rearrange("t a g -> t g a").unsqueeze(3)
                                .broadcast_to((T, NG, 2, 3)))
                        last.then_inc(s_mx, 1)

                def out_copied(b):
                    dve.wait_ge(s_eu, NU * (b + 1))
                    nc.vector.tensor_copy(OC[:, :], pO[:, 0:NG * T]).then_inc(s_oc, 1)

                def normalised(b):
                    dve.wait_ge(s_tt, b + 1)
                    v = pP[0:T, 1, :].rearrange("t (g j r) -> t g j r", g=NG, j=NJ)
                    chain.then(nc.vector.reciprocal(rden[:, :, :], v[:, :, :, HD]))
                    for g in range(NG):
                        last = nc.vector.tensor_tensor(
                            ON[:, :].rearrange("t (j g d) -> t j g d", g=NG, d=HD)[:, :, g, :],
                            v[:, g, :, 0:HD], rden[:, g, :].unsqueeze(2).broadcast_to((T, NJ, HD)), ALU.mult)
                    last.then_inc(s_on, 1)

                def residual(b):
                    dve.wait_ge(s_y, b + 1)
                    nc.vector.tensor_tensor(m.X[:, b, :], m.X[:, b, :], pP[0:T, 1, 128:256], ALU.add)\
                      .then_inc(s_x, 1)

                def query_half(n):
                    if units[n][0] != "Q":
                        return
                    _, p, g, h = units[n]
                    dve.wait_ge(s_t2, n + 1)
                    if n == 0:
                        dve.wait_ge(s_clear, 1)
                    nc.vector.tensor_tensor(QS[0:64, 2 * p, g, h * HALF:(h + 1) * HALF],
                                            X1[0:64, n % 2, 0:HALF], T2[0:64, n % 2, 0:HALF],
                                            ALU.subtract).then_inc(s_qv, 1)

                for n in range(FIRST):
                    read(n)
                    if n >= 1:
                        query_half(n - 1)
                for t in steps:
                    b, u = t // NU, t % NU
                    for n in at.get(t - DELAY, []):
                        read(n)
                    if t + LAG < B * MU:
                        maximum(t + LAG)
                    if b >= 1 and u == 0:
                        out_copied(b - 1)
                    if b >= 1 and u == NORM_AT:
                        normalised(b - 1)
                    if b >= 1 and u == RES_AT:
                        residual(b - 1)
                out_copied(B - 1)
                normalised(B - 1)
                residual(B - 1)

            @block.scalar
            def _(act):
                ln_scalar(nc, act, m, q, banks)
                if bias is not None:
                    act.wait_ge(s_bias, 1)

                def first_terms(n):
                    unit = units[n]
                    if unit[0] == "V":
                        return
                    i = split_before(n)
                    W = width(unit)
                    bank = n % 2 if n < FIRST else 0
                    act.wait_ge(s_up, n + 1)
                    c = MASK + (0 if unit[0] == "K" else 2)
                    if unit[0] == "M":
                        nc.scalar.activation(T1[:, i % 2, 0:W], pP[:, bank, 0:W], ACT.Copy,
                                             scale=bcol[:, c:c + 1]).then_inc(s_t1, 1)
                    else:
                        k = bias_column(unit)
                        nc.scalar.activation(T1[:, i % 2, 0:W], pP[:, bank, 0:W], ACT.Identity,
                                             bias=mcol[:, k:k + 1], scale=bcol[:, c:c + 1]).then_inc(s_t1, 1)

                def second_terms(n):
                    if units[n][0] == "V":
                        return
                    act.wait_ge(s_x1, n + 1)
                    i = split_before(n)
                    if i >= 2:
                        act.wait_ge(s_fin, i - 1)
                        act.wait_ge(s_qv, min(i - 1, NQ))
                    c = MASK + (1 if units[n][0] == "K" else 3)
                    W = width(units[n])
                    nc.scalar.activation(T2[:, i % 2, 0:W], X1[:, i % 2, 0:W], ACT.Copy,
                                         scale=bcol[:, c:c + 1]).then_inc(s_t2, 1)

                def exps(n):
                    k = n % NU // NJ
                    act.wait_ge(s_s, n + 1)
                    if n >= EB:
                        act.wait_ge(s_eu, n - EB + 1)
                    nc.scalar.activation(E[0:tiles[k], n % EB, :], pS[0:tiles[k], n % 2, 0:NG * T],
                                         ACT.Exp, scale=SCALE8).then_inc(s_e, 1)

                def outT(b):
                    act.wait_ge(s_ot, b + 1)
                    nc.scalar.copy(OT[:, :], pP[:, 1, 0:T]).then_inc(s_ots, 1)

                for n in range(FIRST):
                    first_terms(n)
                    if n >= 1:
                        second_terms(n - 1)
                for t in steps:
                    for n in at[t]:
                        first_terms(n)
                    for n in at.get(t - DELAY, []):
                        if not long:
                            second_terms(n)
                    if 0 <= t + NJ < STEPS:
                        exps(t + NJ)
                    if t // NU >= 1 and t % NU == OT_AT:
                        outT(t // NU - 1)
                outT(B - 1)

            @block.tensor
            def _(pe):
                if bias is not None:
                    pe.wait_ge(s_row, 1)
                    for i in range(MASK):
                        last = nc.tensor.matmul(pO[:, i:i + 1], brow[0:1, i, :], m.ones[0:1, 0:1],
                                                start=(i == 0), stop=True, skip_group_check=True)
                    last.then_inc(s_col, 1)
                pe.wait_ge(m.loaded[name], m.load_total[name])
                if not weights_natural:
                    for n in range(4):
                        nc.tensor.transpose(wTs[n], srcs[n][0:rows[n], :], m.ident[0:rows[n], 0:rows[n]])\
                          .then_inc(s_wT, 1)
                if keys == "causal":
                    for b in range(B):
                        pe.wait_ge(m.ctx_loaded[b], 32)
                        last = nc.tensor.transpose(pS[:, b // HB, (b % HB) * T:(b % HB + 1) * T],
                                                   m.ctx_tm[0:T, b, 0, 0:D], m.ident[0:T, 0:T])
                        if b % HB == HB - 1:
                            last.then_inc(s_cx, 1)
                ln_tensor(nc, pe, m, q, banks)
                if keys == "causal":
                    pe.wait_ge(s_cxs, 2)
                pe.wait_ge(s_w, 1)
                pe.wait_ge(q.xTs, 2)
                wv_ap = srcs[2][:, :] if weights_natural else wT[:, 0, 0:KD]
                wo_ap = srcs[3][:, :] if weights_natural else wT[:, 1, :]

                def kv_src(b, n):
                    if keys == "self":
                        return m.XNT[:, b * T:(b + n) * T]
                    return CX[:, b * T:(b + n) * T]

                def unit_matmul(n):
                    unit = units[n]
                    kind = unit[0]
                    bank = n % 2 if n < FIRST else 0
                    if n < FIRST and n >= 2:
                        pe.wait_ge(s_x1, n - 1)
                    if n >= FIRST:
                        pe.wait_ge(s_x1, n)
                    if kind == "Q":
                        last = nc.tensor.matmul(pP[:, bank, 0:HALF], wqe[:, unit[1], unit[2], :],
                                                m.XNT[:, unit[3] * HALF:(unit[3] + 1) * HALF],
                                                start=True, stop=True)
                    elif kind == "K" and long:
                        c0, W = CH[0] * unit[3], width(unit)
                        last = nc.tensor.matmul(pP[:, bank, 0:W], wke[:, unit[1], 0, :],
                                                m.CT[:, unit[2], c0:c0 + W],
                                                start=True, stop=True)
                    elif kind == "K":
                        last = nc.tensor.matmul(pP[:, bank, 0:HALF], wke[:, unit[1], unit[2], :],
                                                kv_src(unit[3] * HB, HB), start=True, stop=True)
                    elif kind == "V" and long:
                        k0 = NKT // 2 * unit[2]
                        for k in range(k0, k0 + NKT // 2):
                            last = nc.tensor.matmul(pP[0:TILES[k], bank, 32 * (k - k0):32 * (k - k0) + 32],
                                                    m.CT[:, unit[1], k * 128:k * 128 + TILES[k]], wv_ap,
                                                    start=True, stop=True)
                    elif kind == "V":
                        last = nc.tensor.matmul(pP[0:T, bank, 0:KD], kv_src(unit[1], 1), wv_ap,
                                                start=True, stop=bias is None)
                        if bias is not None:
                            last = nc.tensor.matmul(pP[0:T, bank, 0:KD], m.ones[0:1, 0:T], bias[2][0:1, :],
                                                    start=False, stop=True)
                    else:
                        pe.wait_ge(s_mx, unit[2] + 1)
                        for g in range(NG):
                            last = nc.tensor.matmul(pP[:, bank, g * T:(g + 1) * T],
                                                    MXP[:, unit[2] % 2, unit[1], g, :], m.ident[0:T, 0:T],
                                                    start=(g == 0), stop=True, skip_group_check=True)
                    last.then_inc(s_up, 1)

                def max_scores(n):
                    b, u = n // MU, n % MU
                    if n >= 3:
                        pe.wait_ge(s_mr, n - 2)
                    if u == 0:
                        pe.wait_ge(s_fin, keys_ready(b))
                    if long:
                        j, g, c = u // (3 * NG), u // 3 % NG, u % 3
                        k0 = sum(CH[:c])
                        last = nc.tensor.matmul(pM[0:T, n % 3, 0:CH[c]], QS[:, j, g, b * T:(b + 1) * T],
                                                KS[:, b % KB, j // 2, k0:k0 + CH[c]], start=True, stop=True)
                    else:
                        if not grouped:
                            nc.tensor.matmul(pM[0:T, n % 3, 0:NG * T], ident16[:, :], mask16[:, 0, :],
                                             start=True, stop=False, skip_group_check=True)
                        for g in range(NG):
                            last = nc.tensor.matmul(
                                pM[0:T, n % 3, g * T:(g + 1) * T], QS[:, u, g, b * T:(b + 1) * T],
                                KS[:, g if NK > 1 else 0, u // 2, b * T:(b + 1) * T],
                                start=(grouped and g == 0), stop=True, skip_group_check=True)
                    last.then_inc(s_m, 1)

                def score(n):
                    b, u = n // NU, n % NU
                    k, j = u // NJ, u % NJ
                    if u == 0:
                        pe.wait_ge(s_fin, rows_split(b))
                    if n >= 2:
                        pe.wait_ge(s_e, n - 1)
                    if long:
                        last = nc.tensor.matmul(pS[0:tiles[k], n % 2, 0:NG * T],
                                                KS[:, b % KB, j // 2, k * 128:k * 128 + tiles[k]],
                                                QS[:, j, :, b * T:(b + 1) * T], start=True, stop=True)
                    elif grouped:
                        last = nc.tensor.matmul(pS[0:T, n % 2, 0:NG * T], KS[:, 0, j // 2, b * T:(b + 1) * T],
                                                QS[:, j, :, b * T:(b + 1) * T], start=True, stop=True)
                    else:
                        nc.tensor.matmul(pS[0:T, n % 2, 0:NG * T], ident16[:, :], mask16[:, 1, :],
                                         start=True, stop=False, skip_group_check=True)
                        for g in range(NG):
                            last = nc.tensor.matmul(pS[0:T, n % 2, g * T:(g + 1) * T],
                                                    KS[:, g, j // 2, b * T:(b + 1) * T],
                                                    QS[:, j, g, b * T:(b + 1) * T], start=False, stop=True,
                                                    skip_group_check=True)
                    last.then_inc(s_s, 1)

                def rows_split(b):
                    n = max(n for n, x in enumerate(units) if x[0] == "M" and x[2] == b)
                    return 1 + split_before(n)

                def weigh(n):
                    b, u = n // NU, n % NU
                    k, j = u // NJ, u % NJ
                    pe.wait_ge(s_e, n + 1)
                    if u == 0:
                        pe.wait_ge(s_x1, values_ready(b))
                        if b >= 1:
                            pe.wait_ge(s_oc, b)
                    out = pO[32 * j:32 * j + 32, 0:NG * T]
                    if grouped:
                        v = V[0:tiles[k], b % 2, k, j, :] if long else V[:, b, j, :]
                        last = nc.tensor.matmul(out, v, E[0:tiles[k], n % EB, :], start=(k == 0),
                                                stop=(k == nt - 1), skip_group_check=True)
                    else:
                        for g in range(NG):
                            last = nc.tensor.matmul(out[:, g * T:(g + 1) * T], V[:, b, NG * j + g, :],
                                                    E[0:T, n % EB, g * T:(g + 1) * T], start=(g == 0),
                                                    stop=True, skip_group_check=True)
                    last.then_inc(s_eu, 1)

                def token_major(b):
                    pe.wait_ge(s_oc, b + 1)
                    if b >= 1:
                        pe.wait_ge(s_x, b)
                    for g in range(NG):
                        last = nc.tensor.transpose(pP[0:T, 1, g * 128:(g + 1) * 128], OC[:, g * T:(g + 1) * T],
                                                   m.ident[:, :])
                    last.then_inc(s_tt, 1)

                def turn(b):
                    pe.wait_ge(s_on, b + 1)
                    nc.tensor.transpose(pP[:, 1, 0:T], ON[:, :], m.ident[0:T, 0:T]).then_inc(s_ot, 1)

                def project(b):
                    pe.wait_ge(s_ots, b + 1)
                    last = nc.tensor.matmul(pP[0:T, 1, 128:256], OT[:, :], wo_ap, start=True,
                                            stop=bias is None)
                    if bias is not None:
                        last = nc.tensor.matmul(pP[0:T, 1, 128:256], m.ones[0:1, 0:T], bias[3][0:1, :],
                                                start=False, stop=True)
                    last.then_inc(s_y, 1)

                for n in range(FIRST):
                    unit_matmul(n)
                pe.wait_ge(s_qv, NQ)
                for t in steps:
                    b, u = t // NU, t % NU
                    for n in at[t]:
                        unit_matmul(n)
                    if t + LAG < B * MU:
                        max_scores(t + LAG)
                    if 0 <= t + NJ < STEPS:
                        score(t + NJ)
                    if b >= 1 and u == TM_AT:
                        token_major(b - 1)
                    if b >= 1 and u == TURN_AT:
                        turn(b - 1)
                    if b >= 1 and u == PROJ_AT:
                        project(b - 1)
                    if t >= 0 and u % NJ == NJ - 1:
                        for n in range(t - NJ + 1, t + 1):
                            weigh(n)
                token_major(B - 1)
                turn(B - 1)
                project(B - 1)



def context_block(nc, m, name, stats):
    VT = 7
    with ExitStack() as ctx:
        s = Stage(nc, ctx, name)
        pT = s.ps("pT", [128, 6, 512])
        junk = s.sb("junk", [128, NKT, D])
        ss = s.sb("ss", [128, B, NKT])
        s_sq, s_sq2, s_ms = s.sem("squares_vector"), s.sem("squares_scalar"), s.sem("mean_squares")
        s_r = s.sem("rstd")
        s_t, s_c, s_c2 = s.sem("transposed"), s.sem("copied_even"), s.sem("copied_odd")
        groups = [(b, g) for b in range(B) for g in range(3)]

        with nc.Block(no_gpsimd_drain=True) as block:

            @block.gpsimd
            def _(pool):
                if stats:
                    for b in range(B):
                        pool.wait_ge(s_ms, b + 1)
                        nc.gpsimd.tensor_tensor(m.ctx_r[:, b, :], ss[:, b, :], m.neg_half[:, 0:NKT], ALU.pow)\
                          .then_inc(s_r, 1)

            @block.vector
            def _(dve):
                def inverse(b):
                    dve.wait_ge(s_r, b + 1)
                    nc.vector.tensor_tensor(m.ctx_tm[:, b, :, D], ss[:, b, :], m.ctx_r[:, b, :], ALU.mult)

                for b in range(B):
                    if stats:
                        dve.wait_ge(m.ctx_loaded[b], 32)
                        if b >= 1:
                            dve.wait_ge(s_sq, b)
                        for k in range(VT):
                            last = nc.vector.scalar_tensor_tensor(
                                out=junk[:, k, :], in0=m.ctx_tm[:, b, k, 0:D], scalar=1.0,
                                in1=m.ctx_tm[:, b, k, 0:D], op0=ALU.mult, op1=ALU.mult,
                                accum_out=ss[:, b, k:k + 1])
                        last.then_inc(s_sq, 1)
                    for g in range(3):
                        i = 3 * b + g
                        if i % 2 == 0:
                            dve.wait_ge(s_t, i + 1)
                            nc.vector.tensor_copy(m.CT[:, b, g * 512:(g + 1) * 512], pT[:, i % 6, :])\
                              .then_inc(s_c, 1)
                    if stats:
                        dve.wait_ge(s_sq, b + 1)
                        dve.wait_ge(s_sq2, b + 1)
                        nc.vector.tensor_scalar(ss[:, b, :], ss[:, b, :], 1.0 / D, 1e-6, ALU.mult, ALU.add)\
                          .then_inc(s_ms, 1)
                        if b >= 1:
                            inverse(b - 1)
                if stats:
                    inverse(B - 1)

            @block.scalar
            def _(act):
                for b in range(B):
                    if stats:
                        act.wait_ge(m.ctx_loaded[b], 32)
                        if b >= 1:
                            act.wait_ge(s_sq2, b)
                        for k in range(VT, NKT):
                            last = nc.scalar.activation(junk[:, k, :], m.ctx_tm[:, b, k, 0:D], ACT.Square,
                                                        accum_out=ss[:, b, k:k + 1])
                        last.then_inc(s_sq2, 1)
                    for g in range(3):
                        i = 3 * b + g
                        if i % 2 == 1:
                            act.wait_ge(s_t, i + 1)
                            nc.scalar.copy(m.CT[:, b, g * 512:(g + 1) * 512], pT[:, i % 6, :])\
                              .then_inc(s_c2, 1)

            @block.tensor
            def _(pe):
                for i, (b, g) in enumerate(groups):
                    pe.wait_ge(m.ctx_loaded[b], 32)
                    if i >= 6:
                        if i % 2 == 0:
                            pe.wait_ge(s_c, (i - 6) // 2 + 1)
                        else:
                            pe.wait_ge(s_c2, (i - 6) // 2 + 1)
                    for k in range(4):
                        last = nc.tensor.transpose(pT[:, i % 6, k * 128:(k + 1) * 128],
                                                   m.ctx_tm[:, b, 4 * g + k, 0:D], m.ident[:, :])
                    last.then_inc(s_t, 1)


def load_context(sp, m, b):
    src = m.a["ctx_1024"]
    sp.dma_start(m.ctx_tm[:, b, 0:KT_FULL, 0:D],
                 src[b, 0:KT_FULL * 128, :].rearrange("(k p) d -> p k d", p=128)).then_inc(m.ctx_loaded[b], 16)
    sp.dma_start(m.ctx_tm[0:TAIL, b, KT_FULL, 0:D], src[b, KT_FULL * 128:SC, :]).then_inc(m.ctx_loaded[b], 16)



def slot_attention(nc, m):
    name = "L0x"
    w = m.w
    ITERS = 3
    N = ITERS * B
    TICKS = range(-4, N + 1)
    SB = 5
    QT, UT_AT = 256, 256
    G4 = 512
    with ExitStack() as ctx:
        s = Stage(nc, ctx, name)
        q = ln_sems(s)
        Mqk = s.sb("Mqk", [128, 128])
        G = s.sb("G", [128, 3 * D])
        wihT = s.sb("wihT", [128, 3 * D])
        whhT = s.sb("whhT", [128, 3 * D])
        grow = s.sb("gate_bias", [1, G4])
        parts = s.sb("gate_bias_parts", [65, G4], BF16)
        part = s.sb("gate_bias_part", [1, G4], BF16)
        ones_b = s.sb("ones_bf16", [65, T], BF16)
        ssq = s.sb("ssq", [T, 2])
        rsl = s.sb("rsl", [T, 2])
        junk = s.sb("junk", [T, D])
        SN = s.sb("SN", [T, 2, D])
        STs = s.sb("STs", [128, 4, 2, T])
        QS = s.sb("QS", [128, 2, T])
        mx = s.sb("mx", [128, 2, 12])
        E = s.sb("E", [128, 3, 12, T])
        Z = s.sb("Z", [128, 2, 12])
        RZ = s.sb("RZ", [128, 2, 12])
        den = s.sb("den", [T, 2])
        U = s.sb("U", [T, D])
        UT = s.sb("UT", [128, T])
        rz = s.sb("rz", [T, 2, 2 * D])
        nn = s.sb("nn", [T, 2, 3, D])
        pS = s.ps("pS", [128, SB, 512])
        pU = s.ps("pU", [128, 512])
        pT = s.ps("pT", [128, 512])
        pG = s.ps("pG", [128, 512])
        vch = s.sem("vector_own")
        gch = s.sem("gpsimd_own")
        s_wt, s_wc, s_w2, s_wr = s.sem("gru_transposed"), s.sem("gru_copied"), s.sem("products"), s.sem("weights")
        s_sq, s_r, s_sn = s.sem("slot_squares"), s.sem("slot_rstd"), s.sem("slots_normalised")
        s_t, s_ts = s.sem("slotsT_psum"), s.sem("slotsT_sbuf")
        s_q, s_qs = s.sem("q_psum"), s.sem("q_sbuf")
        s_s, s_sub, s_e = s.sem("scores"), s.sem("less_max"), s.sem("exps")
        s_rz, s_en = s.sem("rec_of_sums"), s.sem("attention")
        s_u, s_us = s.sem("update_psum"), s.sem("update_sbuf")
        s_ut, s_uts = s.sem("updateT_psum"), s.sem("updateT_sbuf")
        s_g, s_th = s.sem("gates_psum"), s.sem("tanh_rz")
        s_ni, s_n = s.sem("n_argument"), s.sem("n")
        s_slot = s.sem("slots_updated")
        s_mx = s.sem("maxima")

        with nc.Block(no_gpsimd_drain=True) as block:

            @block.gpsimd
            def _(pool):
                ln_gpsimd(nc, pool, m, q)
                chain = Chain(pool, gch)

                def rstd(n):
                    pool.wait_ge(s_sq, n + 1)
                    nc.gpsimd.tensor_tensor(rsl[:, n % 2:n % 2 + 1], ssq[:, n % 2:n % 2 + 1],
                                            m.neg_half[0:T, 0:1], ALU.pow).then_inc(s_r, 1)

                def normalise(n):
                    pool.wait_ge(s_rz, n + 1)
                    nc.gpsimd.tensor_tensor(E[:, n % 3, :, :], E[:, n % 3, :, :],
                                            RZ[:, n % 2, :].unsqueeze(2).broadcast_to((128, 12, T)),
                                            ALU.mult).then_inc(s_en, 1)

                def update(n):
                    b = n % B
                    pool.wait_ge(s_n, n + 1)
                    chain.then(nc.gpsimd.tensor_tensor(nn[:, n % 2, 2, :], m.XN[:, b, :], nn[:, n % 2, 1, :],
                                                       ALU.subtract))
                    chain.then(nc.gpsimd.tensor_tensor(nn[:, n % 2, 2, :], nn[:, n % 2, 2, :],
                                                       rz[:, n % 2, D:2 * D], ALU.mult))
                    nc.gpsimd.tensor_tensor(m.XN[:, b, :], nn[:, n % 2, 2, :], nn[:, n % 2, 1, :],
                                            ALU.add).then_inc(s_slot, 1)

                for i in TICKS:
                    if i + 4 < N:
                        rstd(i + 4)
                    if 0 <= i + 1 < N:
                        normalise(i + 1)
                    if 0 <= i - 1 < N:
                        update(i - 1)

            @block.vector
            def _(dve):
                chain = Chain(dve, vch)
                ln_vector(nc, dve, chain, m, q)
                dve.wait_ge(m.loaded[name], m.load_total[name])
                bi, bh = w["x0bi"], w["x0bh"]
                nc.vector.tensor_tensor(grow[0:1, 0:2 * D], bi[0:1, 0:2 * D], bh[0:1, 0:2 * D], ALU.add)
                nc.vector.tensor_copy(grow[0:1, 2 * D:3 * D], bi[0:1, 2 * D:3 * D])
                nc.vector.tensor_copy(grow[0:1, 3 * D:4 * D], bh[0:1, 2 * D:3 * D])
                chain.then(nc.vector.memset(parts[:, :], 0.0))
                nc.vector.memset(ones_b[:, :], 1.0)
                for row in (0, 32, 64):
                    chain.then(nc.vector.tensor_copy(part[0:1, :], grow[0:1, :]))
                    nc.vector.tensor_copy(parts[row:row + 1, :], part[0:1, :])
                    chain.then(nc.vector.tensor_tensor(grow[0:1, :], grow[0:1, :], part[0:1, :], ALU.subtract))
                dve.wait_ge(s_wt, 2)
                nc.vector.tensor_copy(wihT[:, :], pS[:, 0, 0:3 * D])
                nc.vector.tensor_copy(whhT[:, :], pS[:, 1, 0:3 * D]).then_inc(s_wc, 1)
                dve.wait_ge(s_w2, 1)
                nc.vector.tensor_scalar(G[:, :], pS[:, 2, 0:3 * D], w["x0iw"][:, 0:1], None, ALU.mult)
                nc.vector.tensor_scalar(Mqk[:, :], pS[:, 3, 0:D], w["x0sw"][:, 0:1], float(D) ** -0.5,
                                        ALU.mult, ALU.mult).then_inc(s_wr, 1)
                dve.wait_ge(q.norm, B)

                def slot_stats(n):
                    b = n % B
                    if n >= B:
                        dve.wait_ge(s_slot, n - B + 1)
                    chain.then(nc.vector.scalar_tensor_tensor(
                        out=junk[:, :], in0=m.XN[:, b, :], scalar=1.0, in1=m.XN[:, b, :],
                        op0=ALU.mult, op1=ALU.mult, accum_out=ssq[:, n % 2:n % 2 + 1]))
                    nc.vector.tensor_scalar(ssq[:, n % 2:n % 2 + 1], ssq[:, n % 2:n % 2 + 1], 1.0 / D, 1e-6,
                                            ALU.mult, ALU.add).then_inc(s_sq, 1)

                def slot_norm(n):
                    dve.wait_ge(s_r, n + 1)
                    if n >= 2:
                        dve.wait_ge(s_t, n - 1)
                    nc.vector.tensor_scalar(SN[:, n % 2, :], m.XN[:, n % B, :], rsl[:, n % 2:n % 2 + 1], None,
                                            ALU.mult).then_inc(s_sn, 1)

                def less_max(n):
                    def largest(c):
                        g = 3 * n + c
                        dve.wait_ge(s_s, g + 1)
                        nc.vector.tensor_reduce(mx[:, n % 2, 4 * c:4 * c + 4],
                                                pS[:, g % SB, 0:4 * T].rearrange("p (k t) -> p k t", t=T),
                                                AX.X, ALU.max).then_inc(s_mx, 1)

                    def less(c):
                        g = 3 * n + c
                        dve.wait_ge(s_mx, g + 1)
                        nc.vector.tensor_tensor(
                            E[:, n % 3, 4 * c:4 * c + 4, :],
                            pS[:, g % SB, 0:4 * T].rearrange("p (k t) -> p k t", t=T),
                            mx[:, n % 2, 4 * c:4 * c + 4].unsqueeze(2).broadcast_to((128, 4, T)),
                            ALU.subtract).then_inc(s_sub, 1)

                    if n >= 3:
                        dve.wait_ge(s_u, n - 2)
                    largest(0)
                    largest(1)
                    less(0)
                    largest(2)
                    less(1)
                    less(2)

                def sums(n):
                    dve.wait_ge(s_e, 3 * n + 3)
                    if n >= 2:
                        dve.wait_ge(s_en, n - 1)
                    chain.then(nc.vector.reciprocal(RZ[:, n % 2, :], Z[:, n % 2, :]))
                    nc.vector.tensor_tensor(RZ[:, n % 2, :], RZ[:, n % 2, :], m.ctx_r[:, n % B, :],
                                            ALU.mult).then_inc(s_rz, 1)

                def scale_update(n):
                    dve.wait_ge(s_u, n + 1)
                    chain.then(nc.vector.tensor_scalar(den[:, 0:1], pU[0:T, D:D + 1], 1e-6, None, ALU.add))
                    chain.then(nc.vector.reciprocal(den[:, 1:2], den[:, 0:1]))
                    nc.vector.tensor_scalar(U[:, :], pU[0:T, 0:D], den[:, 1:2], None, ALU.mult).then_inc(s_us, 1)

                def gates(n):
                    dve.wait_ge(s_th, n + 1)
                    if n >= 2:
                        dve.wait_ge(s_slot, n - 1)
                    chain.then(nc.vector.tensor_scalar(rz[:, n % 2, :], rz[:, n % 2, :], 0.5, 0.5,
                                                       ALU.mult, ALU.add))
                    chain.then(nc.vector.tensor_tensor(nn[:, n % 2, 0, :], pG[0:T, 3 * D:4 * D],
                                                       rz[:, n % 2, 0:D], ALU.mult))
                    nc.vector.tensor_tensor(nn[:, n % 2, 0, :], pG[0:T, 2 * D:3 * D], nn[:, n % 2, 0, :],
                                            ALU.add).then_inc(s_ni, 1)

                for i in TICKS:
                    if i + 4 < N:
                        slot_stats(i + 4)
                    if 0 <= i - 1 < N:
                        gates(i - 1)
                    if 0 <= i < N:
                        scale_update(i)
                    if i + 4 < N:
                        slot_norm(i + 4)
                    if 0 <= i + 1 < N:
                        sums(i + 1)
                    if 0 <= i + 2 < N:
                        less_max(i + 2)
                for b in range(B):
                    dve.wait_ge(s_slot, N - B + b + 1)
                    nc.vector.tensor_tensor(m.X[:, b, :], m.X[:, b, :], m.XN[:, b, :], ALU.add)

            @block.scalar
            def _(act):
                def slotsT(n):
                    act.wait_ge(s_t, n + 1)
                    if n >= 4:
                        act.wait_ge(s_g, n - 3)
                    nc.scalar.copy(STs[:, n % 4, :, :],
                                   pT[:, 0:2 * T].rearrange("p (i t) -> p i t", i=2)).then_inc(s_ts, 1)

                def queries(n):
                    act.wait_ge(s_q, n + 1)
                    if n >= 2:
                        act.wait_ge(s_s, 3 * (n - 1))
                    nc.scalar.activation(QS[:, n % 2, :], pT[:, QT:QT + T], ACT.Copy,
                                         scale=w["x0iw"][:, 0:1]).then_inc(s_qs, 1)

                def exps(n, c):
                    if n >= 2 and c == 0:
                        act.wait_ge(s_rz, n - 1)
                    act.wait_ge(s_sub, 3 * n + c + 1)
                    for k in range(4 * c, 4 * c + 4):
                        last = nc.scalar.activation(E[:, n % 3, k, :], E[:, n % 3, k, :], ACT.Exp,
                                                    scale=m.ctx_r[:, n % B, k:k + 1],
                                                    accum_out=Z[:, n % 2, k:k + 1])
                    last.then_inc(s_e, 1)

                def updateT(n):
                    act.wait_ge(s_ut, n + 1)
                    if n >= 1:
                        act.wait_ge(s_g, n)
                    nc.scalar.copy(UT[:, :], pU[:, UT_AT:UT_AT + T]).then_inc(s_uts, 1)

                def reset_update(n):
                    act.wait_ge(s_g, n + 1)
                    if n >= 2:
                        act.wait_ge(s_slot, n - 1)
                    nc.scalar.activation(rz[:, n % 2, :], pG[0:T, 0:2 * D], ACT.Tanh, scale=0.5)\
                      .then_inc(s_th, 1)

                def new(n):
                    act.wait_ge(s_ni, n + 1)
                    nc.scalar.activation(nn[:, n % 2, 1, :], nn[:, n % 2, 0, :], ACT.Tanh).then_inc(s_n, 1)

                act.wait_ge(m.loaded[name], m.load_total[name])
                for i in TICKS:
                    if 0 <= i + 1 < N:
                        exps(i + 1, 0)
                    if 0 <= i - 1 < N:
                        reset_update(i - 1)
                    if 0 <= i + 3 < N:
                        slotsT(i + 3)
                    if 0 <= i + 1 < N:
                        exps(i + 1, 1)
                    if 0 <= i - 1 < N:
                        new(i - 1)
                    if 0 <= i + 1 < N:
                        exps(i + 1, 2)
                    if 0 <= i + 3 < N:
                        queries(i + 3)
                    if 0 <= i < N:
                        updateT(i)

            @block.tensor
            def _(pe):
                pe.wait_ge(m.loaded[name], m.load_total[name])
                for i, key in enumerate(("x0ih", "x0hh")):
                    for c in range(3):
                        last = nc.tensor.transpose(pS[:, i, c * D:(c + 1) * D], w[key][:, c, :], m.ident[:, :])
                    last.then_inc(s_wt, 1)
                nc.tensor.matmul(pS[:, 3, 0:D], w["x0q"][:, :], w["x0k"][:, :], start=True, stop=True)
                pe.wait_ge(s_wc, 1)
                nc.tensor.matmul(pS[:, 2, 0:3 * D], w["x0v"][:, :], wihT[:, :], start=True, stop=True)\
                  .then_inc(s_w2, 1)
                pe.wait_ge(s_wr, 1)

                def slots_turned(n):
                    pe.wait_ge(s_sn, n + 1)
                    if n >= 1:
                        pe.wait_ge(s_qs, n)
                    nc.tensor.transpose(pT[:, 0:T], m.XN[:, n % B, :], m.ident[0:T, 0:T])
                    nc.tensor.transpose(pT[:, T:2 * T], SN[:, n % 2, :], m.ident[0:T, 0:T]).then_inc(s_t, 1)

                def query(n):
                    pe.wait_ge(s_ts, n + 1)
                    nc.tensor.matmul(pT[:, QT:QT + T], Mqk[:, :], STs[:, n % 4, 1, :],
                                     start=True, stop=True).then_inc(s_q, 1)

                def scores(n):
                    pe.wait_ge(s_qs, n + 1)
                    for g in range(3 * n, 3 * n + 3):
                        if g >= SB:
                            pe.wait_ge(s_sub, g - SB + 1)
                        for k in range(4):
                            c = (4 * (g - 3 * n) + k) * 128
                            last = nc.tensor.matmul(pS[:, g % SB, k * T:(k + 1) * T],
                                                    m.CT[:, n % B, c:c + 128], QS[:, n % 2, :],
                                                    start=True, stop=True)
                        last.then_inc(s_s, 1)

                def update(n):
                    pe.wait_ge(s_en, n + 1)
                    if n >= 1:
                        pe.wait_ge(s_uts, n)
                    for k, rows in enumerate(TILES):
                        last = nc.tensor.matmul(pU[0:T, 0:D + 1], E[0:rows, n % 3, k, :],
                                                m.ctx_tm[0:rows, n % B, k, :], start=(k == 0),
                                                stop=(k == NKT - 1))
                    last.then_inc(s_u, 1)

                def update_turned(n):
                    pe.wait_ge(s_us, n + 1)
                    nc.tensor.transpose(pU[:, UT_AT:UT_AT + T], U[:, :], m.ident[0:T, 0:T])\
                      .then_inc(s_ut, 1)

                def gates_of_slots(n):
                    if n >= 1:
                        pe.wait_ge(s_ni, n)
                    nc.tensor.matmul(pG[0:T, :], ones_b[:, :], parts[:, :], start=True, stop=False,
                                     skip_group_check=True)
                    nc.tensor.matmul(pG[0:T, 0:2 * D], STs[:, n % 4, 0, :], whhT[:, 0:2 * D], start=False,
                                     stop=False, skip_group_check=True)
                    nc.tensor.matmul(pG[0:T, 3 * D:4 * D], STs[:, n % 4, 0, :], whhT[:, 2 * D:3 * D],
                                     start=False, stop=True, skip_group_check=True)

                def gates_of_update(n):
                    pe.wait_ge(s_uts, n + 1)
                    nc.tensor.matmul(pG[0:T, 0:3 * D], UT[:, :], G[:, :], start=False, stop=True,
                                     skip_group_check=True).then_inc(s_g, 1)

                for i in TICKS:
                    if 0 <= i - 1 < N:
                        gates_of_update(i - 1)
                    if 0 <= i + 3 < N:
                        slots_turned(i + 3)
                    if 0 <= i < N:
                        update(i)
                    if 0 <= i + 3 < N:
                        query(i + 3)
                    if 0 <= i + 2 < N:
                        scores(i + 2)
                    if 0 <= i < N:
                        update_turned(i)
                        gates_of_slots(i)



NE = 8


def first_largest(nc, chain, m, val, top, eq, best, onehot):
    chain.then(nc.vector.tensor_reduce(top, val, AX.X, ALU.max))
    chain.then(nc.vector.tensor_tensor(eq, val, top.unsqueeze(2).broadcast_to((T, B, NE)), ALU.is_equal))
    chain.then(nc.vector.tensor_tensor(eq, eq, m.order[:, :, :], ALU.mult))
    chain.then(nc.vector.tensor_reduce(best, eq, AX.X, ALU.max))
    chain.then(nc.vector.tensor_tensor(onehot, eq, best.unsqueeze(2).broadcast_to((T, B, NE)), ALU.is_equal))


def mixture_golden(nc, m):
    name = "L0f"
    w = m.w
    CENTER, LOWER, UPPER = 0.36787944117144233, 0.5 - 0.28768207245178085, 0.5
    N = 2 * NE
    with ExitStack() as ctx:
        s = Stage(nc, ctx, name)
        q = ln_sems(s)
        small = [s.sb(f"r{i}", [T, B, NE]) for i in range(8)]
        inh, dist, wz, fb, mask, t1, t2, zone = small
        sums = [s.sb(f"s{i}", [T, B]) for i in range(4)]
        itemp = s.sb("itemp", [T, 1])
        SG = s.sb("SG", [128, 2, HALF])
        H = m.CT[:, :, :].rearrange("p b k -> p (b k)")[:, 0:N * HALF].rearrange("p (n t) -> p n t", n=N)
        pG = s.ps("pG", [128, 2, 512])
        pU = s.ps("pU", [128, 2, 512])
        pW = s.ps("pW", [128, 512])
        pY = s.ps("pY", [128, 3, 512])
        vch = s.sem("vector_own")
        s_tp, s_lg, s_it = s.sem("temperature_psum"), s.sem("logits"), s.sem("inverse_temperature")
        s_ex, s_ds, s_fw = s.sem("exp_of_logits"), s.sem("distances"), s.sem("exp_of_distances")
        s_x = s.sem("added")
        s_g, s_sg, s_h, s_y = s.sem("gate_up"), s.sem("silu"), s.sem("hidden"), s.sem("out")

        with nc.Block(no_gpsimd_drain=True) as block:

            @block.gpsimd
            def _(pool):
                ln_gpsimd(nc, pool, m, q)

            @block.vector
            def _(dve):
                chain = Chain(dve, vch)
                ln_vector(nc, dve, chain, m, q)
                def hidden(n):
                    dve.wait_ge(s_sg, n + 1)
                    nc.vector.tensor_tensor(H[:, n, :], SG[:, n % 2, :], pU[:, n % 2, 0:HALF], ALU.mult)\
                      .then_inc(s_h, 1)

                dve.wait_ge(s_tp, 1)
                chain.then(nc.vector.reciprocal(itemp[:, :], pY[0:T, 0, 0:1]))
                nc.vector.tensor_scalar(itemp[:, :], itemp[:, :], -1.0, None, ALU.mult).then_inc(s_it, 1)
                dve.wait_ge(s_ex, 1)
                chain.then(nc.vector.tensor_scalar(inh[:, :, :], inh[:, :, :], 1.0, None, ALU.add))
                chain.then(nc.vector.reciprocal(inh[:, :, :], inh[:, :, :]))
                chain.then(nc.vector.tensor_scalar(t1[:, :, :], inh[:, :, :], CENTER, None, ALU.subtract))
                nc.vector.scalar_tensor_tensor(out=dist[:, :, :], in0=t1[:, :, :], scalar=-1.0,
                                               in1=t1[:, :, :], op0=ALU.mult, op1=ALU.max).then_inc(s_ds, 1)
                chain.then(nc.vector.tensor_scalar(zone[:, :, :], inh[:, :, :], LOWER, None, ALU.is_ge))
                chain.then(nc.vector.scalar_tensor_tensor(
                    out=zone[:, :, :], in0=inh[:, :, :], scalar=UPPER, in1=zone[:, :, :],
                    op0=ALU.is_le, op1=ALU.mult))
                hidden(0)
                hidden(1)
                dve.wait_ge(s_fw, 2)
                chain.then(nc.vector.tensor_tensor(wz[:, :, :], wz[:, :, :], zone[:, :, :], ALU.mult))
                hidden(2)
                first_largest(nc, chain, m, fb[:, :, :], sums[0][:, :], t1[:, :, :], sums[1][:, :],
                              mask[:, :, :])
                hidden(3)
                hidden(4)
                chain.then(nc.vector.scalar_tensor_tensor(
                    out=zone[:, :, :], in0=mask[:, :, :], scalar=-2.0, in1=fb[:, :, :],
                    op0=ALU.mult, op1=ALU.add))
                first_largest(nc, chain, m, zone[:, :, :], sums[0][:, :], t1[:, :, :], sums[1][:, :],
                              t2[:, :, :])
                hidden(5)
                hidden(6)
                chain.then(nc.vector.tensor_tensor(mask[:, :, :], mask[:, :, :], t2[:, :, :], ALU.add))
                chain.then(nc.vector.tensor_tensor(fb[:, :, :], fb[:, :, :], mask[:, :, :], ALU.mult))

                def over_sum(v, sm):
                    chain.then(nc.vector.tensor_reduce(sm, v, AX.X, ALU.add))
                    chain.then(nc.vector.tensor_scalar(sm, sm, 1e-8, None, ALU.max))
                    chain.then(nc.vector.reciprocal(sm, sm))
                    chain.then(nc.vector.tensor_tensor(v, v, sm.unsqueeze(2).broadcast_to((T, B, NE)), ALU.mult))

                hidden(7)
                over_sum(fb[:, :, :], sums[0][:, :])
                hidden(8)
                hidden(9)
                chain.then(nc.vector.tensor_reduce(sums[2][:, :], wz[:, :, :], AX.X, ALU.add))
                chain.then(nc.vector.tensor_scalar(sums[3][:, :], sums[2][:, :], 1e-8, None, ALU.is_lt))
                chain.then(nc.vector.tensor_tensor(t1[:, :, :], fb[:, :, :], wz[:, :, :], ALU.subtract))
                chain.then(nc.vector.tensor_tensor(
                    t1[:, :, :], t1[:, :, :], sums[3][:, :].unsqueeze(2).broadcast_to((T, B, NE)), ALU.mult))
                chain.then(nc.vector.tensor_tensor(wz[:, :, :], wz[:, :, :], t1[:, :, :], ALU.add))
                hidden(10)
                hidden(11)
                over_sum(wz[:, :, :], sums[0][:, :])
                hidden(12)
                hidden(13)

                def add(n):
                    e, h = n // 2, n % 2
                    dve.wait_ge(s_y, n + 1)
                    if n >= 2:
                        dve.wait_ge(s_x, n - 1)
                    for i in range(HB):
                        b = h * HB + i
                        last = nc.vector.scalar_tensor_tensor(
                            out=m.X[:, b, :], in0=pY[0:T, n % 3, i * D:(i + 1) * D], scalar=wz[:, b, e:e + 1],
                            in1=m.X[:, b, :], op0=ALU.mult, op1=ALU.add)
                    last.then_inc(s_x, 1)

                add(0)
                hidden(14)
                add(1)
                hidden(15)
                for n in range(2, N):
                    add(n)

            @block.scalar
            def _(act):
                ln_scalar(nc, act, m, q, [pG[:, 0, :], pG[:, 1, :]])
                act.wait_ge(s_lg, 1)
                act.wait_ge(s_it, 1)
                nc.scalar.activation(inh[:, :, :], pW[0:T, 0:B * NE].rearrange("p (b e) -> p b e", e=NE),
                                     ACT.Exp, scale=itemp[:, 0:1]).then_inc(s_ex, 1)

                def silu(n):
                    act.wait_ge(s_g, n + 1)
                    if n >= 2:
                        act.wait_ge(s_h, n - 1)
                    nc.scalar.activation(SG[:, n % 2, :], pG[:, n % 2, 0:HALF], ACT.Silu).then_inc(s_sg, 1)

                silu(0)
                silu(1)
                act.wait_ge(s_ds, 1)
                nc.scalar.activation(wz[:, :, :], dist[:, :, :], ACT.Exp, scale=-10.0).then_inc(s_fw, 1)
                nc.scalar.activation(fb[:, :, :], dist[:, :, :], ACT.Exp, scale=-1.0 / 0.3).then_inc(s_fw, 1)
                for n in range(2, N):
                    silu(n)

            @block.tensor
            def _(pe):
                pe.wait_ge(m.loaded[name], m.load_total[name])
                nc.tensor.matmul(pY[0:T, 0, 0:1], m.ones[0:1, 0:T], w["f0t"][:, :], start=True, stop=True)\
                  .then_inc(s_tp, 1)
                ln_tensor(nc, pe, m, q, [pG[:, 0, :], pG[:, 1, :]])
                pe.wait_ge(q.xTs, 2)
                for b in range(B):
                    last = nc.tensor.matmul(pW[0:T, b * NE:(b + 1) * NE], m.XNT[:, b * T:(b + 1) * T],
                                            w["f0r"][:, :], start=True, stop=True)
                last.then_inc(s_lg, 1)

                def up(n):
                    e, h = n // 2, n % 2
                    if n >= 2:
                        pe.wait_ge(s_h, n - 1)
                    x = m.XNT[:, h * HALF:(h + 1) * HALF]
                    nc.tensor.matmul(pG[:, n % 2, 0:HALF], w["f0g"][:, e, :], x, start=True, stop=True)
                    nc.tensor.matmul(pU[:, n % 2, 0:HALF], w["f0u"][:, e, :], x, start=True, stop=True)\
                      .then_inc(s_g, 1)

                def down(n):
                    pe.wait_ge(s_h, n + 1)
                    if n == 0:
                        pe.wait_ge(s_it, 1)
                    if n >= 3:
                        pe.wait_ge(s_x, n - 2)
                    for i in range(HB):
                        last = nc.tensor.matmul(pY[0:T, n % 3, i * D:(i + 1) * D], H[:, n, i * T:(i + 1) * T],
                                                w["f0d"][:, n // 2, :], start=True, stop=True)
                    last.then_inc(s_y, 1)

                for n in range(N - 2):
                    up(n)
                down(0)
                up(N - 2)
                down(1)
                up(N - 1)
                for n in range(2, N):
                    down(n)



def attention_regrouped(nc, m):
    name = "L1a"
    w = m.w
    R = T // 4
    FL = T * 32
    RC = 5
    N = R // RC
    with ExitStack() as ctx:
        s = Stage(nc, ctx, name)
        q = ln_sems(s)
        scr = nc.dram_tensor("regroup_in", (32, 4, FL), F32).ap()
        scr2 = nc.dram_tensor("regroup_out", (32, FL), F32).ap()
        free = m.CT[:, :, :].rearrange("p b k -> p (b k)")
        QK = free[0:T, 0:B * 512].rearrange("t (b c) -> t b c", b=B)
        STEP = RC * NH * NH
        S1 = free[:, B * 512:B * 512 + 3 * STEP].rearrange("p (u r h k) -> p u r h k", u=3, r=RC, h=NH)
        S2 = free[:, B * 512 + 3 * STEP:B * 512 + 5 * STEP].rearrange("p (u r h k) -> p u r h k", u=2, r=RC, h=NH)
        L = s.sb("L", [128, 4, NH, R, 2])
        mx = s.sb("mx", [128, 2, RC, NH])
        den = s.sb("den", [128, 2, RC, NH])
        OA = s.sb("OA", [128, 2, 2, RC, NH])
        O = s.sb("O", [128, NH, R, 2])
        OX = s.sb("OX", [T, B, D])
        pT = s.ps("pT", [128, 2, 512])
        pQ = s.ps("pQ", [128, 4, 512])
        pY = s.ps("pY", [128, 2, 512])
        vch, gch = s.sem("vector_own"), s.sem("gpsimd_own")
        s_q, s_qs = s.sem("qkvw_psum"), s.sem("qkvw_sbuf")
        s_d, s_l = s.sem("in_dram"), s.sem("regrouped")
        s_p0, s_p1, s_sc = s.sem("products_d1"), s.sem("products_d0"), s.sem("less_max")
        s_e, s_pv, s_dn = s.sem("exps"), s.sem("weighted_d1"), s.sem("used")
        s_sum, s_pv0, s_s2 = s.sem("sums"), s.sem("weighted_d0"), s.sem("summed_d1")
        s_o, s_od = s.sem("out_sbuf"), s.sem("out_in_dram")
        s_ox = [s.sem("out_token_major_0"), s.sem("out_token_major_1")]
        s_t, s_ts, s_y = s.sem("outT_psum"), s.sem("outT_sbuf"), s.sem("y_psum")

        def at(i, n, d):
            return L[:, i, :, n * RC:(n + 1) * RC, d].rearrange("p h r -> p r h")

        def rows(ap):
            return ap.unsqueeze(3).broadcast_to((128, RC, NH, NH))

        def cols(ap):
            return ap.unsqueeze(2).broadcast_to((128, RC, NH, NH))

        with nc.Block(no_gpsimd_drain=True) as block:

            @block.sync
            def _(sp):
                for b in range(B):
                    sp.wait_ge(s_qs, b + 1)
                    sp.dma_start(scr[4 * b:4 * b + 4].rearrange("i j (t c) -> t (i j) c", c=32),
                                 QK[:, b, :].rearrange("t (k c) -> t k c", c=32)).then_inc(s_d, 16)
                sp.wait_ge(s_d, 16 * B)
                for rq in range(4):
                    sp.dma_start(L[rq * 32:(rq + 1) * 32, :, :, :, :].rearrange("n j h r d -> n (j h) (r d)"),
                                 scr.rearrange("n j (h x) -> n (j h) x", x=2 * T)[:, :, 2 * R * rq:2 * R * (rq + 1)])\
                      .then_inc(s_l, 16)
                sp.wait_ge(s_o, 1)
                for rq in range(4):
                    sp.dma_start(scr2.rearrange("n (h x) -> n h x", x=2 * T)[:, :, 2 * R * rq:2 * R * (rq + 1)],
                                 O[rq * 32:(rq + 1) * 32, :, :, :].rearrange("n h r d -> n h (r d)"))\
                      .then_inc(s_od, 16)
                sp.wait_ge(s_od, 64)
                for b in range(B):
                    first = (b % 2) * HB
                    sp.dma_start(OX[:, b, :], scr2.rearrange("(b i) (t d) -> i b t d", i=4, d=D)
                                 [b // 2, first:first + HB]).then_inc(s_ox[b // HB], 16)

            @block.gpsimd
            def _(pool):
                ln_gpsimd(nc, pool, m, q)
                pool.wait_ge(s_l, 64)

                def products(n):
                    if n >= 2:
                        pool.wait_ge(s_s2, n - 1)
                    nc.gpsimd.tensor_tensor(S2[:, n % 2], rows(at(0, n, 1)), cols(at(1, n, 1)), ALU.mult)\
                      .then_inc(s_p0, 1)

                products(0)
                for n in range(N):
                    if n + 1 < N:
                        products(n + 1)
                    pool.wait_ge(s_e, n + 1)
                    nc.gpsimd.tensor_tensor(S2[:, n % 2], S1[:, n % 3], cols(at(2, n, 1)), ALU.mult)\
                      .then_inc(s_pv, 1)
                    pool.wait_ge(s_sum, n + 1)
                    pool.wait_ge(s_pv, n + 1)
                    nc.gpsimd.tensor_tensor(S1[:, n % 3], S1[:, n % 3], cols(at(2, n, 0)), ALU.mult)\
                      .then_inc(s_pv0, 1)

            @block.vector
            def _(dve):
                chain = Chain(dve, vch)
                ln_vector(nc, dve, chain, m, q)
                dve.wait_ge(s_l, 64)

                def products(n):
                    nc.vector.tensor_tensor(S1[:, n % 3], rows(at(0, n, 0)), cols(at(1, n, 0)), ALU.mult)\
                      .then_inc(s_p1, 1)

                def scores(n):
                    dve.wait_ge(s_p1, n + 1)
                    dve.wait_ge(s_p0, n + 1)
                    chain.then(nc.vector.tensor_tensor(S1[:, n % 3], S1[:, n % 3], S2[:, n % 2], ALU.add))
                    chain.then(nc.vector.tensor_reduce(mx[:, n % 2], S1[:, n % 3], AX.X, ALU.max))
                    nc.vector.tensor_tensor(S1[:, n % 3], S1[:, n % 3], rows(mx[:, n % 2]),
                                            ALU.subtract).then_inc(s_sc, 1)

                products(0)
                scores(0)
                products(1)
                for n in range(N):
                    if n + 1 < N:
                        scores(n + 1)
                    dve.wait_ge(s_e, n + 1)
                    nc.vector.tensor_reduce(den[:, n % 2], S1[:, n % 3], AX.X, ALU.add).then_inc(s_sum, 1)
                    dve.wait_ge(s_sum, n + 1)
                    chain.then(nc.vector.reciprocal(den[:, n % 2], den[:, n % 2]))
                    dve.wait_ge(s_pv, n + 1)
                    nc.vector.tensor_reduce(OA[:, n % 2, 1], S2[:, n % 2], AX.X, ALU.add).then_inc(s_s2, 1)
                    if n + 2 < N:
                        products(n + 2)
                    dve.wait_ge(s_pv0, n + 1)
                    chain.then(nc.vector.tensor_reduce(OA[:, n % 2, 0], S1[:, n % 3], AX.X, ALU.add))
                    dve.wait_ge(s_s2, n + 1)
                    nc.vector.tensor_tensor(OA[:, n % 2, 0], OA[:, n % 2, 0], den[:, n % 2], ALU.mult)
                    chain.then(nc.vector.tensor_tensor(OA[:, n % 2, 1], OA[:, n % 2, 1], den[:, n % 2], ALU.mult))
                    for d in range(2):
                        last = nc.vector.tensor_tensor(
                            O[:, :, n * RC:(n + 1) * RC, d].rearrange("p h r -> p r h"), OA[:, n % 2, d],
                            at(3, n, d), ALU.mult)
                    last.then_inc(s_dn, 1)
                dve.wait_ge(s_dn, N)
                nc.vector.memset(mx[:, 0], 0.0).then_inc(s_o, 1)
                for h in range(2):
                    dve.wait_ge(s_y, h + 1)
                    nc.vector.tensor_tensor(m.X[:, h * HB:(h + 1) * HB, :], m.X[:, h * HB:(h + 1) * HB, :],
                                            pY[0:T, h, :].rearrange("p (b d) -> p b d", d=D), ALU.add)

            @block.scalar
            def _(act):
                ln_scalar(nc, act, m, q, [pT[:, 0, :], pT[:, 1, :]])
                for b in range(B):
                    act.wait_ge(s_q, b + 1)
                    nc.scalar.copy(QK[:, b, :], pQ[0:T, b % 4, :]).then_inc(s_qs, 1)
                for n in range(N):
                    act.wait_ge(s_sc, n + 1)
                    nc.scalar.activation(S1[:, n % 3], S1[:, n % 3], ACT.Exp, scale=2.0 ** -0.5).then_inc(s_e, 1)
                for h in range(2):
                    act.wait_ge(s_t, h + 1)
                    nc.scalar.copy(m.XNT[:, h * HALF:(h + 1) * HALF], pT[:, h, 0:HALF]).then_inc(s_ts, 1)

            @block.tensor
            def _(pe):
                ln_tensor(nc, pe, m, q, [pT[:, 0, :], pT[:, 1, :]])
                pe.wait_ge(m.loaded[name], m.load_total[name])
                pe.wait_ge(q.xTs, 2)
                for b in range(B):
                    if b >= 4:
                        pe.wait_ge(s_qs, b - 3)
                    nc.tensor.matmul(pQ[0:T, b % 4, :], m.XNT[:, b * T:(b + 1) * T], w["a1w"][:, :],
                                     start=True, stop=True).then_inc(s_q, 1)
                pe.wait_ge(s_qs, B)
                for h in range(2):
                    pe.wait_ge(s_ox[h], 16 * HB)
                    for i in range(HB):
                        last = nc.tensor.transpose(pT[:, h, i * T:(i + 1) * T], OX[:, h * HB + i, :],
                                                   m.ident[0:T, 0:T])
                    last.then_inc(s_t, 1)
                for h in range(2):
                    pe.wait_ge(s_ts, h + 1)
                    for i in range(HB):
                        b = h * HB + i
                        last = nc.tensor.matmul(pY[0:T, h, i * D:(i + 1) * D], m.XNT[:, b * T:(b + 1) * T],
                                                w["a1o"][:, :], start=True, stop=True)
                    last.then_inc(s_y, 1)



def attention_wide(nc, m):
    name = "L2x"
    w = m.w
    C = SC // 4
    SCALE = float(D) ** -0.5
    with ExitStack() as ctx:
        s = Stage(nc, ctx, name)
        q = ln_sems(s)
        Mqk = s.sb("Mqk", [128, 128])
        WvT = s.sb("WvT", [128, 128])
        QS = s.sb("QS", [128, TOK])
        nmx = s.sb("nmx", [T, 2])
        E = s.sb("E", [T, 2, SC])
        sm = s.sb("sm", [T, 4])
        ET = s.sb("ET", [128, NKT, T])
        U = s.sb("U", [T, D])
        UT = s.sb("UT", [128, T])
        pS = s.ps("pS", [128, 4, 512])
        pE = s.ps("pE", [128, 2, 512])
        pY = s.ps("pY", [128, 512])
        pO = s.ps("pO", [128, 512])
        vch = s.sem("vector_own")
        s_w, s_ws = s.sem("weights_psum"), s.sem("weights_ready")
        s_q, s_qs = s.sem("q_psum"), s.sem("q_sbuf")
        s_s, s_m, s_e = s.sem("scores"), s.sem("maximum"), s.sem("exps")
        s_t, s_tc, s_tc2 = s.sem("expsT_psum"), s.sem("expsT_vector"), s.sem("expsT_scalar")
        s_u, s_us = s.sem("sums_psum"), s.sem("sums_scaled")
        s_ut, s_uts, s_y, s_x = s.sem("sumsT_psum"), s.sem("sumsT_sbuf"), s.sem("y_psum"), s.sem("added")

        with nc.Block(no_gpsimd_drain=True) as block:

            @block.gpsimd
            def _(pool):
                ln_gpsimd(nc, pool, m, q)

            @block.vector
            def _(dve):
                chain = Chain(dve, vch)
                dve.wait_ge(s_w, 1)
                nc.vector.tensor_copy(Mqk[:, :], pY[:, 0:128])
                nc.vector.tensor_copy(WvT[:, :], pY[:, 128:256]).then_inc(s_ws, 1)
                ln_vector(nc, dve, chain, m, q)

                def maximum(b):
                    dve.wait_ge(s_s, b + 1)
                    if b >= 2:
                        dve.wait_ge(s_e, b - 1)
                    chain.then(nc.vector.tensor_reduce(nmx[:, b % 2:b % 2 + 1], pS[0:T, :, 0:C], AX.XY,
                                                       ALU.max, negate=True))
                    nc.vector.tensor_scalar(nmx[:, b % 2:b % 2 + 1], nmx[:, b % 2:b % 2 + 1], SCALE, None,
                                            ALU.mult).then_inc(s_m, 1)

                def expsT(b, g):
                    i = 3 * b + g
                    dve.wait_ge(s_t, i + 1)
                    src = pE[:, i % 2, :]
                    if g == 0:
                        if b >= 1:
                            dve.wait_ge(s_u, b)
                        nc.vector.tensor_copy(ET[:, 0:4, :], src[:, 0:4 * T].rearrange("p (k t) -> p k t", t=T))\
                          .then_inc(s_tc, 1)
                    else:
                        nc.vector.tensor_copy(ET[:, 8:11, :], src[:, 0:3 * T].rearrange("p (k t) -> p k t", t=T))
                        nc.vector.tensor_copy(ET[0:TAIL, 11, :], src[0:TAIL, 3 * T:4 * T]).then_inc(s_tc, 1)

                def add(b):
                    dve.wait_ge(s_y, b + 1)
                    nc.vector.tensor_tensor(m.X[:, b, :], m.X[:, b, :], pY[0:T, 128:128 + D], ALU.add)\
                      .then_inc(s_x, 1)

                maximum(0)
                for b in range(B):
                    expsT(b, 0)
                    expsT(b, 2)
                    if b + 1 < B:
                        maximum(b + 1)
                    if b >= 1:
                        add(b - 1)
                    chain.then(nc.vector.reciprocal(sm[:, 2:3], sm[:, b % 2:b % 2 + 1]))
                    dve.wait_ge(s_u, b + 1)
                    nc.vector.tensor_scalar(U[:, :], pO[0:T, 0:D], sm[:, 2:3], None, ALU.mult).then_inc(s_us, 1)
                add(B - 1)

            @block.scalar
            def _(act):
                ln_scalar(nc, act, m, q, [pE[:, 0, :], pE[:, 1, :]])
                for h in range(2):
                    act.wait_ge(s_q, h + 1)
                    nc.scalar.copy(QS[:, h * HALF:(h + 1) * HALF], pS[:, h, 0:HALF]).then_inc(s_qs, 1)

                def exps(b):
                    act.wait_ge(s_m, b + 1)
                    if b >= 2:
                        act.wait_ge(s_us, b - 1)
                        act.wait_ge(s_t, 3 * (b - 1))
                    nc.scalar.activation(E[:, b % 2, :].rearrange("p (c k) -> p c k", k=C), pS[0:T, :, 0:C],
                                         ACT.Exp, bias=nmx[:, b % 2:b % 2 + 1], scale=SCALE,
                                         accum_out=sm[:, b % 2:b % 2 + 1]).then_inc(s_e, 1)

                def sumsT(b):
                    act.wait_ge(s_ut, b + 1)
                    nc.scalar.copy(UT[:, :], pY[:, 0:T]).then_inc(s_uts, 1)

                exps(0)
                for b in range(B):
                    act.wait_ge(s_t, 3 * b + 2)
                    if b >= 1:
                        act.wait_ge(s_u, b)
                    nc.scalar.copy(ET[:, 4:8, :], pE[:, (3 * b + 1) % 2, 0:4 * T]
                                   .rearrange("p (k t) -> p k t", t=T)).then_inc(s_tc2, 1)
                    if b >= 1:
                        sumsT(b - 1)
                    if b + 1 < B:
                        exps(b + 1)
                sumsT(B - 1)

            @block.tensor
            def _(pe):
                pe.wait_ge(m.loaded[name], m.load_total[name])
                nc.tensor.matmul(pY[:, 0:128], w["x2q"][:, :], w["x2k"][:, :], start=True, stop=True)
                nc.tensor.transpose(pY[:, 128:256], w["x2v"][:, :], m.ident[:, :]).then_inc(s_w, 1)
                ln_tensor(nc, pe, m, q, [pE[:, 0, :], pE[:, 1, :]])
                pe.wait_ge(s_ws, 1)
                for h in range(2):
                    pe.wait_ge(q.xTs, h + 1)
                    nc.tensor.matmul(pS[:, h, 0:HALF], Mqk[:, :], m.XNT[:, h * HALF:(h + 1) * HALF],
                                     start=True, stop=True).then_inc(s_q, 1)
                pe.wait_ge(s_qs, 2)

                def scores(b):
                    if b >= 1:
                        pe.wait_ge(s_e, b)
                    for c in range(4):
                        last = nc.tensor.matmul(pS[0:T, c, 0:C], QS[:, b * T:(b + 1) * T],
                                                m.CT[:, b, c * C:(c + 1) * C], start=True, stop=True)
                    last.then_inc(s_s, 1)

                def turn_exps(b, g):
                    i = 3 * b + g
                    if i >= 2:
                        bb, gg = (i - 2) // 3, (i - 2) % 3
                        if gg == 1:
                            pe.wait_ge(s_tc2, bb + 1)
                        else:
                            pe.wait_ge(s_tc, 2 * bb + (1 if gg == 0 else 2))
                    for k in range(4 * g, 4 * g + 4):
                        last = nc.tensor.transpose(pE[0:TILES[k], i % 2, (k % 4) * T:(k % 4 + 1) * T],
                                                   E[:, b % 2, k * 128:k * 128 + TILES[k]],
                                                   m.ident[0:T, 0:T])
                    last.then_inc(s_t, 1)

                def turn_sums(b):
                    pe.wait_ge(s_us, b + 1)
                    if b >= 1:
                        pe.wait_ge(s_x, b)
                    nc.tensor.transpose(pY[:, 0:T], U[:, :], m.ident[0:T, 0:T]).then_inc(s_ut, 1)

                def project(b):
                    pe.wait_ge(s_uts, b + 1)
                    nc.tensor.matmul(pY[0:T, 128:128 + D], UT[:, :], WvT[:, :], start=True, stop=True)\
                      .then_inc(s_y, 1)

                scores(0)
                for b in range(B):
                    pe.wait_ge(s_e, b + 1)
                    turn_exps(b, 0)
                    turn_exps(b, 1)
                    if b >= 1:
                        turn_sums(b - 1)
                    turn_exps(b, 2)
                    if b + 1 < B:
                        scores(b + 1)
                    if b >= 1:
                        project(b - 1)
                    pe.wait_ge(s_tc, 2 * b + 2)
                    pe.wait_ge(s_tc2, b + 1)
                    for k in range(NKT):
                        last = nc.tensor.matmul(pO[0:T, 0:D], ET[0:TILES[k], k, :],
                                                m.ctx_tm[0:TILES[k], b, k, 0:D],
                                                start=(k == 0), stop=(k == NKT - 1))
                    last.then_inc(s_u, 1)
                turn_sums(B - 1)
                project(B - 1)



def two_norms_vector(nc, dve, chain, m, q, q2):
    for b in range(B):
        last = nc.vector.bn_stats(m.stats[:, b, :], m.X[:, b, :])
    chain.then(last)
    for b in range(B):
        last = nc.vector.bn_aggr(m.mv[:, b, :], m.stats[:, b, :])
    chain.then(last)
    nc.vector.tensor_scalar(m.veps[:, 0, :], m.mv[:, :, 1], LN_EPS, None, ALU.add)
    nc.vector.tensor_scalar(m.veps[:, 1, :], m.mv[:, :, 1], 1.0 + LN_EPS, LN_EPS * LN_EPS,
                            ALU.mult, ALU.add).then_inc(q.var, 1)
    dve.wait_ge(q.rstd, 1)
    for i, sem, dst in ((1, q2.norm, m.XN2), (0, q.norm, m.XN)):
        for b in range(B):
            nc.vector.tensor_scalar(dst[:, b, :], m.X[:, b, :], m.mv[:, b, 0:1], m.rstd[:, i, b:b + 1],
                                    ALU.subtract, ALU.mult).then_inc(sem, 1)


def two_norms_gpsimd(nc, pool, m, q):
    pool.wait_ge(q.var, 1)
    nc.gpsimd.tensor_tensor(m.rstd[:, :, :], m.veps[:, :, :],
                            m.neg_half[0:T, 0:2 * B].rearrange("t (i b) -> t i b", i=2),
                            ALU.pow).then_inc(q.rstd, 1)


def add_psum(nc, dve, chain, m, q, h, out):
    dve.wait_ge(q.norm, B)
    x, xn = m.X[:, h * HB:(h + 1) * HB, :], m.XN[:, h * HB:(h + 1) * HB, :]
    chain.then(nc.vector.tensor_tensor(x, x, xn, ALU.add))
    return nc.vector.tensor_tensor(x, x, out.rearrange("p (b d) -> p b d", d=D), ALU.add)



def attention_fixed_keys(nc, m):
    name = "L2a"
    w = m.w
    N = 32
    W = 32
    with ExitStack() as ctx:
        s = Stage(nc, ctx, name)
        q, q2 = ln_sems(s), ln_sems(s, "ln2")
        wf4 = s.sb("wf4", [128, 4, 4, W])
        KF = s.sb("KF", [128, 4, 4, 128])
        OS = s.sb("OS", [128, 2, HALF])
        VF = s.sb("VF", [128, 128])
        RL = s.sb("RL", [128, 4, HALF])
        P = s.sb("P", [128, 8, HALF])
        pT = s.ps("pT", [128, 2, 512])
        pS = s.ps("pS", [128, 4, 512])
        pY = s.ps("pY", [128, 2, 512])
        vch = s.sem("vector_own")
        s_w4, s_wt, s_ws = s.sem("keys_repeated"), s.sem("weights_transposed"), s.sem("weights_ready")
        s_s, s_r, s_p, s_y = s.sem("scores"), s.sem("relu"), s.sem("squares"), s.sem("out")

        s_o, s_ot = s.sem("out_sbuf"), s.sem("out_token_major")

        with nc.Block(no_gpsimd_drain=True) as block:

            @block.gpsimd
            def _(pool):
                two_norms_gpsimd(nc, pool, m, q)

            @block.vector
            def _(dve):
                chain = Chain(dve, vch)
                dve.wait_ge(m.loaded[name], m.load_total[name])
                for h in range(4):
                    last = nc.vector.tensor_copy(wf4[:, :, h, :], w["a2f"][:, :].rearrange("c (j d) -> c j d", d=W))
                last.then_inc(s_w4, 1)
                chain.then(nc.vector.memset(KF[:], 0.0))
                two_norms_vector(nc, dve, chain, m, q, q2)
                dve.wait_ge(s_wt, 1)
                for h in range(4):
                    r = slice(W * h, W * (h + 1))
                    nc.vector.tensor_copy(KF[r, h, :, :], pS[r, 0, :].rearrange("p (j c) -> p j c", c=128))
                nc.vector.tensor_copy(VF[:, :], pS[:, 1, 0:128]).then_inc(s_ws, 1)
                for n in range(N):
                    dve.wait_ge(s_r, n + 1)
                    if n >= 8:
                        dve.wait_ge(s_y, n // 4 - 1)
                    nc.vector.tensor_tensor(P[:, n % 8, :], RL[:, n % 4, :], pS[:, n % 4, 0:HALF],
                                            ALU.mult).then_inc(s_p, 1)
                for h in range(2):
                    dve.wait_ge(s_ot, h + 1)
                    add_psum(nc, dve, chain, m, q, h, pT[0:T, h, :])

            @block.scalar
            def _(act):
                ln_scalar(nc, act, m, q2, [pT[:, 0, :], pT[:, 1, :]], (w["a2g"], w["a2b"]))

                def out(h):
                    act.wait_ge(s_y, 4 * (h + 1))
                    nc.scalar.copy(OS[:, h, :], pY[:, h, 0:HALF]).then_inc(s_o, 1)

                for n in range(N):
                    act.wait_ge(s_s, n + 1)
                    if n >= 4:
                        act.wait_ge(s_p, n - 3)
                    nc.scalar.activation(RL[:, n % 4, :], pS[:, n % 4, 0:HALF], ACT.Relu).then_inc(s_r, 1)
                    if n == N // 2 + 4:
                        out(0)
                out(1)

            @block.tensor
            def _(pe):
                pe.wait_ge(s_w4, 1)
                for j in range(4):
                    nc.tensor.transpose(pS[:, 0, j * 128:(j + 1) * 128], wf4[:, j, :, :], m.ident[:, :])
                nc.tensor.transpose(pS[:, 1, 0:128], w["a2p"][:, :], m.ident[:, :]).then_inc(s_wt, 1)
                ln_tensor(nc, pe, m, q2, [pT[:, 0, :], pT[:, 1, :]], m.XN2)
                pe.wait_ge(s_ws, 1)
                pe.wait_ge(q2.xTs, 2)

                def scores(n):
                    half, j, h = n // 16, n // 4 % 4, n % 4
                    if n >= 4:
                        pe.wait_ge(s_p, n - 3)
                    nc.tensor.matmul(pS[:, n % 4, 0:HALF], KF[:, h, j, :],
                                     m.XNT[:, half * HALF:(half + 1) * HALF],
                                     start=True, stop=True).then_inc(s_s, 1)

                def token_major(half):
                    pe.wait_ge(s_o, half + 1)
                    for i in range(HB):
                        last = nc.tensor.transpose(pT[0:T, half, i * D:(i + 1) * D],
                                                   OS[:, half, i * T:(i + 1) * T], m.ident[:, :])
                    last.then_inc(s_ot, 1)

                for n in range(4):
                    scores(n)
                for g in range(N // 4):
                    for n in range(4 * g + 4, min(4 * g + 8, N)):
                        scores(n)
                    half, j = g // 4, g % 4
                    pe.wait_ge(s_p, 4 * g + 4)
                    for h in range(4):
                        last = nc.tensor.matmul(pY[W * h:W * (h + 1), half, 0:HALF], VF[:, W * j:W * (j + 1)],
                                                P[:, (4 * g + h) % 8, :], start=(j == 0), stop=(j == 3),
                                                skip_group_check=True)
                    last.then_inc(s_y, 1)
                    if g == N // 8 + 1:
                        token_major(0)
                token_major(1)



def mixture_top1(nc, m):
    name = "L2f"
    w = m.w
    CAPACITY = 256
    IT = 4
    N = 2 * NE
    with ExitStack() as ctx:
        s = Stage(nc, ctx, name)
        q, q2 = ln_sems(s), ln_sems(s, "ln2")
        gwT = s.sb("gwT", [128, NE])
        lg, eq, oh, pre, rk = [s.sb(f"r{i}", [T, B, NE]) for i in range(5)]
        top, best, wt, keep = [s.sb(f"s{i}", [T, B]) for i in range(4)]
        OHT = s.sb("OHT", [NE, TOK], BF16)
        SEL = s.sb("SEL", [NE, NE, 128], BF16)
        YT = s.sb("YT", [128, 2, HALF])
        XM = s.sb("XM", [128, 2, HALF])
        H = s.sb("H", [128, 2, IT, HALF])
        YW = s.sb("YW", [T, HB, D])
        pC = s.ps("pC", [128, 2, 512])
        pU = s.ps("pU", [128, 4, 512])
        pY = s.ps("pY", [128, 2, 512])
        vch = s.sem("vector_own")
        s_wt, s_ws, s_lg, s_oh = s.sem("router_transposed"), s.sem("router_ready"), s.sem("logits"), s.sem("one_hot")
        s_dl, s_ex, s_rk = s.sem("logits_less_max"), s.sem("exp_of_logits"), s.sem("ranks")
        s_ot, s_ots = s.sem("one_hotT_psum"), s.sem("one_hotT_sbuf")
        s_c, s_xm = s.sem("mask_spread"), s.sem("tokens_masked")
        s_yt, s_yy = s.sem("out_sbuf"), s.sem("out_token_major")
        s_u, s_h, s_y = s.sem("up"), s.sem("gelu"), s.sem("out")

        free = m.ctx_tm[:, :, :, :].rearrange("p b k d -> p (b k d)")
        wi = free[:, 0:NE * 512].rearrange("p (e i) -> p e i", e=NE)
        wo = free[:, NE * 512:2 * NE * 512].rearrange("p (e i d) -> p e i d", e=NE, d=D)
        s_wi, s_wo = s.sem("wi_loaded"), s.sem("wo_loaded")

        with nc.Block(no_gpsimd_drain=True) as block:

            @block.sync
            def _(sp):
                for b in range(B):
                    sp.wait_ge(m.ctx_loaded[b], 32)
                for e in range(0, NE, 2):
                    sp.dma_start(wi[:, e:e + 2, :], m.a["L2_ffn_wi"][e:e + 2].rearrange("e d i -> d e i"))\
                      .then_inc(s_wi, 16)
                    sp.dma_start(wo[:, e:e + 2, :, :].rearrange("p e i d -> p (e i) d"),
                                 m.a["L2_ffn_wo"][e:e + 2].rearrange("e (i p) d -> p (e i) d", p=128))\
                      .then_inc(s_wo, 16)

            @block.gpsimd
            def _(pool):
                two_norms_gpsimd(nc, pool, m, q)

            @block.vector
            def _(dve):
                chain = Chain(dve, vch)
                dve.wait_ge(s_wt, 1)
                nc.vector.tensor_copy(gwT[:, :], pU[:, 0, 0:NE]).then_inc(s_ws, 1)
                nc.vector.tensor_copy(SEL[:, :, :], m.sel[:, :, :])
                two_norms_vector(nc, dve, chain, m, q, q2)
                dve.wait_ge(s_lg, 1)
                chain.then(nc.vector.tensor_copy(lg[:, :, :], pU[0:T, 1, 0:B * NE].rearrange("p (b e) -> p b e", e=NE)))
                first_largest(nc, chain, m, lg[:, :, :], top[:, :], eq[:, :, :], best[:, :], oh[:, :, :])
                chain.then(nc.vector.memset(pre[:, 0, :], 0.0))
                for b in range(1, B):
                    ins = nc.vector.tensor_tensor(pre[:, b, :], pre[:, b - 1, :], oh[:, b - 1, :], ALU.add)
                    if b < B - 1:
                        chain.then(ins)
                ins.then_inc(s_oh, 1)
                nc.vector.tensor_tensor(lg[:, :, :], lg[:, :, :], top[:, :].unsqueeze(2).broadcast_to((T, B, NE)),
                                        ALU.subtract).then_inc(s_dl, 1)
                dve.wait_ge(s_ot, 1)
                nc.vector.tensor_copy(OHT[:, 0:HALF], pC[0:NE, 0, 0:HALF])
                nc.vector.tensor_copy(OHT[:, HALF:TOK], pC[0:NE, 1, 0:HALF]).then_inc(s_ots, 1)
                dve.wait_ge(s_ex, 1)
                chain.then(nc.vector.tensor_reduce(wt[:, :], eq[:, :, :], AX.X, ALU.add))
                chain.then(nc.vector.reciprocal(wt[:, :], wt[:, :]))
                dve.wait_ge(s_rk, 1)
                chain.then(nc.vector.tensor_tensor(
                    rk[:, :, :], pU[0:T, 2, 0:B * NE].rearrange("p (b e) -> p b e", e=NE), oh[:, :, :], ALU.mult))
                chain.then(nc.vector.tensor_reduce(keep[:, :], rk[:, :, :], AX.X, ALU.add))
                chain.then(nc.vector.tensor_scalar(keep[:, :], keep[:, :], float(CAPACITY), None, ALU.is_lt))
                chain.then(nc.vector.tensor_tensor(wt[:, :], wt[:, :], keep[:, :], ALU.mult))
                for n in range(N):
                    h = n % 2
                    dve.wait_ge(s_c, n + 1)
                    if n >= 2:
                        dve.wait_ge(s_u, IT * (n - 1))
                    nc.vector.tensor_tensor(XM[:, n % 2, :], m.XNT[:, h * HALF:(h + 1) * HALF],
                                            pC[:, n % 2, 0:HALF], ALU.mult).then_inc(s_xm, 1)
                for h in range(2):
                    dve.wait_ge(s_yy, h + 1)
                    x, xn = m.X[:, h * HB:(h + 1) * HB, :], m.XN[:, h * HB:(h + 1) * HB, :]
                    nc.vector.tensor_tensor(x, x, xn, ALU.add)
                    chain.then(nc.vector.tensor_tensor(
                        YW[:, :, :], pC[0:T, h, :].rearrange("p (b d) -> p b d", d=D),
                        wt[:, h * HB:(h + 1) * HB].unsqueeze(2).broadcast_to((T, HB, D)), ALU.mult))
                    chain.then(nc.vector.tensor_tensor(x, x, YW[:, :, :], ALU.add))

            @block.scalar
            def _(act):
                act.wait_ge(m.loaded[name], m.load_total[name])
                ln_scalar(nc, act, m, q2, [pC[:, 0, :], pC[:, 1, :]], (w["f2g"], w["f2b"]))
                act.wait_ge(s_dl, 1)
                nc.scalar.activation(eq[:, :, :], lg[:, :, :], ACT.Exp).then_inc(s_ex, 1)
                for u in range(N * IT):
                    act.wait_ge(s_u, u + 1)
                    n = u // IT
                    if n >= 2:
                        act.wait_ge(s_y, n - 1)
                    nc.scalar.activation(H[:, n % 2, u % IT, :], pU[:, u % 4, 0:HALF], ACT.Gelu).then_inc(s_h, 1)
                for h in range(2):
                    act.wait_ge(s_y, N - 1 + h)
                    nc.scalar.copy(YT[:, h, :], pY[:, h, 0:HALF]).then_inc(s_yt, 1)

            @block.tensor
            def _(pe):
                pe.wait_ge(m.loaded[name], m.load_total[name])
                nc.tensor.transpose(pU[:, 0, 0:NE], w["f2r"][:, :], m.ident[0:NE, 0:NE]).then_inc(s_wt, 1)
                ln_tensor(nc, pe, m, q2, [pC[:, 0, :], pC[:, 1, :]], m.XN2)
                pe.wait_ge(s_ws, 1)
                pe.wait_ge(q2.xTs, 2)
                for b in range(B):
                    last = nc.tensor.matmul(pU[0:T, 1, b * NE:(b + 1) * NE], m.XNT[:, b * T:(b + 1) * T],
                                            gwT[:, :], start=True, stop=True)
                last.then_inc(s_lg, 1)
                pe.wait_ge(s_oh, 1)
                for b in range(B):
                    last = nc.tensor.transpose(pC[0:NE, b // HB, (b % HB) * T:(b % HB + 1) * T], oh[:, b, :],
                                               m.ident[0:T, 0:T])
                last.then_inc(s_ot, 1)
                nc.tensor.matmul(pU[0:T, 2, 0:B * NE], m.before[:, :], oh[:, :, :].rearrange("p b e -> p (b e)"),
                                 start=True, stop=False)
                nc.tensor.matmul(pU[0:T, 2, 0:B * NE], m.ones[0:T, 0:T], pre[:, :, :].rearrange("p b e -> p (b e)"),
                                 start=False, stop=True).then_inc(s_rk, 1)
                pe.wait_ge(s_ots, 1)
                pe.wait_ge(s_ex, 1)

                def spread(n):
                    e, h = n // 2, n % 2
                    if n >= 2:
                        pe.wait_ge(s_xm, n - 1)
                    nc.tensor.matmul(pC[:, n % 2, 0:HALF], SEL[:, e, :], OHT[:, h * HALF:(h + 1) * HALF],
                                     start=True, stop=True).then_inc(s_c, 1)

                def up(n, i):
                    e = n // 2
                    u = n * IT + i
                    if i == 0:
                        pe.wait_ge(s_xm, n + 1)
                    if u >= 4:
                        pe.wait_ge(s_h, u - 3)
                    nc.tensor.matmul(pU[:, u % 4, 0:HALF], wi[:, e, i * 128:(i + 1) * 128],
                                     XM[:, n % 2, :], start=True, stop=True).then_inc(s_u, 1)

                def down(n, i):
                    e, h = n // 2, n % 2
                    pe.wait_ge(s_h, n * IT + i + 1)
                    last = nc.tensor.matmul(pY[:, h, 0:HALF], wo[:, e, i, :], H[:, n % 2, i, :],
                                            start=(e == 0 and i == 0), stop=(e == NE - 1 and i == IT - 1),
                                            skip_group_check=True)
                    if i == IT - 1:
                        last.then_inc(s_y, 1)

                pe.wait_ge(s_wi, 64)
                pe.wait_ge(s_wo, 64)
                spread(0)
                for n in range(N + 1):
                    if n + 1 < N:
                        spread(n + 1)
                    for i in range(IT):
                        if n < N:
                            up(n, i)
                        if n >= 1:
                            down(n - 1, i)
                for h in range(2):
                    pe.wait_ge(s_yt, h + 1)
                    pe.wait_ge(s_xm, N)
                    for k in range(HB):
                        last = nc.tensor.transpose(pC[0:T, h, k * D:(k + 1) * D], YT[:, h, k * T:(k + 1) * T],
                                                   m.ident[:, :])
                    last.then_inc(s_yy, 1)



LEVELS = [1, 2, 4, 8, 16, 32, 64]
TTT_LR = 0.01
DS = 64


def attention_delta_rule(nc, m):
    name = "L3a"
    w = m.w
    NL = len(LEVELS)
    with ExitStack() as ctx:
        s = Stage(nc, ctx, name)
        q, q2 = ln_sems(s), ln_sems(s, "ln2")
        wkT = s.sb("wkT", [128, DS])
        wqT = s.sb("wqT", [128, DS])
        wvT = s.sb("wvT", [128, D])
        KT = s.sb("KT", [DS, TOK])
        QT = s.sb("QT", [DS, TOK])
        V = s.sb("V", [T, B, D])
        LT = m.ctx_tm[0:T, :, :, :].rearrange("p b k d -> p (b k d)")[:, 0:B * NL * T]\
            .rearrange("p (b l t) -> p b l t", b=B, l=NL)
        SQ = s.sb("SQ", [T, B, T])
        X = s.sb("X", [T, 2, HB, T])
        XT = s.sb("XT", [T, 2, HB, T])
        TP = s.sb("TP", [T, 2, HB, T])
        U = s.sb("U", [T, 2, HB, D])
        pA = s.ps("pA", [128, 2, 512])
        pB = s.ps("pB", [128, 2, 512])
        pC = s.ps("pC", [128, 2, 512])
        pD = s.ps("pD", [128, 2, 512])
        vch = s.sem("vector_own")
        s_wt, s_ws = s.sem("weights_transposed"), s.sem("weights_ready")
        s_kq, s_kqs, s_v, s_vs = s.sem("k_q_psum"), s.sem("k_q_sbuf"), s.sem("v_psum"), s.sem("v_sbuf")
        s_kk, s_l = s.sem("k_k_and_k_q"), s.sem("masked")
        s_x0 = s.sem("first_inverse")
        s_t, s_tp = s.sem("l_x_psum"), s.sem("l_x_sbuf")
        s_xx, s_x = s.sem("x_l_x"), s.sem("inverse_updated")
        s_u, s_us, s_y = s.sem("updates_psum"), s.sem("updates_sbuf"), s.sem("y_psum")

        with nc.Block(no_gpsimd_drain=True) as block:

            @block.gpsimd
            def _(pool):
                two_norms_gpsimd(nc, pool, m, q)

            @block.vector
            def _(dve):
                chain = Chain(dve, vch)
                dve.wait_ge(s_wt, 1)
                nc.vector.tensor_copy(wkT[:, :], pB[:, 0, 0:DS])
                nc.vector.tensor_copy(wqT[:, :], pB[:, 0, 128:128 + DS])
                nc.vector.tensor_copy(wvT[:, :], pB[:, 0, 256:256 + D]).then_inc(s_ws, 1)
                two_norms_vector(nc, dve, chain, m, q, q2)
                for h in range(2):
                    dve.wait_ge(s_v, h + 1)
                    nc.vector.tensor_scalar(V[:, h * HB:(h + 1) * HB, :],
                                            pD[0:T, h, :].rearrange("p (b d) -> p b d", d=D), TTT_LR, None,
                                            ALU.mult).then_inc(s_vs, 1)
                for b in range(B):
                    dve.wait_ge(m.ctx_loaded[b], 32)
                for b in range(B):
                    dve.wait_ge(s_kk, b + 1)
                    kk = pC[0:T, b % 2, 0:T].unsqueeze(1)
                    chain.then(nc.vector.tensor_tensor(LT[:, b, :, :], kk.broadcast_to((T, NL, T)),
                                                       m.below[0:T, 1:NL + 1, 0:T], ALU.mult))
                    nc.vector.tensor_tensor(SQ[:, b, :], pC[0:T, b % 2, 128:128 + T], m.before[:, :], ALU.mult)
                    nc.vector.tensor_tensor(X[:, b // HB, b % HB, :], pC[0:T, b % 2, 0:T],
                                            m.below[0:T, 0, 0:T], ALU.mult)
                    chain.then(nc.vector.tensor_tensor(XT[:, b // HB, b % HB, :], m.ident[0:T, 0:T],
                                                       LT[:, b, 0, :], ALU.subtract))
                    nc.vector.tensor_tensor(X[:, b // HB, b % HB, :], m.ident[0:T, 0:T],
                                            X[:, b // HB, b % HB, :], ALU.subtract).then_inc(s_l, 1)
                for l in range(1, NL):
                    for h in range(2):
                        n = 2 * (l - 1) + h
                        dve.wait_ge(s_xx, n + 1)
                        XLX, XLXT = [p[0:T, h, 0:HALF].rearrange("p (b t) -> p b t", t=T) for p in (pB, pC)]
                        if l < NL - 1:
                            nc.vector.tensor_tensor(X[:, h], X[:, h], XLX, ALU.subtract)
                        nc.vector.tensor_tensor(XT[:, h], XT[:, h], XLXT, ALU.subtract).then_inc(s_x, 1)
                for h in range(2):
                    dve.wait_ge(s_y, h + 1)
                    add_psum(nc, dve, chain, m, q, h, pD[0:T, h, :])

            @block.scalar
            def _(act):
                act.wait_ge(m.loaded[name], m.load_total[name])
                ln_scalar(nc, act, m, q2, [pA[:, 0, :], pA[:, 1, :]], (w["a3g"], w["a3b"]))
                for h in range(2):
                    cols = slice(h * HALF, (h + 1) * HALF)
                    act.wait_ge(s_kq, 2 * h + 1)
                    nc.scalar.activation(KT[:, cols], pA[0:DS, h, 0:HALF], ACT.Identity,
                                         bias=w["a3bk"][:, 0:1]).then_inc(s_kqs, 1)
                    act.wait_ge(s_kq, 2 * h + 2)
                    nc.scalar.activation(QT[:, cols], pB[0:DS, h, 0:HALF], ACT.Identity,
                                         bias=w["a3bq"][:, 0:1]).then_inc(s_kqs, 1)
                for n in range(2 * (NL - 1)):
                    act.wait_ge(s_t, n + 1)
                    nc.scalar.copy(TP[:, n % 2], pA[0:T, n % 2, 0:HALF].rearrange("p (b t) -> p b t", t=T))\
                      .then_inc(s_tp, 1)
                for h in range(2):
                    act.wait_ge(s_u, h + 1)
                    nc.scalar.copy(U[:, h], pA[0:T, h, :].rearrange("p (b d) -> p b d", d=D)).then_inc(s_us, 1)

            @block.tensor
            def _(pe):
                pe.wait_ge(m.loaded[name], m.load_total[name])
                nc.tensor.transpose(pB[:, 0, 0:DS], w["a3k"][:, :], m.ident[0:DS, 0:DS])
                nc.tensor.transpose(pB[:, 0, 128:128 + DS], w["a3q"][:, :], m.ident[0:DS, 0:DS])
                nc.tensor.transpose(pB[:, 0, 256:256 + D], w["a3v"][:, :], m.ident[:, :]).then_inc(s_wt, 1)
                ln_tensor(nc, pe, m, q2, [pA[:, 0, :], pA[:, 1, :]], m.XN2)
                pe.wait_ge(s_ws, 1)
                for h in range(2):
                    pe.wait_ge(q2.xTs, 2)
                    x = m.XNT[:, h * HALF:(h + 1) * HALF]
                    nc.tensor.matmul(pA[0:DS, h, 0:HALF], wkT[:, :], x, start=True, stop=True).then_inc(s_kq, 1)
                    nc.tensor.matmul(pB[0:DS, h, 0:HALF], wqT[:, :], x, start=True, stop=True).then_inc(s_kq, 1)
                for h in range(2):
                    for i in range(HB):
                        b = h * HB + i
                        nc.tensor.matmul(pD[0:T, h, i * D:(i + 1) * D], m.XNT[:, b * T:(b + 1) * T], wvT[:, :],
                                         start=(i == 0), stop=False, skip_group_check=True)
                        last = nc.tensor.matmul(pD[0:T, h, i * D:(i + 1) * D], m.ones[0:1, 0:T],
                                                w["a3bv"][:, :], start=False, stop=True, skip_group_check=True)
                    last.then_inc(s_v, 1)
                pe.wait_ge(s_kqs, 4)
                for b in range(B):
                    if b >= 2:
                        pe.wait_ge(s_l, b - 1)
                    c = slice(b * T, (b + 1) * T)
                    nc.tensor.matmul(pC[0:T, b % 2, 0:T], KT[:, c], KT[:, c], start=True, stop=True)
                    nc.tensor.matmul(pC[0:T, b % 2, 128:128 + T], KT[:, c], QT[:, c], start=True, stop=True)\
                      .then_inc(s_kk, 1)
                pe.wait_ge(s_l, B)
                for l in range(1, NL):
                    for h in range(2):
                        n = 2 * (l - 1) + h
                        if n >= 2:
                            pe.wait_ge(s_x, n - 1)
                        for i in range(HB):
                            last = nc.tensor.matmul(pA[0:T, h, i * T:(i + 1) * T], LT[:, h * HB + i, l, :],
                                                    X[:, h, i, :], start=True, stop=True)
                        last.then_inc(s_t, 1)
                    for h in range(2):
                        n = 2 * (l - 1) + h
                        pe.wait_ge(s_tp, n + 1)
                        for i in range(HB):
                            if l < NL - 1:
                                nc.tensor.matmul(pB[0:T, h, i * T:(i + 1) * T], XT[:, h, i, :],
                                                 TP[:, h, i, :], start=True, stop=True)
                            last = nc.tensor.matmul(pC[0:T, h, i * T:(i + 1) * T], TP[:, h, i, :],
                                                    XT[:, h, i, :], start=True, stop=True)
                        last.then_inc(s_xx, 1)
                pe.wait_ge(s_vs, 2)
                for h in range(2):
                    pe.wait_ge(s_x, 2 * (NL - 2) + h + 1)
                    for i in range(HB):
                        last = nc.tensor.matmul(pA[0:T, h, i * D:(i + 1) * D], XT[:, h, i, :],
                                                V[:, h * HB + i, :], start=True, stop=True)
                    last.then_inc(s_u, 1)
                for h in range(2):
                    pe.wait_ge(s_us, h + 1)
                    for i in range(HB):
                        last = nc.tensor.matmul(pD[0:T, h, i * D:(i + 1) * D], SQ[:, h * HB + i, :],
                                                U[:, h, i, :], start=True, stop=True)
                    last.then_inc(s_y, 1)



def ffn_binary(nc, m):
    name = "L3f"
    w = m.w
    IT = 4
    N = 2 * IT
    with ExitStack() as ctx:
        s = Stage(nc, ctx, name)
        q = ln_sems(s)
        S1 = s.sb("S1", [128, IT, D])
        S2 = s.sb("S2", [128, IT * 128])
        S1T = s.sb("S1T", [128, IT, 128])
        S2T = s.sb("S2T", [128, IT, 128])
        al = s.sb("al", [128, IT + 1])
        H = s.sb("H", [128, 2, HALF])
        YT = s.sb("YT", [128, TOK])
        pT = s.ps("pT", [128, 2, 512])
        pW = s.ps("pW", [128, 2, 512])
        pH = s.ps("pH", [128, 2, 512])
        pY = s.ps("pY", [128, 2, 512])
        vch = s.sem("vector_own")
        s_al, s_sg = s.sem("mean_magnitudes"), s.sem("signs")
        s_wt, s_ws, s_h, s_g = s.sem("signs_transposed"), s.sem("weights_ready"), s.sem("hidden"), s.sem("gelu")
        s_y, s_yt, s_yy = s.sem("outT_psum"), s.sem("outT_sbuf"), s.sem("out")

        with nc.Block(no_gpsimd_drain=True) as block:

            @block.gpsimd
            def _(pool):
                ln_gpsimd(nc, pool, m, q)

            @block.vector
            def _(dve):
                chain = Chain(dve, vch)
                dve.wait_ge(m.loaded[name], m.load_total[name])
                nc.vector.tensor_reduce(al[:, 0:IT], w["f31"][:, :, :], AX.X, ALU.add, apply_absolute_value=True)
                chain.then(nc.vector.tensor_reduce(al[:, IT:IT + 1], w["f32"][:, :], AX.X, ALU.add,
                                                   apply_absolute_value=True))
                nc.vector.tensor_scalar(al[:, 0:IT], al[:, 0:IT], 1.0 / D, None, ALU.mult)
                nc.vector.tensor_scalar(al[:, IT:IT + 1], al[:, IT:IT + 1], 1.0 / (IT * 128), None, ALU.mult)\
                  .then_inc(s_al, 1)
                ln_vector(nc, dve, chain, m, q)
                dve.wait_ge(s_wt, 2)
                nc.vector.tensor_copy(S1T[:, :, :], pW[:, 0, :].rearrange("p (i c) -> p i c", c=128))
                nc.vector.tensor_copy(S2T[:, :, :], pW[:, 1, :].rearrange("p (i c) -> p i c", c=128)).then_inc(s_ws, 1)
                for h in range(2):
                    dve.wait_ge(s_y, IT * (h + 1))
                    nc.vector.tensor_scalar(YT[:, h * HALF:(h + 1) * HALF], pY[:, h, 0:HALF],
                                            al[:, IT:IT + 1], w["f3b2"][:, 0:1], ALU.mult, ALU.add)\
                      .then_inc(s_yt, 1)
                for h in range(2):
                    dve.wait_ge(s_yy, h + 1)
                    x = m.X[:, h * HB:(h + 1) * HB, :]
                    nc.vector.tensor_tensor(x, x, pT[0:T, h, :].rearrange("p (b d) -> p b d", d=D), ALU.add)

            @block.scalar
            def _(act):
                act.wait_ge(m.loaded[name], m.load_total[name])
                nc.scalar.activation(S1[:, :, :], w["f31"][:, :, :], ACT.Sign).then_inc(s_sg, 1)
                nc.scalar.activation(S2[:, :], w["f32"][:, :], ACT.Sign).then_inc(s_sg, 1)
                ln_scalar(nc, act, m, q, [pT[:, 0, :], pT[:, 1, :]])
                act.wait_ge(s_al, 1)
                for n in range(N):
                    act.wait_ge(s_h, n + 1)
                    if n >= 2:
                        act.wait_ge(s_y, n - 1)
                    i = n % IT
                    nc.scalar.activation(H[:, n % 2, :], pH[:, n % 2, 0:HALF], ACT.Gelu,
                                         bias=w["f3b1"][:, i:i + 1], scale=al[:, i:i + 1]).then_inc(s_g, 1)

            @block.tensor
            def _(pe):
                pe.wait_ge(s_sg, 2)
                for i in range(IT):
                    last = nc.tensor.transpose(pW[:, 0, i * 128:(i + 1) * 128], S1[:, i, :], m.ident[:, :])
                last.then_inc(s_wt, 1)
                for i in range(IT):
                    last = nc.tensor.transpose(pW[:, 1, i * 128:(i + 1) * 128], S2[:, i * 128:(i + 1) * 128],
                                               m.ident[:, :])
                last.then_inc(s_wt, 1)
                ln_tensor(nc, pe, m, q, [pT[:, 0, :], pT[:, 1, :]])
                pe.wait_ge(s_ws, 1)
                pe.wait_ge(q.xTs, 2)

                def up(n):
                    if n >= 2:
                        pe.wait_ge(s_g, n - 1)
                    h = n // IT
                    nc.tensor.matmul(pH[:, n % 2, 0:HALF], S1T[:, n % IT, :], m.XNT[:, h * HALF:(h + 1) * HALF],
                                     start=True, stop=True).then_inc(s_h, 1)

                up(0)
                for n in range(N):
                    if n + 1 < N:
                        up(n + 1)
                    pe.wait_ge(s_g, n + 1)
                    h, i = n // IT, n % IT
                    last = nc.tensor.matmul(pY[:, h, 0:HALF], S2T[:, i, :], H[:, n % 2, :],
                                            start=(i == 0), stop=(i == IT - 1))
                    last.then_inc(s_y, 1)
                for h in range(2):
                    pe.wait_ge(s_yt, h + 1)
                    for i in range(HB):
                        b = h * HB + i
                        last = nc.tensor.transpose(pT[0:T, h, i * D:(i + 1) * D], YT[:, b * T:(b + 1) * T],
                                                   m.ident[:, :])
                    last.then_inc(s_yy, 1)



def ffn_quantised(nc, m):
    name = "L1f"
    w = m.w
    QMAX = 127.0
    ROWS = [128, 128, 96]
    NI = 352
    N = 6
    with ExitStack() as ctx:
        s = Stage(nc, ctx, name)
        q = ln_sems(s)
        ident16 = s.sb("ident16", [128, 128], BF16)
        scw = s.sb("scw", [128, 7])
        inw = s.sb("inw", [128, 7])
        wq = s.sb("wq", [128, 6, 128])
        wqd = s.sb("wqd", [128, NI])
        wq16 = s.sb("wq16", [128, 6, 128], BF16)
        wqd16 = s.sb("wqd16", [128, NI], BF16)
        WT = s.sb("WT", [128, 6, 128], BF16)
        WDT = s.sb("WDT", [128, 3, 128], BF16)
        col = s.sb("col", [128, 16])
        one = s.sb("one", [1, 4])
        XQ = s.sb("XQ", [128, TOK])
        XQ16 = s.sb("XQ16", [128, TOK], BF16)
        SG = s.sb("SG", [128, 2, HALF])
        H = s.sb("H", [128, N, HALF])
        H16 = s.sb("H16", [128, N, HALF], BF16)
        MH = s.sb("MH", [128, N])
        sg = s.sb("sg", [128, 7])
        YT = s.sb("YT", [128, TOK])
        p16 = s.ps("p16", [128, 2, 1024], BF16)
        pT = s.ps("pT", [128, 2, 512])
        pG = s.ps("pG", [128, 2, 512])
        pU = s.ps("pU", [128, 2, 512])
        vch = s.sem("vector_own")
        s_id, s_q16, s_wt, s_wts = s.sem("ident_bf16"), s.sem("weights_rounded"), s.sem("weights_transposed"), s.sem("weights_sbuf")
        s_cl, s_ce = s.sem("clips_spread"), s.sem("exp_of_clips")
        s_m, s_mt, s_m1, s_mb = s.sem("token_max"), s.sem("max_as_row"), s.sem("overall_max"), s.sem("max_spread")
        s_xq, s_gu, s_si, s_h = s.sem("x_rounded"), s.sem("gate_up"), s.sem("silu"), s.sem("hidden")
        s_hr, s_hq = s.sem("hidden_scaled"), s.sem("hidden_rounded")
        s_y, s_yt, s_yy = s.sem("outT_psum"), s.sem("outT_sbuf"), s.sem("out")
        src = [(w["f1g"], i) for i in range(3)] + [(w["f1u"], i) for i in range(3)]

        def tile(buf, k):
            return buf[0:ROWS[k % 3], k, :]

        with nc.Block(no_gpsimd_drain=True) as block:

            @block.gpsimd
            def _(pool):
                ln_gpsimd(nc, pool, m, q)
                for n in range(N):
                    pool.wait_ge(s_hr, n + 1)
                    r = ROWS[n % 3]
                    nc.gpsimd.tensor_scalar(H16[0:r, n, :], H[0:r, n, :], ROUND, None, ALU.subtract)\
                      .then_inc(s_hq, 1)

            @block.vector
            def _(dve):
                chain = Chain(dve, vch)
                nc.vector.tensor_copy(ident16[:, :], m.ident[:, :]).then_inc(s_id, 1)
                chain.then(nc.vector.memset(scw[:, :], 1.0))
                chain.then(nc.vector.memset(MH[:, :], 0.0))
                dve.wait_ge(m.loaded[name], m.load_total[name])
                for k, (buf, i) in enumerate(src):
                    r = ROWS[i]
                    nc.vector.tensor_reduce(scw[0:r, k:k + 1], buf[0:r, i, :], AX.X, ALU.max,
                                            apply_absolute_value=True)
                chain.then(nc.vector.tensor_reduce(scw[:, 6:7], w["f1d"][:, :], AX.X, ALU.max,
                                                   apply_absolute_value=True))
                chain.then(nc.vector.tensor_scalar(scw[:, :], scw[:, :], 1.0 / QMAX, None, ALU.mult))
                chain.then(nc.vector.reciprocal(inw[:, :], scw[:, :]))

                def clip_above(dst, val, inv):
                    return nc.vector.tensor_scalar(dst, val, inv, QMAX, ALU.mult, ALU.min)

                def clip_below_and_round(dst):
                    return nc.vector.tensor_scalar(dst, dst, -QMAX - 1.0, ROUND, ALU.max, ALU.add)

                def integer(out, dst):
                    return nc.vector.tensor_scalar(out, dst, ROUND, None, ALU.subtract)

                weights = [(tile(wq, k), buf[0:ROWS[i], i, :], inw[0:ROWS[i], k:k + 1], tile(wq16, k))
                           for k, (buf, i) in enumerate(src)]
                weights.append((wqd[:, :], w["f1d"][:, :], inw[:, 6:7], wqd16[:, :]))
                for dst, val, inv, out in weights:
                    last = clip_above(dst, val, inv)
                chain.then(last)
                for dst, val, inv, out in weights:
                    last = clip_below_and_round(dst)
                chain.then(last)
                for dst, val, inv, out in weights:
                    last = integer(out, dst)
                chain.then(last)
                nc.vector.tensor_copy(scw[:, :], scw[:, :]).then_inc(s_q16, 1)
                ln_vector(nc, dve, chain, m, q)
                dve.wait_ge(q.norm, B)
                nc.vector.tensor_reduce(col[0:T, 0:1], m.XN[:, :, :], AX.XY, ALU.max,
                                        apply_absolute_value=True).then_inc(s_m, 1)
                dve.wait_ge(s_wt, 1)
                for k in range(6):
                    nc.vector.tensor_copy(WT[:, k, 0:ROWS[k % 3]], p16[:, 0, k * 128:k * 128 + ROWS[k % 3]])
                for i in range(3):
                    last = nc.vector.tensor_copy(WDT[0:ROWS[i], i, :], p16[0:ROWS[i], 1, i * 128:(i + 1) * 128])
                last.then_inc(s_wts, 1)
                dve.wait_ge(s_ce, 1)
                chain.then(nc.vector.tensor_scalar(col[:, 1:3], col[:, 1:3], 1.0, None, ALU.add))
                chain.then(nc.vector.reciprocal(col[:, 1:3], col[:, 1:3]))
                chain.then(nc.vector.tensor_scalar(col[:, 1:3], col[:, 1:3], 1.0 / QMAX, None, ALU.mult))

                def overall(i):
                    dve.wait_ge(s_mt, i + 1)
                    nc.vector.tensor_reduce(one[0:1, i:i + 1], pU[0:1, 0, 0:128 if i else T], AX.X,
                                            ALU.max).then_inc(s_m1, 1)
                    dve.wait_ge(s_mb, i + 1)
                    chain.then(nc.vector.tensor_tensor(col[:, 3 + 2 * i:4 + 2 * i], pU[:, 1, 0:1],
                                                       col[:, 1 + i:2 + i], ALU.mult))
                    chain.then(nc.vector.reciprocal(col[:, 4 + 2 * i:5 + 2 * i], col[:, 3 + 2 * i:4 + 2 * i]))

                overall(0)
                nc.vector.tensor_scalar(sg[:, 0:6], scw[:, 0:6], col[:, 3:4], None, ALU.mult)
                dve.wait_ge(q.xTs, 2)
                chain.then(clip_above(XQ[:, :], m.XNT[:, :], col[:, 4:5]))
                chain.then(clip_below_and_round(XQ[:, :]))
                chain.then(integer(XQ16[:, :], XQ[:, :]))
                nc.vector.tensor_copy(col[:, 10:11], col[:, 4:5]).then_inc(s_xq, 1)
                for n in range(N):
                    r, k = ROWS[n % 3], n % 3
                    dve.wait_ge(s_si, n + 1)
                    ins = nc.vector.scalar_tensor_tensor(
                        out=H[0:r, n, :], in0=pU[0:r, n % 2, 0:HALF], scalar=sg[0:r, 3 + k:4 + k],
                        in1=SG[0:r, n % 2, :], op0=ALU.mult, op1=ALU.mult)
                    ins.then_inc(s_h, 1)
                    dve.wait_ge(s_h, n + 1)
                    last = nc.vector.tensor_reduce(MH[0:r, n:n + 1], H[0:r, n, :], AX.X, ALU.max,
                                                   apply_absolute_value=True)
                chain.then(last)
                nc.vector.tensor_reduce(col[:, 0:1], MH[:, :], AX.X, ALU.max).then_inc(s_m, 1)
                overall(1)
                for n in range(N):
                    r = ROWS[n % 3]
                    chain.then(clip_above(H[0:r, n, :], H[0:r, n, :], col[0:r, 6:7]))
                    clip_below_and_round(H[0:r, n, :]).then_inc(s_hr, 1)
                chain.then(nc.vector.tensor_tensor(sg[:, 6:7], scw[:, 6:7], col[:, 5:6], ALU.mult))
                for h in range(2):
                    dve.wait_ge(s_y, h + 1)
                    nc.vector.tensor_scalar(YT[:, h * HALF:(h + 1) * HALF], pG[:, h, 0:HALF], sg[:, 6:7],
                                            None, ALU.mult).then_inc(s_yt, 1)
                for h in range(2):
                    dve.wait_ge(s_yy, h + 1)
                    x = m.X[:, h * HB:(h + 1) * HB, :]
                    nc.vector.tensor_tensor(x, x, pT[0:T, h, :].rearrange("p (b d) -> p b d", d=D), ALU.add)

            @block.scalar
            def _(act):
                act.wait_ge(s_cl, 1)
                nc.scalar.activation(col[:, 1:3], pU[:, 0, 128:130], ACT.Exp, scale=-1.0).then_inc(s_ce, 1)
                ln_scalar(nc, act, m, q, [pT[:, 0, :], pT[:, 1, :]])
                act.wait_ge(s_xq, 1)
                for n in range(N):
                    r, k = ROWS[n % 3], n % 3
                    act.wait_ge(s_gu, n + 1)
                    if n >= 2:
                        act.wait_ge(s_h, n - 1)
                    nc.scalar.activation(SG[0:r, n % 2, :], pG[0:r, n % 2, 0:HALF], ACT.Silu,
                                         scale=sg[0:r, k:k + 1]).then_inc(s_si, 1)

            @block.tensor
            def _(pe):
                pe.wait_ge(m.loaded[name], m.load_total[name])
                nc.tensor.matmul(pU[:, 0, 128:130], m.ones[0:1, 0:128], w["f1c"][0:1, :], start=True, stop=True)\
                  .then_inc(s_cl, 1)
                pe.wait_ge(s_id, 1)
                pe.wait_ge(s_q16, 1)
                for k in range(6):
                    r = ROWS[k % 3]
                    nc.tensor.transpose(p16[:, 0, k * 128:k * 128 + r], tile(wq16, k), ident16[0:r, 0:r])
                for i in range(3):
                    last = nc.tensor.transpose(p16[0:ROWS[i], 1, i * 128:(i + 1) * 128],
                                               wqd16[:, i * 128:i * 128 + ROWS[i]], ident16[:, :])
                last.then_inc(s_wt, 1)
                ln_tensor(nc, pe, m, q, [pT[:, 0, :], pT[:, 1, :]])

                def overall(i):
                    n = 128 if i else T
                    pe.wait_ge(s_m, i + 1)
                    if i == 0:
                        pe.wait_ge(s_ce, 1)
                    nc.tensor.transpose(pU[0:1, 0, 0:n], col[0:n, 0:1], m.ident[0:n, 0:n]).then_inc(s_mt, 1)
                    pe.wait_ge(s_m1, i + 1)
                    nc.tensor.matmul(pU[:, 1, 0:1], m.ones[0:1, 0:128], one[0:1, i:i + 1], start=True,
                                     stop=True).then_inc(s_mb, 1)

                overall(0)
                pe.wait_ge(s_wts, 1)
                pe.wait_ge(s_xq, 1)
                for n in range(N):
                    r, k, h = ROWS[n % 3], n % 3, n // 3
                    if n >= 2:
                        pe.wait_ge(s_h, n - 1)
                    x = XQ16[:, h * HALF:(h + 1) * HALF]
                    nc.tensor.matmul(pG[0:r, n % 2, 0:HALF], WT[:, k, 0:r], x, start=True, stop=True)
                    nc.tensor.matmul(pU[0:r, n % 2, 0:HALF], WT[:, 3 + k, 0:r], x, start=True, stop=True)\
                      .then_inc(s_gu, 1)
                overall(1)
                for h in range(2):
                    for k in range(3):
                        n, r = 3 * h + k, ROWS[k]
                        pe.wait_ge(s_hq, n + 1)
                        last = nc.tensor.matmul(pG[:, h, 0:HALF], WDT[0:r, k, :], H16[0:r, n, :],
                                                start=(k == 0), stop=(k == 2))
                    last.then_inc(s_y, 1)
                for h in range(2):
                    pe.wait_ge(s_yt, h + 1)
                    for i in range(HB):
                        b = h * HB + i
                        last = nc.tensor.transpose(pT[0:T, h, i * D:(i + 1) * D], YT[:, b * T:(b + 1) * T],
                                                   m.ident[:, :])
                    last.then_inc(s_yy, 1)



NAMES = ['x', 'ctx_1024', 'L0_attn_Wq', 'L0_attn_Wk', 'L0_attn_Wv', 'L0_attn_Wo', 'L0_xattn_Wq', 'L0_xattn_Wk', 'L0_xattn_Wv', 'L0_xattn_gru_wih', 'L0_xattn_gru_whh', 'L0_xattn_gru_bih', 'L0_xattn_gru_bhh', 'L0_xattn_slot_norm_w', 'L0_xattn_input_norm_w', 'L0_ffn_Wg', 'L0_ffn_Wu', 'L0_ffn_Wd', 'L0_ffn_Wr', 'L0_ffn_temperature', 'L1_attn_w_qkvw', 'L1_attn_w_out', 'L1_xattn_Wq', 'L1_xattn_bq', 'L1_xattn_Wk', 'L1_xattn_bk', 'L1_xattn_Wv', 'L1_xattn_bv', 'L1_xattn_Wo', 'L1_xattn_bo', 'L1_ffn_clip_x', 'L1_ffn_clip_down', 'L1_ffn_w_gate', 'L1_ffn_w_up', 'L1_ffn_w_down', 'L2_attn_w_fc', 'L2_attn_w_proj', 'L2_attn_ln_g', 'L2_attn_ln_b', 'L2_xattn_Wk', 'L2_xattn_Wq', 'L2_xattn_Wv', 'L2_ffn_gate_weight', 'L2_ffn_ln_gamma', 'L2_ffn_ln_beta', 'L2_ffn_wi', 'L2_ffn_wo', 'L3_attn_Wk', 'L3_attn_bk', 'L3_attn_Wv', 'L3_attn_bv', 'L3_attn_Wq', 'L3_attn_bq', 'L3_attn_gamma', 'L3_attn_beta', 'L3_xattn_Wq', 'L3_xattn_Wk', 'L3_xattn_Wv', 'L3_xattn_Wo', 'L3_ffn_w1', 'L3_ffn_b1', 'L3_ffn_w2', 'L3_ffn_b2']

SUBLAYERS = [1, 2, 3, 4, 5, 6, 7, 8, 9, 10, 11, 12]


def decoder(nc, a, out):
    with ExitStack() as ctx:
        def sb(name, shape, dt=F32):
            return ctx.enter_context(nc.sbuf_tensor(name, shape, dt))

        def sem(name):
            return ctx.enter_context(nc.semaphore(name))

        m = Names()
        m.X = sb("X", [T, B, D])
        m.XN = sb("XN", [T, B, D])
        m.XNT = sb("XNT", [128, TOK])
        m.XN2 = sb("XN2", [T, B, D])
        m.stats = sb("stats", [T, B, 6])
        m.mv = sb("mv", [T, B, 2])
        m.veps = sb("veps", [T, 2, B])
        m.rstd = sb("rstd", [T, 2, B])
        m.ident = sb("ident", [128, 128])
        m.ones = sb("ones", [128, 512])
        m.neg_half = sb("neg_half", [128, 96])
        m.mask = sb("mask", [T, 2, NJ * T])
        m.order = sb("order", [T, B, NE])
        m.before = sb("before", [T, T])
        m.below = sb("below", [128, 8, 128])
        m.cols = sb("cols", [128, NCOLS])
        m.mcols = sb("mcols", [128, NCOLS - 4])
        m.sel = sb("sel", [8, 8, 128])
        m.ctx_tm = sb("ctx_tm", [128, B, NKT, D + 1])
        m.ctx_r = sb("ctx_r", [128, B, NKT])
        m.CT = sb("CT", [128, B, NKT * 128])
        m.loaded, m.load_total = {}, {}
        w = {}
        specs = []

        def want(stage, key, shape, src, slot=None, part=None):
            if slot is not None:
                part = (slice(None), slice(slot, slot + 1))
            specs.append((stage, key, shape, src, part if part is not None else slice(None)))

        def row(v):
            return v.rearrange("(a n) -> a n", a=1)

        want_all(a, want, row)
        order = []
        for spec in specs:
            if spec[0] not in order:
                order.append(spec[0])
        held = {stage: ctx.enter_context(ExitStack()) for stage in reversed(order)}
        for stage in reversed(order):
            for st, key, shape, _, _ in specs:
                if st == stage and shape is not None:
                    w[key] = held[stage].enter_context(nc.sbuf_tensor("w_" + key, shape, F32))
        loads = [(stage, w[key][part], src) for stage, key, _, src, part in specs]
        for stage in order:
            m.loaded[stage] = sem("loaded_" + stage)
            m.load_total[stage] = 16 * sum(spec[0] == stage for spec in specs)
        m.w = w
        m.loads = loads
        m.a = a
        m.x_loaded = sem("x_loaded")
        m.stored = sem("result_stored")
        m.padded = sem("context_padded")
        m.ctx_loaded = [sem(f"ctx_loaded_{b}") for b in range(B)]
        first_block(nc, m, a["x"])
        n = SUBLAYERS
        old_CT = m.CT[:, :, :].rearrange("p b k -> p (b k)")
        old_ctx = m.ctx_tm[:, :, :, :].rearrange("p b k d -> p (b k d)")
        if 1 in n:
            attention16(nc, m, "L0a", w["a0q"][:, :], w["a0k"][:, :], w["a0v"][:, :], w["a0o"][:, :], old_CT,
                        beside=(other_loads, other_tables))
        held["L0a"].close()
        if 2 in n:
            context_block(nc, m, "ctxn", True)
            slot_attention(nc, m)
        held["L0x"].close()
        if 3 in n:
            mixture_golden(nc, m)
        held["L0f"].close()
        if 4 in n:
            attention_regrouped(nc, m)
        held["L1a"].close()
        if 5 in n:
            attention16(nc, m, "L1x", w["x1q"][:, :], w["x1k"][:, :], w["x1v"][:, :], w["x1o"][:, :], old_CT,
                        keys="causal", bias=(w["x1bq"], w["x1bk"], w["x1bv"], w["x1bo"]))
        held["L1x"].close()
        if set(n) & {8, 11}:
            context_block(nc, m, "ctxr", False)
        if 6 in n:
            ffn_quantised(nc, m)
        held["L1f"].close()
        if 7 in n:
            attention_fixed_keys(nc, m)
        held["L2a"].close()
        if 8 in n:
            attention_wide(nc, m)
        held["L2x"].close()
        if 9 in n:
            mixture_top1(nc, m)
        held["L2f"].close()
        if 10 in n:
            attention_delta_rule(nc, m)
        held["L3a"].close()
        if 11 in n:
            attention16(nc, m, "L3x", w["x3q"][:, :], w["x3k"][:, :], w["x3v"][:, :], w["x3o"][:, :], old_ctx,
                        weights_natural=True, keys="context")
        held["L3x"].close()
        if 12 in n:
            ffn_binary(nc, m)
        held["L3f"].close()
        store_block(nc, m, out)


def want_all(a, want, row):
    want("L0a", "a0q", [128, 128], a["L0_attn_Wq"])
    want("L0a", "a0k", [32, 128], a["L0_attn_Wk"])
    want("L0a", "a0v", [32, 128], a["L0_attn_Wv"])
    want("L0a", "a0o", [128, 128], a["L0_attn_Wo"])
    want("L0x", "x0q", [128, 128], a["L0_xattn_Wq"])
    want("L0x", "x0k", [128, 128], a["L0_xattn_Wk"])
    want("L0x", "x0v", [128, 128], a["L0_xattn_Wv"])
    want("L0x", "x0ih", [128, 3, 128], a["L0_xattn_gru_wih"].rearrange("(c p) d -> p c d", p=128))
    want("L0x", "x0hh", [128, 3, 128], a["L0_xattn_gru_whh"].rearrange("(c p) d -> p c d", p=128))
    want("L0x", "x0bi", [1, 384], row(a["L0_xattn_gru_bih"]))
    want("L0x", "x0bh", [1, 384], row(a["L0_xattn_gru_bhh"]))
    want("L0x", "x0sw", [128, 1], a["L0_xattn_slot_norm_w"].rearrange("(p a) -> p a", a=1))
    want("L0x", "x0iw", [128, 1], a["L0_xattn_input_norm_w"].rearrange("(p a) -> p a", a=1))
    want("L0f", "f0t", [1, 1], row(a["L0_ffn_temperature"]))
    want("L0f", "f0r", [128, NE], a["L0_ffn_Wr"])
    want("L0f", "f0g", [128, NE, 128], a["L0_ffn_Wg"].rearrange("e d i -> d e i"))
    want("L0f", "f0u", [128, NE, 128], a["L0_ffn_Wu"].rearrange("e d i -> d e i"))
    want("L0f", "f0d", [128, NE, 128], a["L0_ffn_Wd"].rearrange("e i d -> i e d"))
    want("L1a", "a1w", [128, 512], a["L1_attn_w_qkvw"])
    want("L1a", "a1o", [128, 128], a["L1_attn_w_out"])
    for key, src in (("q", "Wq"), ("k", "Wk"), ("v", "Wv"), ("o", "Wo")):
        want("L1x", "x1" + key, [128, 128], a["L1_xattn_" + src])
        want("L1x", "x1b" + key, [1, 128], row(a["L1_xattn_b" + key]))

    def column(v, p=128):
        return v.rearrange("(c p) -> p c", p=p)

    for key, src in (("f1g", "w_gate"), ("f1u", "w_up")):
        v = a["L1_ffn_" + src]
        want("L1f", key, [128, 3, 128], v[0:256, :].rearrange("(i p) d -> p i d", p=128),
             part=(slice(0, 128), slice(0, 2)))
        want("L1f", key, None, v[256:352, :], part=(slice(0, 96), 2))
    want("L1f", "f1d", [128, 352], a["L1_ffn_w_down"])
    want("L1f", "f1c", [1, 2], row(a["L1_ffn_clip_x"]), slot=0)
    want("L1f", "f1c", None, row(a["L1_ffn_clip_down"]), slot=1)
    want("L2a", "a2f", [128, 128], a["L2_attn_w_fc"])
    want("L2a", "a2p", [128, 128], a["L2_attn_w_proj"])
    want("L2a", "a2g", [128, 1], column(a["L2_attn_ln_g"]))
    want("L2a", "a2b", [128, 1], column(a["L2_attn_ln_b"]))
    want("L2x", "x2q", [128, 128], a["L2_xattn_Wq"])
    want("L2x", "x2k", [128, 128], a["L2_xattn_Wk"])
    want("L2x", "x2v", [128, 128], a["L2_xattn_Wv"])
    want("L2f", "f2r", [NE, 128], a["L2_ffn_gate_weight"])
    want("L2f", "f2g", [128, 1], column(a["L2_ffn_ln_gamma"]))
    want("L2f", "f2b", [128, 1], column(a["L2_ffn_ln_beta"]))
    want("L3a", "a3k", [DS, 128], a["L3_attn_Wk"])
    want("L3a", "a3q", [DS, 128], a["L3_attn_Wq"])
    want("L3a", "a3v", [128, 128], a["L3_attn_Wv"])
    want("L3a", "a3bk", [DS, 1], column(a["L3_attn_bk"], DS))
    want("L3a", "a3bq", [DS, 1], column(a["L3_attn_bq"], DS))
    want("L3a", "a3bv", [1, 128], row(a["L3_attn_bv"]))
    want("L3a", "a3g", [128, 1], column(a["L3_attn_gamma"]))
    want("L3a", "a3b", [128, 1], column(a["L3_attn_beta"]))
    for key, src, f in (("q", "Wq", 128), ("k", "Wk", 32), ("v", "Wv", 32), ("o", "Wo", 128)):
        want("L3x", "x3" + key, [128, f], a["L3_xattn_" + src])
    want("L3f", "f31", [128, 4, 128], a["L3_ffn_w1"].rearrange("(i p) d -> p i d", p=128))
    want("L3f", "f32", [128, 512], a["L3_ffn_w2"])
    want("L3f", "f3b1", [128, 4], column(a["L3_ffn_b1"][0:128]), slot=0)
    for i in range(1, 4):
        want("L3f", "f3b1", None, column(a["L3_ffn_b1"][i * 128:(i + 1) * 128]), slot=i)
    want("L3f", "f3b2", [128, 1], column(a["L3_ffn_b2"]))


def first_block(nc, m, x):
    with ExitStack() as ctx:
        s = Stage(nc, ctx, "first")
        brow = s.sb("brow", [1, NCOLS, 128])
        pc = s.ps("columns", [128, NCOLS])
        s_set = s.sem("cleared")
        s_row, s_row1, s_col, s_c = s.sem("rows_cleared"), s.sem("rows"), s.sem("columns_psum"), s.sem("columns")
        with nc.Block(no_gpsimd_drain=True) as block:

            @block.sync
            def _(sp):
                sp.dma_start(m.X[:, :, :], x.rearrange("b t d -> t b d")).then_inc(m.x_loaded, 16)
                for stage, dst, src in m.loads:
                    if stage == "L0a":
                        sp.dma_start(dst, src).then_inc(m.loaded[stage], 16)

            @block.vector
            def _(dve):
                nc.vector.memset(m.ones[:, :], 1.0)
                nc.vector.memset(brow[:], 0.0).then_inc(s_row, 1)
                dve.wait_ge(s_row, 1)
                term_rows(nc, brow).then_inc(s_row1, 1)
                nc.vector.memset(m.ctx_tm[:, :, KT_FULL, :], 0.0).then_inc(m.padded, 1)
                dve.wait_ge(m.padded, 1)
                nc.vector.memset(m.ctx_tm[:, :, :, D], 1.0).then_inc(m.padded, 1)
                dve.wait_ge(s_col, 1)
                nc.vector.tensor_copy(m.cols[:, :], pc[:, :]).then_inc(s_c, 1)
                dve.wait_ge(s_c, 1)
                bias_times_mask(nc, m.mcols, m.cols)
                dve.wait_ge(m.x_loaded, 16)

            @block.tensor
            def _(pe):
                pe.wait_ge(s_row1, 1)
                for i in range(NCOLS):
                    last = nc.tensor.matmul(pc[:, i:i + 1], brow[0:1, i, :], m.ones[0:1, 0:1],
                                            start=(i == 0), stop=True, skip_group_check=True)
                last.then_inc(s_col, 1)

            @block.gpsimd
            def _(pool):
                nc.gpsimd.memset(m.neg_half[:, :], -0.5)
                nc.gpsimd.memset(m.ident[:, :], 0.0).then_inc(s_set, 1)
                pool.wait_ge(s_set, 1)
                nc.gpsimd.affine_select(out=m.ident[:, :], in_=m.ident[:, :], compare_op=ALU.not_equal,
                                        fill=1.0, base=0, pattern=[[-1, 128]], channel_multiplier=1)


def other_loads(sp, m):
    sp.wait_ge(m.padded, 2)
    for b in range(B):
        load_context(sp, m, b)
    for stage, dst, src in m.loads:
        if stage != "L0a":
            sp.dma_start(dst, src).then_inc(m.loaded[stage], 16)


def other_tables(nc, pool, m, s_set):
    nc.gpsimd.memset(m.mask[:, :, :], 0.0)
    nc.gpsimd.memset(m.sel[:, :, :], 0.0)
    nc.gpsimd.memset(m.before[:, :], 1.0)
    nc.gpsimd.memset(m.below[:, :, :], 0.0).then_inc(s_set, 1)
    for e in range(NE):
        last = nc.gpsimd.memset(m.order[:, :, e], float(NE - e))
    last.then_inc(s_set, 1)
    pool.wait_ge(s_set, 2)
    nc.gpsimd.affine_select(out=m.mask[:, 0, :], in_=m.mask[:, 0, :], compare_op=ALU.is_ge,
                            fill=-1e30, base=0, pattern=[[0, NJ], [-1, T]],
                            channel_multiplier=1)
    nc.gpsimd.affine_select(out=m.mask[:, 1, :], in_=m.mask[:, 1, :], compare_op=ALU.is_ge,
                            fill=-1e30, base=0, pattern=[[0, NG], [1, T]],
                            channel_multiplier=-1)
    nc.gpsimd.affine_select(out=m.sel[:, :, :], in_=m.sel[:, :, :], compare_op=ALU.not_equal,
                            fill=1.0, base=0, pattern=[[-1, 8], [0, 128]],
                            channel_multiplier=1).then_inc(s_set, 1)
    nc.gpsimd.affine_select(out=m.before[:, :], in_=m.before[:, :], compare_op=ALU.is_ge,
                            fill=0.0, base=-1, pattern=[[1, T]], channel_multiplier=-1)
    n = 3
    for i, sz in [(0, 1)] + [(k + 1, v) for k, v in enumerate(LEVELS)]:
        blocks = 128 // (2 * sz)
        cols = slice(0, sz) if i == 0 else slice(sz, 2 * sz)
        lo = sz if i == 0 else 0
        kept = [p for p in ([2 * sz, blocks], [0, sz]) if p[1] > 1]
        v = m.below[:, i, :].rearrange("p (k c) -> p k c", c=2 * sz)[:, :, cols]
        pool.wait_ge(s_set, n)
        nc.gpsimd.memset(v, TTT_LR).then_inc(s_set, 1)
        pool.wait_ge(s_set, n + 1)
        nc.gpsimd.affine_select(out=v, in_=v, compare_op=ALU.is_ge, fill=0.0, base=-lo,
                                pattern=[[-p[0], p[1]] for p in kept], channel_multiplier=1)\
            .then_inc(s_set, 1)
        pool.wait_ge(s_set, n + 2)
        nc.gpsimd.affine_select(out=v, in_=v, compare_op=ALU.is_ge, fill=0.0, base=lo + sz - 1,
                                pattern=kept, channel_multiplier=-1)\
            .then_inc(s_set, 1)
        n += 3
    pool.wait_ge(s_set, n)


def store_block(nc, m, out):
    with nc.Block(no_gpsimd_drain=True) as block:

        @block.sync
        def _(sp):
            for stage in m.loaded:
                sp.wait_ge(m.loaded[stage], m.load_total[stage])
            for b in range(B):
                sp.wait_ge(m.ctx_loaded[b], 32)
            sp.dma_start(out.rearrange("b t d -> t b d"), m.X[:, :, :]).then_inc(m.stored, 16)
            sp.wait_ge(m.stored, 16)



def kernel(**inputs):
    import numpy as _np
    import concourse.bacc as _bacc
    from concourse.bass_utils import run_bass_kernel_spmd as _run

    nc = _bacc.Bacc("TRN2", target_bir_lowering=False, num_devices=1)
    arrays, args = {}, {}
    for name in NAMES:
        arr = _np.ascontiguousarray(inputs[name])
        arrays[f"in_{name}"] = arr
        args[name] = nc.dram_tensor(f"in_{name}", arr.shape, mybir.dt.from_np(arr.dtype), kind="ExternalInput").ap()
    out = nc.dram_tensor("decoded", (B, T, D), F32, kind="ExternalOutput").ap()
    decoder(nc, args, out)
    r = _run(nc, [arrays], core_ids=[0])
    return r.results[0]["decoded"]
```
